# Optimizing a Trainium2 kernel written in Bass

```python
import numpy as np
import jax
import jax.numpy as jnp

def _softmax(x, axis=-1):
    return jax.nn.softmax(x, axis=axis)

def _gelu(x):
    return jax.nn.gelu(x, approximate=True)

def _silu(x):
    return jax.nn.silu(x)

def _sigmoid(x):
    return jax.nn.sigmoid(x)

def _layernorm(x, axis=-1, eps=1e-05):
    m = jnp.mean(x, axis=axis, keepdims=True)
    v = jnp.var(x, axis=axis, keepdims=True)
    return (x - m) / jnp.sqrt(v + eps)

def _scatter_add(tgt, idx, src, axis=0):
    return tgt.at[idx].add(src)

def _segment_sum(src, seg, n):
    return jax.ops.segment_sum(src, seg, n)
kernel_name = 'mk_decoder_postln_d4_seqx_r8_5be4a2'

def setup_inputs(seed: int=0):
    np.random.seed(seed)
    _w = jnp.asarray

    def _rec_inputs():
        import jax
        import jax.numpy as jnp
        _rk = jax.random.key(seed)
        x = -0.0005146 + 1 * jax.random.normal(jax.random.fold_in(_rk, 1), (4, 256, 128), jnp.float32)
        _lenS = 256 - jax.random.randint(jax.random.fold_in(_rk, 7), (4,), 0, max(1, 256 // 4) + 1, jnp.int32)
        _lenS2 = 512 - jax.random.randint(jax.random.fold_in(_rk, 8), (4,), 0, max(1, 512 // 4) + 1, jnp.int32)
        _ctx_1024P = jax.random.normal(jax.random.fold_in(_rk, 11), (4, 16, 128), jnp.float32)
        _ctx_1024c = jax.random.dirichlet(jax.random.fold_in(_rk, 511), 0.3 * jnp.ones((16,), jnp.float32), (4, 512))
        _ctx_1024t = jnp.einsum('bsk,bkd->bsd', _ctx_1024c, _ctx_1024P)
        _ctx_1024t = _ctx_1024t * jax.lax.rsqrt(jnp.mean(jnp.square(_ctx_1024t)) + 1e-12) * 0.953939
        ctx_1024 = -0.000125008 + 0.999885 * (_ctx_1024t + 0.3 * jax.random.normal(jax.random.fold_in(_rk, 611), (4, 512, 128), jnp.float32))
        _validS = jnp.arange(256)[None, :] < _lenS[:, None]
        _validS2 = jnp.arange(512)[None, :] < _lenS2[:, None]
        _causal = jnp.tril(jnp.ones((256, 256), dtype=bool))
        mask_BxS2_bf1 = jnp.ones((4, 512), dtype=bool)
        return (x, ctx_1024, mask_BxS2_bf1)
    x, ctx_1024, mask_BxS2_bf1 = _rec_inputs()

    def _L0_attn_setup():
        import jax, jax.numpy as jnp
        import numpy as np
        DIM = 128
        NUM_HEADS = 16
        HEAD_DIM = DIM // NUM_HEADS
        LATENT = 128
        Q_RANK = 32
        B, S = (4, 256)
        key = jax.random.key(seed)
        ks = jax.random.split(key, 12)
        w = lambda k, shape: jax.random.normal(k, shape, dtype=jnp.float32) * 0.02
        x = jax.random.normal(ks[0], (B, S, DIM), dtype=jnp.float32)
        mask = jnp.tril(jnp.ones((S, S), dtype=jnp.int32))[None, None, :, :]
        return {'x': x, 'mask': mask, 'w_kvc': w(ks[1], (DIM, LATENT)), 'b_kvc': jnp.zeros((LATENT,), jnp.float32), 'w_kvu': w(ks[2], (LATENT, 2 * DIM)), 'b_kvu': jnp.zeros((2 * DIM,), jnp.float32), 'w_qc': w(ks[3], (DIM, Q_RANK)), 'b_qc': jnp.zeros((Q_RANK,), jnp.float32), 'w_qu': w(ks[4], (Q_RANK, DIM)), 'b_qu': jnp.zeros((DIM,), jnp.float32), 'w_o': w(ks[5], (DIM, DIM)), 'b_o': jnp.zeros((DIM,), jnp.float32)}
    _L0_attn_all = _L0_attn_setup()
    _L0_attn_in = {k: v for k, v in _L0_attn_all.items() if k in ('mask', 'w_kvc', 'b_kvc', 'w_kvu', 'b_kvu', 'w_qc', 'b_qc', 'w_qu', 'b_qu', 'w_o', 'b_o')}
    del _L0_attn_all

    def _L0_xattn_setup():
        import jax, jax.numpy as jnp
        import numpy as np
        H, DH = (8, 64)
        EPS = 1e-05

        def _ln(x, g, b):
            m = x.mean(-1, keepdims=True)
            v = ((x - m) ** 2).mean(-1, keepdims=True)
            return (x - m) / jnp.sqrt(v + EPS) * g + b
        key = jax.random.key(seed)
        ks = jax.random.split(key, 5)
        B, N, L, D = (4, 1024, 64, 128)
        inner = H * DH
        return {'x': jax.random.normal(ks[0], (B, N, D), jnp.float32), 'latents': jax.random.normal(ks[1], (B, L, D), jnp.float32), 'mask': jnp.ones((B, N), dtype=bool), 'g_x': jnp.ones((D,), jnp.float32), 'b_x': jnp.zeros((D,), jnp.float32), 'g_l': jnp.ones((D,), jnp.float32), 'b_l': jnp.zeros((D,), jnp.float32), 'w_q': jax.random.normal(ks[2], (D, inner), jnp.float32) * D ** (-0.5), 'w_kv': jax.random.normal(ks[3], (D, 2 * inner), jnp.float32) * D ** (-0.5), 'w_out': jax.random.normal(ks[4], (inner, D), jnp.float32) * inner ** (-0.5), 'g_o': jnp.ones((D,), jnp.float32), 'b_o': jnp.zeros((D,), jnp.float32)}
    _L0_xattn_all = _L0_xattn_setup()
    _L0_xattn_in = {k: v for k, v in _L0_xattn_all.items() if k in ('g_x', 'b_x', 'g_l', 'b_l', 'w_q', 'w_kv', 'w_out', 'g_o', 'b_o')}
    del _L0_xattn_all

    def _L0_ffn_setup():
        import jax, jax.numpy as jnp
        import numpy as np
        IN_DIM = 128
        OUT_DIM = 128
        NUM_EXPERTS = 8
        TOP_K = 2
        key = jax.random.key(seed)
        ks = jax.random.split(key, 5)
        s = 1.0 / np.sqrt(IN_DIM)
        x = jax.random.normal(ks[0], (4, 256, IN_DIM), dtype=jnp.float32)
        Wg = jax.random.uniform(ks[1], (IN_DIM, NUM_EXPERTS), jnp.float32, -s, s)
        bg = jnp.zeros((NUM_EXPERTS,), jnp.float32)
        We = jax.random.uniform(ks[2], (NUM_EXPERTS, OUT_DIM, IN_DIM), jnp.float32, -s, s)
        be = jax.random.uniform(ks[3], (NUM_EXPERTS, OUT_DIM), jnp.float32, -s, s)
        return {'x': x, 'Wg': Wg, 'bg': bg, 'We': We, 'be': be}
    _L0_ffn_all = _L0_ffn_setup()
    _L0_ffn_in = {k: v for k, v in _L0_ffn_all.items() if k in ('Wg', 'bg', 'We', 'be')}
    del _L0_ffn_all

    def _L1_attn_setup():
        import jax, jax.numpy as jnp
        import numpy as np
        import math
        EMBED_DIM = 128
        NUM_HEADS = 16
        NUM_KV_HEADS = 16
        DEPTH = 12
        HEAD_DIM = EMBED_DIM // NUM_HEADS // 2
        LAMBDA_INIT = 0.8 - 0.6 * math.exp(-0.3 * DEPTH)
        EPS = 1e-05
        THETA = 0.0001

        def rope(q):
            b, s, h, d = q.shape
            pos = jnp.arange(s, dtype=jnp.float32)[:, None]
            freq = 1.0 / THETA ** (2.0 * jnp.arange(d // 2, dtype=jnp.float32) / d)
            ang = pos * freq
            cos = jnp.cos(ang)[None, :, None, :].astype(q.dtype)
            sin = jnp.sin(ang)[None, :, None, :].astype(q.dtype)
            qr = q.reshape(b, s, h, d // 2, 2)
            q0, q1 = (qr[..., 0], qr[..., 1])
            out = jnp.stack([q0 * cos - q1 * sin, q0 * sin + q1 * cos], axis=-1)
            return out.reshape(q.shape)
        key = jax.random.key(seed)
        ks = jax.random.split(key, 10)
        d = EMBED_DIM
        sd = 1.0 / math.sqrt(d)
        return {'x': jax.random.normal(ks[0], (1, 256, d), dtype=jnp.float32), 'Wq': jax.random.normal(ks[1], (d, d), dtype=jnp.float32) * sd, 'Wk': jax.random.normal(ks[2], (d, d), dtype=jnp.float32) * sd, 'Wv': jax.random.normal(ks[3], (d, d), dtype=jnp.float32) * sd, 'Wo': jax.random.normal(ks[4], (d, d), dtype=jnp.float32) * sd, 'lambda_q1': jax.random.normal(ks[5], (HEAD_DIM,), dtype=jnp.float32) * 0.1, 'lambda_k1': jax.random.normal(ks[6], (HEAD_DIM,), dtype=jnp.float32) * 0.1, 'lambda_q2': jax.random.normal(ks[7], (HEAD_DIM,), dtype=jnp.float32) * 0.1, 'lambda_k2': jax.random.normal(ks[8], (HEAD_DIM,), dtype=jnp.float32) * 0.1, 'subln_g': jnp.ones((2 * HEAD_DIM,), dtype=jnp.float32)}
    _L1_attn_all = _L1_attn_setup()
    _L1_attn_in = {k: v for k, v in _L1_attn_all.items() if k in ('Wq', 'Wk', 'Wv', 'Wo', 'lambda_q1', 'lambda_k1', 'lambda_q2', 'lambda_k2', 'subln_g')}
    del _L1_attn_all

    def _L1_xattn_setup():
        import jax, jax.numpy as jnp
        import numpy as np
        B, S, DIN, DK, DV = (8, 256, 128, 128, 128)
        key = jax.random.key(seed)
        ks = jax.random.split(key, 9)
        s_in = 1.0 / np.sqrt(DIN)
        return {'query': jax.random.normal(ks[0], (B, S, DIN), jnp.float32), 'key_': jax.random.normal(ks[1], (B, S, DIN), jnp.float32), 'value': jax.random.normal(ks[2], (B, S, DIN), jnp.float32), 'Wq_w': jax.random.uniform(ks[3], (DK, DIN), jnp.float32, -s_in, s_in), 'Wq_b': jax.random.uniform(ks[4], (DK,), jnp.float32, -s_in, s_in), 'Wk_w': jax.random.uniform(ks[5], (DK, DIN), jnp.float32, -s_in, s_in), 'Wk_b': jax.random.uniform(ks[6], (DK,), jnp.float32, -s_in, s_in), 'Wv_w': jax.random.uniform(ks[7], (DV, DIN), jnp.float32, -s_in, s_in), 'Wv_b': jax.random.uniform(ks[8], (DV,), jnp.float32, -s_in, s_in)}
    _L1_xattn_all = _L1_xattn_setup()
    _L1_xattn_in = {k: v for k, v in _L1_xattn_all.items() if k in ('Wq_w', 'Wq_b', 'Wk_w', 'Wk_b', 'Wv_w', 'Wv_b')}
    del _L1_xattn_all

    def _L1_ffn_setup():
        import jax, jax.numpy as jnp
        import numpy as np
        DIM = 128
        DEPTH = 6
        HEADS = 16
        DIM_HEAD = 64
        WINDOW = 32
        INNER = HEADS * DIM_HEAD
        DIM_INNER = int(DIM * 4 * 2 / 3)
        QK_SCALE = 8.0

        def shift_tokens(t):
            a, s = jnp.split(t, 2, -1)
            s = jnp.pad(s, ((0, 0), (1, 0), (0, 0)))[:, :-1]
            return jnp.concatenate([a, s], -1)

        def l2norm(t):
            return t / jnp.maximum(jnp.linalg.norm(t, axis=-1, keepdims=True), 1e-12)

        def rotate_half(x):
            x1, x2 = jnp.split(x, 2, -1)
            return jnp.concatenate([-x2, x1], -1)

        def rotary_tables(n):
            half = jnp.arange(0, DIM_HEAD, 2, dtype=jnp.float32)
            inv_freq = 1.0 / 10000.0 ** (half / DIM_HEAD)
            t = jnp.arange(n, dtype=jnp.float32)
            freqs = t[:, None] * inv_freq[None, :]
            freqs = jnp.concatenate([freqs, freqs], -1)
            base_scale = (half + 0.4 * DIM_HEAD) / (1.4 * DIM_HEAD)
            power = (t - n // 2) / (WINDOW // 2)
            scale = base_scale[None, :] ** power[:, None]
            scale = jnp.concatenate([scale, scale], -1)
            return (freqs, scale)

        def local_attention(q, k, v):
            b, h, n, d = q.shape
            w = WINDOW
            nw = n // w
            bq = q.reshape(b, h, nw, w, d)
            bk = k.reshape(b, h, nw, w, d)
            bv = v.reshape(b, h, nw, w, d)

            def look(t):
                p = jnp.pad(t, ((0, 0), (0, 0), (1, 0), (0, 0), (0, 0)))
                return jnp.concatenate([p[:, :, :nw], p[:, :, 1:]], axis=3)
            bk2, bv2 = (look(bk), look(bv))
            seq = jnp.arange(n).reshape(nw, w)
            seq_p = jnp.pad(seq, ((1, 0), (0, 0)), constant_values=-1)
            jt = jnp.concatenate([seq_p[:nw], seq_p[1:]], axis=1)
            it = seq[:, :, None]
            jb = jt[:, None, :]
            mask = (it < jb) | (it > jb + w) | (jb == -1)
            sim = jnp.einsum('bhwie,bhwje->bhwij', bq, bk2) * QK_SCALE
            sim = jnp.where(mask, -jnp.finfo(sim.dtype).max, sim)
            attn = jax.nn.softmax(sim, -1)
            out = jnp.einsum('bhwij,bhwje->bhwie', attn, bv2)
            return out.reshape(b, h, n, d)

        def attn_layer(x, Wqkv, qs, ksc, Wo):
            b, n, _ = x.shape
            qkv = x @ Wqkv
            q, k, v = jnp.split(qkv, 3, -1)
            sh = lambda t: t.reshape(b, n, HEADS, DIM_HEAD).transpose(0, 2, 1, 3)
            q, k, v = (sh(q), sh(k), sh(v))
            q = l2norm(q) * qs
            k = l2norm(k) * ksc
            freqs, scale = rotary_tables(n)
            cos, sin = (jnp.cos(freqs), jnp.sin(freqs))
            q = q * cos * scale + rotate_half(q) * sin * scale
            inv = 1.0 / scale
            k = k * cos * inv + rotate_half(k) * sin * inv
            out = local_attention(q, k, v)
            out = out.transpose(0, 2, 1, 3).reshape(b, n, INNER)
            return out @ Wo

        def ffn_layer(x, g, bln, W1, b1, W2, b2):
            mu = x.mean(-1, keepdims=True)
            var = ((x - mu) ** 2).mean(-1, keepdims=True)
            xn = (x - mu) / jnp.sqrt(var + 1e-05) * g + bln
            hg = xn @ W1 + b1
            a, gate = jnp.split(hg, 2, -1)
            return a * jax.nn.gelu(gate, approximate=False) @ W2 + b2
        key = jax.random.key(seed)
        ks = jax.random.split(key, 8)
        B, N = (2, 256)
        init = lambda k, shape: jax.random.normal(k, shape, jnp.float32) * 0.02
        return {'x': jax.random.normal(ks[0], (B, N, DIM), jnp.float32), 'Wqkv': init(ks[1], (DEPTH, DIM, 3 * INNER)), 'q_scale': jnp.ones((DEPTH, DIM_HEAD), jnp.float32), 'k_scale': jnp.ones((DEPTH, DIM_HEAD), jnp.float32), 'Wo': init(ks[2], (DEPTH, INNER, DIM)), 'ln_g': jnp.ones((DEPTH, DIM), jnp.float32), 'ln_b': jnp.zeros((DEPTH, DIM), jnp.float32), 'W1': init(ks[3], (DEPTH, DIM, 2 * DIM_INNER)), 'b1': jnp.zeros((DEPTH, 2 * DIM_INNER), jnp.float32), 'W2': init(ks[4], (DEPTH, DIM_INNER, DIM)), 'b2': jnp.zeros((DEPTH, DIM), jnp.float32)}
    _L1_ffn_all = _L1_ffn_setup()
    _L1_ffn_in = {k: v for k, v in _L1_ffn_all.items() if k in ('Wqkv', 'q_scale', 'k_scale', 'Wo', 'ln_g', 'ln_b', 'W1', 'b1', 'W2', 'b2')}
    del _L1_ffn_all

    def _L2_attn_setup():
        import jax, jax.numpy as jnp
        import numpy as np
        import math
        EMBED = 128
        HEADS = 16
        HEAD_DIM = EMBED // HEADS
        B, N = (2, 256)
        key = jax.random.key(seed)
        ks = jax.random.split(key, 8)
        s = 1.0 / math.sqrt(EMBED)
        Wq = jax.random.uniform(ks[0], (EMBED, EMBED), jnp.float32, -s, s)
        bq = jax.random.uniform(ks[1], (EMBED,), jnp.float32, -s, s)
        Wk = jax.random.uniform(ks[2], (EMBED, EMBED), jnp.float32, -s, s)
        bk = jax.random.uniform(ks[3], (EMBED,), jnp.float32, -s, s)
        Wv = jax.random.uniform(ks[4], (EMBED, EMBED), jnp.float32, -s, s)
        bv = jax.random.uniform(ks[5], (EMBED,), jnp.float32, -s, s)
        Wp = jax.random.normal(ks[6], (HEAD_DIM, HEAD_DIM), jnp.float32)
        x = jax.random.normal(ks[7], (B, N, EMBED), jnp.float32)
        return {'x': x, 'Wq': Wq, 'bq': bq, 'Wk': Wk, 'bk': bk, 'Wv': Wv, 'bv': bv, 'Wp': Wp}
    _L2_attn_all = _L2_attn_setup()
    _L2_attn_in = {k: v for k, v in _L2_attn_all.items() if k in ('Wq', 'bq', 'Wk', 'bk', 'Wv', 'bv', 'Wp')}
    del _L2_attn_all

    def _L2_xattn_setup():
        import jax, jax.numpy as jnp
        import numpy as np
        B, C_LEN, Q_LEN, D = (8, 256, 64, 128)
        key = jax.random.key(seed)
        ks = jax.random.split(key, 10)
        scale = 1.0 / np.sqrt(D)
        return {'c': jax.random.normal(ks[0], (B, C_LEN, D), dtype=jnp.float32), 'q': jax.random.normal(ks[1], (B, Q_LEN, D), dtype=jnp.float32), 'w_cq': jax.random.normal(ks[2], (D,), dtype=jnp.float32) * scale, 'b_cq': jax.random.normal(ks[3], (), dtype=jnp.float32) * scale, 'w_c': jax.random.normal(ks[4], (D,), dtype=jnp.float32) * scale, 'b_c': jax.random.normal(ks[5], (), dtype=jnp.float32) * scale, 'w_q': jax.random.normal(ks[6], (D,), dtype=jnp.float32) * scale, 'b_q': jax.random.normal(ks[7], (), dtype=jnp.float32) * scale, 'W_l': jax.random.normal(ks[8], (D, 4 * D), dtype=jnp.float32) * (1.0 / np.sqrt(4 * D)), 'b_l': jax.random.normal(ks[9], (D,), dtype=jnp.float32) * (1.0 / np.sqrt(4 * D))}
    _L2_xattn_all = _L2_xattn_setup()
    _L2_xattn_in = {k: v for k, v in _L2_xattn_all.items() if k in ('w_cq', 'b_cq', 'w_c', 'b_c', 'w_q', 'b_q', 'W_l', 'b_l')}
    del _L2_xattn_all

    def _L2_ffn_setup():
        import jax, jax.numpy as jnp
        import numpy as np
        B, T, D, H, E = (4, 256, 128, 512, 8)
        key = jax.random.key(seed)
        ks = jax.random.split(key, 7)
        x = jax.random.normal(ks[0], (B, T, D), dtype=jnp.float32)
        Wg = jax.random.normal(ks[1], (D, E), dtype=jnp.float32) / np.sqrt(D)
        bg = jax.random.normal(ks[2], (E,), dtype=jnp.float32) * 0.01
        W1 = jax.random.normal(ks[3], (E, D, H), dtype=jnp.float32) / np.sqrt(D)
        b1 = jax.random.normal(ks[4], (E, H), dtype=jnp.float32) * 0.01
        W2 = jax.random.normal(ks[5], (E, H, D), dtype=jnp.float32) / np.sqrt(H)
        b2 = jax.random.normal(ks[6], (E, D), dtype=jnp.float32) * 0.01
        return {'x': x, 'Wg': Wg, 'bg': bg, 'W1': W1, 'b1': b1, 'W2': W2, 'b2': b2}
    _L2_ffn_all = _L2_ffn_setup()
    _L2_ffn_in = {k: v for k, v in _L2_ffn_all.items() if k in ('Wg', 'bg', 'W1', 'b1', 'W2', 'b2')}
    del _L2_ffn_all

    def _L3_attn_setup():
        import jax, jax.numpy as jnp
        import numpy as np
        DIM = 128
        HEADS = 16
        HEAD_DIM = DIM // HEADS
        B, N = (4, 512)
        key = jax.random.key(seed)
        ks = jax.random.split(key, 9)
        s = 1.0 / np.sqrt(DIM)
        return {'x': jax.random.normal(ks[0], (B, N, DIM), dtype=jnp.float32), 'Wq': jax.random.uniform(ks[1], (DIM, DIM), jnp.float32, -s, s), 'bq': jax.random.uniform(ks[2], (DIM,), jnp.float32, -s, s), 'Wk': jax.random.uniform(ks[3], (DIM, DIM), jnp.float32, -s, s), 'bk': jax.random.uniform(ks[4], (DIM,), jnp.float32, -s, s), 'Wv': jax.random.uniform(ks[5], (DIM, DIM), jnp.float32, -s, s), 'bv': jax.random.uniform(ks[6], (DIM,), jnp.float32, -s, s), 'Wp': jax.random.uniform(ks[7], (DIM, DIM), jnp.float32, -s, s), 'bp': jax.random.uniform(ks[8], (DIM,), jnp.float32, -s, s)}
    _L3_attn_all = _L3_attn_setup()
    _L3_attn_in = {k: v for k, v in _L3_attn_all.items() if k in ('Wq', 'bq', 'Wk', 'bk', 'Wv', 'bv', 'Wp', 'bp')}
    del _L3_attn_all

    def _L3_xattn_setup():
        import jax, jax.numpy as jnp
        import numpy as np
        EMBED = 128
        HEADS = 16
        HEAD_DIM = EMBED // HEADS
        key = jax.random.key(seed)
        ks = jax.random.split(key, 8)
        N, S, E = (4, 256, EMBED)
        s = 1.0 / np.sqrt(E)
        return {'values': jax.random.normal(ks[0], (N, S, E), jnp.float32), 'keys': jax.random.normal(ks[1], (N, S, E), jnp.float32), 'queries': jax.random.normal(ks[2], (N, S, E), jnp.float32), 'Wv': jax.random.normal(ks[3], (E, E), jnp.float32) * s, 'Wk': jax.random.normal(ks[4], (E, E), jnp.float32) * s, 'Wq': jax.random.normal(ks[5], (E, E), jnp.float32) * s, 'Wo': jax.random.normal(ks[6], (E, E), jnp.float32) * s, 'bo': jax.random.normal(ks[7], (E,), jnp.float32) * s}
    _L3_xattn_all = _L3_xattn_setup()
    _L3_xattn_in = {k: v for k, v in _L3_xattn_all.items() if k in ('Wv', 'Wk', 'Wq', 'Wo', 'bo')}
    del _L3_xattn_all

    def _L3_ffn_setup():
        import jax, jax.numpy as jnp
        import numpy as np
        import math
        D_MODEL = 128
        D_FF = 512
        NUM_EXPERTS = 8
        NUM_SHARED = 1
        E_ROUTED = NUM_EXPERTS - NUM_SHARED
        TOP_K = 2
        CAP_FACTOR = 1.25
        B, S = (4, 256)
        T = B * S
        CAPACITY = math.ceil(CAP_FACTOR * T * TOP_K / E_ROUTED)
        SHARED_SCALE = 1.0

        def _layernorm(x, g, b, eps=1e-05):
            mu = jnp.mean(x, axis=-1, keepdims=True)
            var = jnp.mean((x - mu) ** 2, axis=-1, keepdims=True)
            return (x - mu) * jax.lax.rsqrt(var + eps) * g + b
        key = jax.random.key(seed)
        ks = jax.random.split(key, 10)
        s = 0.02
        return {'x': jax.random.normal(ks[0], (B, S, D_MODEL), dtype=jnp.float32), 'ln_g': jnp.ones((D_MODEL,), jnp.float32), 'ln_b': jnp.zeros((D_MODEL,), jnp.float32), 'Wr': jax.random.normal(ks[1], (D_MODEL, E_ROUTED), jnp.float32) * s, 'W1': jax.random.normal(ks[2], (E_ROUTED, D_MODEL, D_FF), jnp.float32) * s, 'W3': jax.random.normal(ks[3], (E_ROUTED, D_MODEL, D_FF), jnp.float32) * s, 'W2': jax.random.normal(ks[4], (E_ROUTED, D_FF, D_MODEL), jnp.float32) * s, 'W1s': jax.random.normal(ks[5], (D_MODEL, D_FF), jnp.float32) * s, 'W3s': jax.random.normal(ks[6], (D_MODEL, D_FF), jnp.float32) * s, 'W2s': jax.random.normal(ks[7], (D_FF, D_MODEL), jnp.float32) * s}
    _L3_ffn_all = _L3_ffn_setup()
    _L3_ffn_in = {k: v for k, v in _L3_ffn_all.items() if k in ('ln_g', 'ln_b', 'Wr', 'W1', 'W3', 'W2', 'W1s', 'W3s', 'W2s')}
    del _L3_ffn_all
    return {'x': x, 'ctx_1024': ctx_1024, 'mask_BxS2_bf1': mask_BxS2_bf1, 'L0_attn_mask': _L0_attn_in['mask'], 'L0_attn_w_kvc': _L0_attn_in['w_kvc'], 'L0_attn_b_kvc': _L0_attn_in['b_kvc'], 'L0_attn_w_kvu': _L0_attn_in['w_kvu'], 'L0_attn_b_kvu': _L0_attn_in['b_kvu'], 'L0_attn_w_qc': _L0_attn_in['w_qc'], 'L0_attn_b_qc': _L0_attn_in['b_qc'], 'L0_attn_w_qu': _L0_attn_in['w_qu'], 'L0_attn_b_qu': _L0_attn_in['b_qu'], 'L0_attn_w_o': _L0_attn_in['w_o'], 'L0_attn_b_o': _L0_attn_in['b_o'], 'L0_xattn_g_x': _L0_xattn_in['g_x'], 'L0_xattn_b_x': _L0_xattn_in['b_x'], 'L0_xattn_g_l': _L0_xattn_in['g_l'], 'L0_xattn_b_l': _L0_xattn_in['b_l'], 'L0_xattn_w_q': _L0_xattn_in['w_q'], 'L0_xattn_w_kv': _L0_xattn_in['w_kv'], 'L0_xattn_w_out': _L0_xattn_in['w_out'], 'L0_xattn_g_o': _L0_xattn_in['g_o'], 'L0_xattn_b_o': _L0_xattn_in['b_o'], 'L0_ffn_Wg': _L0_ffn_in['Wg'], 'L0_ffn_bg': _L0_ffn_in['bg'], 'L0_ffn_We': _L0_ffn_in['We'], 'L0_ffn_be': _L0_ffn_in['be'], 'L1_attn_Wq': _L1_attn_in['Wq'], 'L1_attn_Wk': _L1_attn_in['Wk'], 'L1_attn_Wv': _L1_attn_in['Wv'], 'L1_attn_Wo': _L1_attn_in['Wo'], 'L1_attn_lambda_q1': _L1_attn_in['lambda_q1'], 'L1_attn_lambda_k1': _L1_attn_in['lambda_k1'], 'L1_attn_lambda_q2': _L1_attn_in['lambda_q2'], 'L1_attn_lambda_k2': _L1_attn_in['lambda_k2'], 'L1_attn_subln_g': _L1_attn_in['subln_g'], 'L1_xattn_Wq_w': _L1_xattn_in['Wq_w'], 'L1_xattn_Wq_b': _L1_xattn_in['Wq_b'], 'L1_xattn_Wk_w': _L1_xattn_in['Wk_w'], 'L1_xattn_Wk_b': _L1_xattn_in['Wk_b'], 'L1_xattn_Wv_w': _L1_xattn_in['Wv_w'], 'L1_xattn_Wv_b': _L1_xattn_in['Wv_b'], 'L1_ffn_Wqkv': _L1_ffn_in['Wqkv'], 'L1_ffn_q_scale': _L1_ffn_in['q_scale'], 'L1_ffn_k_scale': _L1_ffn_in['k_scale'], 'L1_ffn_Wo': _L1_ffn_in['Wo'], 'L1_ffn_ln_g': _L1_ffn_in['ln_g'], 'L1_ffn_ln_b': _L1_ffn_in['ln_b'], 'L1_ffn_W1': _L1_ffn_in['W1'], 'L1_ffn_b1': _L1_ffn_in['b1'], 'L1_ffn_W2': _L1_ffn_in['W2'], 'L1_ffn_b2': _L1_ffn_in['b2'], 'L2_attn_Wq': _L2_attn_in['Wq'], 'L2_attn_bq': _L2_attn_in['bq'], 'L2_attn_Wk': _L2_attn_in['Wk'], 'L2_attn_bk': _L2_attn_in['bk'], 'L2_attn_Wv': _L2_attn_in['Wv'], 'L2_attn_bv': _L2_attn_in['bv'], 'L2_attn_Wp': _L2_attn_in['Wp'], 'L2_xattn_w_cq': _L2_xattn_in['w_cq'], 'L2_xattn_b_cq': _L2_xattn_in['b_cq'], 'L2_xattn_w_c': _L2_xattn_in['w_c'], 'L2_xattn_b_c': _L2_xattn_in['b_c'], 'L2_xattn_w_q': _L2_xattn_in['w_q'], 'L2_xattn_b_q': _L2_xattn_in['b_q'], 'L2_xattn_W_l': _L2_xattn_in['W_l'], 'L2_xattn_b_l': _L2_xattn_in['b_l'], 'L2_ffn_Wg': _L2_ffn_in['Wg'], 'L2_ffn_bg': _L2_ffn_in['bg'], 'L2_ffn_W1': _L2_ffn_in['W1'], 'L2_ffn_b1': _L2_ffn_in['b1'], 'L2_ffn_W2': _L2_ffn_in['W2'], 'L2_ffn_b2': _L2_ffn_in['b2'], 'L3_attn_Wq': _L3_attn_in['Wq'], 'L3_attn_bq': _L3_attn_in['bq'], 'L3_attn_Wk': _L3_attn_in['Wk'], 'L3_attn_bk': _L3_attn_in['bk'], 'L3_attn_Wv': _L3_attn_in['Wv'], 'L3_attn_bv': _L3_attn_in['bv'], 'L3_attn_Wp': _L3_attn_in['Wp'], 'L3_attn_bp': _L3_attn_in['bp'], 'L3_xattn_Wv': _L3_xattn_in['Wv'], 'L3_xattn_Wk': _L3_xattn_in['Wk'], 'L3_xattn_Wq': _L3_xattn_in['Wq'], 'L3_xattn_Wo': _L3_xattn_in['Wo'], 'L3_xattn_bo': _L3_xattn_in['bo'], 'L3_ffn_ln_g': _L3_ffn_in['ln_g'], 'L3_ffn_ln_b': _L3_ffn_in['ln_b'], 'L3_ffn_Wr': _L3_ffn_in['Wr'], 'L3_ffn_W1': _L3_ffn_in['W1'], 'L3_ffn_W3': _L3_ffn_in['W3'], 'L3_ffn_W2': _L3_ffn_in['W2'], 'L3_ffn_W1s': _L3_ffn_in['W1s'], 'L3_ffn_W3s': _L3_ffn_in['W3s'], 'L3_ffn_W2s': _L3_ffn_in['W2s']}

def reference(x, ctx_1024, mask_BxS2_bf1, L0_attn_mask, L0_attn_w_kvc, L0_attn_b_kvc, L0_attn_w_kvu, L0_attn_b_kvu, L0_attn_w_qc, L0_attn_b_qc, L0_attn_w_qu, L0_attn_b_qu, L0_attn_w_o, L0_attn_b_o, L0_xattn_g_x, L0_xattn_b_x, L0_xattn_g_l, L0_xattn_b_l, L0_xattn_w_q, L0_xattn_w_kv, L0_xattn_w_out, L0_xattn_g_o, L0_xattn_b_o, L0_ffn_Wg, L0_ffn_bg, L0_ffn_We, L0_ffn_be, L1_attn_Wq, L1_attn_Wk, L1_attn_Wv, L1_attn_Wo, L1_attn_lambda_q1, L1_attn_lambda_k1, L1_attn_lambda_q2, L1_attn_lambda_k2, L1_attn_subln_g, L1_xattn_Wq_w, L1_xattn_Wq_b, L1_xattn_Wk_w, L1_xattn_Wk_b, L1_xattn_Wv_w, L1_xattn_Wv_b, L1_ffn_Wqkv, L1_ffn_q_scale, L1_ffn_k_scale, L1_ffn_Wo, L1_ffn_ln_g, L1_ffn_ln_b, L1_ffn_W1, L1_ffn_b1, L1_ffn_W2, L1_ffn_b2, L2_attn_Wq, L2_attn_bq, L2_attn_Wk, L2_attn_bk, L2_attn_Wv, L2_attn_bv, L2_attn_Wp, L2_xattn_w_cq, L2_xattn_b_cq, L2_xattn_w_c, L2_xattn_b_c, L2_xattn_w_q, L2_xattn_b_q, L2_xattn_W_l, L2_xattn_b_l, L2_ffn_Wg, L2_ffn_bg, L2_ffn_W1, L2_ffn_b1, L2_ffn_W2, L2_ffn_b2, L3_attn_Wq, L3_attn_bq, L3_attn_Wk, L3_attn_bk, L3_attn_Wv, L3_attn_bv, L3_attn_Wp, L3_attn_bp, L3_xattn_Wv, L3_xattn_Wk, L3_xattn_Wq, L3_xattn_Wo, L3_xattn_bo, L3_ffn_ln_g, L3_ffn_ln_b, L3_ffn_Wr, L3_ffn_W1, L3_ffn_W3, L3_ffn_W2, L3_ffn_W1s, L3_ffn_W3s, L3_ffn_W2s):
    import jax
    import jax.numpy as jnp

    def _L0_attn_ref(x, mask, w_kvc, b_kvc, w_kvu, b_kvu, w_qc, b_qc, w_qu, b_qu, w_o, b_o):
        import jax, jax.numpy as jnp
        import numpy as np
        DIM = 128
        NUM_HEADS = 16
        HEAD_DIM = DIM // NUM_HEADS
        LATENT = 128
        Q_RANK = 32
        B, S = (4, 256)
        b, s, _ = x.shape
        kv_latent = x @ w_kvc + b_kvc
        kv_up = kv_latent @ w_kvu + b_kvu
        K, V = jnp.split(kv_up, 2, axis=-1)
        Q = (x @ w_qc + b_qc) @ w_qu + b_qu

        def split_heads(t):
            return t.reshape(b, s, NUM_HEADS, HEAD_DIM).transpose(0, 2, 1, 3)
        Qh, Kh, Vh = (split_heads(Q), split_heads(K), split_heads(V))
        scores = jnp.einsum('bhsd,bhtd->bhst', Qh, Kh) / np.sqrt(HEAD_DIM).astype(np.float32)
        scores = jnp.where(mask == 0, jnp.float32(-1000000000.0), scores)
        attn = jax.nn.softmax(scores, axis=-1)
        ctx = jnp.einsum('bhst,bhtd->bhsd', attn, Vh)
        ctx = ctx.transpose(0, 2, 1, 3).reshape(b, s, DIM)
        return ctx @ w_o + b_o

    def _L0_xattn_ref(x, latents, mask, g_x, b_x, g_l, b_l, w_q, w_kv, w_out, g_o, b_o):
        import jax, jax.numpy as jnp
        import numpy as np
        H, DH = (8, 64)
        EPS = 1e-05

        def _ln(x, g, b):
            m = x.mean(-1, keepdims=True)
            v = ((x - m) ** 2).mean(-1, keepdims=True)
            return (x - m) / jnp.sqrt(v + EPS) * g + b
        B, Lq = (latents.shape[0], latents.shape[1])
        scale = DH ** (-0.5)
        xn = _ln(x, g_x, b_x)
        ln = _ln(latents, g_l, b_l)
        q = ln @ w_q
        kv_in = jnp.concatenate([xn, ln], axis=1)
        k, v = jnp.split(kv_in @ w_kv, 2, axis=-1)
        split = lambda t: t.reshape(t.shape[0], t.shape[1], H, DH).transpose(0, 2, 1, 3)
        q, k, v = (split(q) * scale, split(k), split(v))
        sim = jnp.einsum('bhid,bhjd->bhij', q, k)
        m = jnp.concatenate([mask, jnp.ones((B, Lq), dtype=bool)], axis=1)[:, None, None, :]
        sim = jnp.where(m, sim, -jnp.finfo(sim.dtype).max)
        attn = jax.nn.softmax(sim, axis=-1)
        out = jnp.einsum('bhij,bhjd->bhid', attn, v)
        out = out.transpose(0, 2, 1, 3).reshape(B, Lq, H * DH)
        return _ln(out @ w_out, g_o, b_o)

    def _L0_ffn_ref(x, Wg, bg, We, be):
        import jax, jax.numpy as jnp
        import numpy as np
        IN_DIM = 128
        OUT_DIM = 128
        NUM_EXPERTS = 8
        TOP_K = 2
        gate = jax.nn.softmax(x @ Wg + bg, axis=-1)
        topk_vals, topk_idx = jax.lax.top_k(gate, TOP_K)
        onehot = jax.nn.one_hot(topk_idx, NUM_EXPERTS, dtype=gate.dtype)
        gate_sparse = jnp.einsum('bsk,bske->bse', topk_vals, onehot)
        gate_sparse = gate_sparse / jnp.sum(gate_sparse, axis=-1, keepdims=True)
        y = jnp.einsum('bsi,eoi->bseo', x, We) + be[None, None, :, :].transpose(0, 1, 2, 3)
        out = jnp.einsum('bseo,bse->bso', y, gate_sparse)
        return out

    def _L1_attn_ref(x, Wq, Wk, Wv, Wo, lambda_q1, lambda_k1, lambda_q2, lambda_k2, subln_g):
        import jax, jax.numpy as jnp
        import numpy as np
        import math
        EMBED_DIM = 128
        NUM_HEADS = 16
        NUM_KV_HEADS = 16
        DEPTH = 12
        HEAD_DIM = EMBED_DIM // NUM_HEADS // 2
        LAMBDA_INIT = 0.8 - 0.6 * math.exp(-0.3 * DEPTH)
        EPS = 1e-05
        THETA = 0.0001

        def rope(q):
            b, s, h, d = q.shape
            pos = jnp.arange(s, dtype=jnp.float32)[:, None]
            freq = 1.0 / THETA ** (2.0 * jnp.arange(d // 2, dtype=jnp.float32) / d)
            ang = pos * freq
            cos = jnp.cos(ang)[None, :, None, :].astype(q.dtype)
            sin = jnp.sin(ang)[None, :, None, :].astype(q.dtype)
            qr = q.reshape(b, s, h, d // 2, 2)
            q0, q1 = (qr[..., 0], qr[..., 1])
            out = jnp.stack([q0 * cos - q1 * sin, q0 * sin + q1 * cos], axis=-1)
            return out.reshape(q.shape)
        b, s, d = x.shape
        H, hd = (NUM_HEADS, HEAD_DIM)
        scaling = hd ** (-0.5)
        q = (x @ Wq).reshape(b, s, 2 * H, hd)
        k = (x @ Wk).reshape(b, s, 2 * NUM_KV_HEADS, hd)
        v = (x @ Wv).reshape(b, s, NUM_KV_HEADS, 2 * hd)
        q = rope(q).transpose(0, 2, 1, 3) * scaling
        k = rope(k).transpose(0, 2, 1, 3)
        v = v.transpose(0, 2, 1, 3)
        scores = jnp.einsum('bhqd,bhkd->bhqk', q, k)
        probs = jax.nn.softmax(scores.astype(jnp.float32), axis=-1).astype(scores.dtype)
        lam1 = jnp.exp(jnp.sum(lambda_q1 * lambda_k1))
        lam2 = jnp.exp(jnp.sum(lambda_q2 * lambda_k2))
        lam = (lam1 - lam2 + LAMBDA_INIT).astype(q.dtype)
        probs = probs.reshape(b, H, 2, s, s)
        w = probs[:, :, 0] - lam * probs[:, :, 1]
        attn = jnp.einsum('bhqk,bhkd->bhqd', w, v)
        rms = jax.lax.rsqrt(jnp.mean(attn * attn, axis=-1, keepdims=True) + EPS)
        attn = attn * rms * subln_g
        attn = attn * (1.0 - LAMBDA_INIT)
        attn = attn.transpose(0, 2, 1, 3).reshape(b, s, H * 2 * hd)
        return attn @ Wo

    def _L1_xattn_ref(query, key_, value, Wq_w, Wq_b, Wk_w, Wk_b, Wv_w, Wv_b):
        import jax, jax.numpy as jnp
        import numpy as np
        B, S, DIN, DK, DV = (8, 256, 128, 128, 128)
        Q = jnp.einsum('bsd,kd->bsk', query, Wq_w) + Wq_b
        K = jnp.einsum('bsd,kd->bsk', key_, Wk_w) + Wk_b
        V = jnp.einsum('bsd,vd->bsv', value, Wv_w) + Wv_b
        scale = 1.0 / jnp.sqrt(jnp.asarray(Q.shape[-1], Q.dtype))
        scores = jnp.einsum('bqk,bsk->bqs', Q, K) * scale
        attn = jax.nn.softmax(scores, axis=-1)
        return jnp.einsum('bqs,bsv->bqv', attn, V)

    def _L1_ffn_ref(x, Wqkv, q_scale, k_scale, Wo, ln_g, ln_b, W1, b1, W2, b2):
        import jax, jax.numpy as jnp
        import numpy as np
        DIM = 128
        DEPTH = 6
        HEADS = 16
        DIM_HEAD = 64
        WINDOW = 32
        INNER = HEADS * DIM_HEAD
        DIM_INNER = int(DIM * 4 * 2 / 3)
        QK_SCALE = 8.0

        def shift_tokens(t):
            a, s = jnp.split(t, 2, -1)
            s = jnp.pad(s, ((0, 0), (1, 0), (0, 0)))[:, :-1]
            return jnp.concatenate([a, s], -1)

        def l2norm(t):
            return t / jnp.maximum(jnp.linalg.norm(t, axis=-1, keepdims=True), 1e-12)

        def rotate_half(x):
            x1, x2 = jnp.split(x, 2, -1)
            return jnp.concatenate([-x2, x1], -1)

        def rotary_tables(n):
            half = jnp.arange(0, DIM_HEAD, 2, dtype=jnp.float32)
            inv_freq = 1.0 / 10000.0 ** (half / DIM_HEAD)
            t = jnp.arange(n, dtype=jnp.float32)
            freqs = t[:, None] * inv_freq[None, :]
            freqs = jnp.concatenate([freqs, freqs], -1)
            base_scale = (half + 0.4 * DIM_HEAD) / (1.4 * DIM_HEAD)
            power = (t - n // 2) / (WINDOW // 2)
            scale = base_scale[None, :] ** power[:, None]
            scale = jnp.concatenate([scale, scale], -1)
            return (freqs, scale)

        def local_attention(q, k, v):
            b, h, n, d = q.shape
            w = WINDOW
            nw = n // w
            bq = q.reshape(b, h, nw, w, d)
            bk = k.reshape(b, h, nw, w, d)
            bv = v.reshape(b, h, nw, w, d)

            def look(t):
                p = jnp.pad(t, ((0, 0), (0, 0), (1, 0), (0, 0), (0, 0)))
                return jnp.concatenate([p[:, :, :nw], p[:, :, 1:]], axis=3)
            bk2, bv2 = (look(bk), look(bv))
            seq = jnp.arange(n).reshape(nw, w)
            seq_p = jnp.pad(seq, ((1, 0), (0, 0)), constant_values=-1)
            jt = jnp.concatenate([seq_p[:nw], seq_p[1:]], axis=1)
            it = seq[:, :, None]
            jb = jt[:, None, :]
            mask = (it < jb) | (it > jb + w) | (jb == -1)
            sim = jnp.einsum('bhwie,bhwje->bhwij', bq, bk2) * QK_SCALE
            sim = jnp.where(mask, -jnp.finfo(sim.dtype).max, sim)
            attn = jax.nn.softmax(sim, -1)
            out = jnp.einsum('bhwij,bhwje->bhwie', attn, bv2)
            return out.reshape(b, h, n, d)

        def attn_layer(x, Wqkv, qs, ksc, Wo):
            b, n, _ = x.shape
            qkv = x @ Wqkv
            q, k, v = jnp.split(qkv, 3, -1)
            sh = lambda t: t.reshape(b, n, HEADS, DIM_HEAD).transpose(0, 2, 1, 3)
            q, k, v = (sh(q), sh(k), sh(v))
            q = l2norm(q) * qs
            k = l2norm(k) * ksc
            freqs, scale = rotary_tables(n)
            cos, sin = (jnp.cos(freqs), jnp.sin(freqs))
            q = q * cos * scale + rotate_half(q) * sin * scale
            inv = 1.0 / scale
            k = k * cos * inv + rotate_half(k) * sin * inv
            out = local_attention(q, k, v)
            out = out.transpose(0, 2, 1, 3).reshape(b, n, INNER)
            return out @ Wo

        def ffn_layer(x, g, bln, W1, b1, W2, b2):
            mu = x.mean(-1, keepdims=True)
            var = ((x - mu) ** 2).mean(-1, keepdims=True)
            xn = (x - mu) / jnp.sqrt(var + 1e-05) * g + bln
            hg = xn @ W1 + b1
            a, gate = jnp.split(hg, 2, -1)
            return a * jax.nn.gelu(gate, approximate=False) @ W2 + b2
        for i in range(DEPTH):
            x = attn_layer(shift_tokens(x), Wqkv[i], q_scale[i], k_scale[i], Wo[i]) + x
            x = ffn_layer(shift_tokens(x), ln_g[i], ln_b[i], W1[i], b1[i], W2[i], b2[i]) + x
        return x

    def _L2_attn_ref(x, Wq, bq, Wk, bk, Wv, bv, Wp):
        import jax, jax.numpy as jnp
        import numpy as np
        import math
        EMBED = 128
        HEADS = 16
        HEAD_DIM = EMBED // HEADS
        B, N = (2, 256)
        Bb, Nn, E = x.shape
        H, D = (HEADS, HEAD_DIM)
        q = (x @ Wq + bq).reshape(Bb, Nn, H, D)
        k = (x @ Wk + bk).reshape(Bb, Nn, H, D)
        v = (x @ Wv + bv).reshape(Bb, Nn, H, D)
        q = jnp.einsum('bnhe,ei->bnhi', q, Wp)
        k = jnp.einsum('bnhe,ei->bnhi', k, Wp)
        scores = jnp.einsum('bnhi,bmhi->bnhm', q, k) / math.sqrt(D)
        attn = jax.nn.softmax(scores, axis=-1)
        out = jnp.einsum('bnhm,bmhe->bnhe', attn, v).reshape(Bb, Nn, E)
        return out

    def _L2_xattn_ref(c, q, w_cq, b_cq, w_c, b_c, w_q, b_q, W_l, b_l):
        import jax, jax.numpy as jnp
        import numpy as np
        B, C_LEN, Q_LEN, D = (8, 256, 64, 128)
        cq = jnp.einsum('bcd,bqd,d->bcq', c, q, w_cq) + b_cq
        s = (c @ w_c + b_c)[:, :, None] + (q @ w_q + b_q)[:, None, :] + cq
        a = jax.nn.softmax(s, axis=2)
        c2q_att = jnp.einsum('bcq,bqd->bcd', a, q)
        b_att = jax.nn.softmax(jnp.max(s, axis=2), axis=1)
        q2c_att = jnp.einsum('bc,bcd->bd', b_att, c)[:, None, :]
        x = jnp.concatenate([c, c2q_att, c * c2q_att, c * q2c_att], axis=-1)
        z = x @ W_l.T + b_l
        return z

    def _L2_ffn_ref(x, Wg, bg, W1, b1, W2, b2):
        import jax, jax.numpy as jnp
        import numpy as np
        B, T, D, H, E = (4, 256, 128, 512, 8)
        gate_scores = x @ Wg + bg
        top1 = jnp.argmax(gate_scores, axis=-1)
        onehot = jax.nn.one_hot(top1, Wg.shape[-1], dtype=x.dtype)
        h = jax.nn.relu(jnp.einsum('btd,edh->beth', x, W1) + b1[None, :, None, :])
        y = jnp.einsum('beth,ehd->betd', h, W2) + b2[None, :, None, :]
        out = jnp.einsum('betd,bte->btd', y, onehot)
        return out

    def _L3_attn_ref(x, Wq, bq, Wk, bk, Wv, bv, Wp, bp):
        import jax, jax.numpy as jnp
        import numpy as np
        DIM = 128
        HEADS = 16
        HEAD_DIM = DIM // HEADS
        B, N = (4, 512)
        b, n, d = x.shape
        q = x @ Wq + bq
        k = x @ Wk + bk
        v = x @ Wv + bv
        split = lambda t: t.reshape(b, n, HEADS, HEAD_DIM).transpose(0, 2, 1, 3)
        q, k, v = (split(q), split(k), split(v))
        q = jax.nn.elu(q) + 1.0
        k = jax.nn.elu(k) + 1.0
        kv = jnp.einsum('bhnd,bhnf->bhdf', k, v)
        out = jnp.einsum('bhnd,bhdf->bhnf', q, kv)
        out = out.transpose(0, 2, 1, 3).reshape(b, n, d)
        return out @ Wp + bp

    def _L3_xattn_ref(values, keys, queries, Wv, Wk, Wq, Wo, bo):
        import jax, jax.numpy as jnp
        import numpy as np
        EMBED = 128
        HEADS = 16
        HEAD_DIM = EMBED // HEADS
        N = queries.shape[0]
        H, D, E = (HEADS, HEAD_DIM, EMBED)
        v = (values @ Wv.T).reshape(N, -1, H, D)
        k = (keys @ Wk.T).reshape(N, -1, H, D)
        q = (queries @ Wq.T).reshape(N, -1, H, D)
        energy = jnp.einsum('nqhd,nkhd->nhqk', q, k)
        attn = jax.nn.softmax(energy / jnp.sqrt(jnp.float32(E)), axis=3)
        out = jnp.einsum('nhql,nlhd->nqhd', attn, v).reshape(N, -1, H * D)
        return out @ Wo.T + bo

    def _L3_ffn_ref(x, ln_g, ln_b, Wr, W1, W3, W2, W1s, W3s, W2s):
        import jax, jax.numpy as jnp
        import numpy as np
        import math
        D_MODEL = 128
        D_FF = 512
        NUM_EXPERTS = 8
        NUM_SHARED = 1
        E_ROUTED = NUM_EXPERTS - NUM_SHARED
        TOP_K = 2
        CAP_FACTOR = 1.25
        B, S = (4, 256)
        T = B * S
        CAPACITY = math.ceil(CAP_FACTOR * T * TOP_K / E_ROUTED)
        SHARED_SCALE = 1.0

        def _layernorm(x, g, b, eps=1e-05):
            mu = jnp.mean(x, axis=-1, keepdims=True)
            var = jnp.mean((x - mu) ** 2, axis=-1, keepdims=True)
            return (x - mu) * jax.lax.rsqrt(var + eps) * g + b
        Bx, Sx, D = x.shape
        Tn = Bx * Sx
        h = _layernorm(x, ln_g, ln_b).reshape(Tn, D)
        logits = h @ Wr
        top_vals, top_idx = jax.lax.top_k(logits, TOP_K)
        gates = jax.nn.softmax(top_vals, axis=-1)
        idx = top_idx.T.reshape(-1)
        gat = gates.T.reshape(-1)
        tok = jnp.tile(jnp.arange(Tn), TOP_K)
        onehot = jax.nn.one_hot(idx, E_ROUTED, dtype=jnp.int32)
        pos = jnp.sum(jnp.cumsum(onehot, axis=0) * onehot, axis=-1) - 1
        keep = pos < CAPACITY
        pos_c = jnp.where(keep, pos, CAPACITY)
        xe = jnp.zeros((E_ROUTED, CAPACITY, D), h.dtype).at[idx, pos_c].set(h[tok], mode='drop')
        a = jnp.einsum('ecd,edf->ecf', xe, W1)
        b = jnp.einsum('ecd,edf->ecf', xe, W3)
        ye = jnp.einsum('ecf,efd->ecd', jax.nn.silu(a) * b, W2)
        out_slots = ye[jnp.clip(idx, 0, E_ROUTED - 1), jnp.clip(pos_c, 0, CAPACITY - 1)]
        out_slots = out_slots * (gat * keep.astype(gat.dtype))[:, None]
        routed = jnp.zeros((Tn, D), h.dtype).at[tok].add(out_slots)
        shared = jax.nn.silu(h @ W1s) * (h @ W3s) @ W2s
        out = routed + SHARED_SCALE * shared
        return out.reshape(Bx, Sx, D)
    x = _layernorm(x + _L0_attn_ref(x, L0_attn_mask, L0_attn_w_kvc, L0_attn_b_kvc, L0_attn_w_kvu, L0_attn_b_kvu, L0_attn_w_qc, L0_attn_b_qc, L0_attn_w_qu, L0_attn_b_qu, L0_attn_w_o, L0_attn_b_o), axis=-1)
    x = _layernorm(x + _L0_xattn_ref(ctx_1024, x, mask_BxS2_bf1, L0_xattn_g_x, L0_xattn_b_x, L0_xattn_g_l, L0_xattn_b_l, L0_xattn_w_q, L0_xattn_w_kv, L0_xattn_w_out, L0_xattn_g_o, L0_xattn_b_o), axis=-1)
    x = _layernorm(x + _L0_ffn_ref(x, L0_ffn_Wg, L0_ffn_bg, L0_ffn_We, L0_ffn_be), axis=-1)
    x = _layernorm(x + _L1_attn_ref(x, L1_attn_Wq, L1_attn_Wk, L1_attn_Wv, L1_attn_Wo, L1_attn_lambda_q1, L1_attn_lambda_k1, L1_attn_lambda_q2, L1_attn_lambda_k2, L1_attn_subln_g), axis=-1)
    x = _layernorm(x + _L1_xattn_ref(x, ctx_1024, ctx_1024, L1_xattn_Wq_w, L1_xattn_Wq_b, L1_xattn_Wk_w, L1_xattn_Wk_b, L1_xattn_Wv_w, L1_xattn_Wv_b), axis=-1)
    x = _layernorm(x + _L1_ffn_ref(x, L1_ffn_Wqkv, L1_ffn_q_scale, L1_ffn_k_scale, L1_ffn_Wo, L1_ffn_ln_g, L1_ffn_ln_b, L1_ffn_W1, L1_ffn_b1, L1_ffn_W2, L1_ffn_b2), axis=-1)
    x = _layernorm(x + _L2_attn_ref(x, L2_attn_Wq, L2_attn_bq, L2_attn_Wk, L2_attn_bk, L2_attn_Wv, L2_attn_bv, L2_attn_Wp), axis=-1)
    x = _layernorm(x + _L2_xattn_ref(x, ctx_1024, L2_xattn_w_cq, L2_xattn_b_cq, L2_xattn_w_c, L2_xattn_b_c, L2_xattn_w_q, L2_xattn_b_q, L2_xattn_W_l, L2_xattn_b_l), axis=-1)
    x = _layernorm(x + _L2_ffn_ref(x, L2_ffn_Wg, L2_ffn_bg, L2_ffn_W1, L2_ffn_b1, L2_ffn_W2, L2_ffn_b2), axis=-1)
    x = _layernorm(x + _L3_attn_ref(x, L3_attn_Wq, L3_attn_bq, L3_attn_Wk, L3_attn_bk, L3_attn_Wv, L3_attn_bv, L3_attn_Wp, L3_attn_bp), axis=-1)
    x = _layernorm(x + _L3_xattn_ref(ctx_1024, ctx_1024, x, L3_xattn_Wv, L3_xattn_Wk, L3_xattn_Wq, L3_xattn_Wo, L3_xattn_bo), axis=-1)
    x = _layernorm(x + _L3_ffn_ref(x, L3_ffn_ln_g, L3_ffn_ln_b, L3_ffn_Wr, L3_ffn_W1, L3_ffn_W3, L3_ffn_W2, L3_ffn_W1s, L3_ffn_W3s, L3_ffn_W2s), axis=-1)
    return x

_drawn_inputs = setup_inputs


def setup_inputs(seed=0):
    import zlib

    import numpy as np

    out = dict(_drawn_inputs(seed))
    spreads = {'L0_attn_b_kvc': (0.0, 0.498),
     'L0_attn_b_kvu': (0.0, 0.1),
     'L0_attn_b_qc': (0.0, 0.8),
     'L0_attn_b_qu': (0.0, 0.8),
     'L0_attn_b_o': (0.0, 0.1),
     'L0_xattn_g_x': (1.0, 0.2),
     'L0_xattn_b_x': (0.0, 0.1),
     'L0_xattn_g_l': (1.0, 0.2),
     'L0_xattn_b_l': (0.0, 0.1),
     'L0_xattn_g_o': (1.0, 0.2),
     'L0_xattn_b_o': (0.0, 0.1),
     'L0_ffn_bg': (0.0, 0.1),
     'L1_attn_subln_g': (1.0, 0.2),
     'L1_ffn_q_scale': (1.0, 0.6),
     'L1_ffn_k_scale': (1.0, 0.6),
     'L1_ffn_ln_g': (1.0, 0.6),
     'L1_ffn_ln_b': (0.0, 0.8),
     'L1_ffn_b1': (0.0, 0.794),
     'L1_ffn_b2': (0.0, 0.1),
     'L3_ffn_ln_g': (1.0, 0.6),
     'L3_ffn_ln_b': (0.0, 0.8)}
    factors = {'L0_attn_w_kvc': 8.0,
     'L0_attn_w_kvu': 5.578,
     'L0_attn_w_qc': 8.0,
     'L0_attn_w_qu': 8.0,
     'L1_attn_lambda_q1': 8.0,
     'L1_attn_lambda_k1': 8.0,
     'L1_attn_lambda_q2': 5.637,
     'L1_attn_lambda_k2': 5.637,
     'L1_xattn_Wq_b': 8.0,
     'L1_xattn_Wk_b': 200.0,
     'L1_ffn_W1': 3.368,
     'L1_ffn_W2': 3.495,
     'L2_attn_bq': 2.687,
     'L2_attn_bk': 200.0,
     'L2_ffn_bg': 4.765,
     'L2_ffn_b1': 8.0,
     'L2_ffn_b2': 6.394,
     'L3_attn_bq': 4.807,
     'L3_attn_bk': 5.157,
     'L3_attn_bp': 200.0,
     'L3_ffn_Wr': 7.326,
     'L3_ffn_W1': 6.648,
     'L3_ffn_W3': 6.585,
     'L3_ffn_W2': 6.439,
     'L3_ffn_W1s': 4.603,
     'L3_ffn_W3s': 4.187,
     'L3_ffn_W2s': 4.53}
    for name, (base, spread) in spreads.items():
        noise = np.random.default_rng([zlib.crc32(name.encode()), seed]).standard_normal(out[name].shape)
        drawn = base * np.exp(spread * noise) if base else spread * noise
        out[name] = jnp.asarray(drawn.astype(out[name].dtype))
    for name, factor in factors.items():
        out[name] = (out[name] * factor).astype(out[name].dtype)
    return out
```

```python
from contextlib import ExitStack

import numpy as np

import concourse.bass as bass
from concourse import mybir

F32 = mybir.dt.float32
BF16 = mybir.dt.bfloat16
I32 = mybir.dt.int32
U8 = mybir.dt.uint8
ALU = mybir.AluOpType
ACT = mybir.ActivationFunctionType
AX = mybir.AxisListType

P = 128
D = 128
B = 4
S = 256
QT = S // P
S2 = 512
CT = S2 // P
EPS = 1e-5
MASKED = -1e30
STRIP = 32


class Steps:

    def __init__(self, sem, names):
        self.sem, self.names, self.turn = sem, list(names), 0
        self.place = {n: k + 1 for k, n in enumerate(self.names)}
        assert len(self.place) == len(self.names)

    def end(self, name):
        assert self.names[self.turn % len(self.names)] == name, (self.names[self.turn % len(self.names)], name)
        self.turn += 1
        return self.sem, 1

    def done(self, name, turn=0):
        return self.sem, turn * len(self.names) + self.place[name]

    def passed(self, turn):
        return self.sem, turn * len(self.names)


class Chip:
    pass


def fp(handle):
    return handle[tuple(slice(None) for _ in handle.shape)]


def stage_sems(nc, ctx, label):
    return [ctx.enter_context(nc.semaphore(f"{label}_{e}_steps")) for e in ("pe", "dve", "act", "pool")] + \
        [ctx.enter_context(nc.semaphore(f"{label}_loads"))]



TAIL_DVE = ["sum", "stats", "var", "normed"]
TAIL_POOL = ["rstd"]


class Tail:

    def __init__(self, nc, ctx, label):
        sb = lambda n, s: ctx.enter_context(nc.sbuf_tensor(f"{label}_{n}", s, F32))
        self.y = sb("y", [P, QT, D])
        self.stats = sb("stats", [P, QT, 6])
        self.mv = sb("mv", [P, QT, 2])
        self.rstd = sb("rstd", [P, QT])


def tail_dve(nc, eng, chip, t, dve, pool, b, addend, residual):
    nc.vector.tensor_tensor(fp(t.y), addend, residual, ALU.add).then_inc(*dve.end("sum"))
    eng.wait_ge(*dve.done("sum", b))
    for q in range(QT):
        last = nc.vector.bn_stats(t.stats[:, q, :], t.y[:, q, :])
    last.then_inc(*dve.end("stats"))
    eng.wait_ge(*dve.done("stats", b))
    nc.vector.memset(chip.scratch[:, 0:1], 0.0)
    for q in range(QT):
        last = nc.vector.bn_aggr(t.mv[:, q, :], t.stats[:, q, :])
    last.then_inc(*dve.end("var"))
    eng.wait_ge(*pool.done("rstd", b))
    for q in range(QT):
        last = nc.vector.tensor_scalar(chip.x_tok[:, b, q, :], t.y[:, q, :], t.mv[:, q, 0:1], t.rstd[:, q:q + 1],
                                       ALU.subtract, ALU.mult)
    last.then_inc(*dve.end("normed"))


RSTD_POOL = ["vareps"]


def tail_pool(nc, eng, chip, t, dve, pool, b):
    eng.wait_ge(*dve.done("var", b))
    nc.gpsimd.tensor_tensor(fp(t.rstd), t.mv[:, :, 1], chip.eps[:, 0:QT], ALU.add).then_inc(*pool.end("vareps"))
    eng.wait_ge(*pool.done("vareps", b))
    nc.gpsimd.tensor_tensor(fp(t.rstd), fp(t.rstd), chip.neghalf[:, 0:QT], ALU.pow).then_inc(*pool.end("rstd"))


TAIL_POOL = ["vareps", "rstd"]


class Heads:

    def __init__(self, nc, ctx, label, G, NK):
        sb = lambda n, s, dt=F32: ctx.enter_context(nc.sbuf_tensor(f"{label}_{n}", s, dt))
        self.G, self.NK, self.KT = G, NK, NK // P
        self.qT = sb("qT", [P, G, S])
        self.kT = sb("kT", [P, G, NK])
        self.v = sb("v", [P, NK // P, 16, STRIP])
        self.nm = sb("nm", [P, QT, G, P])
        self.e = sb("e", [P, 2, 2, 512])
        self.oT = sb("oT", [P, G, S])
        self.rec = sb("rec", [P, QT, 16])
        self.att = sb("att", [P, QT, 4 * G, 8])
        self.s_units = [(g, p, q) for g in range(G) for p in range(2) for q in ([None] if NK == S else range(QT))]
        self.t_units = [(g, p, k) for g in range(G) for p in range(2) for k in range(NK // S)]
        self.rounds = G // 4

    def pe_steps(self):
        names = [f"scores{u}" for u in range(len(self.s_units))] + [f"negmax{g}" for g in range(self.G)]
        n = len(self.t_units)
        for u in range(n + 1):
            names += ([f"scoresT{u}"] if u < n else []) + ([f"pv{u - 1}"] if u else [])
        return names + [f"heads{r}" for r in range(self.rounds)]

    def dve_steps(self):
        names = [f"max{u}" for u in range(len(self.s_units))] + [f"guarded{g}" for g in range(self.G)]
        names += [f"out{g}" for g in range(self.G)]
        for r in range(self.rounds):
            names += [f"rec{r}", f"att{r}"]
        return names

    def act_steps(self):
        return [f"exp{u}" for u in range(len(self.t_units))]


def heads_pe(nc, eng, chip, h, pe, dve, act, b, vhead, mask=None):
    ps = chip.ps
    for u, (g, pair, q) in enumerate(h.s_units):
        if u >= 2:
            eng.wait_ge(*dve.done(f"max{u - 2}", b))
        for j in range(2):
            s0 = STRIP * (2 * pair + j)
            for qt in (range(QT) if q is None else [q]):
                col = 0 if q is not None else qt * S
                out = ps[:, 2 * (u % 2) + j, col:col + h.NK]
                last = nc.tensor.matmul(out, h.qT[s0:s0 + STRIP, g, qt * P:(qt + 1) * P], h.kT[s0:s0 + STRIP, g, :],
                                        start=True, stop=mask is None, tile_position=(s0, 0))
                if mask is not None:
                    last = nc.tensor.matmul(out, chip.ident_b[:, :], mask[0][:, qt, :], start=False, stop=True)
        last.then_inc(*pe.end(f"scores{u}"))
    for g in range(h.G):
        last_unit = max(u for u, x in enumerate(h.s_units) if x[0] == g)
        eng.wait_ge(*dve.done(f"max{last_unit}", b))
        if g >= 2:
            eng.wait_ge(*dve.done(f"guarded{g - 2}", b))
        for qt in range(QT):
            last = nc.tensor.transpose(ps[:, 4 + g % 2, qt * P:(qt + 1) * P], h.nm[:, qt, g, :], chip.ident[:, :])
        last.then_inc(*pe.end(f"negmax{g}"))
    n = len(h.t_units)
    per = h.NK // S
    for u in range(n + 1):
        if u < n:
            g, pair, kh = h.t_units[u]
            eng.wait_ge(*dve.done(f"guarded{g}", b))
            if u >= 2:
                eng.wait_ge(*act.done(f"exp{u - 2}", b))
            for j in range(2):
                s0 = STRIP * (2 * pair + j)
                for i in range(2):
                    kt = 2 * kh + i
                    out = ps[:, 2 * (u % 2) + j, i * S:(i + 1) * S]
                    last = nc.tensor.matmul(out, h.kT[s0:s0 + STRIP, g, kt * P:(kt + 1) * P],
                                            h.qT[s0:s0 + STRIP, g, :], start=True, stop=mask is None,
                                            tile_position=(s0, 0))
                    if mask is not None:
                        last = nc.tensor.matmul(out, chip.ident_b[:, :], mask[1][:, kt, :], start=False, stop=True)
            last.then_inc(*pe.end(f"scoresT{u}"))
        if u:
            w = u - 1
            g, pair, kh = h.t_units[w]
            eng.wait_ge(*act.done(f"exp{w}", b))
            if pair == 0 and kh == 0 and g >= 2:
                eng.wait_ge(*dve.done(f"out{g - 2}", b))
            for j in range(2):
                s0 = STRIP * (2 * pair + j)
                for i in range(2):
                    kt = 2 * kh + i
                    last = nc.tensor.matmul(ps[s0:s0 + STRIP, 6 + g % 2, 0:S], h.v[:, kt, vhead(4 * g + 2 * pair + j), :],
                                            h.e[:, w % 2, j, i * S:(i + 1) * S], start=(kt == 0),
                                            stop=(kt == h.KT - 1), tile_position=(0, s0))
            last.then_inc(*pe.end(f"pv{w}"))
    for r in range(h.rounds):
        if r:
            eng.wait_ge(*dve.done(f"att{r - 1}", b))
        for g in range(4 * r, 4 * r + 4):
            eng.wait_ge(*dve.done(f"out{g}", b))
            for qt in range(QT):
                last = nc.tensor.transpose(ps[:, 4 + qt, (g % 4) * P:(g % 4 + 1) * P], h.oT[:, g, qt * P:(qt + 1) * P],
                                           chip.ident[:, :])
        last.then_inc(*pe.end(f"heads{r}"))


def heads_dve(nc, eng, chip, h, pe, dve, b, hd):
    ps = chip.ps
    for u, (g, pair, q) in enumerate(h.s_units):
        eng.wait_ge(*pe.done(f"scores{u}", b))
        c0 = STRIP * 2 * pair + hd
        bank = 2 * (u % 2)
        if q is None:
            src = ps[:, bank:bank + 2, :].rearrange("p j (t k) -> p j t k", t=QT)
            dst = h.nm[:, :, g, c0:c0 + STRIP + 1:STRIP].rearrange("p t j -> p j t")
        else:
            src, dst = ps[:, bank:bank + 2, :], h.nm[:, q, g, c0:c0 + STRIP + 1:STRIP]
        nc.vector.tensor_reduce(dst, src, AX.X, ALU.max, negate=True).then_inc(*dve.end(f"max{u}"))
    for g in range(h.G):
        eng.wait_ge(*pe.done(f"negmax{g}", b))
        nc.vector.tensor_tensor(h.qT[:, g, :], h.qT[:, g, :], ps[:, 4 + g % 2, 0:S], ALU.add)\
            .then_inc(*dve.end(f"guarded{g}"))
    for g in range(h.G):
        eng.wait_ge(*pe.done(f"pv{max(u for u, x in enumerate(h.t_units) if x[0] == g)}", b))
        nc.vector.tensor_copy(h.oT[:, g, :], ps[:, 6 + g % 2, 0:S]).then_inc(*dve.end(f"out{g}"))
    for r in range(h.rounds):
        eng.wait_ge(*pe.done(f"heads{r}", b))
        o = ps[:, 4:6, :].rearrange("p t (h c) -> p t h c", c=STRIP)
        nc.vector.reciprocal(h.rec[:, :, :], o[:, :, :, 8]).then_inc(*dve.end(f"rec{r}"))
        eng.wait_ge(*dve.done(f"rec{r}", b))
        nc.vector.tensor_tensor(h.att[:, :, 16 * r:16 * r + 16, :], o[:, :, :, 0:8],
                                h.rec[:, :, :].unsqueeze(3).to_broadcast([P, QT, 16, 8]), ALU.mult)\
            .then_inc(*dve.end(f"att{r}"))


def heads_act(nc, eng, chip, h, pe, act, b):
    for u in range(len(h.t_units)):
        eng.wait_ge(*pe.done(f"scoresT{u}", b))
        if u >= 2:
            eng.wait_ge(*pe.done(f"pv{u - 2}", b))
        bank = 2 * (u % 2)
        nc.scalar.activation(h.e[:, u % 2, :, :], chip.ps[:, bank:bank + 2, :], ACT.Exp).then_inc(*act.end(f"exp{u}"))


def clear_heads(nc, eng, h, hd, cleared):
    nc.gpsimd.memset(fp(h.nm), 0.0).then_inc(cleared, 1)
    nc.gpsimd.memset(h.v[:, :, :, 0:8], 0.0)
    nc.gpsimd.memset(h.v[:, :, :, 9:STRIP], 0.0)
    nc.gpsimd.memset(h.v[:, :, :, 8:9], 1.0).then_inc(cleared, 1)


def pad_heads(dst, hd):
    return dst.rearrange("k g (j c) -> k (g j) c", c=STRIP)[:, :, 0:hd]



LOADS = {
    "L0_attn_w_kvc": (P, D), "L0_attn_w_kvu": (P, 2 * D), "L0_attn_w_qc": (P, 32), "L0_attn_w_qu": (32, D),
    "L0_attn_w_o": (P, D), "L0_xattn_w_q": (P, 512), "L0_xattn_w_kv": (P, 1024), "L0_ffn_Wg": (P, 8),
    "L1_attn_Wq": (P, D), "L1_attn_Wk": (P, D), "L1_attn_Wv": (P, D), "L1_attn_Wo": (P, D),
    "L2_attn_Wq": (P, D), "L2_attn_Wk": (P, D), "L2_attn_Wv": (P, D),
    "L2_ffn_Wg": (P, 8), "L2_ffn_b2": (8, D),
    "L3_attn_Wq": (P, D), "L3_attn_Wk": (P, D), "L3_attn_Wv": (P, D), "L3_attn_Wp": (P, D),
    "L3_ffn_Wr": (P, 7),
}
ROWS = {
    "L0_attn_b_kvc": D, "L0_attn_b_kvu": 2 * D, "L0_attn_b_qc": 32, "L0_attn_b_qu": D, "L0_attn_b_o": D,
    "L0_ffn_bg": 8, "L0_ffn_be": 8 * D, "L1_xattn_Wv_b": D, "L2_attn_bv": D, "L2_xattn_b_l": D, "L2_ffn_bg": 8,
    "L3_attn_bq": D, "L3_attn_bk": D, "L3_attn_bv": D, "L3_attn_bp": D, "L3_xattn_bo": D,
}
COLS = [
    "L0_xattn_g_x", "L0_xattn_b_x", "L0_xattn_g_l", "L0_xattn_b_l", "L1_xattn_Wq_b", "L1_xattn_Wk_b",
    "L2_attn_bq", "L2_attn_bk", "L2_xattn_w_cq", "L2_xattn_w_c", "L2_xattn_w_q", "L3_ffn_ln_g", "L3_ffn_ln_b",
]
SPREAD = {
    "L0_xattn_g_o": D, "L0_xattn_b_o": D, "L1_attn_lambda_q1": 4, "L1_attn_lambda_k1": 4, "L1_attn_lambda_q2": 4,
    "L1_attn_lambda_k2": 4, "L1_attn_subln_g": 8, "L2_xattn_b_cq": 1, "L2_xattn_b_c": 1, "L2_xattn_b_q": 1,
}
TURNED = {
    "L0_ffn_We": 8, "L1_xattn_Wq_w": 1, "L1_xattn_Wk_w": 1, "L1_xattn_Wv_w": 1, "L2_xattn_W_l": 4,
    "L3_xattn_Wv": 1, "L3_xattn_Wk": 1, "L3_xattn_Wq": 1, "L3_xattn_Wo": 1,
}


def setup(nc, chip, a):
    with ExitStack() as ctx:
        pe_s, dve_s, act_s, pool_s, loads = stage_sems(nc, ctx, "setup")
        fetched = []

        block = ctx.enter_context(nc.Block())

        @block.sync
        def _(sp):
            n = 0
            for dst, src in chip.initial_loads:
                sp.dma_start(dst, src).then_inc(loads, 16)
                n += 16
            sp.wait_ge(loads, n)

        @block.gpsimd
        def _(pool):
            nc.gpsimd.memset(fp(chip.neghalf), -0.5)
            nc.gpsimd.memset(fp(chip.eps), EPS)
            nc.gpsimd.memset(fp(chip.zeros), 0.0)
            nc.gpsimd.memset(fp(chip.ones), 1.0)


def context_stage(nc, chip):
    with ExitStack() as ctx:
        pe_s, dve_s, act_s, pool_s, loads = stage_sems(nc, ctx, "context")
        jobs = [(chip.ctxT[:, b, c * P:(c + 1) * P], chip.ctx_tok[:, b, c, :]) for b in range(B) for c in range(CT)]
        jobs += chip.turned_weights
        full = 4
        units = [jobs[i:i + full] for i in range(0, len(jobs), full)]
        pe = Steps(pe_s, [f"turn{u}" for u in range(len(units))])
        dve = Steps(dve_s, [f"copy{u}" for u in range(len(units))])
        block = ctx.enter_context(nc.Block())

        @block.tensor
        def _(eng):
            for u, unit in enumerate(units):
                if u >= 8:
                    eng.wait_ge(*dve.done(f"copy{u - 8}"))
                for i, (dst, src) in enumerate(unit):
                    n = src.shape[0]
                    last = nc.tensor.transpose(chip.ps[:, u % 8, i * P:i * P + n], src, chip.ident[0:n, 0:n])
                last.then_inc(*pe.end(f"turn{u}"))

        @block.vector
        def _(eng):
            nc.vector.tensor_copy(fp(chip.ident_b), fp(chip.ident))
            for u, unit in enumerate(units):
                eng.wait_ge(*pe.done(f"turn{u}"))
                for i, (dst, src) in enumerate(unit):
                    last = nc.vector.tensor_copy(dst, chip.ps[:, u % 8, i * P:i * P + src.shape[0]])
                last.then_inc(*dve.end(f"copy{u}"))


def l0_attn(nc, chip):
    with ExitStack() as ctx:
        sb = lambda n, s, dt=F32: ctx.enter_context(nc.sbuf_tensor(f"l0a_{n}", s, dt))
        pe_s, dve_s, act_s, pool_s, ready = stage_sems(nc, ctx, "l0a")
        hd, G = 8, 4
        h = Heads(nc, ctx, "l0a", G, S)
        t = Tail(nc, ctx, "l0a")
        wq, wk = sb("wq", [32, G, P]), sb("wk", [P, G, P])
        bq, bk = sb("bq", [1, G, P]), sb("bk", [1, G, P])
        mq, mf, mk = sb("mq", [P, QT, S], BF16), sb("mf", [P, QT, S]), sb("mk", [P, QT, S], BF16)
        xb, xT = sb("xb", [P, QT, D]), sb("xT", [P, S])
        latent, low, attT = sb("latent", [P, S]), sb("low", [32, S]), sb("attT", [P, S])
        ps, w = chip.ps, chip.w
        pre_dve = ["mask", "maskb", "maskT", "wq", "wk", "bq", "bk"]
        pre = Steps(ctx.enter_context(nc.semaphore("l0a_prepared")), pre_dve)
        turned = ctx.enter_context(nc.semaphore("l0a_mask_turned"))
        pe = Steps(pe_s, ["xT", "latent", "low", "q", "k", "v"] + h.pe_steps() + ["attT", "y"])
        dve = Steps(dve_s, ["x", "xT", "latent", "low", "q", "k", "v"] + h.dve_steps() + ["attT"] + TAIL_DVE)
        act = Steps(act_s, h.act_steps())
        pool = Steps(pool_s, TAIL_POOL)
        block = ctx.enter_context(nc.Block())

        @block.gpsimd
        def _(eng):
            clear_heads(nc, eng, h, hd, ready)
            nc.gpsimd.memset(fp(wq), 0.0)
            nc.gpsimd.memset(fp(wk), 0.0)
            nc.gpsimd.memset(fp(bq), 0.0)
            nc.gpsimd.memset(fp(bk), 0.0).then_inc(ready, 1)
            with eng.Fori(0, B) as b:
                tail_pool(nc, eng, chip, t, dve, pool, b)

        @block.vector
        def _(eng):
            nc.vector.tensor_scalar(fp(mf), w["L0_attn_mask"], 0, MASKED, ALU.is_equal, ALU.mult).then_inc(*pre.end("mask"))
            eng.wait_ge(*pre.done("mask"))
            nc.vector.tensor_copy(fp(mq), fp(mf)).then_inc(*pre.end("maskb"))
            eng.wait_ge(turned, 1)
            nc.vector.tensor_copy(fp(mk), ps[:, 0:2, 0:S]).then_inc(*pre.end("maskT"))
            eng.wait_ge(ready, 3)
            nc.vector.tensor_copy(pad_heads(fp(wq), hd), w["L0_attn_w_qu"].rearrange("k (h c) -> k h c", c=hd))\
                .then_inc(*pre.end("wq"))
            nc.vector.tensor_copy(pad_heads(fp(wk), hd), w["L0_attn_w_kvu"][:, 0:D].rearrange("k (h c) -> k h c", c=hd))\
                .then_inc(*pre.end("wk"))
            nc.vector.tensor_copy(pad_heads(fp(bq), hd), w["L0_attn_b_qu"].rearrange("k (h c) -> k h c", c=hd))\
                .then_inc(*pre.end("bq"))
            nc.vector.tensor_copy(pad_heads(fp(bk), hd), w["L0_attn_b_kvu"][:, 0:D].rearrange("k (h c) -> k h c", c=hd))
            nc.vector.memset(fp(bk).rearrange("k g (j c) -> k (g j) c", c=STRIP)[:, :, hd:hd + 1], 1.0)\
                .then_inc(*pre.end("bk"))
            with eng.Fori(0, B) as b:
                nc.vector.tensor_copy(fp(xb), chip.x_tok[:, b, :, :]).then_inc(*dve.end("x"))
                eng.wait_ge(*pe.done("xT", b))
                nc.vector.tensor_copy(fp(xT), ps[:, 6, 0:S]).then_inc(*dve.end("xT"))
                eng.wait_ge(*pe.done("latent", b))
                nc.vector.tensor_copy(fp(latent), ps[:, 7, 0:S]).then_inc(*dve.end("latent"))
                eng.wait_ge(*pe.done("low", b))
                nc.vector.tensor_copy(fp(low), ps[0:32, 6, 0:S]).then_inc(*dve.end("low"))
                eng.wait_ge(*pe.done("q", b))
                nc.vector.tensor_scalar(fp(h.qT), ps[:, 4:6, :].rearrange("p a (g t) -> p (a g) t", t=S),
                                        float(1 / np.sqrt(np.float32(hd))), None, ALU.mult).then_inc(*dve.end("q"))
                eng.wait_ge(*pe.done("k", b))
                nc.vector.tensor_copy(fp(h.kT), ps[:, 0:2, :].rearrange("p a (g t) -> p (a g) t", t=S))\
                    .then_inc(*dve.end("k"))
                eng.wait_ge(*pe.done("v", b))
                nc.vector.tensor_copy(h.v[:, :, :, 0:hd], ps[:, 2, 0:S].rearrange("p (t h c) -> p t h c", t=QT, c=hd))\
                    .then_inc(*dve.end("v"))
                heads_dve(nc, eng, chip, h, pe, dve, b, hd)
                eng.wait_ge(*pe.done("attT", b))
                nc.vector.tensor_copy(fp(attT), ps[:, 6, 0:S]).then_inc(*dve.end("attT"))
                eng.wait_ge(*pe.done("y", b))
                tail_dve(nc, eng, chip, t, dve, pool, b, ps[:, 7, 0:S].rearrange("p (t d) -> p t d", t=QT), fp(xb))

        @block.scalar
        def _(eng):
            with eng.Fori(0, B) as b:
                heads_act(nc, eng, chip, h, pe, act, b)

        @block.tensor
        def _(eng):
            eng.wait_ge(*pre.done("mask"))
            for kt in range(QT):
                for qt in range(QT):
                    last = nc.tensor.transpose(ps[:, kt, qt * P:(qt + 1) * P], mf[:, qt, kt * P:(kt + 1) * P],
                                               chip.ident[:, :])
            last.then_inc(turned, 1)
            eng.wait_ge(*pre.done("bk"))
            eng.wait_ge(ready, 3)
            with eng.Fori(0, B) as b:
                eng.wait_ge(*dve.done("x", b))
                for qt in range(QT):
                    last = nc.tensor.transpose(ps[:, 6, qt * P:(qt + 1) * P], xb[:, qt, :], chip.ident[:, :])
                last.then_inc(*pe.end("xT"))
                eng.wait_ge(*dve.done("xT", b))
                nc.tensor.matmul(ps[:, 7, 0:S], w["L0_attn_w_kvc"], fp(xT), start=True, stop=False)
                nc.tensor.matmul(ps[:, 7, 0:S], w["L0_attn_b_kvc"], chip.ones[0:1, 0:S], start=False, stop=True)\
                    .then_inc(*pe.end("latent"))
                nc.tensor.matmul(ps[0:32, 6, 0:S], w["L0_attn_w_qc"], fp(xT), start=True, stop=False)
                nc.tensor.matmul(ps[0:32, 6, 0:S], w["L0_attn_b_qc"], chip.ones[0:1, 0:S], start=False, stop=True)\
                    .then_inc(*pe.end("low"))
                eng.wait_ge(*dve.done("low", b))
                for g in range(G):
                    out = ps[:, 4 + g // 2, (g % 2) * S:(g % 2 + 1) * S]
                    nc.tensor.matmul(out, wq[:, g, :], fp(low), start=True, stop=False)
                    last = nc.tensor.matmul(out, bq[:, g, :], chip.ones[0:1, 0:S], start=False, stop=True)
                last.then_inc(*pe.end("q"))
                for g in range(G):
                    out = ps[:, g // 2, (g % 2) * S:(g % 2 + 1) * S]
                    nc.tensor.matmul(out, wk[:, g, :], fp(latent), start=True, stop=False)
                    last = nc.tensor.matmul(out, bk[:, g, :], chip.ones[0:1, 0:S], start=False, stop=True)
                last.then_inc(*pe.end("k"))
                for kt in range(QT):
                    out = ps[:, 2, kt * P:(kt + 1) * P]
                    nc.tensor.matmul(out, latent[:, kt * P:(kt + 1) * P], w["L0_attn_w_kvu"][:, D:2 * D], start=True, stop=False)
                    last = nc.tensor.matmul(out, chip.ones[0:1, 0:P], w["L0_attn_b_kvu"][:, D:2 * D], start=False, stop=True)
                last.then_inc(*pe.end("v"))
                eng.wait_ge(*dve.done("v", b))
                heads_pe(nc, eng, chip, h, pe, dve, act, b, lambda i: i, mask=(mq, mk))
                project_out(nc, eng, chip, h.att, attT, pe, dve, b, h.rounds, w["L0_attn_w_o"], w["L0_attn_b_o"])


def project_out(nc, eng, chip, att, attT, pe, dve, b, rounds, wo, bo, ready="att"):
    ps = chip.ps
    eng.wait_ge(*dve.done(f"att{rounds - 1}" if ready == "att" else ready, b))
    for qt in range(QT):
        src = att[:, qt, :, :].rearrange("p h c -> p (h c)") if len(att.shape) == 4 else att[:, qt, :]
        last = nc.tensor.transpose(chip.ps[:, 6, qt * P:(qt + 1) * P], src, chip.ident[:, :])
    last.then_inc(*pe.end("attT"))
    eng.wait_ge(*dve.done("attT", b))
    for qt in range(QT):
        out = ps[:, 7, qt * P:(qt + 1) * P]
        last = nc.tensor.matmul(out, attT[:, qt * P:(qt + 1) * P], wo, start=True, stop=bo is None)
        if bo is not None:
            last = nc.tensor.matmul(out, chip.ones[0:1, 0:P], bo, start=False, stop=True)
    last.then_inc(*pe.end("y"))


def l3_xattn(nc, chip):
    with ExitStack() as ctx:
        sb = lambda n, s, dt=F32: ctx.enter_context(nc.sbuf_tensor(f"l3x_{n}", s, dt))
        pe_s, dve_s, act_s, pool_s, ready = stage_sems(nc, ctx, "l3x")
        hd, G = 8, 4
        h = Heads(nc, ctx, "l3x", G, S2)
        t = Tail(nc, ctx, "l3x")
        wq, wk, bk = sb("wq", [P, G, P]), sb("wk", [P, G, P]), sb("bk", [1, G, P])
        xb, xT, cT, attT = sb("xb", [P, QT, D]), sb("xT", [P, S]), sb("cT", [P, S2]), sb("attT", [P, S])
        ps, w = chip.ps, chip.w
        padded = ctx.enter_context(nc.semaphore("l3x_padded"))
        pe = Steps(pe_s, ["xT", "v", "k", "q"] + h.pe_steps() + ["attT", "y"])
        dve = Steps(dve_s, ["x", "xT", "v", "k", "q"] + h.dve_steps() + ["attT"] + TAIL_DVE)
        act = Steps(act_s, h.act_steps())
        pool = Steps(pool_s, TAIL_POOL)
        block = ctx.enter_context(nc.Block())

        @block.gpsimd
        def _(eng):
            clear_heads(nc, eng, h, hd, ready)
            nc.gpsimd.memset(fp(wq), 0.0)
            nc.gpsimd.memset(fp(wk), 0.0)
            nc.gpsimd.memset(fp(bk), 0.0).then_inc(ready, 1)
            with eng.Fori(0, B) as b:
                tail_pool(nc, eng, chip, t, dve, pool, b)

        @block.vector
        def _(eng):
            eng.wait_ge(ready, 3)
            for dst, src in ((wq, w["L3_xattn_Wq"]), (wk, w["L3_xattn_Wk"])):
                nc.vector.tensor_copy(pad_heads(fp(dst), hd), src[:, 0, :].rearrange("k (h c) -> k h c", c=hd))
            nc.vector.memset(fp(bk).rearrange("k g (j c) -> k (g j) c", c=STRIP)[:, :, hd:hd + 1], 1.0)\
                .then_inc(padded, 1)
            with eng.Fori(0, B) as b:
                nc.vector.tensor_copy(fp(xb), chip.x_tok[:, b, :, :])
                nc.vector.tensor_copy(fp(cT), chip.ctxT[:, b, :]).then_inc(*dve.end("x"))
                eng.wait_ge(*pe.done("xT", b))
                nc.vector.tensor_copy(fp(xT), ps[:, 6, 0:S]).then_inc(*dve.end("xT"))
                eng.wait_ge(*pe.done("v", b))
                nc.vector.tensor_copy(h.v[:, :, :, 0:hd], ps[:, 7, :].rearrange("p (t h c) -> p t h c", t=CT, c=hd))\
                    .then_inc(*dve.end("v"))
                eng.wait_ge(*pe.done("k", b))
                nc.vector.tensor_copy(fp(h.kT), ps[:, 0:4, :]).then_inc(*dve.end("k"))
                eng.wait_ge(*pe.done("q", b))
                nc.vector.tensor_scalar(fp(h.qT), ps[:, 4:6, :].rearrange("p a (g t) -> p (a g) t", t=S),
                                        float(np.float32(1) / np.sqrt(np.float32(D))), None, ALU.mult)\
                    .then_inc(*dve.end("q"))
                heads_dve(nc, eng, chip, h, pe, dve, b, hd)
                eng.wait_ge(*pe.done("attT", b))
                nc.vector.tensor_copy(fp(attT), ps[:, 6, 0:S]).then_inc(*dve.end("attT"))
                eng.wait_ge(*pe.done("y", b))
                tail_dve(nc, eng, chip, t, dve, pool, b, ps[:, 7, 0:S].rearrange("p (t d) -> p t d", t=QT), fp(xb))

        @block.scalar
        def _(eng):
            with eng.Fori(0, B) as b:
                heads_act(nc, eng, chip, h, pe, act, b)

        @block.tensor
        def _(eng):
            eng.wait_ge(padded, 1)
            eng.wait_ge(ready, 3)
            with eng.Fori(0, B) as b:
                eng.wait_ge(*dve.done("x", b))
                for qt in range(QT):
                    last = nc.tensor.transpose(ps[:, 6, qt * P:(qt + 1) * P], xb[:, qt, :], chip.ident[:, :])
                last.then_inc(*pe.end("xT"))
                for kt in range(CT):
                    last = nc.tensor.matmul(ps[:, 7, kt * P:(kt + 1) * P], cT[:, kt * P:(kt + 1) * P],
                                            w["L3_xattn_Wv"][:, 0, :], start=True, stop=True)
                last.then_inc(*pe.end("v"))
                for g in range(G):
                    nc.tensor.matmul(ps[:, g, :], wk[:, g, :], fp(cT), start=True, stop=False)
                    last = nc.tensor.matmul(ps[:, g, :], bk[:, g, :], chip.ones[0:1, :], start=False, stop=True)
                last.then_inc(*pe.end("k"))
                eng.wait_ge(*dve.done("xT", b))
                for g in range(G):
                    last = nc.tensor.matmul(ps[:, 4 + g // 2, (g % 2) * S:(g % 2 + 1) * S], wq[:, g, :], fp(xT),
                                            start=True, stop=True)
                last.then_inc(*pe.end("q"))
                eng.wait_ge(*dve.done("q", b))
                heads_pe(nc, eng, chip, h, pe, dve, act, b, lambda i: i)
                project_out(nc, eng, chip, h.att, attT, pe, dve, b, h.rounds, w["L3_xattn_Wo"][:, 0, :], w["L3_xattn_bo"])


def l2_attn(nc, chip):
    with ExitStack() as ctx:
        sb = lambda n, s, dt=F32: ctx.enter_context(nc.sbuf_tensor(f"l2a_{n}", s, dt))
        pe_s, dve_s, act_s, pool_s, ready = stage_sems(nc, ctx, "l2a")
        hd, G = 8, 4
        h = Heads(nc, ctx, "l2a", G, S)
        t = Tail(nc, ctx, "l2a")
        wp, bk = sb("wp", [P, G, P]), sb("bk", [1, G, P])
        xb, xT = sb("xb", [P, QT, D]), sb("xT", [P, S])
        q0, k0 = sb("q0", [P, S]), sb("k0", [P, S])
        ps, w = chip.ps, chip.w
        padded = ctx.enter_context(nc.semaphore("l2a_padded"))
        pe = Steps(pe_s, ["xT", "q0", "k0", "v", "q", "k"] + h.pe_steps())
        dve = Steps(dve_s, ["x", "xT", "q0", "k0", "v", "q", "k"] + h.dve_steps() + TAIL_DVE)
        act = Steps(act_s, h.act_steps())
        pool = Steps(pool_s, TAIL_POOL)
        block = ctx.enter_context(nc.Block())

        @block.gpsimd
        def _(eng):
            clear_heads(nc, eng, h, hd, ready)
            nc.gpsimd.memset(fp(wp), 0.0)
            nc.gpsimd.memset(fp(bk), 0.0).then_inc(ready, 1)
            with eng.Fori(0, B) as b:
                tail_pool(nc, eng, chip, t, dve, pool, b)

        @block.vector
        def _(eng):
            eng.wait_ge(ready, 3)
            nc.vector.tensor_tensor(pad_heads(fp(wp), hd), w["L2_attn_Wp"].unsqueeze(1).to_broadcast([P, 16, hd]),
                                    w["c_heads"].unsqueeze(2).to_broadcast([P, 16, hd]), ALU.mult)
            nc.vector.memset(fp(bk).rearrange("k g (j c) -> k (g j) c", c=STRIP)[:, :, hd:hd + 1], 1.0)\
                .then_inc(padded, 1)
            with eng.Fori(0, B) as b:
                nc.vector.tensor_copy(fp(xb), chip.x_tok[:, b, :, :]).then_inc(*dve.end("x"))
                eng.wait_ge(*pe.done("xT", b))
                nc.vector.tensor_copy(fp(xT), ps[:, 6, 0:S]).then_inc(*dve.end("xT"))
                eng.wait_ge(*pe.done("q0", b))
                nc.vector.tensor_scalar(fp(q0), ps[:, 3, 0:S], w["L2_attn_bq"], None, ALU.add).then_inc(*dve.end("q0"))
                eng.wait_ge(*pe.done("k0", b))
                nc.vector.tensor_scalar(fp(k0), ps[:, 7, 0:S], w["L2_attn_bk"], None, ALU.add).then_inc(*dve.end("k0"))
                eng.wait_ge(*pe.done("v", b))
                nc.vector.tensor_copy(h.v[:, :, :, 0:hd], ps[:, 2, 0:S].rearrange("p (t h c) -> p t h c", t=QT, c=hd))\
                    .then_inc(*dve.end("v"))
                eng.wait_ge(*pe.done("q", b))
                nc.vector.tensor_scalar(fp(h.qT), ps[:, 4:6, :].rearrange("p a (g t) -> p (a g) t", t=S),
                                        float(1 / np.sqrt(hd)), None, ALU.mult).then_inc(*dve.end("q"))
                eng.wait_ge(*pe.done("k", b))
                nc.vector.tensor_copy(fp(h.kT), ps[:, 0:2, :].rearrange("p a (g t) -> p (a g) t", t=S))\
                    .then_inc(*dve.end("k"))
                heads_dve(nc, eng, chip, h, pe, dve, b, hd)
                eng.wait_ge(*dve.done(f"att{h.rounds - 1}", b))
                tail_dve(nc, eng, chip, t, dve, pool, b, fp(h.att).rearrange("p t h c -> p t (h c)"), fp(xb))

        @block.scalar
        def _(eng):
            with eng.Fori(0, B) as b:
                heads_act(nc, eng, chip, h, pe, act, b)

        @block.tensor
        def _(eng):
            eng.wait_ge(padded, 1)
            eng.wait_ge(ready, 3)
            with eng.Fori(0, B) as b:
                eng.wait_ge(*dve.done("x", b))
                for qt in range(QT):
                    last = nc.tensor.transpose(ps[:, 6, qt * P:(qt + 1) * P], xb[:, qt, :], chip.ident[:, :])
                last.then_inc(*pe.end("xT"))
                eng.wait_ge(*dve.done("xT", b))
                nc.tensor.matmul(ps[:, 3, 0:S], w["L2_attn_Wq"], fp(xT), start=True, stop=True).then_inc(*pe.end("q0"))
                nc.tensor.matmul(ps[:, 7, 0:S], w["L2_attn_Wk"], fp(xT), start=True, stop=True).then_inc(*pe.end("k0"))
                for kt in range(QT):
                    out = ps[:, 2, kt * P:(kt + 1) * P]
                    nc.tensor.matmul(out, xT[:, kt * P:(kt + 1) * P], w["L2_attn_Wv"], start=True, stop=False)
                    last = nc.tensor.matmul(out, chip.ones[0:1, 0:P], w["L2_attn_bv"], start=False, stop=True)
                last.then_inc(*pe.end("v"))
                eng.wait_ge(*dve.done("q0", b))
                for g in range(G):
                    last = nc.tensor.matmul(ps[:, 4 + g // 2, (g % 2) * S:(g % 2 + 1) * S], wp[:, g, :], fp(q0),
                                            start=True, stop=True)
                last.then_inc(*pe.end("q"))
                eng.wait_ge(*dve.done("k0", b))
                for g in range(G):
                    out = ps[:, g // 2, (g % 2) * S:(g % 2 + 1) * S]
                    nc.tensor.matmul(out, wp[:, g, :], fp(k0), start=True, stop=False)
                    last = nc.tensor.matmul(out, bk[:, g, :], chip.ones[0:1, 0:S], start=False, stop=True)
                last.then_inc(*pe.end("k"))
                eng.wait_ge(*dve.done("k", b))
                heads_pe(nc, eng, chip, h, pe, dve, act, b, lambda i: i)


LAMBDA_INIT = 0.8 - 0.6 * float(np.exp(-0.3 * 12))


def l1_attn(nc, chip):
    with ExitStack() as ctx:
        sb = lambda n, s, dt=F32: ctx.enter_context(nc.sbuf_tensor(f"l1a_{n}", s, dt))
        pe_s, dve_s, act_s, pool_s, ready = stage_sems(nc, ctx, "l1a")
        hd, G = 4, 8
        h = Heads(nc, ctx, "l1a", G, S)
        t = Tail(nc, ctx, "l1a")
        xb, xT, attT = sb("xb", [P, QT, D]), sb("xT", [P, S]), sb("attT", [P, S])
        pad = sb("pad", [P, 2, QT, 32, STRIP])
        rot, rot2 = sb("rot", [P, QT, D]), sb("rot2", [P, QT, D])
        lam, lam2, neglam = sb("lam", [P, 2, 4]), sb("lam2", [P, 2]), sb("neglam", [P, 1])
        gain = sb("gain", [P, 8])
        diff, sq = sb("diff", [P, QT, 16, 8]), sb("sq", [P, QT, 16, 8])
        ms, rms = sb("ms", [P, QT, 16]), sb("rms", [P, QT, 16])
        heads = sb("heads", [P, QT, D])
        ps, w = chip.ps, chip.w
        lam_steps = Steps(ctx.enter_context(nc.semaphore("l1a_lambda_steps")), ["products", "sums", "neglam"])
        lam_exp = ctx.enter_context(nc.semaphore("l1a_lambda_exp"))
        pe = Steps(pe_s, ["xT", "qkv", "qTkT0", "qTkT1"] + h.pe_steps() + ["attT", "y"])
        dve = Steps(dve_s, ["x", "xT", "v"] + [f"{k}{n}" for k in "qk" for n in ("cos", "sin", "turned")] + ["qT", "kT"]
                    + h.dve_steps() + ["diff", "sq", "ms", "rms", "gained", "heads"] + ["attT"] + TAIL_DVE)
        act = Steps(act_s, h.act_steps())
        pool = Steps(pool_s, ["rmseps", "rmspow"] + TAIL_POOL)
        block = ctx.enter_context(nc.Block())

        @block.gpsimd
        def _(eng):
            clear_heads(nc, eng, h, hd, ready)
            nc.gpsimd.memset(pad[:, 0, :, :, :], 0.0)
            nc.gpsimd.memset(pad[:, 1, :, :, 0:hd], 0.0)
            nc.gpsimd.memset(pad[:, 1, :, :, hd + 1:STRIP], 0.0)
            nc.gpsimd.memset(pad[:, 1, :, :, hd:hd + 1], 1.0).then_inc(ready, 1)
            with eng.Fori(0, B) as b:
                eng.wait_ge(*dve.done("ms", b))
                nc.gpsimd.tensor_tensor(fp(rms), fp(ms), chip.eps[:, 0:1].unsqueeze(2).to_broadcast([P, QT, 16]), ALU.add)\
                    .then_inc(*pool.end("rmseps"))
                eng.wait_ge(*pool.done("rmseps", b))
                nc.gpsimd.tensor_tensor(fp(rms), fp(rms), chip.neghalf[:, 0:32].rearrange("p (t h) -> p t h", t=QT), ALU.pow)\
                    .then_inc(*pool.end("rmspow"))
                tail_pool(nc, eng, chip, t, dve, pool, b)

        @block.vector
        def _(eng):
            nc.vector.tensor_tensor(lam[:, 0, :], w["L1_attn_lambda_q1"], w["L1_attn_lambda_k1"], ALU.mult)
            nc.vector.tensor_tensor(lam[:, 1, :], w["L1_attn_lambda_q2"], w["L1_attn_lambda_k2"], ALU.mult)\
                .then_inc(*lam_steps.end("products"))
            nc.vector.tensor_scalar(fp(gain), w["L1_attn_subln_g"], 1.0 - LAMBDA_INIT, None, ALU.mult)
            eng.wait_ge(*lam_steps.done("products"))
            nc.vector.tensor_reduce(fp(lam2), fp(lam), AX.X, ALU.add).then_inc(*lam_steps.end("sums"))
            eng.wait_ge(lam_exp, 1)
            nc.vector.scalar_tensor_tensor(fp(neglam), lam2[:, 1:2], -LAMBDA_INIT, lam2[:, 0:1], ALU.add, ALU.subtract)\
                .then_inc(*lam_steps.end("neglam"))
            eng.wait_ge(*lam_steps.done("neglam"))
            eng.wait_ge(ready, 3)
            with eng.Fori(0, B) as b:
                nc.vector.tensor_copy(fp(xb), chip.x_tok[:, b, :, :]).then_inc(*dve.end("x"))
                eng.wait_ge(*pe.done("xT", b))
                nc.vector.tensor_copy(fp(xT), ps[:, 6, 0:S]).then_inc(*dve.end("xT"))
                eng.wait_ge(*pe.done("qkv", b))
                nc.vector.tensor_copy(h.v[:, :, :, 0:8], ps[:, 2, 0:S].rearrange("p (t h c) -> p t h c", t=QT, c=8))\
                    .then_inc(*dve.end("v"))
                for i, k in enumerate("qk"):
                    src = ps[:, i, 0:S].rearrange("p (t d) -> p t d", t=QT)
                    pairs = ps[:, i, 0:S].rearrange("p (n c) -> p n c", c=2)
                    sin = w["c_rope"][:, i, 1, :, :].rearrange("p t (n c) -> p (t n) c", c=2)
                    out = fp(rot2).rearrange("p t (n c) -> p (t n) c", c=2)
                    if i:
                        eng.wait_ge(*dve.done("qturned", b))
                    nc.vector.tensor_tensor(fp(rot), src, w["c_rope"][:, i, 0, :, :], ALU.mult).then_inc(*dve.end(k + "cos"))
                    nc.vector.tensor_tensor(out[:, :, 0], pairs[:, :, 1], sin[:, :, 0], ALU.mult)
                    nc.vector.tensor_tensor(out[:, :, 1], pairs[:, :, 0], sin[:, :, 1], ALU.mult).then_inc(*dve.end(k + "sin"))
                    eng.wait_ge(*dve.done(k + "sin", b))
                    nc.vector.tensor_tensor(pad[:, i, :, :, 0:hd], fp(rot).rearrange("p t (h c) -> p t h c", c=hd),
                                            fp(rot2).rearrange("p t (h c) -> p t h c", c=hd), ALU.add)\
                        .then_inc(*dve.end(k + "turned"))
                for i, dst in enumerate((h.qT, h.kT)):
                    eng.wait_ge(*pe.done(f"qTkT{i}", b))
                    nc.vector.tensor_copy(fp(dst), ps[:, 4 * i:4 * i + 4, :].rearrange("p a (g t) -> p (a g) t", t=S))\
                        .then_inc(*dve.end("qk"[i] + "T"))
                heads_dve(nc, eng, chip, h, pe, dve, b, hd)
                eng.wait_ge(*dve.done(f"att{h.rounds - 1}", b))
                pair = fp(h.att).rearrange("p t (h two) c -> p (t h) two c", two=2)
                nc.vector.scalar_tensor_tensor(fp(diff).rearrange("p t h c -> p (t h) c"), pair[:, :, 1, :], neglam[:, 0:1],
                                               pair[:, :, 0, :], ALU.mult, ALU.add).then_inc(*dve.end("diff"))
                eng.wait_ge(*dve.done("diff", b))
                nc.vector.scalar_tensor_tensor(fp(sq), fp(diff), 1.0 / 8, fp(diff), ALU.mult, ALU.mult).then_inc(*dve.end("sq"))
                eng.wait_ge(*dve.done("sq", b))
                nc.vector.tensor_reduce(fp(ms), fp(sq), AX.X, ALU.add).then_inc(*dve.end("ms"))
                eng.wait_ge(*pool.done("rmspow", b))
                nc.vector.tensor_tensor(fp(sq), fp(diff), fp(rms).unsqueeze(3).to_broadcast([P, QT, 16, 8]), ALU.mult)\
                    .then_inc(*dve.end("rms"))
                eng.wait_ge(*dve.done("rms", b))
                nc.vector.tensor_tensor(fp(heads).rearrange("p t (h c) -> p (t h) c", c=8),
                                        fp(sq).rearrange("p t h c -> p (t h) c"),
                                        fp(gain).unsqueeze(1).to_broadcast([P, 32, 8]), ALU.mult).then_inc(*dve.end("gained"))
                eng.wait_ge(*dve.done("gained", b))
                nc.vector.memset(chip.scratch[:, 1:2], 0.0).then_inc(*dve.end("heads"))
                eng.wait_ge(*pe.done("attT", b))
                nc.vector.tensor_copy(fp(attT), ps[:, 6, 0:S]).then_inc(*dve.end("attT"))
                eng.wait_ge(*pe.done("y", b))
                tail_dve(nc, eng, chip, t, dve, pool, b, ps[:, 7, 0:S].rearrange("p (t d) -> p t d", t=QT), fp(xb))

        @block.scalar
        def _(eng):
            eng.wait_ge(*lam_steps.done("sums"))
            nc.scalar.activation(fp(lam2), fp(lam2), ACT.Exp).then_inc(lam_exp, 1)
            with eng.Fori(0, B) as b:
                heads_act(nc, eng, chip, h, pe, act, b)

        @block.tensor
        def _(eng):
            eng.wait_ge(ready, 3)
            with eng.Fori(0, B) as b:
                eng.wait_ge(*dve.done("x", b))
                for qt in range(QT):
                    last = nc.tensor.transpose(ps[:, 6, qt * P:(qt + 1) * P], xb[:, qt, :], chip.ident[:, :])
                last.then_inc(*pe.end("xT"))
                eng.wait_ge(*dve.done("xT", b))
                for i, name in enumerate(("L1_attn_Wq", "L1_attn_Wk", "L1_attn_Wv")):
                    for qt in range(QT):
                        last = nc.tensor.matmul(ps[:, i, qt * P:(qt + 1) * P], xT[:, qt * P:(qt + 1) * P], w[name],
                                                start=True, stop=True)
                last.then_inc(*pe.end("qkv"))
                for i, k in enumerate("qk"):
                    eng.wait_ge(*dve.done("kturned", b))
                    for g in range(G):
                        for qt in range(QT):
                            at = (g % 2) * S + qt * P
                            last = nc.tensor.transpose(ps[:, 4 * i + g // 2, at:at + P],
                                                       pad[:, i, qt, 4 * g:4 * g + 4, :].rearrange("p h c -> p (h c)"),
                                                       chip.ident[:, :])
                    last.then_inc(*pe.end(f"qTkT{i}"))
                eng.wait_ge(*dve.done("kT", b))
                heads_pe(nc, eng, chip, h, pe, dve, act, b, lambda i: i // 2)
                project_out(nc, eng, chip, heads, attT, pe, dve, b, h.rounds, w["L1_attn_Wo"], None, ready="heads")


def l3_attn(nc, chip):
    with ExitStack() as ctx:
        sb = lambda n, s, dt=F32: ctx.enter_context(nc.sbuf_tensor(f"l3a_{n}", s, dt))
        pe_s, dve_s, act_s, pool_s, ready = stage_sems(nc, ctx, "l3a")
        t = Tail(nc, ctx, "l3a")
        xb, xT = sb("xb", [P, QT, D]), sb("xT", [P, S])
        low, qk, v = sb("low", [P, 2, S]), sb("qk", [P, 2, S]), sb("v", [P, S])
        ex = sb("ex", [P, 2, S])
        kv, oT = sb("kv", [P, D]), sb("oT", [P, S])
        ps, w = chip.ps, chip.w
        pe = Steps(pe_s, ["xT", "qkv", "kv", "oT", "y"])
        dve = Steps(dve_s, ["x", "xT", "low", "v", "qk", "kv", "oT"] + TAIL_DVE)
        act = Steps(act_s, ["exp"])
        pool = Steps(pool_s, TAIL_POOL)
        block = ctx.enter_context(nc.Block())

        @block.gpsimd
        def _(eng):
            with eng.Fori(0, B) as b:
                tail_pool(nc, eng, chip, t, dve, pool, b)

        @block.scalar
        def _(eng):
            with eng.Fori(0, B) as b:
                eng.wait_ge(*dve.done("low", b))
                nc.scalar.activation(fp(ex), fp(low), ACT.Exp).then_inc(*act.end("exp"))

        @block.vector
        def _(eng):
            with eng.Fori(0, B) as b:
                nc.vector.tensor_copy(fp(xb), chip.x_tok[:, b, :, :]).then_inc(*dve.end("x"))
                eng.wait_ge(*pe.done("xT", b))
                nc.vector.tensor_copy(fp(xT), ps[:, 6, 0:S]).then_inc(*dve.end("xT"))
                eng.wait_ge(*pe.done("qkv", b))
                nc.vector.tensor_scalar(fp(low), ps[:, 0:2, 0:S], 0.0, None, ALU.min).then_inc(*dve.end("low"))
                nc.vector.tensor_copy(fp(v), ps[:, 2, 0:S]).then_inc(*dve.end("v"))
                eng.wait_ge(*act.done("exp", b))
                nc.vector.scalar_tensor_tensor(fp(qk), ps[:, 0:2, 0:S], 0.0, fp(ex), ALU.max, ALU.add)\
                    .then_inc(*dve.end("qk"))
                eng.wait_ge(*pe.done("kv", b))
                nc.vector.tensor_tensor(fp(kv).rearrange("p (h c) -> p h c", c=8),
                                        ps[:, 3, 0:D].rearrange("p (h c) -> p h c", c=8),
                                        w["c_heads"].unsqueeze(2).to_broadcast([P, 16, 8]), ALU.mult).then_inc(*dve.end("kv"))
                eng.wait_ge(*pe.done("oT", b))
                nc.vector.tensor_copy(fp(oT), ps[:, 4, 0:S]).then_inc(*dve.end("oT"))
                eng.wait_ge(*pe.done("y", b))
                tail_dve(nc, eng, chip, t, dve, pool, b, ps[:, 7, 0:S].rearrange("p (t d) -> p t d", t=QT), fp(xb))

        @block.tensor
        def _(eng):
            with eng.Fori(0, B) as b:
                eng.wait_ge(*dve.done("x", b))
                for qt in range(QT):
                    last = nc.tensor.transpose(ps[:, 6, qt * P:(qt + 1) * P], xb[:, qt, :], chip.ident[:, :])
                last.then_inc(*pe.end("xT"))
                eng.wait_ge(*dve.done("xT", b))
                nc.tensor.matmul(ps[:, 0, 0:S], w["L3_attn_Wq"], fp(xT), start=True, stop=False)
                nc.tensor.matmul(ps[:, 0, 0:S], w["L3_attn_bq"], chip.ones[0:1, 0:S], start=False, stop=True)
                for i, k in ((1, "k"), (2, "v")):
                    for kt in range(QT):
                        out = ps[:, i, kt * P:(kt + 1) * P]
                        nc.tensor.matmul(out, xT[:, kt * P:(kt + 1) * P], w[f"L3_attn_W{k}"], start=True, stop=False)
                        last = nc.tensor.matmul(out, chip.ones[0:1, 0:P], w[f"L3_attn_b{k}"], start=False, stop=True)
                last.then_inc(*pe.end("qkv"))
                eng.wait_ge(*dve.done("qk", b))
                for kt in range(QT):
                    last = nc.tensor.matmul(ps[:, 3, 0:D], qk[:, 1, kt * P:(kt + 1) * P], v[:, kt * P:(kt + 1) * P],
                                            start=(kt == 0), stop=(kt == QT - 1))
                last.then_inc(*pe.end("kv"))
                eng.wait_ge(*dve.done("kv", b))
                nc.tensor.matmul(ps[:, 4, 0:S], fp(kv), qk[:, 0, :], start=True, stop=True).then_inc(*pe.end("oT"))
                eng.wait_ge(*dve.done("oT", b))
                for qt in range(QT):
                    out = ps[:, 7, qt * P:(qt + 1) * P]
                    nc.tensor.matmul(out, oT[:, qt * P:(qt + 1) * P], w["L3_attn_Wp"], start=True, stop=False)
                    last = nc.tensor.matmul(out, chip.ones[0:1, 0:P], w["L3_attn_bp"], start=False, stop=True)
                last.then_inc(*pe.end("y"))


class Pick:

    def __init__(self, nc, ctx, label, n):
        sb = lambda k, s: ctx.enter_context(nc.sbuf_tensor(f"{label}_{k}", s, F32))
        self.n = n
        self.m, self.eq, self.best = sb("m", [P, QT]), sb("eq", [P, QT, n]), sb("best", [P, QT])


def pick_steps(p):
    return [p + s for s in ("max", "eq", "cand", "best", "pick")]


def pick_first(nc, eng, chip, k, dve, b, p, v, out):
    wide = lambda x: fp(x).unsqueeze(2).to_broadcast([P, QT, k.n])
    nc.vector.tensor_reduce(fp(k.m), v, AX.X, ALU.max).then_inc(*dve.end(p + "max"))
    eng.wait_ge(*dve.done(p + "max", b))
    nc.vector.tensor_tensor(fp(k.eq), v, wide(k.m), ALU.is_equal).then_inc(*dve.end(p + "eq"))
    eng.wait_ge(*dve.done(p + "eq", b))
    nc.vector.tensor_tensor(fp(k.eq), fp(k.eq), chip.w["c_rank"][:, 0:k.n].unsqueeze(1).to_broadcast([P, QT, k.n]), ALU.mult)\
        .then_inc(*dve.end(p + "cand"))
    eng.wait_ge(*dve.done(p + "cand", b))
    nc.vector.tensor_reduce(fp(k.best), fp(k.eq), AX.X, ALU.max).then_inc(*dve.end(p + "best"))
    eng.wait_ge(*dve.done(p + "best", b))
    nc.vector.tensor_tensor(out, fp(k.eq), wide(k.best), ALU.is_equal).then_inc(*dve.end(p + "pick"))


def l0_ffn(nc, chip):
    E = 8
    with ExitStack() as ctx:
        sb = lambda n, s, dt=F32: ctx.enter_context(nc.sbuf_tensor(f"l0f_{n}", s, dt))
        pe_s, dve_s, act_s, pool_s, ready = stage_sems(nc, ctx, "l0f")
        t, k = Tail(nc, ctx, "l0f"), Pick(nc, ctx, "l0f", E)
        xb, xT = sb("xb", [P, QT, D]), sb("xT", [P, S])
        gate, one, two = sb("gate", [P, QT, E]), sb("one", [P, QT, E]), sb("two", [P, QT, E])
        mx, den = sb("mx", [P, QT]), sb("den", [P, QT])
        prod, mixed = sb("prod", [P, QT, E, D]), sb("mixed", [P, QT, D])
        ps, w = chip.ps, chip.w
        pe = Steps(pe_s, ["xT", "logits", "experts"])
        dve = Steps(dve_s, ["x", "xT", "gmax", "shift", "den", "rden", "gate"] + pick_steps("first") + ["rest"]
                    + pick_steps("second") + ["sel", "kept", "kden", "rkden", "weight", "prod", "mixed"] + TAIL_DVE)
        act = Steps(act_s, ["exp"])
        pool = Steps(pool_s, TAIL_POOL)
        wide = lambda x: fp(x).unsqueeze(2).to_broadcast([P, QT, E])
        block = ctx.enter_context(nc.Block())

        @block.gpsimd
        def _(eng):
            with eng.Fori(0, B) as b:
                tail_pool(nc, eng, chip, t, dve, pool, b)

        @block.scalar
        def _(eng):
            with eng.Fori(0, B) as b:
                eng.wait_ge(*dve.done("shift", b))
                nc.scalar.activation(fp(gate), fp(gate), ACT.Exp).then_inc(*act.end("exp"))

        @block.vector
        def _(eng):
            with eng.Fori(0, B) as b:
                nc.vector.tensor_copy(fp(xb), chip.x_tok[:, b, :, :]).then_inc(*dve.end("x"))
                eng.wait_ge(*pe.done("xT", b))
                nc.vector.tensor_copy(fp(xT), ps[:, 6, 0:S]).then_inc(*dve.end("xT"))
                eng.wait_ge(*pe.done("logits", b))
                logits = ps[:, 7, 0:QT * E].rearrange("p (t e) -> p t e", e=E)
                nc.vector.tensor_reduce(fp(mx), logits, AX.X, ALU.max).then_inc(*dve.end("gmax"))
                eng.wait_ge(*dve.done("gmax", b))
                nc.vector.tensor_tensor(fp(gate), logits, wide(mx), ALU.subtract).then_inc(*dve.end("shift"))
                eng.wait_ge(*act.done("exp", b))
                nc.vector.tensor_reduce(fp(den), fp(gate), AX.X, ALU.add).then_inc(*dve.end("den"))
                eng.wait_ge(*dve.done("den", b))
                nc.vector.reciprocal(fp(den), fp(den)).then_inc(*dve.end("rden"))
                eng.wait_ge(*dve.done("rden", b))
                nc.vector.tensor_tensor(fp(gate), fp(gate), wide(den), ALU.mult).then_inc(*dve.end("gate"))
                eng.wait_ge(*dve.done("gate", b))
                pick_first(nc, eng, chip, k, dve, b, "first", fp(gate), fp(one))
                eng.wait_ge(*dve.done("firstpick", b))
                nc.vector.scalar_tensor_tensor(fp(two), fp(one), -2.0, fp(gate), ALU.mult, ALU.add).then_inc(*dve.end("rest"))
                eng.wait_ge(*dve.done("rest", b))
                pick_first(nc, eng, chip, k, dve, b, "second", fp(two), fp(two))
                eng.wait_ge(*dve.done("secondpick", b))
                nc.vector.tensor_tensor(fp(one), fp(one), fp(two), ALU.add).then_inc(*dve.end("sel"))
                eng.wait_ge(*dve.done("sel", b))
                nc.vector.tensor_tensor(fp(gate), fp(gate), fp(one), ALU.mult).then_inc(*dve.end("kept"))
                eng.wait_ge(*dve.done("kept", b))
                nc.vector.tensor_reduce(fp(den), fp(gate), AX.X, ALU.add).then_inc(*dve.end("kden"))
                eng.wait_ge(*dve.done("kden", b))
                nc.vector.reciprocal(fp(den), fp(den)).then_inc(*dve.end("rkden"))
                eng.wait_ge(*dve.done("rkden", b))
                nc.vector.tensor_tensor(fp(gate), fp(gate), wide(den), ALU.mult).then_inc(*dve.end("weight"))
                eng.wait_ge(*dve.done("weight", b))
                eng.wait_ge(*pe.done("experts", b))
                for qt in range(QT):
                    last = nc.vector.tensor_tensor(prod[:, qt, :, :],
                                                   ps[:, 2 * qt:2 * qt + 2, :].rearrange("p a (e d) -> p (a e) d", d=D),
                                                   gate[:, qt, :].unsqueeze(2).to_broadcast([P, E, D]), ALU.mult)
                last.then_inc(*dve.end("prod"))
                eng.wait_ge(*dve.done("prod", b))
                for qt in range(QT):
                    last = nc.vector.tensor_reduce(mixed[:, qt, :], prod[:, qt, :, :].rearrange("p e d -> p d e"), AX.X, ALU.add)
                last.then_inc(*dve.end("mixed"))
                eng.wait_ge(*dve.done("mixed", b))
                tail_dve(nc, eng, chip, t, dve, pool, b, fp(mixed), fp(xb))

        @block.tensor
        def _(eng):
            with eng.Fori(0, B) as b:
                eng.wait_ge(*dve.done("x", b))
                for qt in range(QT):
                    last = nc.tensor.transpose(ps[:, 6, qt * P:(qt + 1) * P], xb[:, qt, :], chip.ident[:, :])
                last.then_inc(*pe.end("xT"))
                eng.wait_ge(*dve.done("xT", b))
                for qt in range(QT):
                    out = ps[:, 7, qt * E:(qt + 1) * E]
                    nc.tensor.matmul(out, xT[:, qt * P:(qt + 1) * P], w["L0_ffn_Wg"], start=True, stop=False)
                    last = nc.tensor.matmul(out, chip.ones[0:1, 0:P], w["L0_ffn_bg"], start=False, stop=True)
                last.then_inc(*pe.end("logits"))
                for qt in range(QT):
                    for a in range(2):
                        out = ps[:, 2 * qt + a, :]
                        nc.tensor.matmul(out, xT[:, qt * P:(qt + 1) * P],
                                         w["L0_ffn_We"][:, 4 * a:4 * a + 4, :].rearrange("p e d -> p (e d)"), start=True, stop=False)
                        last = nc.tensor.matmul(out, chip.ones[0:1, 0:P], w["L0_ffn_be"][:, 512 * a:512 * a + 512],
                                                start=False, stop=True)
                last.then_inc(*pe.end("experts"))


def l1_xattn(nc, chip):
    with ExitStack() as ctx:
        sb = lambda n, s, dt=F32: ctx.enter_context(nc.sbuf_tensor(f"l1x_{n}", s, dt))
        pe_s, dve_s, act_s, pool_s, ready = stage_sems(nc, ctx, "l1x")
        t = Tail(nc, ctx, "l1x")
        xb, xT, cT = sb("xb", [P, QT, D]), sb("xT", [P, S]), sb("cT", [P, S2])
        qT, kT, v = sb("qT", [P, S]), sb("kT", [P, S2]), sb("v", [P, CT, D])
        nm, den, rden = sb("nm", [P, QT]), sb("den", [P, QT]), sb("rden", [P, QT])
        pr, prT, out_sb = sb("pr", [P, QT, S2]), sb("prT", [P, QT, CT, P]), sb("out", [P, QT, D])
        ps, w = chip.ps, chip.w
        pe = Steps(pe_s, ["xT", "kv", "q", "s", "prT", "o"])
        dve = Steps(dve_s, ["x", "xT", "k", "v", "q", "nm", "rden", "prT", "o"] + TAIL_DVE)
        act = Steps(act_s, ["exp"])
        pool = Steps(pool_s, TAIL_POOL)
        block = ctx.enter_context(nc.Block())

        @block.gpsimd
        def _(eng):
            with eng.Fori(0, B) as b:
                tail_pool(nc, eng, chip, t, dve, pool, b)

        @block.scalar
        def _(eng):
            with eng.Fori(0, B) as b:
                eng.wait_ge(*dve.done("nm", b))
                for qt in range(QT):
                    last = nc.scalar.activation(pr[:, qt, :], ps[:, 3 + qt, :], ACT.Exp, bias=nm[:, qt:qt + 1],
                                                accum_out=den[:, qt:qt + 1])
                last.then_inc(*act.end("exp"))

        @block.vector
        def _(eng):
            with eng.Fori(0, B) as b:
                nc.vector.tensor_copy(fp(xb), chip.x_tok[:, b, :, :])
                nc.vector.tensor_copy(fp(cT), chip.ctxT[:, b, :]).then_inc(*dve.end("x"))
                eng.wait_ge(*pe.done("xT", b))
                nc.vector.tensor_copy(fp(xT), ps[:, 6, 0:S]).then_inc(*dve.end("xT"))
                eng.wait_ge(*pe.done("kv", b))
                nc.vector.tensor_scalar(fp(kT), ps[:, 0, :], w["L1_xattn_Wk_b"], None, ALU.add).then_inc(*dve.end("k"))
                nc.vector.tensor_copy(fp(v), ps[:, 1, :].rearrange("p (t d) -> p t d", t=CT)).then_inc(*dve.end("v"))
                eng.wait_ge(*pe.done("q", b))
                nc.vector.tensor_scalar(fp(qT), ps[:, 2, 0:S], w["L1_xattn_Wq_b"], float(np.float32(1) / np.sqrt(np.float32(D))),
                                        ALU.add, ALU.mult).then_inc(*dve.end("q"))
                eng.wait_ge(*pe.done("s", b))
                nc.vector.tensor_reduce(fp(nm), ps[:, 3:5, :], AX.X, ALU.max, negate=True).then_inc(*dve.end("nm"))
                eng.wait_ge(*act.done("exp", b))
                nc.vector.reciprocal(fp(rden), fp(den)).then_inc(*dve.end("rden"))
                eng.wait_ge(*pe.done("prT", b))
                for qt, bank in enumerate((5, 0)):
                    last = nc.vector.tensor_copy(prT[:, qt, :, :], ps[:, bank, :].rearrange("p (t q) -> p t q", t=CT))
                last.then_inc(*dve.end("prT"))
                eng.wait_ge(*pe.done("o", b))
                eng.wait_ge(*dve.done("rden", b))
                for qt in range(QT):
                    last = nc.vector.tensor_scalar(out_sb[:, qt, :], ps[:, 7, qt * P:(qt + 1) * P], rden[:, qt:qt + 1], None, ALU.mult)
                last.then_inc(*dve.end("o"))
                eng.wait_ge(*dve.done("o", b))
                tail_dve(nc, eng, chip, t, dve, pool, b, fp(out_sb), fp(xb))

        @block.tensor
        def _(eng):
            with eng.Fori(0, B) as b:
                eng.wait_ge(*dve.done("x", b))
                for qt in range(QT):
                    last = nc.tensor.transpose(ps[:, 6, qt * P:(qt + 1) * P], xb[:, qt, :], chip.ident[:, :])
                last.then_inc(*pe.end("xT"))
                nc.tensor.matmul(ps[:, 0, :], w["L1_xattn_Wk_w"][:, 0, :], fp(cT), start=True, stop=True)
                for kt in range(CT):
                    out = ps[:, 1, kt * P:(kt + 1) * P]
                    nc.tensor.matmul(out, cT[:, kt * P:(kt + 1) * P], w["L1_xattn_Wv_w"][:, 0, :], start=True, stop=False)
                    last = nc.tensor.matmul(out, chip.ones[0:1, 0:P], w["L1_xattn_Wv_b"], start=False, stop=True)
                last.then_inc(*pe.end("kv"))
                eng.wait_ge(*dve.done("xT", b))
                nc.tensor.matmul(ps[:, 2, 0:S], w["L1_xattn_Wq_w"][:, 0, :], fp(xT), start=True, stop=True).then_inc(*pe.end("q"))
                eng.wait_ge(*dve.done("q", b))
                for qt in range(QT):
                    last = nc.tensor.matmul(ps[:, 3 + qt, :], qT[:, qt * P:(qt + 1) * P], fp(kT), start=True, stop=True)
                last.then_inc(*pe.end("s"))
                eng.wait_ge(*act.done("exp", b))
                for qt, bank in enumerate((5, 0)):
                    for kt in range(CT):
                        last = nc.tensor.transpose(ps[:, bank, kt * P:(kt + 1) * P], pr[:, qt, kt * P:(kt + 1) * P], chip.ident[:, :])
                last.then_inc(*pe.end("prT"))
                eng.wait_ge(*dve.done("prT", b))
                for qt in range(QT):
                    for kt in range(CT):
                        last = nc.tensor.matmul(ps[:, 7, qt * P:(qt + 1) * P], prT[:, qt, kt, :], v[:, kt, :],
                                                start=(kt == 0), stop=(kt == CT - 1))
                last.then_inc(*pe.end("o"))


def l2_xattn(nc, chip):
    with ExitStack() as ctx:
        sb = lambda n, s, dt=F32: ctx.enter_context(nc.sbuf_tensor(f"l2x_{n}", s, dt))
        pe_s, dve_s, act_s, pool_s, ready = stage_sems(nc, ctx, "l2x")
        t = Tail(nc, ctx, "l2x")
        xb, xT, cT, cb = sb("xb", [P, QT, D]), sb("xT", [P, S]), sb("cT", [P, S2]), sb("cb", [P, CT, D])
        xw, bsum = sb("xw", [P, S]), sb("bsum", [P, 1])
        nm, den, rden, top = sb("nm", [P, QT]), sb("den", [P, QT]), sb("rden", [P, QT]), sb("top", [P, QT])
        pr, prT = sb("pr", [P, QT, S2]), sb("prT", [P, CT, QT, P])
        att, xatt, xq = sb("att", [P, S]), sb("xatt", [P, S]), sb("xq", [P, S])
        rowmax, rowden, row = sb("rowmax", [1, 1]), sb("rowden", [1, 2]), sb("row", [1, S])
        col, q2c = sb("col", [P, QT]), sb("q2c", [P, 1])
        ps, w = chip.ps, chip.w
        pe = Steps(pe_s, ["xT", "s", "toprow", "prT", "att", "col", "q2c", "z"])
        dve = Steps(dve_s, ["bsum1", "x", "xT", "xw", "nm", "top", "rowmax", "rden", "norm", "prT", "att", "xatt",
                            "rowden", "rown", "col", "q2c", "xq"] + TAIL_DVE)
        act = Steps(act_s, ["exp", "rowexp"])
        pool = Steps(pool_s, TAIL_POOL)
        block = ctx.enter_context(nc.Block())

        @block.gpsimd
        def _(eng):
            with eng.Fori(0, B) as b:
                tail_pool(nc, eng, chip, t, dve, pool, b)

        @block.scalar
        def _(eng):
            with eng.Fori(0, B) as b:
                eng.wait_ge(*dve.done("nm", b))
                for qt in range(QT):
                    last = nc.scalar.activation(pr[:, qt, :], ps[:, 3 + qt, :], ACT.Exp, bias=nm[:, qt:qt + 1],
                                                accum_out=den[:, qt:qt + 1])
                last.then_inc(*act.end("exp"))
                eng.wait_ge(*dve.done("rowmax", b))
                nc.scalar.activation(fp(row), ps[0:1, 2, 0:S], ACT.Exp, bias=fp(rowmax), accum_out=rowden[:, 0:1])\
                    .then_inc(*act.end("rowexp"))

        @block.vector
        def _(eng):
            with eng.Fori(0, B) as b:
                nc.vector.tensor_copy(fp(xb), chip.x_tok[:, b, :, :])
                nc.vector.tensor_copy(fp(cb), chip.ctx_tok[:, b, :, :])
                nc.vector.tensor_copy(fp(cT), chip.ctxT[:, b, :])
                nc.vector.tensor_tensor(fp(bsum), w["L2_xattn_b_c"], w["L2_xattn_b_q"], ALU.add).then_inc(*dve.end("bsum1"))
                eng.wait_ge(*dve.done("bsum1", b))
                nc.vector.tensor_tensor(fp(bsum), fp(bsum), w["L2_xattn_b_cq"], ALU.add).then_inc(*dve.end("x"))
                eng.wait_ge(*pe.done("xT", b))
                nc.vector.tensor_copy(fp(xT), ps[:, 6, 0:S]).then_inc(*dve.end("xT"))
                nc.vector.tensor_scalar(fp(xw), ps[:, 6, 0:S], w["L2_xattn_w_cq"], w["L2_xattn_w_q"], ALU.mult, ALU.add)\
                    .then_inc(*dve.end("xw"))
                eng.wait_ge(*pe.done("s", b))
                nc.vector.tensor_reduce(fp(nm), ps[:, 3:5, :], AX.X, ALU.max, negate=True).then_inc(*dve.end("nm"))
                eng.wait_ge(*dve.done("nm", b))
                eng.wait_ge(*dve.done("x", b))
                nc.vector.scalar_tensor_tensor(fp(top), ps[:, 7, 0:QT], bsum[:, 0:1], fp(nm), ALU.add, ALU.subtract)\
                    .then_inc(*dve.end("top"))
                eng.wait_ge(*pe.done("toprow", b))
                nc.vector.tensor_reduce(fp(rowmax), ps[0:1, 2, 0:S], AX.X, ALU.max, negate=True).then_inc(*dve.end("rowmax"))
                eng.wait_ge(*act.done("exp", b))
                nc.vector.reciprocal(fp(rden), fp(den)).then_inc(*dve.end("rden"))
                eng.wait_ge(*dve.done("rden", b))
                for qt in range(QT):
                    last = nc.vector.tensor_scalar(pr[:, qt, :], pr[:, qt, :], rden[:, qt:qt + 1], None, ALU.mult)
                last.then_inc(*dve.end("norm"))
                eng.wait_ge(*pe.done("prT", b))
                for qt, bank in enumerate((5, 0)):
                    last = nc.vector.tensor_copy(prT[:, :, qt, :], ps[:, bank, :].rearrange("p (t q) -> p t q", t=CT))
                last.then_inc(*dve.end("prT"))
                eng.wait_ge(*pe.done("att", b))
                nc.vector.tensor_copy(fp(att), ps[:, 1, 0:S]).then_inc(*dve.end("att"))
                nc.vector.tensor_tensor(fp(xatt), ps[:, 1, 0:S], fp(xT), ALU.mult).then_inc(*dve.end("xatt"))
                eng.wait_ge(*act.done("rowexp", b))
                nc.vector.reciprocal(rowden[:, 1:2], rowden[:, 0:1]).then_inc(*dve.end("rowden"))
                eng.wait_ge(*dve.done("rowden", b))
                nc.vector.tensor_scalar(fp(row), fp(row), rowden[:, 1:2], None, ALU.mult).then_inc(*dve.end("rown"))
                eng.wait_ge(*pe.done("col", b))
                nc.vector.tensor_copy(fp(col), ps[:, 2, 0:QT]).then_inc(*dve.end("col"))
                eng.wait_ge(*pe.done("q2c", b))
                nc.vector.tensor_copy(fp(q2c), ps[:, 2, 4:5]).then_inc(*dve.end("q2c"))
                eng.wait_ge(*dve.done("q2c", b))
                nc.vector.tensor_scalar(fp(xq), fp(xT), q2c[:, 0:1], None, ALU.mult).then_inc(*dve.end("xq"))
                eng.wait_ge(*pe.done("z", b))
                tail_dve(nc, eng, chip, t, dve, pool, b, ps[:, 7, 0:S].rearrange("p (t d) -> p t d", t=QT), fp(xb))

        @block.tensor
        def _(eng):
            with eng.Fori(0, B) as b:
                eng.wait_ge(*dve.done("x", b))
                for qt in range(QT):
                    last = nc.tensor.transpose(ps[:, 6, qt * P:(qt + 1) * P], xb[:, qt, :], chip.ident[:, :])
                last.then_inc(*pe.end("xT"))
                eng.wait_ge(*dve.done("xw", b))
                for qt in range(QT):
                    nc.tensor.matmul(ps[:, 3 + qt, :], xw[:, qt * P:(qt + 1) * P], fp(cT), start=True, stop=True)
                    last = nc.tensor.matmul(ps[:, 7, qt:qt + 1], xT[:, qt * P:(qt + 1) * P], w["L2_xattn_w_c"], start=True, stop=True)
                last.then_inc(*pe.end("s"))
                eng.wait_ge(*dve.done("top", b))
                for qt in range(QT):
                    last = nc.tensor.transpose(ps[0:1, 2, qt * P:(qt + 1) * P], top[:, qt:qt + 1], chip.ident[:, :])
                last.then_inc(*pe.end("toprow"))
                eng.wait_ge(*dve.done("norm", b))
                for qt, bank in enumerate((5, 0)):
                    for kt in range(CT):
                        last = nc.tensor.transpose(ps[:, bank, kt * P:(kt + 1) * P], pr[:, qt, kt * P:(kt + 1) * P], chip.ident[:, :])
                last.then_inc(*pe.end("prT"))
                eng.wait_ge(*dve.done("prT", b))
                for kt in range(CT):
                    last = nc.tensor.matmul(ps[:, 1, 0:S], cb[:, kt, :], prT[:, kt, :, :].rearrange("p t q -> p (t q)"),
                                            start=(kt == 0), stop=(kt == CT - 1))
                last.then_inc(*pe.end("att"))
                eng.wait_ge(*dve.done("rown", b))
                for qt in range(QT):
                    last = nc.tensor.matmul(ps[:, 2, qt:qt + 1], row[:, qt * P:(qt + 1) * P], chip.ones[0:1, 0:1], start=True, stop=True)
                last.then_inc(*pe.end("col"))
                eng.wait_ge(*dve.done("col", b))
                for qt in range(QT):
                    last = nc.tensor.matmul(ps[:, 2, 4:5], xb[:, qt, :], col[:, qt:qt + 1], start=(qt == 0), stop=(qt == QT - 1))
                last.then_inc(*pe.end("q2c"))
                eng.wait_ge(*dve.done("xq", b))
                for qt in range(QT):
                    out = ps[:, 7, qt * P:(qt + 1) * P]
                    for c, part in enumerate((xT, att, xatt, xq)):
                        nc.tensor.matmul(out, part[:, qt * P:(qt + 1) * P], w["L2_xattn_W_l"][:, c, :], start=(c == 0), stop=False)
                    last = nc.tensor.matmul(out, chip.ones[0:1, 0:P], w["L2_xattn_b_l"], start=False, stop=True)
                last.then_inc(*pe.end("z"))


def l0_xattn(nc, chip):
    H, DH, NK = 8, 64, S2 + S
    KT = NK // P
    with ExitStack() as ctx:
        sb = lambda n, s, dt=F32: ctx.enter_context(nc.sbuf_tensor(f"l0x_{n}", s, dt))
        pe_s, dve_s, act_s, pool_s, ready = stage_sems(nc, ctx, "l0x")
        t = Tail(nc, ctx, "l0x")
        xb = sb("xb", [P, QT, D])
        z = sb("z", [P, KT, D])
        zs, zmv, zr = sb("zs", [P, KT, 6]), sb("zmv", [P, KT, 2]), sb("zr", [P, KT])
        kvT = sb("kvT", [P, NK])
        qT, kT = sb("qT", [P, H, S]), sb("kT", [P, H, NK])
        v = sb("v", [P, KT, H, P])
        nm, e = sb("nm", [P, QT, H, P]), sb("e", [P, 4, 512])
        rec, attT = sb("rec", [P, 2, S]), sb("attT", [P, H // 2, S])
        mask_rows, rows = sb("mask_rows", [2, B, NK]), sb("rows", [2, NK])
        mask_u8 = sb("mask_u8", [1, B, S2], U8)
        ys, ymv, yr = sb("ys", [P, QT, 6]), sb("ymv", [P, QT, 2]), sb("yr", [P, QT])
        yn = sb("yn", [P, QT, D])
        ps, w = chip.ps, chip.w
        wq, wkv = w["L0_xattn_w_q"], w["L0_xattn_w_kv"]
        masked = ctx.enter_context(nc.semaphore("l0x_mask_rows"))
        units = [(h, kp) for h in range(H) for kp in range(KT // 2)]
        names = []
        for u in range(len(units) + 1):
            names += ([f"sT{u}"] if u < len(units) else []) + ([f"pv{u - 1}"] if u else [])
        pe = Steps(pe_s, ["zT", "rows", "q"] + [f"k{h}" for h in range(H)] + [f"v{i}" for i in range(KT)]
                   + [f"s{h}" for h in range(H)] + ["nmT"] + names + ["y"])
        dve = Steps(dve_s, ["x", "zstats", "zvar", "zn", "kvT", "qrows", "q"] + [f"k{h}" for h in range(0, H, 2)]
                    + [f"v{i}" for i in range(0, KT, 2)] + [f"max{h}" for h in range(H)] + ["guarded"]
                    + [f"{s}{h}" for h in range(H) for s in ("rec", "att")]
                    + ["ystats", "yvar", "yn", "yg", "yb"] + TAIL_DVE)
        act = Steps(act_s, ["rows"] + [f"k{h}" for h in range(1, H, 2)] + [f"v{i}" for i in range(1, KT, 2)]
                    + [f"exp{u}" for u in range(len(units))])
        pool = Steps(pool_s, ["zeps", "zr", "yeps", "yr"] + TAIL_POOL)
        kd = lambda h: dve.done if h % 2 == 0 else act.done
        block = ctx.enter_context(nc.Block())

        @block.sync
        def _(sp):
            sp.dma_start(fp(mask_u8), chip.a["mask_BxS2_bf1"].rearrange("(o b) k -> o b k", o=1)).then_inc(ready, 16)
            sp.wait_ge(ready, 16)

        @block.gpsimd
        def _(eng):
            nc.gpsimd.memset(fp(nm), 0.0)
            nc.gpsimd.memset(v[:, :, 0:H:2, DH:P], 1.0)
            nc.gpsimd.memset(v[:, :, 1:H:2, 0:DH], 1.0).then_inc(masked, 1)
            with eng.Fori(0, B) as b:
                eng.wait_ge(*dve.done("zvar", b))
                nc.gpsimd.tensor_tensor(fp(zr), zmv[:, :, 1], chip.eps[:, 0:KT], ALU.add).then_inc(*pool.end("zeps"))
                eng.wait_ge(*pool.done("zeps", b))
                nc.gpsimd.tensor_tensor(fp(zr), fp(zr), chip.neghalf[:, 0:KT], ALU.pow).then_inc(*pool.end("zr"))
                eng.wait_ge(*dve.done("yvar", b))
                nc.gpsimd.tensor_tensor(fp(yr), ymv[:, :, 1], chip.eps[:, 0:QT], ALU.add).then_inc(*pool.end("yeps"))
                eng.wait_ge(*pool.done("yeps", b))
                nc.gpsimd.tensor_tensor(fp(yr), fp(yr), chip.neghalf[:, 0:QT], ALU.pow).then_inc(*pool.end("yr"))
                tail_pool(nc, eng, chip, t, dve, pool, b)

        @block.vector
        def _(eng):
            nc.vector.memset(fp(mask_rows), 1.0).then_inc(masked, 1)
            eng.wait_ge(masked, 2)
            nc.vector.memset(mask_rows[0:1, :, S2:NK], 0.0)
            eng.wait_ge(ready, 16)
            nc.vector.tensor_scalar(mask_rows[0:1, :, 0:S2], fp(mask_u8), 0, MASKED, ALU.is_equal, ALU.mult).then_inc(masked, 1)
            eng.wait_ge(masked, 3)
            with eng.Fori(0, B) as b:
                nc.vector.tensor_copy(fp(rows), mask_rows[:, b, :])
                nc.vector.tensor_copy(fp(xb), chip.x_tok[:, b, :, :])
                nc.vector.tensor_copy(z[:, CT:KT, :], chip.x_tok[:, b, :, :])
                nc.vector.tensor_copy(z[:, 0:CT, :], chip.ctx_tok[:, b, :, :]).then_inc(*dve.end("x"))
                eng.wait_ge(*dve.done("x", b))
                for i in range(KT):
                    last = nc.vector.bn_stats(zs[:, i, :], z[:, i, :])
                last.then_inc(*dve.end("zstats"))
                eng.wait_ge(*dve.done("zstats", b))
                nc.vector.memset(chip.scratch[:, 2:3], 0.0)
                for i in range(KT):
                    last = nc.vector.bn_aggr(zmv[:, i, :], zs[:, i, :])
                last.then_inc(*dve.end("zvar"))
                eng.wait_ge(*pool.done("zr", b))
                for i in range(KT):
                    last = nc.vector.tensor_scalar(z[:, i, :], z[:, i, :], zmv[:, i, 0:1], zr[:, i:i + 1], ALU.subtract, ALU.mult)
                last.then_inc(*dve.end("zn"))
                eng.wait_ge(*pe.done("zT", b))
                nc.vector.tensor_scalar(kvT[:, 0:S2], ps[:, 0, :], w["L0_xattn_g_x"], w["L0_xattn_b_x"], ALU.mult, ALU.add)
                nc.vector.tensor_scalar(kvT[:, S2:NK], ps[:, 1, 0:S], w["L0_xattn_g_l"], w["L0_xattn_b_l"], ALU.mult, ALU.add)\
                    .then_inc(*dve.end("kvT"))
                wide_const = w["c_qrows"][DH:P, :].unsqueeze(1).to_broadcast([P - DH, H, S])
                nc.vector.tensor_copy(qT[DH:P, :, :], wide_const).then_inc(*dve.end("qrows"))
                eng.wait_ge(*pe.done("q", b))
                nc.vector.tensor_scalar(qT[0:DH, :, :], ps[0:DH, 4:8, :].rearrange("p a (h q) -> p (a h) q", q=S),
                                        DH ** -0.5, None, ALU.mult).then_inc(*dve.end("q"))
                for h in range(0, H, 2):
                    eng.wait_ge(*pe.done(f"k{h}", b))
                    nc.vector.tensor_copy(kT[0:DH, h, :], ps[0:DH, 0:2, :].rearrange("p a k -> p (a k)")[:, 0:NK])\
                        .then_inc(*dve.end(f"k{h}"))
                for i in range(0, KT, 2):
                    eng.wait_ge(*pe.done(f"v{i}", b))
                    src = ps[:, 4 + i % 4, :].rearrange("p (h d) -> p h d", d=DH)
                    nc.vector.tensor_copy(v[:, i, 0:H:2, 0:DH], src[:, 0:H:2, :])
                    nc.vector.tensor_copy(v[:, i, 1:H:2, DH:P], src[:, 1:H:2, :]).then_inc(*dve.end(f"v{i}"))
                for h in range(H):
                    eng.wait_ge(*pe.done(f"s{h}", b))
                    bank = 4 * (h % 2)
                    nc.vector.tensor_reduce(nm[:, :, h, DH], ps[:, bank:bank + 4, :].rearrange("p (q a) k -> p q (a k)", a=2)[:, :, 0:NK],
                                            AX.X, ALU.max, negate=True).then_inc(*dve.end(f"max{h}"))
                eng.wait_ge(*pe.done("nmT", b))
                nc.vector.tensor_tensor(qT[DH:P, :, :], ps[DH:P, 0:4, :].rearrange("p a (h q) -> p (a h) q", q=S), wide_const, ALU.add)\
                    .then_inc(*dve.end("guarded"))
                for h in range(H):
                    eng.wait_ge(*pe.done(f"pv{(KT // 2) * h + KT // 2 - 1}", b))
                    dims, den = (slice(0, DH), slice(DH, P)) if h % 2 == 0 else (slice(DH, P), slice(0, DH))
                    nc.vector.reciprocal(rec[dims, h % 2, :], ps[den, 4 + h % 2, 0:S]).then_inc(*dve.end(f"rec{h}"))
                    eng.wait_ge(*dve.done(f"rec{h}", b))
                    nc.vector.tensor_tensor(attT[dims, h // 2, :], ps[dims, 4 + h % 2, 0:S], rec[dims, h % 2, :], ALU.mult)\
                        .then_inc(*dve.end(f"att{h}"))
                eng.wait_ge(*pe.done("y", b))
                for q in range(QT):
                    last = nc.vector.bn_stats(ys[:, q, :], ps[:, 6, q * P:(q + 1) * P])
                last.then_inc(*dve.end("ystats"))
                eng.wait_ge(*dve.done("ystats", b))
                nc.vector.memset(chip.scratch[:, 3:4], 0.0)
                for q in range(QT):
                    last = nc.vector.bn_aggr(ymv[:, q, :], ys[:, q, :])
                last.then_inc(*dve.end("yvar"))
                eng.wait_ge(*pool.done("yr", b))
                for q in range(QT):
                    last = nc.vector.tensor_scalar(yn[:, q, :], ps[:, 6, q * P:(q + 1) * P], ymv[:, q, 0:1], yr[:, q:q + 1],
                                                   ALU.subtract, ALU.mult)
                last.then_inc(*dve.end("yn"))
                eng.wait_ge(*dve.done("yn", b))
                nc.vector.tensor_tensor(fp(yn), fp(yn), w["L0_xattn_g_o"].unsqueeze(1).to_broadcast([P, QT, D]), ALU.mult)\
                    .then_inc(*dve.end("yg"))
                eng.wait_ge(*dve.done("yg", b))
                nc.vector.tensor_tensor(fp(yn), fp(yn), w["L0_xattn_b_o"].unsqueeze(1).to_broadcast([P, QT, D]), ALU.add)\
                    .then_inc(*dve.end("yb"))
                eng.wait_ge(*dve.done("yb", b))
                tail_dve(nc, eng, chip, t, dve, pool, b, fp(yn), fp(xb))

        @block.scalar
        def _(eng):
            with eng.Fori(0, B) as b:
                eng.wait_ge(*pe.done("rows", b))
                nc.scalar.activation(kT[DH:P, :, :], ps[DH:P, 2:4, :].rearrange("p a k -> p (a k)")[:, 0:NK].unsqueeze(1)
                                     .to_broadcast([P - DH, H, NK]), ACT.Copy).then_inc(*act.end("rows"))
                for h in range(1, H, 2):
                    eng.wait_ge(*pe.done(f"k{h}", b))
                    nc.scalar.activation(kT[0:DH, h, :], ps[0:DH, 2:4, :].rearrange("p a k -> p (a k)")[:, 0:NK], ACT.Copy)\
                        .then_inc(*act.end(f"k{h}"))
                for i in range(1, KT, 2):
                    eng.wait_ge(*pe.done(f"v{i}", b))
                    src = ps[:, 4 + i % 4, :].rearrange("p (h d) -> p h d", d=DH)
                    nc.scalar.activation(v[:, i, 0:H:2, 0:DH], src[:, 0:H:2, :], ACT.Copy)
                    nc.scalar.activation(v[:, i, 1:H:2, DH:P], src[:, 1:H:2, :], ACT.Copy).then_inc(*act.end(f"v{i}"))
                for u in range(len(units)):
                    eng.wait_ge(*pe.done(f"sT{u}", b))
                    if u >= 4:
                        eng.wait_ge(*pe.done(f"pv{u - 4}", b))
                    nc.scalar.activation(e[:, u % 4, :], ps[:, u % 4, :], ACT.Exp).then_inc(*act.end(f"exp{u}"))

        @block.tensor
        def _(eng):
            eng.wait_ge(masked, 3)
            with eng.Fori(0, B) as b:
                eng.wait_ge(*dve.done("zn", b))
                for i in range(KT):
                    last = nc.tensor.transpose(ps[:, i // 4, (i % 4) * P:(i % 4 + 1) * P], z[:, i, :], chip.ident[:, :])
                last.then_inc(*pe.end("zT"))
                nc.tensor.matmul(ps[:, 2, :], w["c_krows"], rows[:, 0:512], start=True, stop=True)
                nc.tensor.matmul(ps[:, 3, 0:S], w["c_krows"], rows[:, 512:NK], start=True, stop=True).then_inc(*pe.end("rows"))
                eng.wait_ge(*dve.done("kvT", b))
                for h in range(H):
                    last = nc.tensor.matmul(ps[0:DH, 4 + h // 2, (h % 2) * S:(h % 2 + 1) * S], wq[:, h * DH:(h + 1) * DH],
                                            kvT[:, S2:NK], start=True, stop=True)
                last.then_inc(*pe.end("q"))
                for h in range(H):
                    if h == 1:
                        eng.wait_ge(*act.done("rows", b))
                    if h >= 2:
                        eng.wait_ge(*kd(h)(f"k{h - 2}", b))
                    wk = wkv[:, h * DH:(h + 1) * DH]
                    bank = 2 * (h % 2)
                    nc.tensor.matmul(ps[0:DH, bank, :], wk, kvT[:, 0:512], start=True, stop=True)
                    nc.tensor.matmul(ps[0:DH, bank + 1, 0:S], wk, kvT[:, 512:NK], start=True, stop=True).then_inc(*pe.end(f"k{h}"))
                eng.wait_ge(*dve.done("q", b))
                for i in range(KT):
                    if i >= 4:
                        eng.wait_ge(*kd(i)(f"v{i - 4}", b))
                    nc.tensor.matmul(ps[:, 4 + i % 4, :], kvT[:, i * P:(i + 1) * P], wkv[:, 512:1024], start=True, stop=True)\
                        .then_inc(*pe.end(f"v{i}"))
                eng.wait_ge(*dve.done(f"v{KT - 2}", b))
                eng.wait_ge(*act.done(f"v{KT - 1}", b))
                for h in range(H):
                    if h >= 2:
                        eng.wait_ge(*dve.done(f"max{h - 2}", b))
                    for q in range(QT):
                        bank = 4 * (h % 2) + 2 * q
                        lhs = qT[:, h, q * P:(q + 1) * P]
                        nc.tensor.matmul(ps[:, bank, :], lhs, kT[:, h, 0:512], start=True, stop=True)
                        last = nc.tensor.matmul(ps[:, bank + 1, 0:S], lhs, kT[:, h, 512:NK], start=True, stop=True)
                    last.then_inc(*pe.end(f"s{h}"))
                eng.wait_ge(*dve.done(f"max{H - 1}", b))
                for h in range(H):
                    for q in range(QT):
                        at = (h % 2) * S + q * P
                        last = nc.tensor.transpose(ps[:, h // 2, at:at + P], nm[:, q, h, :], chip.ident[:, :])
                last.then_inc(*pe.end("nmT"))
                eng.wait_ge(*dve.done("guarded", b))
                for u in range(len(units) + 1):
                    if u < len(units):
                        h, kp = units[u]
                        if u >= 4:
                            eng.wait_ge(*act.done(f"exp{u - 4}", b))
                        for i in range(2):
                            kt = 2 * kp + i
                            last = nc.tensor.matmul(ps[:, u % 4, i * S:(i + 1) * S], kT[:, h, kt * P:(kt + 1) * P], qT[:, h, :],
                                                    start=True, stop=True)
                        last.then_inc(*pe.end(f"sT{u}"))
                    if u:
                        h, kp = units[u - 1]
                        eng.wait_ge(*act.done(f"exp{u - 1}", b))
                        if kp == 0 and h >= 2:
                            eng.wait_ge(*dve.done(f"att{h - 2}", b))
                        for i in range(2):
                            kt = 2 * kp + i
                            last = nc.tensor.matmul(ps[:, 4 + h % 2, 0:S], v[:, kt, h, :], e[:, (u - 1) % 4, i * S:(i + 1) * S],
                                                    start=(kt == 0), stop=(kt == KT - 1))
                        last.then_inc(*pe.end(f"pv{u - 1}"))
                eng.wait_ge(*dve.done(f"att{H - 1}", b))
                for q in range(QT):
                    for c in range(H // 2):
                        last = nc.tensor.matmul(ps[:, 6, q * P:(q + 1) * P], attT[:, c, q * P:(q + 1) * P],
                                                w["L0_xattn_w_out"][:, c, :], start=(c == 0), stop=(c == H // 2 - 1))
                last.then_inc(*pe.end("y"))


def l2_ffn(nc, chip):
    E, F, T = 8, 512, B * S
    C = F // P
    with ExitStack() as ctx:
        sb = lambda n, s, dt=F32: ctx.enter_context(nc.sbuf_tensor(f"l2f_{n}", s, dt))
        pe_s, dve_s, act_s, pool_s, ready = stage_sems(nc, ctx, "l2f")
        t, k = Tail(nc, ctx, "l2f"), Pick(nc, ctx, "l2f", E)
        xb, xTb, xT = sb("xb", [P, QT, D]), sb("xTb", [P, S]), sb("xT", [P, T])
        logits, one = sb("logits", [P, QT, E]), sb("one", [P, QT, E])
        oneT, shut, sel = sb("oneT", [E, T]), sb("shut", [P, T], BF16), sb("sel", [P, E, P], BF16)
        w1, w2 = sb("w1", [P, 2, F]), sb("w2", [P, 2, C, D])
        b1 = sb("b1", [P, 2 * C])
        hT, yT = sb("hT", [P, 4, 512]), sb("yT", [P, T])
        ps, w = chip.ps, chip.w
        nxt = [ctx.enter_context(nc.semaphore(f"l2f_{e}")) for e in ("gate_pe", "gate_dve", "main_pe", "main_dve", "main_act",
                                                                      "end_pe", "weights0", "weights1", "bias")]
        gpe, gdve = Steps(nxt[0], ["xT", "logits", "oneT"]), Steps(nxt[1], ["x", "xT", "xTall", "logits"] + pick_steps("top") + ["oneT", "shut"])
        units = [(e, c, half) for e in range(2) for c in range(C) for half in range(2)]
        n = len(units)
        names = []
        for u in range(n + 2):
            names += ([f"h{u}"] if u < n else []) + ([f"acc{u - 2}"] if u >= 2 else [])
        mpe = Steps(nxt[2], names)
        mdve, mact = Steps(nxt[3], ["b1"] + [f"r{u}" for u in range(1, n, 2)]), Steps(nxt[4], [f"r{u}" for u in range(0, n, 2)])
        relu = lambda u: (mact if u % 2 == 0 else mdve).done
        pe, dve, pool = Steps(pe_s, ["y"]), Steps(dve_s, ["x"] + TAIL_DVE), Steps(pool_s, TAIL_POOL)
        weights = nxt[6:8]
        block = ctx.enter_context(nc.Block())

        @block.sync
        def _(sp):
            for e in range(E):
                if e >= 2:
                    sp.wait_ge(*mpe.done(f"acc{n // 2 * (e % 2 + 1) - 1}", e // 2 - 1))
                sp.dma_start(w1[:, e % 2, :], chip.a["L2_ffn_W1"][e, :, :]).then_inc(weights[e % 2], 16)
                sp.dma_start(w2[:, e % 2, :, :], chip.a["L2_ffn_W2"][e, :, :].rearrange("(c p) d -> p c d", p=P))\
                    .then_inc(weights[e % 2], 16)

        @block.gpsimd
        def _(eng):
            nc.gpsimd.memset(fp(shut), 0.0)
            nc.gpsimd.memset(fp(sel), 0.0).then_inc(ready, 1)
            with eng.Fori(0, B) as b:
                tail_pool(nc, eng, chip, t, dve, pool, b)

        @block.vector
        def _(eng):
            eng.wait_ge(ready, 1)
            nc.vector.tensor_copy(sel[0:E, :, :], w["c_sel8"]).then_inc(ready, 1)
            with eng.Fori(0, B) as b:
                nc.vector.tensor_copy(fp(xb), chip.x_tok[:, b, :, :]).then_inc(*gdve.end("x"))
                eng.wait_ge(*gpe.done("xT", b))
                nc.vector.tensor_copy(fp(xTb), ps[:, 6, 0:S]).then_inc(*gdve.end("xT"))
                nc.vector.tensor_copy(xT[:, bass.ts(b, S)], ps[:, 6, 0:S]).then_inc(*gdve.end("xTall"))
                eng.wait_ge(*gpe.done("logits", b))
                nc.vector.tensor_copy(fp(logits), ps[:, 7, 0:QT * E].rearrange("p (t e) -> p t e", e=E)).then_inc(*gdve.end("logits"))
                eng.wait_ge(*gdve.done("logits", b))
                pick_first(nc, eng, chip, k, gdve, b, "top", fp(logits), fp(one))
                eng.wait_ge(*gpe.done("oneT", b))
                nc.vector.tensor_scalar(oneT[:, bass.ts(b, S)], ps[0:E, 5, 0:S], 1.0, None, ALU.mult).then_inc(*gdve.end("oneT"))
                nc.vector.tensor_scalar(shut[0:E, bass.ts(b, S)], ps[0:E, 5, 0:S], -1.0, -MASKED, ALU.add, ALU.mult)\
                    .then_inc(*gdve.end("shut"))
            with eng.Fori(0, E // 2) as i:
                nc.vector.tensor_copy(fp(b1), w["L2_ffn_b1"][:, bass.ts(i, 2 * C)]).then_inc(*mdve.end("b1"))
                eng.wait_ge(*mdve.done("b1", i))
                for u, (e, c, half) in enumerate(units):
                    if u % 2:
                        eng.wait_ge(*mpe.done(f"h{u}", i))
                        if u >= 4:
                            eng.wait_ge(*mpe.done(f"acc{u - 4}", i))
                        nc.vector.tensor_scalar(hT[:, u % 4, :], ps[:, u % 4, :], b1[:, e * C + c:e * C + c + 1], 0.0, ALU.add, ALU.max)\
                            .then_inc(*mdve.end(f"r{u}"))
                eng.wait_ge(*mdve.done(f"r{n - 1}", i))
                eng.wait_ge(*mact.done(f"r{n - 2}", i))
            eng.wait_ge(*mpe.passed(E // 2))
            eng.wait_ge(nxt[5], 1)
            nc.vector.tensor_copy(fp(yT), ps[:, 6:8, :].rearrange("p a t -> p (a t)")).then_inc(nxt[8], 1)
            for b in range(B):
                nc.vector.tensor_copy(fp(xb), chip.x_tok[:, b, :, :]).then_inc(*dve.end("x"))
                eng.wait_ge(*dve.done("x", b))
                eng.wait_ge(*pe.done("y", b))
                tail_dve(nc, eng, chip, t, dve, pool, b, ps[:, b % 2, 0:S].rearrange("p (t d) -> p t d", t=QT), fp(xb))

        @block.scalar
        def _(eng):
            with eng.Fori(0, E // 2) as i:
                eng.wait_ge(*mdve.done("b1", i))
                for u, (e, c, half) in enumerate(units):
                    if u % 2 == 0:
                        eng.wait_ge(*mpe.done(f"h{u}", i))
                        if u >= 4:
                            eng.wait_ge(*mpe.done(f"acc{u - 4}", i))
                        nc.scalar.activation(hT[:, u % 4, :], ps[:, u % 4, :], ACT.Relu, bias=b1[:, e * C + c:e * C + c + 1])\
                            .then_inc(*mact.end(f"r{u}"))

        @block.tensor
        def _(eng):
            with eng.Fori(0, B) as b:
                eng.wait_ge(*gdve.done("x", b))
                for qt in range(QT):
                    last = nc.tensor.transpose(ps[:, 6, qt * P:(qt + 1) * P], xb[:, qt, :], chip.ident[:, :])
                last.then_inc(*gpe.end("xT"))
                eng.wait_ge(*gdve.done("xT", b))
                for qt in range(QT):
                    out = ps[:, 7, qt * E:(qt + 1) * E]
                    nc.tensor.matmul(out, xTb[:, qt * P:(qt + 1) * P], w["L2_ffn_Wg"], start=True, stop=False)
                    last = nc.tensor.matmul(out, chip.ones[0:1, 0:P], w["L2_ffn_bg"], start=False, stop=True)
                last.then_inc(*gpe.end("logits"))
                eng.wait_ge(*gdve.done("toppick", b))
                for qt in range(QT):
                    last = nc.tensor.transpose(ps[0:E, 5, qt * P:(qt + 1) * P], one[:, qt, :], chip.ident[:, :])
                last.then_inc(*gpe.end("oneT"))
            eng.wait_ge(*gdve.passed(B))
            eng.wait_ge(ready, 2)
            for half in range(2):
                nc.tensor.matmul(ps[:, 6 + half, :], w["L2_ffn_b2"], oneT[:, half * 512:(half + 1) * 512], start=True, stop=False)
            with eng.Fori(0, E // 2) as i:
                for u in range(n + 2):
                    if u < n:
                        e, c, half = units[u]
                        if u % (n // 2) == 0:
                            eng.wait_ge(weights[e], i * 32 + 32)
                        if u >= 4:
                            eng.wait_ge(*relu(u)(f"r{u - 4}", i))
                        cols = slice(half * 512, (half + 1) * 512)
                        nc.tensor.matmul(ps[:, u % 4, :], w1[:, e, c * P:(c + 1) * P], xT[:, cols], start=True, stop=False)
                        nc.tensor.matmul(ps[:, u % 4, :], sel[:, i * 2 + e, :], shut[:, cols], start=False, stop=True)\
                            .then_inc(*mpe.end(f"h{u}"))
                    if u >= 2:
                        e, c, half = units[u - 2]
                        eng.wait_ge(*relu(u)(f"r{u - 2}", i))
                        nc.tensor.matmul(ps[:, 6 + half, :], w2[:, e, c, :], hT[:, (u - 2) % 4, :], start=False, stop=False)\
                            .then_inc(*mpe.end(f"acc{u - 2}"))
            for half in range(2):
                last = nc.tensor.matmul(ps[:, 6 + half, :], chip.zeros[0:1, 0:P], chip.ones[0:1, 0:512], start=False, stop=True)
            last.then_inc(nxt[5], 1)
            eng.wait_ge(nxt[8], 1)
            for b in range(B):
                if b >= 2:
                    eng.wait_ge(*dve.done("sum", b - 2))
                for qt in range(QT):
                    last = nc.tensor.transpose(ps[:, b % 2, qt * P:(qt + 1) * P], yT[:, b * S + qt * P:b * S + (qt + 1) * P], chip.ident[:, :])
                last.then_inc(*pe.end("y"))


def l3_ffn(nc, chip):
    E, F, T, TILES = 7, 512, B * S, B * QT
    C = F // P
    CAPACITY = -(-5 * T * 2 // (4 * E))
    with ExitStack() as ctx:
        sb = lambda n, s, dt=F32: ctx.enter_context(nc.sbuf_tensor(f"l3f_{n}", s, dt))
        pe_s, dve_s, act_s, pool_s, ready = stage_sems(nc, ctx, "l3f")
        t, k = Tail(nc, ctx, "l3f"), Pick(nc, ctx, "l3f", E)
        xb, z = sb("xb", [P, QT, D]), sb("z", [P, QT, D])
        zs, zmv, zr = sb("zs", [P, QT, 6]), sb("zmv", [P, QT, 2]), sb("zr", [P, QT])
        hb, hT = sb("hb", [P, S]), sb("hT", [P, T])
        lg, one, two = sb("lg", [P, QT, E]), sb("one", [P, QT, E]), sb("two", [P, QT, E])
        m1, ex, den = sb("m1", [P, QT]), sb("ex", [P, QT]), sb("den", [P, QT])
        picks, gates = sb("picks", [P, 2 * TILES, E]), sb("gates", [P, 2, TILES])
        offs, keep = sb("offs", [P, 2 * TILES, E]), sb("keep", [P, 2 * TILES, E])
        weight, weightT = sb("weight", [P, TILES, 8]), sb("weightT", [8, T])
        mine, hg = sb("mine", [8, 2, T]), sb("hg", [P, 2, T])
        w1, w3, w2 = sb("w1", [P, 2, F]), sb("w3", [P, 2, F]), sb("w2", [P, 2, C, D])
        act1, mid = sb("act1", [P, 2, 512]), sb("mid", [P, 2, 512])
        yT = sb("yT", [P, T])
        ps, w = chip.ps, chip.w
        sem = lambda n: ctx.enter_context(nc.semaphore(f"l3f_{n}"))
        weights = [sem("weights0"), sem("weights1")]
        closed, copied = sem("closed"), sem("copied")
        rpe = Steps(sem("route_pe"), ["zT", "logits"])
        rdve = Steps(sem("route_dve"), ["x", "stats", "var", "z", "hb", "hT", "logits"] + pick_steps("first") + ["m1", "rest"]
                     + pick_steps("second") + ["gap", "den", "gate1", "gate2", "picks"])
        ract, rpool = Steps(sem("route_act"), ["exp"]), Steps(sem("route_pool"), ["eps", "rstd"])
        cpe = Steps(sem("count_pe"), ["counts", "weightT"])
        cdve = Steps(sem("count_dve"), ["shared", "off0"] + [f"off{i}" for i in range(1, 2 * TILES)]
                     + ["pos", "keep", "kept", "weighed", "weight", "weightT"])
        units = [(e, c, half) for e in range(2) for c in range(C) for half in range(2)]
        n = len(units)
        names = []
        for u in range(n + 2):
            if u < n and u % (n // 2) == 0:
                names.append(f"spread{units[u][0]}")
            names += ([f"ab{u}"] if u < n else []) + ([f"acc{u - 2}"] if u >= 2 else [])
        mpe = Steps(sem("main_pe"), names)
        names = []
        for u in range(n):
            if u % (n // 2) == 0:
                names += [f"mine{units[u][0]}", f"hg{units[u][0]}"]
            names.append(f"mid{u}")
        mdve, mact = Steps(sem("main_dve"), names), Steps(sem("main_act"), [f"silu{u}" for u in range(n)])
        pe, dve, pool = Steps(pe_s, ["y"]), Steps(dve_s, ["x"] + TAIL_DVE), Steps(pool_s, TAIL_POOL)
        a = chip.a
        block = ctx.enter_context(nc.Block())

        @block.sync
        def _(sp):
            for e in range(E + 1):
                if e >= 2:
                    sp.wait_ge(*mpe.done(f"acc{n // 2 * (e % 2 + 1) - 1}", e // 2 - 1))
                one_of = lambda m: a[f"L3_ffn_{m}"][e, :, :] if e < E else a[f"L3_ffn_{m}s"]
                sp.dma_start(w1[:, e % 2, :], one_of("W1")).then_inc(weights[e % 2], 16)
                sp.dma_start(w3[:, e % 2, :], one_of("W3")).then_inc(weights[e % 2], 16)
                sp.dma_start(w2[:, e % 2, :, :], one_of("W2").rearrange("(c p) d -> p c d", p=P)).then_inc(weights[e % 2], 16)

        @block.gpsimd
        def _(eng):
            with eng.Fori(0, B) as b:
                eng.wait_ge(*rdve.done("var", b))
                nc.gpsimd.tensor_tensor(fp(zr), zmv[:, :, 1], chip.eps[:, 0:QT], ALU.add).then_inc(*rpool.end("eps"))
                eng.wait_ge(*rpool.done("eps", b))
                nc.gpsimd.tensor_tensor(fp(zr), fp(zr), chip.neghalf[:, 0:QT], ALU.pow).then_inc(*rpool.end("rstd"))
            with eng.Fori(0, B) as b:
                tail_pool(nc, eng, chip, t, dve, pool, b)

        @block.vector
        def _(eng):
            with eng.Fori(0, B) as b:
                nc.vector.tensor_copy(fp(xb), chip.x_tok[:, b, :, :]).then_inc(*rdve.end("x"))
                eng.wait_ge(*rdve.done("x", b))
                for q in range(QT):
                    last = nc.vector.bn_stats(zs[:, q, :], xb[:, q, :])
                last.then_inc(*rdve.end("stats"))
                eng.wait_ge(*rdve.done("stats", b))
                nc.vector.memset(chip.scratch[:, 4:5], 0.0)
                for q in range(QT):
                    last = nc.vector.bn_aggr(zmv[:, q, :], zs[:, q, :])
                last.then_inc(*rdve.end("var"))
                eng.wait_ge(*rpool.done("rstd", b))
                for q in range(QT):
                    last = nc.vector.tensor_scalar(z[:, q, :], xb[:, q, :], zmv[:, q, 0:1], zr[:, q:q + 1], ALU.subtract, ALU.mult)
                last.then_inc(*rdve.end("z"))
                eng.wait_ge(*rpe.done("zT", b))
                nc.vector.tensor_scalar(fp(hb), ps[:, 6, 0:S], w["L3_ffn_ln_g"], w["L3_ffn_ln_b"], ALU.mult, ALU.add)\
                    .then_inc(*rdve.end("hb"))
                nc.vector.tensor_scalar(hT[:, bass.ts(b, S)], ps[:, 6, 0:S], w["L3_ffn_ln_g"], w["L3_ffn_ln_b"], ALU.mult, ALU.add)\
                    .then_inc(*rdve.end("hT"))
                eng.wait_ge(*rpe.done("logits", b))
                nc.vector.tensor_copy(fp(lg), ps[:, 7, 0:QT * E].rearrange("p (t e) -> p t e", e=E)).then_inc(*rdve.end("logits"))
                eng.wait_ge(*rdve.done("logits", b))
                pick_first(nc, eng, chip, k, rdve, b, "first", fp(lg), fp(one))
                nc.vector.tensor_copy(fp(m1), fp(k.m)).then_inc(*rdve.end("m1"))
                eng.wait_ge(*rdve.done("m1", b))
                nc.vector.scalar_tensor_tensor(fp(two), fp(one), MASKED, fp(lg), ALU.mult, ALU.add).then_inc(*rdve.end("rest"))
                eng.wait_ge(*rdve.done("rest", b))
                pick_first(nc, eng, chip, k, rdve, b, "second", fp(two), fp(two))
                nc.vector.tensor_tensor(fp(ex), fp(k.m), fp(m1), ALU.subtract).then_inc(*rdve.end("gap"))
                eng.wait_ge(*ract.done("exp", b))
                nc.vector.tensor_scalar(fp(den), fp(ex), 1.0, None, ALU.add).then_inc(*rdve.end("den"))
                eng.wait_ge(*rdve.done("den", b))
                nc.vector.reciprocal(fp(den), fp(den)).then_inc(*rdve.end("gate1"))
                eng.wait_ge(*rdve.done("gate1", b))
                nc.vector.tensor_scalar(gates[:, 0, bass.ts(b, QT)], fp(den), 1.0, None, ALU.mult)
                nc.vector.tensor_tensor(gates[:, 1, bass.ts(b, QT)], fp(ex), fp(den), ALU.mult).then_inc(*rdve.end("gate2"))
                eng.wait_ge(*rdve.done("gate2", b))
                nc.vector.tensor_scalar(picks[:, bass.ts(b, QT), :], fp(one), 1.0, None, ALU.mult)
                nc.vector.tensor_scalar(picks[:, bass.ds(b * QT + TILES, QT), :], fp(two), 1.0, None, ALU.mult)\
                    .then_inc(*rdve.end("picks"))
            nc.vector.memset(weight[:, :, E:8], 1.0).then_inc(*cdve.end("shared"))
            nc.vector.memset(offs[:, 0, :], 0.0).then_inc(*cdve.end("off0"))
            eng.wait_ge(*cpe.done("counts"))
            totals = ps[:, 1, 0:2 * TILES * E].rearrange("p (i e) -> p i e", e=E)
            for i in range(1, 2 * TILES):
                eng.wait_ge(*cdve.done(f"off{i - 1}"))
                nc.vector.tensor_tensor(offs[:, i, :], offs[:, i - 1, :], totals[:, i - 1, :], ALU.add).then_inc(*cdve.end(f"off{i}"))
            eng.wait_ge(*cdve.done(f"off{2 * TILES - 1}"))
            nc.vector.tensor_tensor(fp(offs), ps[:, 0, 0:2 * TILES * E].rearrange("p (i e) -> p i e", e=E), fp(offs), ALU.add)\
                .then_inc(*cdve.end("pos"))
            eng.wait_ge(*cdve.done("pos"))
            nc.vector.tensor_scalar(fp(keep), fp(offs), float(CAPACITY), None, ALU.is_lt).then_inc(*cdve.end("keep"))
            eng.wait_ge(*cdve.done("keep"))
            nc.vector.tensor_tensor(fp(keep), fp(keep), fp(picks), ALU.mult).then_inc(*cdve.end("kept"))
            eng.wait_ge(*cdve.done("kept"))
            nc.vector.tensor_tensor(fp(keep), fp(keep), fp(gates).rearrange("p s t -> p (s t)").unsqueeze(2)
                                    .to_broadcast([P, 2 * TILES, E]), ALU.mult).then_inc(*cdve.end("weighed"))
            eng.wait_ge(*cdve.done("weighed"))
            nc.vector.tensor_tensor(weight[:, :, 0:E], keep[:, 0:TILES, :], keep[:, TILES:2 * TILES, :], ALU.add)\
                .then_inc(*cdve.end("weight"))
            eng.wait_ge(*cpe.done("weightT"))
            nc.vector.tensor_copy(fp(weightT), ps[0:8, 2:4, :].rearrange("p a t -> p (a t)")).then_inc(*cdve.end("weightT"))
            eng.wait_ge(*cdve.done("weightT"))
            with eng.Fori(0, (E + 1) // 2) as i:
                for u, (e, c, half) in enumerate(units):
                    if u % (n // 2) == 0:
                        nc.vector.tensor_scalar(mine[:, e, :], fp(weightT), chip.ident[0:8, bass.ds(i * 2 + e, 1)], None, ALU.mult)\
                            .then_inc(*mdve.end(f"mine{e}"))
                        eng.wait_ge(*mpe.done(f"spread{e}", i))
                        nc.vector.tensor_tensor(hg[:, e, :], ps[:, 4:6, :].rearrange("p a t -> p (a t)"), fp(hT), ALU.mult)\
                            .then_inc(*mdve.end(f"hg{e}"))
                    eng.wait_ge(*mact.done(f"silu{u}", i))
                    if u >= 2:
                        eng.wait_ge(*mpe.done(f"acc{u - 2}", i))
                    nc.vector.tensor_tensor(mid[:, u % 2, :], ps[:, 2 + u % 2, :], act1[:, u % 2, :], ALU.mult)\
                        .then_inc(*mdve.end(f"mid{u}"))
                eng.wait_ge(*mpe.done(f"acc{n - 1}", i))
            eng.wait_ge(closed, 1)
            nc.vector.tensor_copy(fp(yT), ps[:, 6:8, :].rearrange("p a t -> p (a t)")).then_inc(copied, 1)
            for b in range(B):
                nc.vector.tensor_copy(fp(xb), chip.x_tok[:, b, :, :]).then_inc(*dve.end("x"))
                eng.wait_ge(*dve.done("x", b))
                eng.wait_ge(*pe.done("y", b))
                tail_dve(nc, eng, chip, t, dve, pool, b, ps[:, b % 2, 0:S].rearrange("p (t d) -> p t d", t=QT), fp(xb))

        @block.scalar
        def _(eng):
            with eng.Fori(0, B) as b:
                eng.wait_ge(*rdve.done("gap", b))
                nc.scalar.activation(fp(ex), fp(ex), ACT.Exp).then_inc(*ract.end("exp"))
            with eng.Fori(0, (E + 1) // 2) as i:
                for u, (e, c, half) in enumerate(units):
                    eng.wait_ge(*mpe.done(f"ab{u}", i))
                    if u >= 2:
                        eng.wait_ge(*mdve.done(f"mid{u - 2}", i))
                    nc.scalar.activation(act1[:, u % 2, :], ps[:, u % 2, :], ACT.Silu).then_inc(*mact.end(f"silu{u}"))

        @block.tensor
        def _(eng):
            with eng.Fori(0, B) as b:
                eng.wait_ge(*rdve.done("z", b))
                for q in range(QT):
                    last = nc.tensor.transpose(ps[:, 6, q * P:(q + 1) * P], z[:, q, :], chip.ident[:, :])
                last.then_inc(*rpe.end("zT"))
                eng.wait_ge(*rdve.done("hb", b))
                for q in range(QT):
                    last = nc.tensor.matmul(ps[:, 7, q * E:(q + 1) * E], hb[:, q * P:(q + 1) * P], w["L3_ffn_Wr"], start=True, stop=True)
                last.then_inc(*rpe.end("logits"))
            eng.wait_ge(*rdve.passed(B))
            flat = fp(picks).rearrange("p i e -> p (i e)")
            nc.tensor.matmul(ps[:, 0, 0:2 * TILES * E], w["c_before"], flat, start=True, stop=True)
            nc.tensor.matmul(ps[:, 1, 0:2 * TILES * E], chip.ones[:, 0:P], flat, start=True, stop=True).then_inc(*cpe.end("counts"))
            eng.wait_ge(*cdve.done("weight"))
            for i in range(TILES):
                last = nc.tensor.transpose(ps[0:8, 2 + i // 4, (i % 4) * P:(i % 4 + 1) * P], weight[:, i, :], chip.ident[:, :])
            last.then_inc(*cpe.end("weightT"))
            for half in range(2):
                nc.tensor.matmul(ps[:, 6 + half, :], chip.zeros[0:1, 0:P], chip.ones[0:1, 0:512], start=True, stop=False)
            eng.wait_ge(*cdve.done("weightT"))
            with eng.Fori(0, (E + 1) // 2) as i:
                for u in range(n + 2):
                    if u < n:
                        e, c, half = units[u]
                        cols = slice(half * 512, (half + 1) * 512)
                        if u % (n // 2) == 0:
                            eng.wait_ge(*mdve.done(f"mine{e}", i))
                            for x in range(2):
                                last = nc.tensor.matmul(ps[:, 4 + x, :], chip.ones[0:8, 0:P], mine[:, e, x * 512:(x + 1) * 512],
                                                        start=True, stop=True)
                            last.then_inc(*mpe.end(f"spread{e}"))
                            eng.wait_ge(weights[e], i * 48 + 48)
                            eng.wait_ge(*mdve.done(f"hg{e}", i))
                        if u >= 2:
                            eng.wait_ge(*mdve.done(f"mid{u - 2}", i))
                        nc.tensor.matmul(ps[:, u % 2, :], w1[:, e, c * P:(c + 1) * P], hT[:, cols], start=True, stop=True)
                        nc.tensor.matmul(ps[:, 2 + u % 2, :], w3[:, e, c * P:(c + 1) * P], hg[:, e, cols], start=True, stop=True)\
                            .then_inc(*mpe.end(f"ab{u}"))
                    if u >= 2:
                        e, c, half = units[u - 2]
                        eng.wait_ge(*mdve.done(f"mid{u - 2}", i))
                        nc.tensor.matmul(ps[:, 6 + half, :], w2[:, e, c, :], mid[:, (u - 2) % 2, :], start=False, stop=False)\
                            .then_inc(*mpe.end(f"acc{u - 2}"))
            for half in range(2):
                last = nc.tensor.matmul(ps[:, 6 + half, :], chip.zeros[0:1, 0:P], chip.ones[0:1, 0:512], start=False, stop=True)
            last.then_inc(closed, 1)
            eng.wait_ge(copied, 1)
            for b in range(B):
                if b >= 2:
                    eng.wait_ge(*dve.done("sum", b - 2))
                for q in range(QT):
                    last = nc.tensor.transpose(ps[:, b % 2, q * P:(q + 1) * P], yT[:, b * S + q * P:b * S + (q + 1) * P], chip.ident[:, :])
                last.then_inc(*pe.end("y"))


FFN_LAYERS, FFN_HEADS, FFN_DH, FFN_IN = 6, 16, 64, 341
FFN_CHUNKS = [(0, P), (P, P), (2 * P, FFN_IN - 2 * P)]
EDGE = 32


def l1_ffn_constants():
    f = np.float32
    half = np.arange(0, FFN_DH, 2, dtype=f)
    inv_freq = (f(1) / np.power(f(10000), half / f(FFN_DH)).astype(f)).astype(f)
    t = np.arange(S, dtype=f)
    freqs = (t[:, None] * inv_freq[None, :]).astype(f)
    freqs = np.concatenate([freqs, freqs], -1)
    base = ((half + f(0.4 * FFN_DH)) / f(1.4 * FFN_DH)).astype(f)
    power = ((t - S // 2) / f(EDGE // 2)).astype(f)
    scale = np.power(base[None, :], power[:, None]).astype(f)
    scale = np.concatenate([scale, scale], -1)
    inv = (f(1) / scale).astype(f)
    sign = np.where(np.arange(FFN_DH) < FFN_DH // 2, f(-1), f(1))[None, :]
    cos, sin = np.cos(freqs).astype(f), (np.sin(freqs) * sign).astype(f)
    tab = np.stack([np.stack([cos * scale * f(8), sin * scale * f(8)]), np.stack([cos * inv, sin * inv])]).astype(f)
    return {"c_xpos": np.ascontiguousarray(tab.reshape(2, 2, QT, P, FFN_DH).transpose(3, 0, 1, 2, 4))}


class FfnState:
    pass


def l1_ffn(nc, chip):
    with ExitStack() as ctx:
        sb = lambda n, s, dt=F32: ctx.enter_context(nc.sbuf_tensor(f"l1f_{n}", s, dt))
        f = FfnState()
        f.xr = sb("xr", [P, B, S])
        f.cols = sb("cols", [P, 9, FFN_LAYERS])
        f.spread = sb("spread", [P, 2, FFN_LAYERS, FFN_DH])
        f.xpos = sb("xpos", [P, 2, 2, QT, FFN_DH])
        f.band = sb("band", [P, QT, 160], BF16)
        f.mean_w = sb("mean_w", [P, P])
        l1_ffn_enter(nc, chip, f)
        l1_ffn_layers(nc, chip, f)
        l1_ffn_leave(nc, chip, f)


def l1_ffn_enter(nc, chip, f):
    with ExitStack() as ctx:
        sb = lambda n, s, dt=F32: ctx.enter_context(nc.sbuf_tensor(f"l1fe_{n}", s, dt))
        pe_s, dve_s, act_s, pool_s, loads = stage_sems(nc, ctx, "l1fe")
        raw = sb("raw", [FFN_LAYERS, 3, P])
        raw_b1 = sb("raw_b1", [FFN_LAYERS, 2 * FFN_IN])
        pe, dve = Steps(pe_s, [f"x{b}" for b in range(B)] + ["cols"]), Steps(dve_s, ["clear"] + [f"x{b}" for b in range(B)])
        vectors = [(i, raw[:, i, :], P) for i in range(3)]
        vectors += [(3 + 3 * g + i, raw_b1[:, g * FFN_IN + at:g * FFN_IN + at + n], n)
                    for g in range(2) for i, (at, n) in enumerate(FFN_CHUNKS)]
        a, ps = chip.a, chip.ps
        block = ctx.enter_context(nc.Block())

        @block.sync
        def _(sp):
            n = 0
            for dst, src in [(raw[:, 0, :], a["L1_ffn_ln_g"]), (raw[:, 1, :], a["L1_ffn_ln_b"]), (raw[:, 2, :], a["L1_ffn_b2"]),
                             (fp(raw_b1), a["L1_ffn_b1"]), (fp(f.xpos), a["c_xpos"])]:
                sp.dma_start(dst, src).then_inc(loads, 16)
                n += 16
            for i, k in enumerate("qk"):
                sp.dma_start(f.spread[:, i, :, :].rearrange("p l d -> p (l d)"),
                             a[f"L1_ffn_{k}_scale"].rearrange("l d -> (l d)").partition_broadcast(P)).then_inc(loads, 16)
                n += 16
            sp.wait_ge(loads, n)

        @block.tensor
        def _(eng):
            for b in range(B):
                for q in range(QT):
                    last = nc.tensor.transpose(ps[:, b, q * P:(q + 1) * P], chip.x_tok[:, b, q, :], chip.ident[:, :])
                last.then_inc(*pe.end(f"x{b}"))
            eng.wait_ge(loads, 7 * 16)
            for i, src, n in vectors:
                last = nc.tensor.transpose(ps[0:n, 4, 8 * i:8 * i + FFN_LAYERS], src, chip.ident[0:FFN_LAYERS, 0:FFN_LAYERS])
            last.then_inc(*pe.end("cols"))

        @block.vector
        def _(eng):
            nc.vector.tensor_copy(fp(f.band), chip.w["c_band"])
            nc.vector.memset(fp(f.mean_w), 1.0 / D)
            nc.vector.memset(fp(f.cols), 0.0).then_inc(*dve.end("clear"))
            for b in range(B):
                eng.wait_ge(*pe.done(f"x{b}"))
                nc.vector.tensor_copy(f.xr[:, b, :], ps[:, b, 0:S]).then_inc(*dve.end(f"x{b}"))
            eng.wait_ge(*pe.done("cols"))
            eng.wait_ge(*dve.done("clear"))
            for i, src, n in vectors:
                nc.vector.tensor_copy(f.cols[0:n, i, :], ps[0:n, 4, 8 * i:8 * i + FFN_LAYERS])


def l1_ffn_leave(nc, chip, f):
    with ExitStack() as ctx:
        sb = lambda n, s, dt=F32: ctx.enter_context(nc.sbuf_tensor(f"l1fl_{n}", s, dt))
        pe_s, dve_s, act_s, pool_s, loads = stage_sems(nc, ctx, "l1fl")
        t = Tail(nc, ctx, "l1fl")
        xb = sb("xb", [P, QT, D])
        pe, dve, pool = Steps(pe_s, ["y"]), Steps(dve_s, ["x"] + TAIL_DVE), Steps(pool_s, TAIL_POOL)
        block = ctx.enter_context(nc.Block())

        @block.gpsimd
        def _(eng):
            with eng.Fori(0, B) as b:
                tail_pool(nc, eng, chip, t, dve, pool, b)

        @block.vector
        def _(eng):
            for b in range(B):
                nc.vector.tensor_copy(fp(xb), chip.x_tok[:, b, :, :]).then_inc(*dve.end("x"))
                eng.wait_ge(*dve.done("x", b))
                eng.wait_ge(*pe.done("y", b))
                tail_dve(nc, eng, chip, t, dve, pool, b, chip.ps[:, b, 0:S].rearrange("p (t d) -> p t d", t=QT), fp(xb))

        @block.tensor
        def _(eng):
            for b in range(B):
                for q in range(QT):
                    last = nc.tensor.transpose(chip.ps[:, b, q * P:(q + 1) * P], f.xr[:, b, q * P:(q + 1) * P], chip.ident[:, :])
                last.then_inc(*pe.end("y"))


def l1_ffn_layers(nc, chip, f):
    H, DH, L = FFN_HEADS, FFN_DH, FFN_LAYERS
    PAIRS = H // 2
    with ExitStack() as ctx:
        sb = lambda n, s, dt=F32: ctx.enter_context(nc.sbuf_tensor(f"l1fb_{n}", s, dt))
        pe_s, dve_s, act_s, pool_s, ready = stage_sems(nc, ctx, "l1fb")
        wqkv, wo = sb("wqkv", [P, 2, 3 * H * DH]), sb("wo", [P, 2, PAIRS, D])
        w1, w2 = sb("w1", [P, 2, 2 * FFN_IN]), sb("w2", [P, 2, 3, D])
        turn_tab, col = sb("turn_tab", [P, 2, 2, QT, DH]), sb("col", [P, 9])
        xc, xs = sb("xc", [P, S]), sb("xs", [P, S])
        sq, ssq = sb("sq", [P, 2, 512]), sb("ssq", [P, 8, 8])
        rinv = sb("rinv", [P, 8, 8])
        r1, r2 = sb("r1", [P, 2, 512]), sb("r2", [P, 2, 512])
        qk = sb("qk", [P, 2, QT, H, DH])
        qT, kT = sb("qT", [P, H, S]), sb("kT", [P, PAIRS, S])
        v, ve = sb("v", [P, QT, H, DH]), sb("ve", [EDGE, H, DH])
        nm, den, rden = sb("nm", [P, H, QT]), sb("den", [P, H, QT]), sb("rden", [P, H, QT])
        pr, prT = sb("pr", [P, 2, 2, 288]), sb("prT", [P, 2, 2, 384])
        attT = sb("attT", [P, PAIRS, S])
        x1, x1s, diff, dsq = sb("x1", [P, S]), sb("x1s", [P, S]), sb("diff", [P, S]), sb("dsq", [P, S])
        rstd, xn, gl, g = sb("rstd", [P, S]), sb("xn", [P, S]), sb("gl", [P, 3, S]), sb("g", [P, 3, S])
        ps, a = chip.ps, chip.a
        weights = [ctx.enter_context(nc.semaphore(f"l1fb_weights{i}")) for i in range(2)]

        proj = [(k, q, hh) for k in range(3) for q in range(QT) for hh in range(2)]
        QK = 4 * QT
        turns = [(k, cp) for k in range(2) for cp in range(PAIRS // 2)]
        names = [f"proj{u}" for u in range(len(proj))] + [f"turn{u}" for u in range(len(turns))] + ["s0", "s1"]
        for c in range(PAIRS + 1):
            if c < PAIRS:
                names += [f"pT{2 * c}", f"pT{2 * c + 1}"] + ([f"s{c + 2}"] if c + 2 < PAIRS else [])
            if c:
                names.append(f"pv{c - 1}")
        pe = Steps(pe_s, names + ["y1", "mean", "var", "h0", "h1", "h2", "y2"])
        names = ["xs"]
        for u in range(QK):
            names += [f"rot{u}", f"ssq{u}", f"clamp{u}"]
        names += [f"q{cp}" for cp in range(PAIRS // 2)]
        for c in range(PAIRS):
            names += [f"max{c}", f"rden{c}"]
            if c:
                names += [f"pT{2 * c - 1}", f"att{c - 1}"]
        names += [f"pT{2 * PAIRS - 1}", f"att{PAIRS - 1}"]
        dve = Steps(dve_s, names + ["x1", "x1s", "diff", "dsq", "vareps", "xn0", "xn", "g0", "g1", "g2", "x2"])
        names = [f"sq{u}" for u in range(QK)] + [f"v{u}" for u in range(QK, len(proj))]
        names += [f"q{cp}" for cp in range(PAIRS // 2)] + [f"k{cp}" for cp in range(PAIRS // 2)]
        for c in range(PAIRS):
            names += [f"exp{c}"] + ([f"pT{2 * c - 2}"] if c else [])
        act = Steps(act_s, names + [f"pT{2 * PAIRS - 2}", "gelu0", "gelu1", "gelu2"])
        names = []
        for u in range(QK):
            names += [f"add{u}", f"rinv{u}", f"qk{u}"]
        pool = Steps(pool_s, names + [f"pn{c}" for c in range(PAIRS)] + ["rstd"])
        lay = Steps(ctx.enter_context(nc.semaphore("l1fb_layer_steps")), ["tables"])
        block = ctx.enter_context(nc.Block())

        def layers(eng, body, per_layer=None):
            with eng.Fori(0, L // 2) as half:
                for par in range(2):
                    if per_layer is not None:
                        per_layer(half * 2 + par)
                    with eng.Fori(0, B) as b:
                        body(par, half, b, half * (2 * B) + par * B + b)

        @block.sync
        def _(sp):
            for l in range(L):
                if l >= 2:
                    sp.wait_ge(*pe.passed(B * (l - 1)))
                for dst, src in [(wqkv[:, l % 2, :], a["L1_ffn_Wqkv"][l, :, :]),
                                 (wo[:, l % 2, :, :], a["L1_ffn_Wo"][l, :, :].rearrange("(c p) d -> p c d", p=P)),
                                 (w1[:, l % 2, :], a["L1_ffn_W1"][l, :, :]),
                                 (w2[:, l % 2, 0:2, :], a["L1_ffn_W2"][l, 0:2 * P, :].rearrange("(c p) d -> p c d", p=P)),
                                 (w2[0:FFN_IN - 2 * P, l % 2, 2, :], a["L1_ffn_W2"][l, 2 * P:FFN_IN, :])]:
                    sp.dma_start(dst, src).then_inc(weights[l % 2], 16)

        @block.gpsimd
        def _(eng):
            nc.gpsimd.memset(qT[0:DH, 1:H:2, :], 0.0)
            nc.gpsimd.memset(qT[DH:P, 0:H:2, :], 0.0)
            nc.gpsimd.memset(xs[DH:P, 0:1], 0.0)
            nc.gpsimd.memset(x1s[DH:P, 0:1], 0.0).then_inc(ready, 1)
            eng.wait_ge(ready, 1)

            def body(par, half, b, turn):
                for u in range(QK):
                    k, q, hh = proj[u]
                    eng.wait_ge(*dve.done(f"rot{u}", turn))
                    nc.gpsimd.tensor_tensor(r1[:, u % 2, :], r1[:, u % 2, :], r2[:, u % 2, :], ALU.add).then_inc(*pool.end(f"add{u}"))
                    eng.wait_ge(*dve.done(f"clamp{u}", turn))
                    nc.gpsimd.tensor_tensor(rinv[:, u, :], ssq[:, u, :], chip.neghalf[:, 0:8], ALU.pow).then_inc(*pool.end(f"rinv{u}"))
                    eng.wait_ge(*pool.done(f"rinv{u}", turn))
                    nc.gpsimd.tensor_tensor(qk[:, k, q, 8 * hh:8 * hh + 8, :], r1[:, u % 2, :].rearrange("p (h d) -> p h d", d=DH),
                                            rinv[:, u, :].unsqueeze(2).to_broadcast([P, 8, DH]), ALU.mult).then_inc(*pool.end(f"qk{u}"))
                for c in range(PAIRS):
                    eng.wait_ge(*dve.done(f"rden{c}", turn))
                    for q, (lo, hi) in enumerate(((0, P), (P, 288))):
                        part = pr[:, c % 2, :, lo:hi]
                        last = nc.gpsimd.tensor_tensor(part, part, rden[:, 2 * c:2 * c + 2, q].unsqueeze(2).to_broadcast([P, 2, hi - lo]),
                                                       ALU.mult)
                    last.then_inc(*pool.end(f"pn{c}"))
                eng.wait_ge(*dve.done("vareps", turn))
                nc.gpsimd.tensor_tensor(fp(rstd), fp(rstd), chip.neghalf[:, 0:S], ALU.pow).then_inc(*pool.end("rstd"))

            layers(eng, body)

        @block.vector
        def _(eng):
            eng.wait_ge(ready, 1)

            def tables(l):
                for k in range(2):
                    for part, (lo, hi) in ((0, (0, DH)), (1, (DH // 2, DH)), (1, (0, DH // 2))):
                        o = slice(0, DH) if part == 0 else slice(DH // 2 - lo, DH - lo)
                        nc.vector.tensor_tensor(turn_tab[:, k, part, :, o], f.xpos[:, k, part, :, o],
                                                f.spread[:, k, l, lo:hi].unsqueeze(1).to_broadcast([P, QT, hi - lo]), ALU.mult)
                nc.vector.tensor_copy(fp(col), f.cols[:, :, l]).then_inc(*lay.end("tables"))

            def body(par, half, b, turn):
                nc.vector.tensor_copy(fp(xc), f.xr[:, b, :])
                nc.vector.tensor_copy(xs[0:DH, :], f.xr[0:DH, b, :])
                nc.vector.tensor_copy(xs[DH:P, 1:S], f.xr[DH:P, b, 0:S - 1]).then_inc(*dve.end("xs"))
                eng.wait_ge(*lay.done("tables", half * 2 + par))
                for u in range(QK):
                    k, q, hh = proj[u]
                    eng.wait_ge(*act.done(f"sq{u}", turn))
                    if u >= 2:
                        eng.wait_ge(*pool.done(f"qk{u - 2}", turn))
                    src = ps[:, u % 4, :].rearrange("p (h d) -> p h d", d=DH)
                    tab = lambda part, o: turn_tab[:, k, part, q, o].unsqueeze(1).to_broadcast([P, 8, o.stop - o.start])
                    nc.vector.tensor_tensor(r1[:, u % 2, :].rearrange("p (h d) -> p h d", d=DH), src, tab(0, slice(0, DH)), ALU.mult)
                    out = r2[:, u % 2, :].rearrange("p (h d) -> p h d", d=DH)
                    lo, hi = slice(0, DH // 2), slice(DH // 2, DH)
                    nc.vector.tensor_tensor(out[:, :, lo], src[:, :, hi], tab(1, lo), ALU.mult)
                    nc.vector.tensor_tensor(out[:, :, hi], src[:, :, lo], tab(1, hi), ALU.mult).then_inc(*dve.end(f"rot{u}"))
                    eng.wait_ge(*act.done(f"sq{u}", turn))
                    nc.vector.tensor_reduce(ssq[:, u, :], sq[:, u % 2, :].rearrange("p (h d) -> p h d", d=DH), AX.X, ALU.add)\
                        .then_inc(*dve.end(f"ssq{u}"))
                    eng.wait_ge(*dve.done(f"ssq{u}", turn))
                    nc.vector.tensor_scalar(ssq[:, u, :], ssq[:, u, :], 1e-24, None, ALU.max).then_inc(*dve.end(f"clamp{u}"))
                for cp in range(PAIRS // 2):
                    eng.wait_ge(*pe.done(f"turn{cp}", turn))
                    nc.vector.tensor_copy(qT[DH:P, 4 * cp + 1:4 * cp + 4:2, :], ps[DH:P, 4 + cp % 2, :].rearrange("p (h t) -> p h t", t=S))\
                        .then_inc(*dve.end(f"q{cp}"))

                def second_head(c):
                    u = 2 * c + 1
                    eng.wait_ge(*pe.done(f"pT{u}", turn))
                    if c >= 2:
                        eng.wait_ge(*pe.done(f"pv{c - 2}", turn))
                    nc.vector.tensor_copy(prT[:, c % 2, 1, 0:S], ps[:, 5, 0:S])
                    nc.vector.tensor_copy(prT[0:EDGE, c % 2, 1, S:384], ps[0:EDGE, 5, S:384]).then_inc(*dve.end(f"pT{u}"))
                    eng.wait_ge(*pe.done(f"pv{c}", turn))
                    nc.vector.tensor_copy(attT[:, c, :], ps[:, 6 + c % 2, 0:S]).then_inc(*dve.end(f"att{c}"))

                for c in range(PAIRS):
                    eng.wait_ge(*pe.done(f"s{c}", turn))
                    bank = 2 * (c % 2)
                    nc.vector.tensor_reduce(nm[:, 2 * c:2 * c + 2, 0], ps[:, bank:bank + 2, 0:P], AX.X, ALU.max, negate=True)
                    nc.vector.tensor_reduce(nm[:, 2 * c:2 * c + 2, 1], ps[:, bank:bank + 2, P:288], AX.X, ALU.max, negate=True)\
                        .then_inc(*dve.end(f"max{c}"))
                    eng.wait_ge(*act.done(f"exp{c}", turn))
                    nc.vector.reciprocal(rden[:, 2 * c:2 * c + 2, :], den[:, 2 * c:2 * c + 2, :]).then_inc(*dve.end(f"rden{c}"))
                    if c:
                        second_head(c - 1)
                second_head(PAIRS - 1)
                eng.wait_ge(*pe.done("y1", turn))
                nc.vector.tensor_tensor(fp(x1), ps[:, 0, 0:S], fp(xc), ALU.add).then_inc(*dve.end("x1"))
                eng.wait_ge(*dve.done("x1", turn))
                nc.vector.tensor_copy(x1s[0:DH, :], x1[0:DH, :])
                nc.vector.tensor_copy(x1s[DH:P, 1:S], x1[DH:P, 0:S - 1]).then_inc(*dve.end("x1s"))
                eng.wait_ge(*pe.done("mean", turn))
                eng.wait_ge(*dve.done("x1s", turn))
                nc.vector.tensor_tensor(fp(diff), fp(x1s), ps[:, 1, 0:S], ALU.subtract).then_inc(*dve.end("diff"))
                eng.wait_ge(*dve.done("diff", turn))
                nc.vector.tensor_tensor(fp(dsq), fp(diff), fp(diff), ALU.mult).then_inc(*dve.end("dsq"))
                eng.wait_ge(*pe.done("var", turn))
                nc.vector.tensor_scalar(fp(rstd), ps[:, 2, 0:S], EPS, None, ALU.add).then_inc(*dve.end("vareps"))
                eng.wait_ge(*pool.done("rstd", turn))
                nc.vector.tensor_tensor(fp(xn), fp(diff), fp(rstd), ALU.mult).then_inc(*dve.end("xn0"))
                eng.wait_ge(*dve.done("xn0", turn))
                nc.vector.tensor_scalar(fp(xn), fp(xn), col[:, 0:1], col[:, 1:2], ALU.mult, ALU.add).then_inc(*dve.end("xn"))
                for i, (at, n) in enumerate(FFN_CHUNKS):
                    eng.wait_ge(*act.done(f"gelu{i}", turn))
                    nc.vector.scalar_tensor_tensor(g[0:n, i, :], ps[0:n, 3 + i, 0:S], col[0:n, 3 + i:4 + i], gl[0:n, i, :], ALU.add, ALU.mult)\
                        .then_inc(*dve.end(f"g{i}"))
                eng.wait_ge(*pe.done("y2", turn))
                nc.vector.scalar_tensor_tensor(f.xr[:, b, :], ps[:, 1, 0:S], col[:, 2:3], fp(x1), ALU.add, ALU.add).then_inc(*dve.end("x2"))
                eng.wait_ge(*dve.done("x2", turn))

            layers(eng, body, tables)

        @block.scalar
        def _(eng):
            def body(par, half, b, turn):
                for u in range(QK):
                    eng.wait_ge(*pe.done(f"proj{u}", turn))
                    if u >= 2:
                        eng.wait_ge(*dve.done(f"ssq{u - 2}", turn))
                    nc.scalar.activation(sq[:, u % 2, :], ps[:, u % 4, :], ACT.Square).then_inc(*act.end(f"sq{u}"))
                for u in range(QK, len(proj)):
                    k, q, hh = proj[u]
                    eng.wait_ge(*pe.done(f"proj{u}", turn))
                    src = ps[:, u % 4, :].rearrange("p (h d) -> p h d", d=DH)
                    if q == 0:
                        nc.scalar.activation(ve[:, 8 * hh:8 * hh + 8, :], src[P - EDGE:P, :, :], ACT.Copy)
                    nc.scalar.activation(v[:, q, 8 * hh:8 * hh + 8, :], src, ACT.Copy).then_inc(*act.end(f"v{u}"))
                for u, (k, cp) in enumerate(turns):
                    eng.wait_ge(*pe.done(f"turn{u}", turn))
                    src = ps[:, 4 + u % 2, :].rearrange("p (h t) -> p h t", t=S)
                    if k == 0:
                        nc.scalar.activation(qT[0:DH, 4 * cp:4 * cp + 4:2, :], src[0:DH, :, :], ACT.Copy).then_inc(*act.end(f"q{cp}"))
                    else:
                        nc.scalar.activation(kT[:, 2 * cp:2 * cp + 2, :], src, ACT.Copy).then_inc(*act.end(f"k{cp}"))

                def first_head(c):
                    eng.wait_ge(*pe.done(f"pT{2 * c}", turn))
                    if c >= 2:
                        eng.wait_ge(*pe.done(f"pv{c - 2}", turn))
                    nc.scalar.activation(prT[:, c % 2, 0, 0:S], ps[:, 4, 0:S], ACT.Copy)
                    nc.scalar.activation(prT[0:EDGE, c % 2, 0, S:384], ps[0:EDGE, 4, S:384], ACT.Copy).then_inc(*act.end(f"pT{2 * c}"))

                for c in range(PAIRS):
                    eng.wait_ge(*dve.done(f"max{c}", turn))
                    if c >= 2:
                        eng.wait_ge(*pe.done(f"pT{2 * c - 3}", turn))
                    for j in range(2):
                        for q, (lo, hi) in enumerate(((0, P), (P, 288))):
                            h = 2 * c + j
                            last = nc.scalar.activation(pr[:, c % 2, j, lo:hi], ps[:, 2 * (c % 2) + j, lo:hi], ACT.Exp,
                                                        bias=nm[:, h, q:q + 1], accum_out=den[:, h, q:q + 1])
                    last.then_inc(*act.end(f"exp{c}"))
                    if c:
                        first_head(c - 1)
                first_head(PAIRS - 1)
                for i, (at, n) in enumerate(FFN_CHUNKS):
                    eng.wait_ge(*pe.done(f"h{i}", turn))
                    nc.scalar.activation(gl[0:n, i, :], ps[0:n, 3 + i, S:2 * S], ACT.Gelu, bias=col[0:n, 6 + i:7 + i])\
                        .then_inc(*act.end(f"gelu{i}"))

            layers(eng, body)

        @block.tensor
        def _(eng):
            eng.wait_ge(ready, 1)

            def body(par, half, b, turn):
                eng.wait_ge(weights[par], half * 80 + 80)
                eng.wait_ge(*dve.done("xs", turn))
                for u, (k, q, hh) in enumerate(proj):
                    if u >= 4:
                        w = u - 4
                        eng.wait_ge(*act.done(f"sq{w}" if w < QK else f"v{w}", turn))
                        if w < QK:
                            eng.wait_ge(*dve.done(f"rot{w}", turn))
                    at = k * H * DH + hh * 512
                    nc.tensor.matmul(ps[:, u % 4, :], xs[:, q * P:(q + 1) * P], wqkv[:, par, at:at + 512], start=True, stop=True)\
                        .then_inc(*pe.end(f"proj{u}"))
                for u, (k, cp) in enumerate(turns):
                    eng.wait_ge(*pool.done(f"qk{4 * k + 2 + cp // 2}", turn))
                    if u >= 2:
                        w, (kw, cw) = u - 2, turns[u - 2]
                        eng.wait_ge(*act.done(f"{'qk'[kw]}{cw}", turn))
                        if kw == 0:
                            eng.wait_ge(*dve.done(f"q{cw}", turn))
                    for c in range(2):
                        for q in range(QT):
                            h = 4 * cp + 2 * c
                            last = nc.tensor.transpose(ps[:, 4 + u % 2, c * S + q * P:c * S + (q + 1) * P],
                                                       qk[:, k, q, h:h + 2, :].rearrange("p h d -> p (h d)"), chip.ident[:, :])
                    last.then_inc(*pe.end(f"turn{u}"))

                def scores(c):
                    if c >= 2:
                        eng.wait_ge(*act.done(f"exp{c - 2}", turn))
                    for j in range(2):
                        h, bank = 2 * c + j, 2 * (c % 2) + j
                        for q, (lo, hi, key) in enumerate(((0, P, 0), (P, 288, P - EDGE))):
                            nc.tensor.matmul(ps[:, bank, lo:hi], qT[:, h, q * P:(q + 1) * P], kT[:, c, key:key + hi - lo],
                                             start=True, stop=False)
                            last = nc.tensor.matmul(ps[:, bank, lo:hi], chip.ident_b[:, :], f.band[:, q, 0:hi - lo], start=False, stop=True)
                    last.then_inc(*pe.end(f"s{c}"))

                eng.wait_ge(*act.done(f"k{PAIRS // 2 - 1}", turn))
                eng.wait_ge(*dve.done(f"q{PAIRS // 2 - 1}", turn))
                scores(0)
                scores(1)
                for c in range(PAIRS + 1):
                    if c < PAIRS:
                        eng.wait_ge(*pool.done(f"pn{c}", turn))
                        for j in range(2):
                            u, p = 2 * c + j, pr[:, c % 2, j, :]
                            if u >= 2:
                                eng.wait_ge(*(dve if j else act).done(f"pT{u - 2}", turn))
                            nc.tensor.transpose(ps[:, 4 + j, 0:P], p[:, 0:P], chip.ident[:, :])
                            nc.tensor.transpose(ps[:, 4 + j, P:S], p[:, P + EDGE:288], chip.ident[:, :])
                            nc.tensor.transpose(ps[0:EDGE, 4 + j, S:384], p[:, P:P + EDGE], chip.ident[:, :]).then_inc(*pe.end(f"pT{u}"))
                        if c + 2 < PAIRS:
                            scores(c + 2)
                    if c:
                        w = c - 1
                        eng.wait_ge(*act.done(f"pT{2 * w}", turn))
                        eng.wait_ge(*dve.done(f"pT{2 * w + 1}", turn))
                        if w >= 2:
                            eng.wait_ge(*dve.done(f"att{w - 2}", turn))
                        for j in range(2):
                            h, rows, out = 2 * w + j, prT[:, w % 2, j, :], ps[DH * j:DH * j + DH, 6 + w % 2, 0:S]
                            nc.tensor.matmul(out[:, 0:P], v[:, 0, h, :], rows[:, 0:P], start=True, stop=True, tile_position=(0, DH * j))
                            nc.tensor.matmul(out[:, P:S], v[:, 1, h, :], rows[:, P:S], start=True, stop=False, tile_position=(0, DH * j))
                            last = nc.tensor.matmul(out[:, P:S], ve[:, h, :], rows[0:EDGE, S:384], start=False, stop=True,
                                                    tile_position=(0, DH * j))
                        last.then_inc(*pe.end(f"pv{w}"))
                eng.wait_ge(*dve.done(f"att{PAIRS - 1}", turn))
                for c in range(PAIRS):
                    last = nc.tensor.matmul(ps[:, 0, 0:S], wo[:, par, c, :], attT[:, c, :], start=(c == 0), stop=(c == PAIRS - 1))
                last.then_inc(*pe.end("y1"))
                eng.wait_ge(*dve.done("x1s", turn))
                nc.tensor.matmul(ps[:, 1, 0:S], fp(f.mean_w), fp(x1s), start=True, stop=True).then_inc(*pe.end("mean"))
                eng.wait_ge(*dve.done("dsq", turn))
                nc.tensor.matmul(ps[:, 2, 0:S], fp(f.mean_w), fp(dsq), start=True, stop=True).then_inc(*pe.end("var"))
                eng.wait_ge(*dve.done("xn", turn))
                for i, (at, n) in enumerate(FFN_CHUNKS):
                    nc.tensor.matmul(ps[0:n, 3 + i, S:2 * S], w1[:, par, FFN_IN + at:FFN_IN + at + n], fp(xn), start=True, stop=True)
                    nc.tensor.matmul(ps[0:n, 3 + i, 0:S], w1[:, par, at:at + n], fp(xn), start=True, stop=True).then_inc(*pe.end(f"h{i}"))
                for i, (at, n) in enumerate(FFN_CHUNKS):
                    eng.wait_ge(*dve.done(f"g{i}", turn))
                    last = nc.tensor.matmul(ps[:, 1, 0:S], w2[0:n, par, i, :], g[0:n, i, :], start=(i == 0), stop=(i == 2))
                last.then_inc(*pe.end("y2"))

            layers(eng, body)



def constants():
    f = np.float32
    pos, feat = np.arange(S, dtype=f)[:, None], np.arange(D)
    freq = (f(1) / np.power(f(0.0001), f(2) * np.arange(2, dtype=f) / f(4)).astype(f)).astype(f)
    ang = (pos * freq[(feat % 4) // 2][None, :]).astype(f)
    sign = np.where(feat % 2 == 0, f(-1), f(1))[None, :]
    turn = np.stack([np.cos(ang), np.sin(ang) * sign]).astype(f)
    rope = np.stack([turn * f(0.5), turn])
    rope = rope.reshape(2, 2, QT, P, D).transpose(3, 0, 1, 2, 4)
    heads = (np.arange(P)[:, None] // 8 == np.arange(16)[None, :]).astype(f)
    see = lambda i, j: np.where((j <= i) & (j >= i - 32), f(0), f(MASKED))
    p = np.arange(P)[:, None]
    w = np.arange(160)[None, :]
    band = np.stack([see(p, w), see(P + p, 96 + w)], axis=1)
    sel8 = np.repeat(np.eye(8, dtype=f)[:, :, None], P, axis=2)
    before = (np.arange(P)[:, None] < np.arange(P)[None, :]).astype(f)
    qrows = np.zeros((P, S), f)
    qrows[65] = 1
    krows = np.zeros((2, P), f)
    krows[0, 65], krows[1, 64] = 1, 1
    return {"c_ident": np.eye(P, dtype=f), "c_rope": np.ascontiguousarray(rope), "c_heads": heads,
            "c_band": band.astype(f), "c_sel8": sel8, "c_before": before, "c_qrows": qrows, "c_krows": krows, "c_rank": np.tile(np.arange(8, 0, -1, dtype=f), (P, 1)),
            **l1_ffn_constants()}


def program(nc, a, out, stages):
    with ExitStack() as ctx:
        sb = lambda n, s, dt=F32: ctx.enter_context(nc.sbuf_tensor(n, s, dt))
        chip = Chip()
        chip.a = a
        chip.ps = ctx.enter_context(nc.psum_tensor("ps", [P, 8, 512], F32))
        chip.x_tok = sb("x_tok", [P, B, QT, D])
        chip.ctx_tok = sb("ctx_tok", [P, B, CT, D])
        chip.ctxT = sb("ctxT", [P, B, S2])
        chip.ident, chip.ident_b = sb("ident", [P, P]), sb("ident_b", [P, P], BF16)
        chip.ones = sb("ones", [P, 512])
        chip.neghalf, chip.eps = sb("neghalf", [P, S]), sb("eps", [P, 8])
        chip.zeros = sb("zeros", [P, P])
        chip.scratch = sb("scratch", [P, 8])
        chip.w = {}
        chip.initial_loads = [
            (fp(chip.ident), a["c_ident"]),
            (fp(chip.x_tok), a["x"].rearrange("b (t p) d -> p b t d", p=P)),
            (fp(chip.ctx_tok), a["ctx_1024"].rearrange("b (t p) d -> p b t d", p=P)),
        ]
        chip.turned_weights = []
        early = ExitStack()
        shared = lambda name: not name.startswith(("L0_", "L1_", "c_rope", "c_qrows", "c_krows"))
        for of_all in (True, False):
            stack = ctx if of_all else early
            add = lambda name, shape, dt=F32: chip.w.__setitem__(name, fp(stack.enter_context(nc.sbuf_tensor(f"w_{name}", list(shape), dt))))
            load = lambda name, src: chip.initial_loads.append((chip.w[name], src))
            for name, shape in LOADS.items():
                if shared(name) == of_all:
                    add(name, shape)
                    load(name, a[name])
            for name, n in ROWS.items():
                if shared(name) == of_all:
                    add(name, [1, n])
                    flat = a[name] if len(a[name].shape) == 1 else a[name].rearrange("e n -> (e n)")
                    load(name, flat.rearrange("(o n) -> o n", o=1))
            for name in COLS:
                if shared(name) == of_all:
                    add(name, [P, 1])
                    load(name, a[name].rearrange("(d o) -> d o", o=1))
            for name, n in SPREAD.items():
                if shared(name) == of_all:
                    add(name, [P, n])
                    load(name, a[name].partition_broadcast(P))
            for name, n in TURNED.items():
                if shared(name) == of_all:
                    add(name, [P, n, D])
            for name in ("c_rope", "c_heads", "c_band", "c_sel8", "c_before", "c_rank", "c_qrows", "c_krows"):
                if shared(name) == of_all:
                    add(name, a[name].shape)
                    load(name, a[name])
            if of_all:
                add("L2_ffn_b1", [P, 32])
                add("L2_attn_Wp", [P, 8])
                for head in range(16):
                    chip.initial_loads.append((chip.w["L2_attn_Wp"][8 * head:8 * head + 8, :], a["L2_attn_Wp"]))
            else:
                add("L0_xattn_w_out", [P, 4, D])
                load("L0_xattn_w_out", a["L0_xattn_w_out"].rearrange("(c p) d -> p c d", p=P))
                add("L0_attn_mask", [P, QT, S], I32)
                load("L0_attn_mask", a["L0_attn_mask"][0, 0, :, :].rearrange("(t p) k -> p t k", p=P))
        with ExitStack() as stay:
            for name, n in TURNED.items():
                raw = stay.enter_context(nc.sbuf_tensor(f"raw_{name}", [P, n, D], F32))
                src = {"L0_ffn_We": "e o i -> o e i"}.get(name)
                chip.initial_loads.append((fp(raw), a[name].rearrange(src) if src else
                                           a[name].rearrange("o (c i) -> o c i", i=D)))
                chip.turned_weights += [(chip.w[name][:, c, :], raw[:, c, :]) for c in range(n)]
            raw = stay.enter_context(nc.sbuf_tensor("raw_b1", [32, D], F32))
            chip.initial_loads.append((fp(raw), a["L2_ffn_b1"].rearrange("e (c p) -> (e c) p", p=P)))
            chip.turned_weights.append((chip.w["L2_ffn_b1"], fp(raw)))
            setup(nc, chip, a)
            context_stage(nc, chip)
        for stage in stages:
            if stage is l1_ffn:
                early.close()
            stage(nc, chip)
        early.close()
        stored = ctx.enter_context(nc.semaphore("stored"))
        with nc.Block() as block:
            @block.sync
            def _(sp):
                sp.dma_start(out.rearrange("b (t p) d -> p b t d", p=P), fp(chip.x_tok)).then_inc(stored, 16)
                sp.wait_ge(stored, 16)


def kernel(**inputs):
    import concourse.bacc as bacc
    from concourse.bass_utils import run_bass_kernel_spmd

    nc = bacc.Bacc("TRN2", target_bir_lowering=False, num_devices=1)
    arrays, aps = {}, {}
    for name, value in list(inputs.items()) + list(constants().items()):
        v = np.ascontiguousarray(value)
        if v.dtype == np.bool_:
            v = v.view(np.uint8)
        arrays[f"in_{name}"] = v
        shape = v.shape if v.shape else (1,)
        arrays[f"in_{name}"] = v.reshape(shape)
        aps[name] = nc.dram_tensor(f"in_{name}", shape, mybir.dt.from_np(v.dtype), kind="ExternalInput").ap()
    out = nc.dram_tensor("out_0", (B, S, D), F32, kind="ExternalOutput").ap()
    program(nc, aps, out, STAGES)
    r = run_bass_kernel_spmd(nc, [arrays], core_ids=[0])
    return r.results[0]["out_0"]
STAGES = [l0_attn, l0_xattn, l0_ffn, l1_attn, l1_xattn, l1_ffn, l2_attn, l2_xattn, l2_ffn, l3_attn, l3_xattn, l3_ffn]
```

```python
from contextlib import ExitStack

import numpy as np

import concourse.bass as bass
from concourse import mybir

F32 = mybir.dt.float32
BF16 = mybir.dt.bfloat16
I32 = mybir.dt.int32
U8 = mybir.dt.uint8
ALU = mybir.AluOpType
ACT = mybir.ActivationFunctionType
AX = mybir.AxisListType

P = 128
D = 128
B = 4
S = 256
QT = S // P
S2 = 512
CT = S2 // P
EPS = 1e-5
MASKED = -1e30
STRIP = 32


class Steps:

    def __init__(self, sem, names):
        self.sem, self.names, self.turn = sem, list(names), 0
        self.place = {n: k + 1 for k, n in enumerate(self.names)}
        assert len(self.place) == len(self.names)

    def end(self, name):
        assert self.names[self.turn % len(self.names)] == name, (self.names[self.turn % len(self.names)], name)
        self.turn += 1
        return self.sem, 1

    def done(self, name, turn=0):
        return self.sem, turn * len(self.names) + self.place[name]

    def passed(self, turn):
        return self.sem, turn * len(self.names)


class Chip:
    pass


def fp(handle):
    return handle[tuple(slice(None) for _ in handle.shape)]


def stage_sems(nc, ctx, label):
    return [ctx.enter_context(nc.semaphore(f"{label}_{e}_steps")) for e in ("pe", "dve", "act", "pool")] + \
        [ctx.enter_context(nc.semaphore(f"{label}_loads"))]



TAIL_DVE = ["sum", "stats", "var", "normed"]
TAIL_POOL = ["rstd"]


class Tail:

    def __init__(self, nc, ctx, label):
        sb = lambda n, s: ctx.enter_context(nc.sbuf_tensor(f"{label}_{n}", s, F32))
        self.y = sb("y", [P, QT, D])
        self.stats = sb("stats", [P, QT, 6])
        self.mv = sb("mv", [P, QT, 2])
        self.rstd = sb("rstd", [P, QT])


def tail_dve(nc, eng, chip, t, dve, pool, b, addend, residual):
    nc.vector.tensor_tensor(fp(t.y), addend, residual, ALU.add).then_inc(*dve.end("sum"))
    eng.wait_ge(*dve.done("sum", b))
    for q in range(QT):
        last = nc.vector.bn_stats(t.stats[:, q, :], t.y[:, q, :])
    last.then_inc(*dve.end("stats"))
    eng.wait_ge(*dve.done("stats", b))
    nc.vector.memset(chip.scratch[:, 0:1], 0.0)
    for q in range(QT):
        last = nc.vector.bn_aggr(t.mv[:, q, :], t.stats[:, q, :])
    last.then_inc(*dve.end("var"))
    eng.wait_ge(*pool.done("rstd", b))
    for q in range(QT):
        last = nc.vector.tensor_scalar(chip.x_tok[:, b, q, :], t.y[:, q, :], t.mv[:, q, 0:1], t.rstd[:, q:q + 1],
                                       ALU.subtract, ALU.mult)
    last.then_inc(*dve.end("normed"))


RSTD_POOL = ["vareps"]


def tail_pool(nc, eng, chip, t, dve, pool, b):
    eng.wait_ge(*dve.done("var", b))
    nc.gpsimd.tensor_tensor(fp(t.rstd), t.mv[:, :, 1], chip.eps[:, 0:QT], ALU.add).then_inc(*pool.end("vareps"))
    eng.wait_ge(*pool.done("vareps", b))
    nc.gpsimd.tensor_tensor(fp(t.rstd), fp(t.rstd), chip.neghalf[:, 0:QT], ALU.pow).then_inc(*pool.end("rstd"))


TAIL_POOL = ["vareps", "rstd"]


class Heads:

    def __init__(self, nc, ctx, label, G, NK):
        sb = lambda n, s, dt=F32: ctx.enter_context(nc.sbuf_tensor(f"{label}_{n}", s, dt))
        self.G, self.NK, self.KT = G, NK, NK // P
        self.qT = sb("qT", [P, G, S])
        self.kT = sb("kT", [P, G, NK])
        self.v = sb("v", [P, NK // P, 16, STRIP])
        self.nm = sb("nm", [P, QT, G, P])
        self.e = sb("e", [P, 2, 2, 512])
        self.oT = sb("oT", [P, G, S])
        self.rec = sb("rec", [P, QT, 16])
        self.att = sb("att", [P, QT, 4 * G, 8])
        self.s_units = [(g, p, q) for g in range(G) for p in range(2) for q in ([None] if NK == S else range(QT))]
        self.t_units = [(g, p, k) for g in range(G) for p in range(2) for k in range(NK // S)]
        self.rounds = G // 4

    def pe_steps(self):
        names = [f"scores{u}" for u in range(len(self.s_units))] + [f"negmax{g}" for g in range(self.G)]
        n = len(self.t_units)
        for u in range(n + 1):
            names += ([f"scoresT{u}"] if u < n else []) + ([f"pv{u - 1}"] if u else [])
        return names + [f"heads{r}" for r in range(self.rounds)]

    def dve_steps(self):
        names = [f"max{u}" for u in range(len(self.s_units))] + [f"guarded{g}" for g in range(self.G)]
        names += [f"out{g}" for g in range(self.G)]
        for r in range(self.rounds):
            names += [f"rec{r}", f"att{r}"]
        return names

    def act_steps(self):
        return [f"exp{u}" for u in range(len(self.t_units))]


def heads_pe(nc, eng, chip, h, pe, dve, act, b, vhead, mask=None):
    ps = chip.ps
    for u, (g, pair, q) in enumerate(h.s_units):
        if u >= 2:
            eng.wait_ge(*dve.done(f"max{u - 2}", b))
        for j in range(2):
            s0 = STRIP * (2 * pair + j)
            for qt in (range(QT) if q is None else [q]):
                col = 0 if q is not None else qt * S
                out = ps[:, 2 * (u % 2) + j, col:col + h.NK]
                last = nc.tensor.matmul(out, h.qT[s0:s0 + STRIP, g, qt * P:(qt + 1) * P], h.kT[s0:s0 + STRIP, g, :],
                                        start=True, stop=mask is None, tile_position=(s0, 0))
                if mask is not None:
                    last = nc.tensor.matmul(out, chip.ident_b[:, :], mask[0][:, qt, :], start=False, stop=True)
        last.then_inc(*pe.end(f"scores{u}"))
    for g in range(h.G):
        last_unit = max(u for u, x in enumerate(h.s_units) if x[0] == g)
        eng.wait_ge(*dve.done(f"max{last_unit}", b))
        if g >= 2:
            eng.wait_ge(*dve.done(f"guarded{g - 2}", b))
        for qt in range(QT):
            last = nc.tensor.transpose(ps[:, 4 + g % 2, qt * P:(qt + 1) * P], h.nm[:, qt, g, :], chip.ident[:, :])
        last.then_inc(*pe.end(f"negmax{g}"))
    n = len(h.t_units)
    per = h.NK // S
    for u in range(n + 1):
        if u < n:
            g, pair, kh = h.t_units[u]
            eng.wait_ge(*dve.done(f"guarded{g}", b))
            if u >= 2:
                eng.wait_ge(*act.done(f"exp{u - 2}", b))
            for j in range(2):
                s0 = STRIP * (2 * pair + j)
                for i in range(2):
                    kt = 2 * kh + i
                    out = ps[:, 2 * (u % 2) + j, i * S:(i + 1) * S]
                    last = nc.tensor.matmul(out, h.kT[s0:s0 + STRIP, g, kt * P:(kt + 1) * P],
                                            h.qT[s0:s0 + STRIP, g, :], start=True, stop=mask is None,
                                            tile_position=(s0, 0))
                    if mask is not None:
                        last = nc.tensor.matmul(out, chip.ident_b[:, :], mask[1][:, kt, :], start=False, stop=True)
            last.then_inc(*pe.end(f"scoresT{u}"))
        if u:
            w = u - 1
            g, pair, kh = h.t_units[w]
            eng.wait_ge(*act.done(f"exp{w}", b))
            if pair == 0 and kh == 0 and g >= 2:
                eng.wait_ge(*dve.done(f"out{g - 2}", b))
            for j in range(2):
                s0 = STRIP * (2 * pair + j)
                for i in range(2):
                    kt = 2 * kh + i
                    last = nc.tensor.matmul(ps[s0:s0 + STRIP, 6 + g % 2, 0:S], h.v[:, kt, vhead(4 * g + 2 * pair + j), :],
                                            h.e[:, w % 2, j, i * S:(i + 1) * S], start=(kt == 0),
                                            stop=(kt == h.KT - 1), tile_position=(0, s0))
            last.then_inc(*pe.end(f"pv{w}"))
    for r in range(h.rounds):
        if r:
            eng.wait_ge(*dve.done(f"att{r - 1}", b))
        for g in range(4 * r, 4 * r + 4):
            eng.wait_ge(*dve.done(f"out{g}", b))
            for qt in range(QT):
                last = nc.tensor.transpose(ps[:, 4 + qt, (g % 4) * P:(g % 4 + 1) * P], h.oT[:, g, qt * P:(qt + 1) * P],
                                           chip.ident[:, :])
        last.then_inc(*pe.end(f"heads{r}"))


def heads_dve(nc, eng, chip, h, pe, dve, b, hd):
    ps = chip.ps
    for u, (g, pair, q) in enumerate(h.s_units):
        eng.wait_ge(*pe.done(f"scores{u}", b))
        c0 = STRIP * 2 * pair + hd
        bank = 2 * (u % 2)
        if q is None:
            src = ps[:, bank:bank + 2, :].rearrange("p j (t k) -> p j t k", t=QT)
            dst = h.nm[:, :, g, c0:c0 + STRIP + 1:STRIP].rearrange("p t j -> p j t")
        else:
            src, dst = ps[:, bank:bank + 2, :], h.nm[:, q, g, c0:c0 + STRIP + 1:STRIP]
        nc.vector.tensor_reduce(dst, src, AX.X, ALU.max, negate=True).then_inc(*dve.end(f"max{u}"))
    for g in range(h.G):
        eng.wait_ge(*pe.done(f"negmax{g}", b))
        nc.vector.tensor_tensor(h.qT[:, g, :], h.qT[:, g, :], ps[:, 4 + g % 2, 0:S], ALU.add)\
            .then_inc(*dve.end(f"guarded{g}"))
    for g in range(h.G):
        eng.wait_ge(*pe.done(f"pv{max(u for u, x in enumerate(h.t_units) if x[0] == g)}", b))
        nc.vector.tensor_copy(h.oT[:, g, :], ps[:, 6 + g % 2, 0:S]).then_inc(*dve.end(f"out{g}"))
    for r in range(h.rounds):
        eng.wait_ge(*pe.done(f"heads{r}", b))
        o = ps[:, 4:6, :].rearrange("p t (h c) -> p t h c", c=STRIP)
        nc.vector.reciprocal(h.rec[:, :, :], o[:, :, :, 8]).then_inc(*dve.end(f"rec{r}"))
        eng.wait_ge(*dve.done(f"rec{r}", b))
        nc.vector.tensor_tensor(h.att[:, :, 16 * r:16 * r + 16, :], o[:, :, :, 0:8],
                                h.rec[:, :, :].unsqueeze(3).to_broadcast([P, QT, 16, 8]), ALU.mult)\
            .then_inc(*dve.end(f"att{r}"))


def heads_act(nc, eng, chip, h, pe, act, b):
    for u in range(len(h.t_units)):
        eng.wait_ge(*pe.done(f"scoresT{u}", b))
        if u >= 2:
            eng.wait_ge(*pe.done(f"pv{u - 2}", b))
        bank = 2 * (u % 2)
        nc.scalar.activation(h.e[:, u % 2, :, :], chip.ps[:, bank:bank + 2, :], ACT.Exp).then_inc(*act.end(f"exp{u}"))


def clear_heads(nc, eng, h, hd, cleared):
    nc.gpsimd.memset(fp(h.nm), 0.0).then_inc(cleared, 1)
    nc.gpsimd.memset(h.v[:, :, :, 0:8], 0.0)
    nc.gpsimd.memset(h.v[:, :, :, 9:STRIP], 0.0)
    nc.gpsimd.memset(h.v[:, :, :, 8:9], 1.0).then_inc(cleared, 1)


def pad_heads(dst, hd):
    return dst.rearrange("k g (j c) -> k (g j) c", c=STRIP)[:, :, 0:hd]



LOADS = {
    "L0_attn_w_kvc": (P, D), "L0_attn_w_kvu": (P, 2 * D), "L0_attn_w_qc": (P, 32), "L0_attn_w_qu": (32, D),
    "L0_attn_w_o": (P, D), "L0_xattn_w_q": (P, 512), "L0_xattn_w_kv": (P, 1024), "L0_ffn_Wg": (P, 8),
    "L1_attn_Wq": (P, D), "L1_attn_Wk": (P, D), "L1_attn_Wv": (P, D), "L1_attn_Wo": (P, D),
    "L2_attn_Wq": (P, D), "L2_attn_Wk": (P, D), "L2_attn_Wv": (P, D),
    "L2_ffn_Wg": (P, 8), "L2_ffn_b2": (8, D),
    "L3_attn_Wq": (P, D), "L3_attn_Wk": (P, D), "L3_attn_Wv": (P, D), "L3_attn_Wp": (P, D),
    "L3_ffn_Wr": (P, 7),
}
ROWS = {
    "L0_attn_b_kvc": D, "L0_attn_b_kvu": 2 * D, "L0_attn_b_qc": 32, "L0_attn_b_qu": D, "L0_attn_b_o": D,
    "L0_ffn_bg": 8, "L0_ffn_be": 8 * D, "L1_xattn_Wv_b": D, "L2_attn_bv": D, "L2_xattn_b_l": D, "L2_ffn_bg": 8,
    "L3_attn_bq": D, "L3_attn_bk": D, "L3_attn_bv": D, "L3_attn_bp": D, "L3_xattn_bo": D,
}
COLS = [
    "L0_xattn_g_x", "L0_xattn_b_x", "L0_xattn_g_l", "L0_xattn_b_l", "L1_xattn_Wq_b", "L1_xattn_Wk_b",
    "L2_attn_bq", "L2_attn_bk", "L2_xattn_w_cq", "L2_xattn_w_c", "L2_xattn_w_q", "L3_ffn_ln_g", "L3_ffn_ln_b",
]
SPREAD = {
    "L0_xattn_g_o": D, "L0_xattn_b_o": D, "L1_attn_lambda_q1": 4, "L1_attn_lambda_k1": 4, "L1_attn_lambda_q2": 4,
    "L1_attn_lambda_k2": 4, "L1_attn_subln_g": 8, "L2_xattn_b_cq": 1, "L2_xattn_b_c": 1, "L2_xattn_b_q": 1,
}
TURNED = {
    "L0_ffn_We": 8, "L1_xattn_Wq_w": 1, "L1_xattn_Wk_w": 1, "L1_xattn_Wv_w": 1, "L2_xattn_W_l": 4,
    "L3_xattn_Wv": 1, "L3_xattn_Wk": 1, "L3_xattn_Wq": 1, "L3_xattn_Wo": 1,
}


def setup(nc, chip, a):
    with ExitStack() as ctx:
        pe_s, dve_s, act_s, pool_s, loads = stage_sems(nc, ctx, "setup")
        fetched = []

        block = ctx.enter_context(nc.Block())

        @block.sync
        def _(sp):
            n = 0
            for dst, src in chip.initial_loads:
                sp.dma_start(dst, src).then_inc(loads, 16)
                n += 16
            sp.wait_ge(loads, n)

        @block.gpsimd
        def _(pool):
            nc.gpsimd.memset(fp(chip.neghalf), -0.5)
            nc.gpsimd.memset(fp(chip.eps), EPS)
            nc.gpsimd.memset(fp(chip.zeros), 0.0)
            nc.gpsimd.memset(fp(chip.ones), 1.0)


def context_stage(nc, chip):
    with ExitStack() as ctx:
        pe_s, dve_s, act_s, pool_s, loads = stage_sems(nc, ctx, "context")
        jobs = [(chip.ctxT[:, b, c * P:(c + 1) * P], chip.ctx_tok[:, b, c, :]) for b in range(B) for c in range(CT)]
        jobs += chip.turned_weights
        full = 4
        units = [jobs[i:i + full] for i in range(0, len(jobs), full)]
        pe = Steps(pe_s, [f"turn{u}" for u in range(len(units))])
        dve = Steps(dve_s, [f"copy{u}" for u in range(len(units))])
        block = ctx.enter_context(nc.Block())

        @block.tensor
        def _(eng):
            for u, unit in enumerate(units):
                if u >= 8:
                    eng.wait_ge(*dve.done(f"copy{u - 8}"))
                for i, (dst, src) in enumerate(unit):
                    n = src.shape[0]
                    last = nc.tensor.transpose(chip.ps[:, u % 8, i * P:i * P + n], src, chip.ident[0:n, 0:n])
                last.then_inc(*pe.end(f"turn{u}"))

        @block.vector
        def _(eng):
            nc.vector.tensor_copy(fp(chip.ident_b), fp(chip.ident))
            for u, unit in enumerate(units):
                eng.wait_ge(*pe.done(f"turn{u}"))
                for i, (dst, src) in enumerate(unit):
                    last = nc.vector.tensor_copy(dst, chip.ps[:, u % 8, i * P:i * P + src.shape[0]])
                last.then_inc(*dve.end(f"copy{u}"))


def l0_attn(nc, chip):
    with ExitStack() as ctx:
        sb = lambda n, s, dt=F32: ctx.enter_context(nc.sbuf_tensor(f"l0a_{n}", s, dt))
        pe_s, dve_s, act_s, pool_s, ready = stage_sems(nc, ctx, "l0a")
        hd, G = 8, 4
        h = Heads(nc, ctx, "l0a", G, S)
        t = Tail(nc, ctx, "l0a")
        wq, wk = sb("wq", [32, G, P]), sb("wk", [P, G, P])
        bq, bk = sb("bq", [1, G, P]), sb("bk", [1, G, P])
        mq, mf, mk = sb("mq", [P, QT, S], BF16), sb("mf", [P, QT, S]), sb("mk", [P, QT, S], BF16)
        xb, xT = sb("xb", [P, QT, D]), sb("xT", [P, S])
        latent, low, attT = sb("latent", [P, S]), sb("low", [32, S]), sb("attT", [P, S])
        ps, w = chip.ps, chip.w
        pre_dve = ["mask", "maskb", "maskT", "wq", "wk", "bq", "bk"]
        pre = Steps(ctx.enter_context(nc.semaphore("l0a_prepared")), pre_dve)
        turned = ctx.enter_context(nc.semaphore("l0a_mask_turned"))
        pe = Steps(pe_s, ["xT", "latent", "low", "q", "k", "v"] + h.pe_steps() + ["attT", "y"])
        dve = Steps(dve_s, ["x", "xT", "latent", "low", "q", "k", "v"] + h.dve_steps() + ["attT"] + TAIL_DVE)
        act = Steps(act_s, h.act_steps())
        pool = Steps(pool_s, TAIL_POOL)
        block = ctx.enter_context(nc.Block())

        @block.gpsimd
        def _(eng):
            clear_heads(nc, eng, h, hd, ready)
            nc.gpsimd.memset(fp(wq), 0.0)
            nc.gpsimd.memset(fp(wk), 0.0)
            nc.gpsimd.memset(fp(bq), 0.0)
            nc.gpsimd.memset(fp(bk), 0.0).then_inc(ready, 1)
            with eng.Fori(0, B) as b:
                tail_pool(nc, eng, chip, t, dve, pool, b)

        @block.vector
        def _(eng):
            nc.vector.tensor_scalar(fp(mf), w["L0_attn_mask"], 0, MASKED, ALU.is_equal, ALU.mult).then_inc(*pre.end("mask"))
            eng.wait_ge(*pre.done("mask"))
            nc.vector.tensor_copy(fp(mq), fp(mf)).then_inc(*pre.end("maskb"))
            eng.wait_ge(turned, 1)
            nc.vector.tensor_copy(fp(mk), ps[:, 0:2, 0:S]).then_inc(*pre.end("maskT"))
            eng.wait_ge(ready, 3)
            nc.vector.tensor_copy(pad_heads(fp(wq), hd), w["L0_attn_w_qu"].rearrange("k (h c) -> k h c", c=hd))\
                .then_inc(*pre.end("wq"))
            nc.vector.tensor_copy(pad_heads(fp(wk), hd), w["L0_attn_w_kvu"][:, 0:D].rearrange("k (h c) -> k h c", c=hd))\
                .then_inc(*pre.end("wk"))
            nc.vector.tensor_copy(pad_heads(fp(bq), hd), w["L0_attn_b_qu"].rearrange("k (h c) -> k h c", c=hd))\
                .then_inc(*pre.end("bq"))
            nc.vector.tensor_copy(pad_heads(fp(bk), hd), w["L0_attn_b_kvu"][:, 0:D].rearrange("k (h c) -> k h c", c=hd))
            nc.vector.memset(fp(bk).rearrange("k g (j c) -> k (g j) c", c=STRIP)[:, :, hd:hd + 1], 1.0)\
                .then_inc(*pre.end("bk"))
            with eng.Fori(0, B) as b:
                nc.vector.tensor_copy(fp(xb), chip.x_tok[:, b, :, :]).then_inc(*dve.end("x"))
                eng.wait_ge(*pe.done("xT", b))
                nc.vector.tensor_copy(fp(xT), ps[:, 6, 0:S]).then_inc(*dve.end("xT"))
                eng.wait_ge(*pe.done("latent", b))
                nc.vector.tensor_copy(fp(latent), ps[:, 7, 0:S]).then_inc(*dve.end("latent"))
                eng.wait_ge(*pe.done("low", b))
                nc.vector.tensor_copy(fp(low), ps[0:32, 6, 0:S]).then_inc(*dve.end("low"))
                eng.wait_ge(*pe.done("q", b))
                nc.vector.tensor_scalar(fp(h.qT), ps[:, 4:6, :].rearrange("p a (g t) -> p (a g) t", t=S),
                                        float(1 / np.sqrt(np.float32(hd))), None, ALU.mult).then_inc(*dve.end("q"))
                eng.wait_ge(*pe.done("k", b))
                nc.vector.tensor_copy(fp(h.kT), ps[:, 0:2, :].rearrange("p a (g t) -> p (a g) t", t=S))\
                    .then_inc(*dve.end("k"))
                eng.wait_ge(*pe.done("v", b))
                nc.vector.tensor_copy(h.v[:, :, :, 0:hd], ps[:, 2, 0:S].rearrange("p (t h c) -> p t h c", t=QT, c=hd))\
                    .then_inc(*dve.end("v"))
                heads_dve(nc, eng, chip, h, pe, dve, b, hd)
                eng.wait_ge(*pe.done("attT", b))
                nc.vector.tensor_copy(fp(attT), ps[:, 6, 0:S]).then_inc(*dve.end("attT"))
                eng.wait_ge(*pe.done("y", b))
                tail_dve(nc, eng, chip, t, dve, pool, b, ps[:, 7, 0:S].rearrange("p (t d) -> p t d", t=QT), fp(xb))

        @block.scalar
        def _(eng):
            with eng.Fori(0, B) as b:
                heads_act(nc, eng, chip, h, pe, act, b)

        @block.tensor
        def _(eng):
            eng.wait_ge(*pre.done("mask"))
            for kt in range(QT):
                for qt in range(QT):
                    last = nc.tensor.transpose(ps[:, kt, qt * P:(qt + 1) * P], mf[:, qt, kt * P:(kt + 1) * P],
                                               chip.ident[:, :])
            last.then_inc(turned, 1)
            eng.wait_ge(*pre.done("bk"))
            eng.wait_ge(ready, 3)
            with eng.Fori(0, B) as b:
                eng.wait_ge(*dve.done("x", b))
                for qt in range(QT):
                    last = nc.tensor.transpose(ps[:, 6, qt * P:(qt + 1) * P], xb[:, qt, :], chip.ident[:, :])
                last.then_inc(*pe.end("xT"))
                eng.wait_ge(*dve.done("xT", b))
                nc.tensor.matmul(ps[:, 7, 0:S], w["L0_attn_w_kvc"], fp(xT), start=True, stop=False)
                nc.tensor.matmul(ps[:, 7, 0:S], w["L0_attn_b_kvc"], chip.ones[0:1, 0:S], start=False, stop=True)\
                    .then_inc(*pe.end("latent"))
                nc.tensor.matmul(ps[0:32, 6, 0:S], w["L0_attn_w_qc"], fp(xT), start=True, stop=False)
                nc.tensor.matmul(ps[0:32, 6, 0:S], w["L0_attn_b_qc"], chip.ones[0:1, 0:S], start=False, stop=True)\
                    .then_inc(*pe.end("low"))
                eng.wait_ge(*dve.done("low", b))
                for g in range(G):
                    out = ps[:, 4 + g // 2, (g % 2) * S:(g % 2 + 1) * S]
                    nc.tensor.matmul(out, wq[:, g, :], fp(low), start=True, stop=False)
                    last = nc.tensor.matmul(out, bq[:, g, :], chip.ones[0:1, 0:S], start=False, stop=True)
                last.then_inc(*pe.end("q"))
                for g in range(G):
                    out = ps[:, g // 2, (g % 2) * S:(g % 2 + 1) * S]
                    nc.tensor.matmul(out, wk[:, g, :], fp(latent), start=True, stop=False)
                    last = nc.tensor.matmul(out, bk[:, g, :], chip.ones[0:1, 0:S], start=False, stop=True)
                last.then_inc(*pe.end("k"))
                for kt in range(QT):
                    out = ps[:, 2, kt * P:(kt + 1) * P]
                    nc.tensor.matmul(out, latent[:, kt * P:(kt + 1) * P], w["L0_attn_w_kvu"][:, D:2 * D], start=True, stop=False)
                    last = nc.tensor.matmul(out, chip.ones[0:1, 0:P], w["L0_attn_b_kvu"][:, D:2 * D], start=False, stop=True)
                last.then_inc(*pe.end("v"))
                eng.wait_ge(*dve.done("v", b))
                heads_pe(nc, eng, chip, h, pe, dve, act, b, lambda i: i, mask=(mq, mk))
                project_out(nc, eng, chip, h.att, attT, pe, dve, b, h.rounds, w["L0_attn_w_o"], w["L0_attn_b_o"])


def project_out(nc, eng, chip, att, attT, pe, dve, b, rounds, wo, bo, ready="att"):
    ps = chip.ps
    eng.wait_ge(*dve.done(f"att{rounds - 1}" if ready == "att" else ready, b))
    for qt in range(QT):
        src = att[:, qt, :, :].rearrange("p h c -> p (h c)") if len(att.shape) == 4 else att[:, qt, :]
        last = nc.tensor.transpose(chip.ps[:, 6, qt * P:(qt + 1) * P], src, chip.ident[:, :])
    last.then_inc(*pe.end("attT"))
    eng.wait_ge(*dve.done("attT", b))
    for qt in range(QT):
        out = ps[:, 7, qt * P:(qt + 1) * P]
        last = nc.tensor.matmul(out, attT[:, qt * P:(qt + 1) * P], wo, start=True, stop=bo is None)
        if bo is not None:
            last = nc.tensor.matmul(out, chip.ones[0:1, 0:P], bo, start=False, stop=True)
    last.then_inc(*pe.end("y"))


def l3_xattn(nc, chip):
    with ExitStack() as ctx:
        sb = lambda n, s, dt=F32: ctx.enter_context(nc.sbuf_tensor(f"l3x_{n}", s, dt))
        pe_s, dve_s, act_s, pool_s, ready = stage_sems(nc, ctx, "l3x")
        hd, G = 8, 4
        h = Heads(nc, ctx, "l3x", G, S2)
        t = Tail(nc, ctx, "l3x")
        wq, wk, bk = sb("wq", [P, G, P]), sb("wk", [P, G, P]), sb("bk", [1, G, P])
        xb, xT, cT, attT = sb("xb", [P, QT, D]), sb("xT", [P, S]), sb("cT", [P, S2]), sb("attT", [P, S])
        ps, w = chip.ps, chip.w
        padded = ctx.enter_context(nc.semaphore("l3x_padded"))
        pe = Steps(pe_s, ["xT", "v", "k", "q"] + h.pe_steps() + ["attT", "y"])
        dve = Steps(dve_s, ["x", "xT", "v", "k", "q"] + h.dve_steps() + ["attT"] + TAIL_DVE)
        act = Steps(act_s, h.act_steps())
        pool = Steps(pool_s, TAIL_POOL)
        block = ctx.enter_context(nc.Block())

        @block.gpsimd
        def _(eng):
            clear_heads(nc, eng, h, hd, ready)
            nc.gpsimd.memset(fp(wq), 0.0)
            nc.gpsimd.memset(fp(wk), 0.0)
            nc.gpsimd.memset(fp(bk), 0.0).then_inc(ready, 1)
            with eng.Fori(0, B) as b:
                tail_pool(nc, eng, chip, t, dve, pool, b)

        @block.vector
        def _(eng):
            eng.wait_ge(ready, 3)
            for dst, src in ((wq, w["L3_xattn_Wq"]), (wk, w["L3_xattn_Wk"])):
                nc.vector.tensor_copy(pad_heads(fp(dst), hd), src[:, 0, :].rearrange("k (h c) -> k h c", c=hd))
            nc.vector.memset(fp(bk).rearrange("k g (j c) -> k (g j) c", c=STRIP)[:, :, hd:hd + 1], 1.0)\
                .then_inc(padded, 1)
            with eng.Fori(0, B) as b:
                nc.vector.tensor_copy(fp(xb), chip.x_tok[:, b, :, :])
                nc.vector.tensor_copy(fp(cT), chip.ctxT[:, b, :]).then_inc(*dve.end("x"))
                eng.wait_ge(*pe.done("xT", b))
                nc.vector.tensor_copy(fp(xT), ps[:, 6, 0:S]).then_inc(*dve.end("xT"))
                eng.wait_ge(*pe.done("v", b))
                nc.vector.tensor_copy(h.v[:, :, :, 0:hd], ps[:, 7, :].rearrange("p (t h c) -> p t h c", t=CT, c=hd))\
                    .then_inc(*dve.end("v"))
                eng.wait_ge(*pe.done("k", b))
                nc.vector.tensor_copy(fp(h.kT), ps[:, 0:4, :]).then_inc(*dve.end("k"))
                eng.wait_ge(*pe.done("q", b))
                nc.vector.tensor_scalar(fp(h.qT), ps[:, 4:6, :].rearrange("p a (g t) -> p (a g) t", t=S),
                                        float(np.float32(1) / np.sqrt(np.float32(D))), None, ALU.mult)\
                    .then_inc(*dve.end("q"))
                heads_dve(nc, eng, chip, h, pe, dve, b, hd)
                eng.wait_ge(*pe.done("attT", b))
                nc.vector.tensor_copy(fp(attT), ps[:, 6, 0:S]).then_inc(*dve.end("attT"))
                eng.wait_ge(*pe.done("y", b))
                tail_dve(nc, eng, chip, t, dve, pool, b, ps[:, 7, 0:S].rearrange("p (t d) -> p t d", t=QT), fp(xb))

        @block.scalar
        def _(eng):
            with eng.Fori(0, B) as b:
                heads_act(nc, eng, chip, h, pe, act, b)

        @block.tensor
        def _(eng):
            eng.wait_ge(padded, 1)
            eng.wait_ge(ready, 3)
            with eng.Fori(0, B) as b:
                eng.wait_ge(*dve.done("x", b))
                for qt in range(QT):
                    last = nc.tensor.transpose(ps[:, 6, qt * P:(qt + 1) * P], xb[:, qt, :], chip.ident[:, :])
                last.then_inc(*pe.end("xT"))
                for kt in range(CT):
                    last = nc.tensor.matmul(ps[:, 7, kt * P:(kt + 1) * P], cT[:, kt * P:(kt + 1) * P],
                                            w["L3_xattn_Wv"][:, 0, :], start=True, stop=True)
                last.then_inc(*pe.end("v"))
                for g in range(G):
                    nc.tensor.matmul(ps[:, g, :], wk[:, g, :], fp(cT), start=True, stop=False)
                    last = nc.tensor.matmul(ps[:, g, :], bk[:, g, :], chip.ones[0:1, :], start=False, stop=True)
                last.then_inc(*pe.end("k"))
                eng.wait_ge(*dve.done("xT", b))
                for g in range(G):
                    last = nc.tensor.matmul(ps[:, 4 + g // 2, (g % 2) * S:(g % 2 + 1) * S], wq[:, g, :], fp(xT),
                                            start=True, stop=True)
                last.then_inc(*pe.end("q"))
                eng.wait_ge(*dve.done("q", b))
                heads_pe(nc, eng, chip, h, pe, dve, act, b, lambda i: i)
                project_out(nc, eng, chip, h.att, attT, pe, dve, b, h.rounds, w["L3_xattn_Wo"][:, 0, :], w["L3_xattn_bo"])


def l2_attn(nc, chip):
    with ExitStack() as ctx:
        sb = lambda n, s, dt=F32: ctx.enter_context(nc.sbuf_tensor(f"l2a_{n}", s, dt))
        pe_s, dve_s, act_s, pool_s, ready = stage_sems(nc, ctx, "l2a")
        hd, G = 8, 4
        h = Heads(nc, ctx, "l2a", G, S)
        t = Tail(nc, ctx, "l2a")
        wp, bk = sb("wp", [P, G, P]), sb("bk", [1, G, P])
        xb, xT = sb("xb", [P, QT, D]), sb("xT", [P, S])
        q0, k0 = sb("q0", [P, S]), sb("k0", [P, S])
        ps, w = chip.ps, chip.w
        padded = ctx.enter_context(nc.semaphore("l2a_padded"))
        pe = Steps(pe_s, ["xT", "q0", "k0", "v", "q", "k"] + h.pe_steps())
        dve = Steps(dve_s, ["x", "xT", "q0", "k0", "v", "q", "k"] + h.dve_steps() + TAIL_DVE)
        act = Steps(act_s, h.act_steps())
        pool = Steps(pool_s, TAIL_POOL)
        block = ctx.enter_context(nc.Block())

        @block.gpsimd
        def _(eng):
            clear_heads(nc, eng, h, hd, ready)
            nc.gpsimd.memset(fp(wp), 0.0)
            nc.gpsimd.memset(fp(bk), 0.0).then_inc(ready, 1)
            with eng.Fori(0, B) as b:
                tail_pool(nc, eng, chip, t, dve, pool, b)

        @block.vector
        def _(eng):
            eng.wait_ge(ready, 3)
            nc.vector.tensor_tensor(pad_heads(fp(wp), hd), w["L2_attn_Wp"].unsqueeze(1).to_broadcast([P, 16, hd]),
                                    w["c_heads"].unsqueeze(2).to_broadcast([P, 16, hd]), ALU.mult)
            nc.vector.memset(fp(bk).rearrange("k g (j c) -> k (g j) c", c=STRIP)[:, :, hd:hd + 1], 1.0)\
                .then_inc(padded, 1)
            with eng.Fori(0, B) as b:
                nc.vector.tensor_copy(fp(xb), chip.x_tok[:, b, :, :]).then_inc(*dve.end("x"))
                eng.wait_ge(*pe.done("xT", b))
                nc.vector.tensor_copy(fp(xT), ps[:, 6, 0:S]).then_inc(*dve.end("xT"))
                eng.wait_ge(*pe.done("q0", b))
                nc.vector.tensor_scalar(fp(q0), ps[:, 3, 0:S], w["L2_attn_bq"], None, ALU.add).then_inc(*dve.end("q0"))
                eng.wait_ge(*pe.done("k0", b))
                nc.vector.tensor_scalar(fp(k0), ps[:, 7, 0:S], w["L2_attn_bk"], None, ALU.add).then_inc(*dve.end("k0"))
                eng.wait_ge(*pe.done("v", b))
                nc.vector.tensor_copy(h.v[:, :, :, 0:hd], ps[:, 2, 0:S].rearrange("p (t h c) -> p t h c", t=QT, c=hd))\
                    .then_inc(*dve.end("v"))
                eng.wait_ge(*pe.done("q", b))
                nc.vector.tensor_scalar(fp(h.qT), ps[:, 4:6, :].rearrange("p a (g t) -> p (a g) t", t=S),
                                        float(1 / np.sqrt(hd)), None, ALU.mult).then_inc(*dve.end("q"))
                eng.wait_ge(*pe.done("k", b))
                nc.vector.tensor_copy(fp(h.kT), ps[:, 0:2, :].rearrange("p a (g t) -> p (a g) t", t=S))\
                    .then_inc(*dve.end("k"))
                heads_dve(nc, eng, chip, h, pe, dve, b, hd)
                eng.wait_ge(*dve.done(f"att{h.rounds - 1}", b))
                tail_dve(nc, eng, chip, t, dve, pool, b, fp(h.att).rearrange("p t h c -> p t (h c)"), fp(xb))

        @block.scalar
        def _(eng):
            with eng.Fori(0, B) as b:
                heads_act(nc, eng, chip, h, pe, act, b)

        @block.tensor
        def _(eng):
            eng.wait_ge(padded, 1)
            eng.wait_ge(ready, 3)
            with eng.Fori(0, B) as b:
                eng.wait_ge(*dve.done("x", b))
                for qt in range(QT):
                    last = nc.tensor.transpose(ps[:, 6, qt * P:(qt + 1) * P], xb[:, qt, :], chip.ident[:, :])
                last.then_inc(*pe.end("xT"))
                eng.wait_ge(*dve.done("xT", b))
                nc.tensor.matmul(ps[:, 3, 0:S], w["L2_attn_Wq"], fp(xT), start=True, stop=True).then_inc(*pe.end("q0"))
                nc.tensor.matmul(ps[:, 7, 0:S], w["L2_attn_Wk"], fp(xT), start=True, stop=True).then_inc(*pe.end("k0"))
                for kt in range(QT):
                    out = ps[:, 2, kt * P:(kt + 1) * P]
                    nc.tensor.matmul(out, xT[:, kt * P:(kt + 1) * P], w["L2_attn_Wv"], start=True, stop=False)
                    last = nc.tensor.matmul(out, chip.ones[0:1, 0:P], w["L2_attn_bv"], start=False, stop=True)
                last.then_inc(*pe.end("v"))
                eng.wait_ge(*dve.done("q0", b))
                for g in range(G):
                    last = nc.tensor.matmul(ps[:, 4 + g // 2, (g % 2) * S:(g % 2 + 1) * S], wp[:, g, :], fp(q0),
                                            start=True, stop=True)
                last.then_inc(*pe.end("q"))
                eng.wait_ge(*dve.done("k0", b))
                for g in range(G):
                    out = ps[:, g // 2, (g % 2) * S:(g % 2 + 1) * S]
                    nc.tensor.matmul(out, wp[:, g, :], fp(k0), start=True, stop=False)
                    last = nc.tensor.matmul(out, bk[:, g, :], chip.ones[0:1, 0:S], start=False, stop=True)
                last.then_inc(*pe.end("k"))
                eng.wait_ge(*dve.done("k", b))
                heads_pe(nc, eng, chip, h, pe, dve, act, b, lambda i: i)


LAMBDA_INIT = 0.8 - 0.6 * float(np.exp(-0.3 * 12))


def l1_attn(nc, chip):
    with ExitStack() as ctx:
        sb = lambda n, s, dt=F32: ctx.enter_context(nc.sbuf_tensor(f"l1a_{n}", s, dt))
        pe_s, dve_s, act_s, pool_s, ready = stage_sems(nc, ctx, "l1a")
        hd, G = 4, 8
        h = Heads(nc, ctx, "l1a", G, S)
        t = Tail(nc, ctx, "l1a")
        xb, xT, attT = sb("xb", [P, QT, D]), sb("xT", [P, S]), sb("attT", [P, S])
        pad = sb("pad", [P, 2, QT, 32, STRIP])
        rot, rot2 = sb("rot", [P, QT, D]), sb("rot2", [P, QT, D])
        lam, lam2, neglam = sb("lam", [P, 2, 4]), sb("lam2", [P, 2]), sb("neglam", [P, 1])
        gain = sb("gain", [P, 8])
        diff, sq = sb("diff", [P, QT, 16, 8]), sb("sq", [P, QT, 16, 8])
        ms, rms = sb("ms", [P, QT, 16]), sb("rms", [P, QT, 16])
        heads = sb("heads", [P, QT, D])
        ps, w = chip.ps, chip.w
        lam_steps = Steps(ctx.enter_context(nc.semaphore("l1a_lambda_steps")), ["products", "sums", "neglam"])
        lam_exp = ctx.enter_context(nc.semaphore("l1a_lambda_exp"))
        pe = Steps(pe_s, ["xT", "qkv", "qTkT0", "qTkT1"] + h.pe_steps() + ["attT", "y"])
        dve = Steps(dve_s, ["x", "xT", "v"] + [f"{k}{n}" for k in "qk" for n in ("cos", "sin", "turned")] + ["qT", "kT"]
                    + h.dve_steps() + ["diff", "sq", "ms", "rms", "gained", "heads"] + ["attT"] + TAIL_DVE)
        act = Steps(act_s, h.act_steps())
        pool = Steps(pool_s, ["rmseps", "rmspow"] + TAIL_POOL)
        block = ctx.enter_context(nc.Block())

        @block.gpsimd
        def _(eng):
            clear_heads(nc, eng, h, hd, ready)
            nc.gpsimd.memset(pad[:, 0, :, :, :], 0.0)
            nc.gpsimd.memset(pad[:, 1, :, :, 0:hd], 0.0)
            nc.gpsimd.memset(pad[:, 1, :, :, hd + 1:STRIP], 0.0)
            nc.gpsimd.memset(pad[:, 1, :, :, hd:hd + 1], 1.0).then_inc(ready, 1)
            with eng.Fori(0, B) as b:
                eng.wait_ge(*dve.done("ms", b))
                nc.gpsimd.tensor_tensor(fp(rms), fp(ms), chip.eps[:, 0:1].unsqueeze(2).to_broadcast([P, QT, 16]), ALU.add)\
                    .then_inc(*pool.end("rmseps"))
                eng.wait_ge(*pool.done("rmseps", b))
                nc.gpsimd.tensor_tensor(fp(rms), fp(rms), chip.neghalf[:, 0:32].rearrange("p (t h) -> p t h", t=QT), ALU.pow)\
                    .then_inc(*pool.end("rmspow"))
                tail_pool(nc, eng, chip, t, dve, pool, b)

        @block.vector
        def _(eng):
            nc.vector.tensor_tensor(lam[:, 0, :], w["L1_attn_lambda_q1"], w["L1_attn_lambda_k1"], ALU.mult)
            nc.vector.tensor_tensor(lam[:, 1, :], w["L1_attn_lambda_q2"], w["L1_attn_lambda_k2"], ALU.mult)\
                .then_inc(*lam_steps.end("products"))
            nc.vector.tensor_scalar(fp(gain), w["L1_attn_subln_g"], 1.0 - LAMBDA_INIT, None, ALU.mult)
            eng.wait_ge(*lam_steps.done("products"))
            nc.vector.tensor_reduce(fp(lam2), fp(lam), AX.X, ALU.add).then_inc(*lam_steps.end("sums"))
            eng.wait_ge(lam_exp, 1)
            nc.vector.scalar_tensor_tensor(fp(neglam), lam2[:, 1:2], -LAMBDA_INIT, lam2[:, 0:1], ALU.add, ALU.subtract)\
                .then_inc(*lam_steps.end("neglam"))
            eng.wait_ge(*lam_steps.done("neglam"))
            eng.wait_ge(ready, 3)
            with eng.Fori(0, B) as b:
                nc.vector.tensor_copy(fp(xb), chip.x_tok[:, b, :, :]).then_inc(*dve.end("x"))
                eng.wait_ge(*pe.done("xT", b))
                nc.vector.tensor_copy(fp(xT), ps[:, 6, 0:S]).then_inc(*dve.end("xT"))
                eng.wait_ge(*pe.done("qkv", b))
                nc.vector.tensor_copy(h.v[:, :, :, 0:8], ps[:, 2, 0:S].rearrange("p (t h c) -> p t h c", t=QT, c=8))\
                    .then_inc(*dve.end("v"))
                for i, k in enumerate("qk"):
                    src = ps[:, i, 0:S].rearrange("p (t d) -> p t d", t=QT)
                    pairs = ps[:, i, 0:S].rearrange("p (n c) -> p n c", c=2)
                    sin = w["c_rope"][:, i, 1, :, :].rearrange("p t (n c) -> p (t n) c", c=2)
                    out = fp(rot2).rearrange("p t (n c) -> p (t n) c", c=2)
                    if i:
                        eng.wait_ge(*dve.done("qturned", b))
                    nc.vector.tensor_tensor(fp(rot), src, w["c_rope"][:, i, 0, :, :], ALU.mult).then_inc(*dve.end(k + "cos"))
                    nc.vector.tensor_tensor(out[:, :, 0], pairs[:, :, 1], sin[:, :, 0], ALU.mult)
                    nc.vector.tensor_tensor(out[:, :, 1], pairs[:, :, 0], sin[:, :, 1], ALU.mult).then_inc(*dve.end(k + "sin"))
                    eng.wait_ge(*dve.done(k + "sin", b))
                    nc.vector.tensor_tensor(pad[:, i, :, :, 0:hd], fp(rot).rearrange("p t (h c) -> p t h c", c=hd),
                                            fp(rot2).rearrange("p t (h c) -> p t h c", c=hd), ALU.add)\
                        .then_inc(*dve.end(k + "turned"))
                for i, dst in enumerate((h.qT, h.kT)):
                    eng.wait_ge(*pe.done(f"qTkT{i}", b))
                    nc.vector.tensor_copy(fp(dst), ps[:, 4 * i:4 * i + 4, :].rearrange("p a (g t) -> p (a g) t", t=S))\
                        .then_inc(*dve.end("qk"[i] + "T"))
                heads_dve(nc, eng, chip, h, pe, dve, b, hd)
                eng.wait_ge(*dve.done(f"att{h.rounds - 1}", b))
                pair = fp(h.att).rearrange("p t (h two) c -> p (t h) two c", two=2)
                nc.vector.scalar_tensor_tensor(fp(diff).rearrange("p t h c -> p (t h) c"), pair[:, :, 1, :], neglam[:, 0:1],
                                               pair[:, :, 0, :], ALU.mult, ALU.add).then_inc(*dve.end("diff"))
                eng.wait_ge(*dve.done("diff", b))
                nc.vector.scalar_tensor_tensor(fp(sq), fp(diff), 1.0 / 8, fp(diff), ALU.mult, ALU.mult).then_inc(*dve.end("sq"))
                eng.wait_ge(*dve.done("sq", b))
                nc.vector.tensor_reduce(fp(ms), fp(sq), AX.X, ALU.add).then_inc(*dve.end("ms"))
                eng.wait_ge(*pool.done("rmspow", b))
                nc.vector.tensor_tensor(fp(sq), fp(diff), fp(rms).unsqueeze(3).to_broadcast([P, QT, 16, 8]), ALU.mult)\
                    .then_inc(*dve.end("rms"))
                eng.wait_ge(*dve.done("rms", b))
                nc.vector.tensor_tensor(fp(heads).rearrange("p t (h c) -> p (t h) c", c=8),
                                        fp(sq).rearrange("p t h c -> p (t h) c"),
                                        fp(gain).unsqueeze(1).to_broadcast([P, 32, 8]), ALU.mult).then_inc(*dve.end("gained"))
                eng.wait_ge(*dve.done("gained", b))
                nc.vector.memset(chip.scratch[:, 1:2], 0.0).then_inc(*dve.end("heads"))
                eng.wait_ge(*pe.done("attT", b))
                nc.vector.tensor_copy(fp(attT), ps[:, 6, 0:S]).then_inc(*dve.end("attT"))
                eng.wait_ge(*pe.done("y", b))
                tail_dve(nc, eng, chip, t, dve, pool, b, ps[:, 7, 0:S].rearrange("p (t d) -> p t d", t=QT), fp(xb))

        @block.scalar
        def _(eng):
            eng.wait_ge(*lam_steps.done("sums"))
            nc.scalar.activation(fp(lam2), fp(lam2), ACT.Exp).then_inc(lam_exp, 1)
            with eng.Fori(0, B) as b:
                heads_act(nc, eng, chip, h, pe, act, b)

        @block.tensor
        def _(eng):
            eng.wait_ge(ready, 3)
            with eng.Fori(0, B) as b:
                eng.wait_ge(*dve.done("x", b))
                for qt in range(QT):
                    last = nc.tensor.transpose(ps[:, 6, qt * P:(qt + 1) * P], xb[:, qt, :], chip.ident[:, :])
                last.then_inc(*pe.end("xT"))
                eng.wait_ge(*dve.done("xT", b))
                for i, name in enumerate(("L1_attn_Wq", "L1_attn_Wk", "L1_attn_Wv")):
                    for qt in range(QT):
                        last = nc.tensor.matmul(ps[:, i, qt * P:(qt + 1) * P], xT[:, qt * P:(qt + 1) * P], w[name],
                                                start=True, stop=True)
                last.then_inc(*pe.end("qkv"))
                for i, k in enumerate("qk"):
                    eng.wait_ge(*dve.done("kturned", b))
                    for g in range(G):
                        for qt in range(QT):
                            at = (g % 2) * S + qt * P
                            last = nc.tensor.transpose(ps[:, 4 * i + g // 2, at:at + P],
                                                       pad[:, i, qt, 4 * g:4 * g + 4, :].rearrange("p h c -> p (h c)"),
                                                       chip.ident[:, :])
                    last.then_inc(*pe.end(f"qTkT{i}"))
                eng.wait_ge(*dve.done("kT", b))
                heads_pe(nc, eng, chip, h, pe, dve, act, b, lambda i: i // 2)
                project_out(nc, eng, chip, heads, attT, pe, dve, b, h.rounds, w["L1_attn_Wo"], None, ready="heads")


def l3_attn(nc, chip):
    with ExitStack() as ctx:
        sb = lambda n, s, dt=F32: ctx.enter_context(nc.sbuf_tensor(f"l3a_{n}", s, dt))
        pe_s, dve_s, act_s, pool_s, ready = stage_sems(nc, ctx, "l3a")
        t = Tail(nc, ctx, "l3a")
        xb, xT = sb("xb", [P, QT, D]), sb("xT", [P, S])
        low, qk, v = sb("low", [P, 2, S]), sb("qk", [P, 2, S]), sb("v", [P, S])
        ex = sb("ex", [P, 2, S])
        kv, oT = sb("kv", [P, D]), sb("oT", [P, S])
        ps, w = chip.ps, chip.w
        pe = Steps(pe_s, ["xT", "qkv", "kv", "oT", "y"])
        dve = Steps(dve_s, ["x", "xT", "low", "v", "qk", "kv", "oT"] + TAIL_DVE)
        act = Steps(act_s, ["exp"])
        pool = Steps(pool_s, TAIL_POOL)
        block = ctx.enter_context(nc.Block())

        @block.gpsimd
        def _(eng):
            with eng.Fori(0, B) as b:
                tail_pool(nc, eng, chip, t, dve, pool, b)

        @block.scalar
        def _(eng):
            with eng.Fori(0, B) as b:
                eng.wait_ge(*dve.done("low", b))
                nc.scalar.activation(fp(ex), fp(low), ACT.Exp).then_inc(*act.end("exp"))

        @block.vector
        def _(eng):
            with eng.Fori(0, B) as b:
                nc.vector.tensor_copy(fp(xb), chip.x_tok[:, b, :, :]).then_inc(*dve.end("x"))
                eng.wait_ge(*pe.done("xT", b))
                nc.vector.tensor_copy(fp(xT), ps[:, 6, 0:S]).then_inc(*dve.end("xT"))
                eng.wait_ge(*pe.done("qkv", b))
                nc.vector.tensor_scalar(fp(low), ps[:, 0:2, 0:S], 0.0, None, ALU.min).then_inc(*dve.end("low"))
                nc.vector.tensor_copy(fp(v), ps[:, 2, 0:S]).then_inc(*dve.end("v"))
                eng.wait_ge(*act.done("exp", b))
                nc.vector.scalar_tensor_tensor(fp(qk), ps[:, 0:2, 0:S], 0.0, fp(ex), ALU.max, ALU.add)\
                    .then_inc(*dve.end("qk"))
                eng.wait_ge(*pe.done("kv", b))
                nc.vector.tensor_tensor(fp(kv).rearrange("p (h c) -> p h c", c=8),
                                        ps[:, 3, 0:D].rearrange("p (h c) -> p h c", c=8),
                                        w["c_heads"].unsqueeze(2).to_broadcast([P, 16, 8]), ALU.mult).then_inc(*dve.end("kv"))
                eng.wait_ge(*pe.done("oT", b))
                nc.vector.tensor_copy(fp(oT), ps[:, 4, 0:S]).then_inc(*dve.end("oT"))
                eng.wait_ge(*pe.done("y", b))
                tail_dve(nc, eng, chip, t, dve, pool, b, ps[:, 7, 0:S].rearrange("p (t d) -> p t d", t=QT), fp(xb))

        @block.tensor
        def _(eng):
            with eng.Fori(0, B) as b:
                eng.wait_ge(*dve.done("x", b))
                for qt in range(QT):
                    last = nc.tensor.transpose(ps[:, 6, qt * P:(qt + 1) * P], xb[:, qt, :], chip.ident[:, :])
                last.then_inc(*pe.end("xT"))
                eng.wait_ge(*dve.done("xT", b))
                nc.tensor.matmul(ps[:, 0, 0:S], w["L3_attn_Wq"], fp(xT), start=True, stop=False)
                nc.tensor.matmul(ps[:, 0, 0:S], w["L3_attn_bq"], chip.ones[0:1, 0:S], start=False, stop=True)
                for i, k in ((1, "k"), (2, "v")):
                    for kt in range(QT):
                        out = ps[:, i, kt * P:(kt + 1) * P]
                        nc.tensor.matmul(out, xT[:, kt * P:(kt + 1) * P], w[f"L3_attn_W{k}"], start=True, stop=False)
                        last = nc.tensor.matmul(out, chip.ones[0:1, 0:P], w[f"L3_attn_b{k}"], start=False, stop=True)
                last.then_inc(*pe.end("qkv"))
                eng.wait_ge(*dve.done("qk", b))
                for kt in range(QT):
                    last = nc.tensor.matmul(ps[:, 3, 0:D], qk[:, 1, kt * P:(kt + 1) * P], v[:, kt * P:(kt + 1) * P],
                                            start=(kt == 0), stop=(kt == QT - 1))
                last.then_inc(*pe.end("kv"))
                eng.wait_ge(*dve.done("kv", b))
                nc.tensor.matmul(ps[:, 4, 0:S], fp(kv), qk[:, 0, :], start=True, stop=True).then_inc(*pe.end("oT"))
                eng.wait_ge(*dve.done("oT", b))
                for qt in range(QT):
                    out = ps[:, 7, qt * P:(qt + 1) * P]
                    nc.tensor.matmul(out, oT[:, qt * P:(qt + 1) * P], w["L3_attn_Wp"], start=True, stop=False)
                    last = nc.tensor.matmul(out, chip.ones[0:1, 0:P], w["L3_attn_bp"], start=False, stop=True)
                last.then_inc(*pe.end("y"))


class Pick:

    def __init__(self, nc, ctx, label, n):
        sb = lambda k, s: ctx.enter_context(nc.sbuf_tensor(f"{label}_{k}", s, F32))
        self.n = n
        self.m, self.eq, self.best = sb("m", [P, QT]), sb("eq", [P, QT, n]), sb("best", [P, QT])


def pick_steps(p):
    return [p + s for s in ("max", "eq", "cand", "best", "pick")]


def pick_first(nc, eng, chip, k, dve, b, p, v, out):
    wide = lambda x: fp(x).unsqueeze(2).to_broadcast([P, QT, k.n])
    nc.vector.tensor_reduce(fp(k.m), v, AX.X, ALU.max).then_inc(*dve.end(p + "max"))
    eng.wait_ge(*dve.done(p + "max", b))
    nc.vector.tensor_tensor(fp(k.eq), v, wide(k.m), ALU.is_equal).then_inc(*dve.end(p + "eq"))
    eng.wait_ge(*dve.done(p + "eq", b))
    nc.vector.tensor_tensor(fp(k.eq), fp(k.eq), chip.w["c_rank"][:, 0:k.n].unsqueeze(1).to_broadcast([P, QT, k.n]), ALU.mult)\
        .then_inc(*dve.end(p + "cand"))
    eng.wait_ge(*dve.done(p + "cand", b))
    nc.vector.tensor_reduce(fp(k.best), fp(k.eq), AX.X, ALU.max).then_inc(*dve.end(p + "best"))
    eng.wait_ge(*dve.done(p + "best", b))
    nc.vector.tensor_tensor(out, fp(k.eq), wide(k.best), ALU.is_equal).then_inc(*dve.end(p + "pick"))


def l0_ffn(nc, chip):
    E = 8
    with ExitStack() as ctx:
        sb = lambda n, s, dt=F32: ctx.enter_context(nc.sbuf_tensor(f"l0f_{n}", s, dt))
        pe_s, dve_s, act_s, pool_s, ready = stage_sems(nc, ctx, "l0f")
        t, k = Tail(nc, ctx, "l0f"), Pick(nc, ctx, "l0f", E)
        xb, xT = sb("xb", [P, QT, D]), sb("xT", [P, S])
        gate, one, two = sb("gate", [P, QT, E]), sb("one", [P, QT, E]), sb("two", [P, QT, E])
        mx, den = sb("mx", [P, QT]), sb("den", [P, QT])
        prod, mixed = sb("prod", [P, QT, E, D]), sb("mixed", [P, QT, D])
        ps, w = chip.ps, chip.w
        pe = Steps(pe_s, ["xT", "logits", "experts"])
        dve = Steps(dve_s, ["x", "xT", "gmax", "shift", "den", "rden", "gate"] + pick_steps("first") + ["rest"]
                    + pick_steps("second") + ["sel", "kept", "kden", "rkden", "weight", "prod", "mixed"] + TAIL_DVE)
        act = Steps(act_s, ["exp"])
        pool = Steps(pool_s, TAIL_POOL)
        wide = lambda x: fp(x).unsqueeze(2).to_broadcast([P, QT, E])
        block = ctx.enter_context(nc.Block())

        @block.gpsimd
        def _(eng):
            with eng.Fori(0, B) as b:
                tail_pool(nc, eng, chip, t, dve, pool, b)

        @block.scalar
        def _(eng):
            with eng.Fori(0, B) as b:
                eng.wait_ge(*dve.done("shift", b))
                nc.scalar.activation(fp(gate), fp(gate), ACT.Exp).then_inc(*act.end("exp"))

        @block.vector
        def _(eng):
            with eng.Fori(0, B) as b:
                nc.vector.tensor_copy(fp(xb), chip.x_tok[:, b, :, :]).then_inc(*dve.end("x"))
                eng.wait_ge(*pe.done("xT", b))
                nc.vector.tensor_copy(fp(xT), ps[:, 6, 0:S]).then_inc(*dve.end("xT"))
                eng.wait_ge(*pe.done("logits", b))
                logits = ps[:, 7, 0:QT * E].rearrange("p (t e) -> p t e", e=E)
                nc.vector.tensor_reduce(fp(mx), logits, AX.X, ALU.max).then_inc(*dve.end("gmax"))
                eng.wait_ge(*dve.done("gmax", b))
                nc.vector.tensor_tensor(fp(gate), logits, wide(mx), ALU.subtract).then_inc(*dve.end("shift"))
                eng.wait_ge(*act.done("exp", b))
                nc.vector.tensor_reduce(fp(den), fp(gate), AX.X, ALU.add).then_inc(*dve.end("den"))
                eng.wait_ge(*dve.done("den", b))
                nc.vector.reciprocal(fp(den), fp(den)).then_inc(*dve.end("rden"))
                eng.wait_ge(*dve.done("rden", b))
                nc.vector.tensor_tensor(fp(gate), fp(gate), wide(den), ALU.mult).then_inc(*dve.end("gate"))
                eng.wait_ge(*dve.done("gate", b))
                pick_first(nc, eng, chip, k, dve, b, "first", fp(gate), fp(one))
                eng.wait_ge(*dve.done("firstpick", b))
                nc.vector.scalar_tensor_tensor(fp(two), fp(one), -2.0, fp(gate), ALU.mult, ALU.add).then_inc(*dve.end("rest"))
                eng.wait_ge(*dve.done("rest", b))
                pick_first(nc, eng, chip, k, dve, b, "second", fp(two), fp(two))
                eng.wait_ge(*dve.done("secondpick", b))
                nc.vector.tensor_tensor(fp(one), fp(one), fp(two), ALU.add).then_inc(*dve.end("sel"))
                eng.wait_ge(*dve.done("sel", b))
                nc.vector.tensor_tensor(fp(gate), fp(gate), fp(one), ALU.mult).then_inc(*dve.end("kept"))
                eng.wait_ge(*dve.done("kept", b))
                nc.vector.tensor_reduce(fp(den), fp(gate), AX.X, ALU.add).then_inc(*dve.end("kden"))
                eng.wait_ge(*dve.done("kden", b))
                nc.vector.reciprocal(fp(den), fp(den)).then_inc(*dve.end("rkden"))
                eng.wait_ge(*dve.done("rkden", b))
                nc.vector.tensor_tensor(fp(gate), fp(gate), wide(den), ALU.mult).then_inc(*dve.end("weight"))
                eng.wait_ge(*dve.done("weight", b))
                eng.wait_ge(*pe.done("experts", b))
                for qt in range(QT):
                    last = nc.vector.tensor_tensor(prod[:, qt, :, :],
                                                   ps[:, 2 * qt:2 * qt + 2, :].rearrange("p a (e d) -> p (a e) d", d=D),
                                                   gate[:, qt, :].unsqueeze(2).to_broadcast([P, E, D]), ALU.mult)
                last.then_inc(*dve.end("prod"))
                eng.wait_ge(*dve.done("prod", b))
                for qt in range(QT):
                    last = nc.vector.tensor_reduce(mixed[:, qt, :], prod[:, qt, :, :].rearrange("p e d -> p d e"), AX.X, ALU.add)
                last.then_inc(*dve.end("mixed"))
                eng.wait_ge(*dve.done("mixed", b))
                tail_dve(nc, eng, chip, t, dve, pool, b, fp(mixed), fp(xb))

        @block.tensor
        def _(eng):
            with eng.Fori(0, B) as b:
                eng.wait_ge(*dve.done("x", b))
                for qt in range(QT):
                    last = nc.tensor.transpose(ps[:, 6, qt * P:(qt + 1) * P], xb[:, qt, :], chip.ident[:, :])
                last.then_inc(*pe.end("xT"))
                eng.wait_ge(*dve.done("xT", b))
                for qt in range(QT):
                    out = ps[:, 7, qt * E:(qt + 1) * E]
                    nc.tensor.matmul(out, xT[:, qt * P:(qt + 1) * P], w["L0_ffn_Wg"], start=True, stop=False)
                    last = nc.tensor.matmul(out, chip.ones[0:1, 0:P], w["L0_ffn_bg"], start=False, stop=True)
                last.then_inc(*pe.end("logits"))
                for qt in range(QT):
                    for a in range(2):
                        out = ps[:, 2 * qt + a, :]
                        nc.tensor.matmul(out, xT[:, qt * P:(qt + 1) * P],
                                         w["L0_ffn_We"][:, 4 * a:4 * a + 4, :].rearrange("p e d -> p (e d)"), start=True, stop=False)
                        last = nc.tensor.matmul(out, chip.ones[0:1, 0:P], w["L0_ffn_be"][:, 512 * a:512 * a + 512],
                                                start=False, stop=True)
                last.then_inc(*pe.end("experts"))


def l1_xattn(nc, chip):
    with ExitStack() as ctx:
        sb = lambda n, s, dt=F32: ctx.enter_context(nc.sbuf_tensor(f"l1x_{n}", s, dt))
        pe_s, dve_s, act_s, pool_s, ready = stage_sems(nc, ctx, "l1x")
        t = Tail(nc, ctx, "l1x")
        xb, xT, cT = sb("xb", [P, QT, D]), sb("xT", [P, S]), sb("cT", [P, S2])
        qT, kT, v = sb("qT", [P, S]), sb("kT", [P, S2]), sb("v", [P, CT, D])
        nm, den, rden = sb("nm", [P, QT]), sb("den", [P, QT]), sb("rden", [P, QT])
        pr, prT, out_sb = sb("pr", [P, QT, S2]), sb("prT", [P, QT, CT, P]), sb("out", [P, QT, D])
        ps, w = chip.ps, chip.w
        pe = Steps(pe_s, ["xT", "kv", "q", "s", "prT", "o"])
        dve = Steps(dve_s, ["x", "xT", "k", "v", "q", "nm", "rden", "prT", "o"] + TAIL_DVE)
        act = Steps(act_s, ["exp"])
        pool = Steps(pool_s, TAIL_POOL)
        block = ctx.enter_context(nc.Block())

        @block.gpsimd
        def _(eng):
            with eng.Fori(0, B) as b:
                tail_pool(nc, eng, chip, t, dve, pool, b)

        @block.scalar
        def _(eng):
            with eng.Fori(0, B) as b:
                eng.wait_ge(*dve.done("nm", b))
                for qt in range(QT):
                    last = nc.scalar.activation(pr[:, qt, :], ps[:, 3 + qt, :], ACT.Exp, bias=nm[:, qt:qt + 1],
                                                accum_out=den[:, qt:qt + 1])
                last.then_inc(*act.end("exp"))

        @block.vector
        def _(eng):
            with eng.Fori(0, B) as b:
                nc.vector.tensor_copy(fp(xb), chip.x_tok[:, b, :, :])
                nc.vector.tensor_copy(fp(cT), chip.ctxT[:, b, :]).then_inc(*dve.end("x"))
                eng.wait_ge(*pe.done("xT", b))
                nc.vector.tensor_copy(fp(xT), ps[:, 6, 0:S]).then_inc(*dve.end("xT"))
                eng.wait_ge(*pe.done("kv", b))
                nc.vector.tensor_scalar(fp(kT), ps[:, 0, :], w["L1_xattn_Wk_b"], None, ALU.add).then_inc(*dve.end("k"))
                nc.vector.tensor_copy(fp(v), ps[:, 1, :].rearrange("p (t d) -> p t d", t=CT)).then_inc(*dve.end("v"))
                eng.wait_ge(*pe.done("q", b))
                nc.vector.tensor_scalar(fp(qT), ps[:, 2, 0:S], w["L1_xattn_Wq_b"], float(np.float32(1) / np.sqrt(np.float32(D))),
                                        ALU.add, ALU.mult).then_inc(*dve.end("q"))
                eng.wait_ge(*pe.done("s", b))
                nc.vector.tensor_reduce(fp(nm), ps[:, 3:5, :], AX.X, ALU.max, negate=True).then_inc(*dve.end("nm"))
                eng.wait_ge(*act.done("exp", b))
                nc.vector.reciprocal(fp(rden), fp(den)).then_inc(*dve.end("rden"))
                eng.wait_ge(*pe.done("prT", b))
                for qt, bank in enumerate((5, 0)):
                    last = nc.vector.tensor_copy(prT[:, qt, :, :], ps[:, bank, :].rearrange("p (t q) -> p t q", t=CT))
                last.then_inc(*dve.end("prT"))
                eng.wait_ge(*pe.done("o", b))
                eng.wait_ge(*dve.done("rden", b))
                for qt in range(QT):
                    last = nc.vector.tensor_scalar(out_sb[:, qt, :], ps[:, 7, qt * P:(qt + 1) * P], rden[:, qt:qt + 1], None, ALU.mult)
                last.then_inc(*dve.end("o"))
                eng.wait_ge(*dve.done("o", b))
                tail_dve(nc, eng, chip, t, dve, pool, b, fp(out_sb), fp(xb))

        @block.tensor
        def _(eng):
            with eng.Fori(0, B) as b:
                eng.wait_ge(*dve.done("x", b))
                for qt in range(QT):
                    last = nc.tensor.transpose(ps[:, 6, qt * P:(qt + 1) * P], xb[:, qt, :], chip.ident[:, :])
                last.then_inc(*pe.end("xT"))
                nc.tensor.matmul(ps[:, 0, :], w["L1_xattn_Wk_w"][:, 0, :], fp(cT), start=True, stop=True)
                for kt in range(CT):
                    out = ps[:, 1, kt * P:(kt + 1) * P]
                    nc.tensor.matmul(out, cT[:, kt * P:(kt + 1) * P], w["L1_xattn_Wv_w"][:, 0, :], start=True, stop=False)
                    last = nc.tensor.matmul(out, chip.ones[0:1, 0:P], w["L1_xattn_Wv_b"], start=False, stop=True)
                last.then_inc(*pe.end("kv"))
                eng.wait_ge(*dve.done("xT", b))
                nc.tensor.matmul(ps[:, 2, 0:S], w["L1_xattn_Wq_w"][:, 0, :], fp(xT), start=True, stop=True).then_inc(*pe.end("q"))
                eng.wait_ge(*dve.done("q", b))
                for qt in range(QT):
                    last = nc.tensor.matmul(ps[:, 3 + qt, :], qT[:, qt * P:(qt + 1) * P], fp(kT), start=True, stop=True)
                last.then_inc(*pe.end("s"))
                eng.wait_ge(*act.done("exp", b))
                for qt, bank in enumerate((5, 0)):
                    for kt in range(CT):
                        last = nc.tensor.transpose(ps[:, bank, kt * P:(kt + 1) * P], pr[:, qt, kt * P:(kt + 1) * P], chip.ident[:, :])
                last.then_inc(*pe.end("prT"))
                eng.wait_ge(*dve.done("prT", b))
                for qt in range(QT):
                    for kt in range(CT):
                        last = nc.tensor.matmul(ps[:, 7, qt * P:(qt + 1) * P], prT[:, qt, kt, :], v[:, kt, :],
                                                start=(kt == 0), stop=(kt == CT - 1))
                last.then_inc(*pe.end("o"))


def l2_xattn(nc, chip):
    with ExitStack() as ctx:
        sb = lambda n, s, dt=F32: ctx.enter_context(nc.sbuf_tensor(f"l2x_{n}", s, dt))
        pe_s, dve_s, act_s, pool_s, ready = stage_sems(nc, ctx, "l2x")
        t = Tail(nc, ctx, "l2x")
        xb, xT, cT, cb = sb("xb", [P, QT, D]), sb("xT", [P, S]), sb("cT", [P, S2]), sb("cb", [P, CT, D])
        xw, bsum = sb("xw", [P, S]), sb("bsum", [P, 1])
        nm, den, rden, top = sb("nm", [P, QT]), sb("den", [P, QT]), sb("rden", [P, QT]), sb("top", [P, QT])
        pr, prT = sb("pr", [P, QT, S2]), sb("prT", [P, CT, QT, P])
        att, xatt, xq = sb("att", [P, S]), sb("xatt", [P, S]), sb("xq", [P, S])
        rowmax, rowden, row = sb("rowmax", [1, 1]), sb("rowden", [1, 2]), sb("row", [1, S])
        col, q2c = sb("col", [P, QT]), sb("q2c", [P, 1])
        ps, w = chip.ps, chip.w
        pe = Steps(pe_s, ["xT", "s", "toprow", "prT", "att", "col", "q2c", "z"])
        dve = Steps(dve_s, ["bsum1", "x", "xT", "xw", "nm", "top", "rowmax", "rden", "norm", "prT", "att", "xatt",
                            "rowden", "rown", "col", "q2c", "xq"] + TAIL_DVE)
        act = Steps(act_s, ["exp", "rowexp"])
        pool = Steps(pool_s, TAIL_POOL)
        block = ctx.enter_context(nc.Block())

        @block.gpsimd
        def _(eng):
            with eng.Fori(0, B) as b:
                tail_pool(nc, eng, chip, t, dve, pool, b)

        @block.scalar
        def _(eng):
            with eng.Fori(0, B) as b:
                eng.wait_ge(*dve.done("nm", b))
                for qt in range(QT):
                    last = nc.scalar.activation(pr[:, qt, :], ps[:, 3 + qt, :], ACT.Exp, bias=nm[:, qt:qt + 1],
                                                accum_out=den[:, qt:qt + 1])
                last.then_inc(*act.end("exp"))
                eng.wait_ge(*dve.done("rowmax", b))
                nc.scalar.activation(fp(row), ps[0:1, 2, 0:S], ACT.Exp, bias=fp(rowmax), accum_out=rowden[:, 0:1])\
                    .then_inc(*act.end("rowexp"))

        @block.vector
        def _(eng):
            with eng.Fori(0, B) as b:
                nc.vector.tensor_copy(fp(xb), chip.x_tok[:, b, :, :])
                nc.vector.tensor_copy(fp(cb), chip.ctx_tok[:, b, :, :])
                nc.vector.tensor_copy(fp(cT), chip.ctxT[:, b, :])
                nc.vector.tensor_tensor(fp(bsum), w["L2_xattn_b_c"], w["L2_xattn_b_q"], ALU.add).then_inc(*dve.end("bsum1"))
                eng.wait_ge(*dve.done("bsum1", b))
                nc.vector.tensor_tensor(fp(bsum), fp(bsum), w["L2_xattn_b_cq"], ALU.add).then_inc(*dve.end("x"))
                eng.wait_ge(*pe.done("xT", b))
                nc.vector.tensor_copy(fp(xT), ps[:, 6, 0:S]).then_inc(*dve.end("xT"))
                nc.vector.tensor_scalar(fp(xw), ps[:, 6, 0:S], w["L2_xattn_w_cq"], w["L2_xattn_w_q"], ALU.mult, ALU.add)\
                    .then_inc(*dve.end("xw"))
                eng.wait_ge(*pe.done("s", b))
                nc.vector.tensor_reduce(fp(nm), ps[:, 3:5, :], AX.X, ALU.max, negate=True).then_inc(*dve.end("nm"))
                eng.wait_ge(*dve.done("nm", b))
                eng.wait_ge(*dve.done("x", b))
                nc.vector.scalar_tensor_tensor(fp(top), ps[:, 7, 0:QT], bsum[:, 0:1], fp(nm), ALU.add, ALU.subtract)\
                    .then_inc(*dve.end("top"))
                eng.wait_ge(*pe.done("toprow", b))
                nc.vector.tensor_reduce(fp(rowmax), ps[0:1, 2, 0:S], AX.X, ALU.max, negate=True).then_inc(*dve.end("rowmax"))
                eng.wait_ge(*act.done("exp", b))
                nc.vector.reciprocal(fp(rden), fp(den)).then_inc(*dve.end("rden"))
                eng.wait_ge(*dve.done("rden", b))
                for qt in range(QT):
                    last = nc.vector.tensor_scalar(pr[:, qt, :], pr[:, qt, :], rden[:, qt:qt + 1], None, ALU.mult)
                last.then_inc(*dve.end("norm"))
                eng.wait_ge(*pe.done("prT", b))
                for qt, bank in enumerate((5, 0)):
                    last = nc.vector.tensor_copy(prT[:, :, qt, :], ps[:, bank, :].rearrange("p (t q) -> p t q", t=CT))
                last.then_inc(*dve.end("prT"))
                eng.wait_ge(*pe.done("att", b))
                nc.vector.tensor_copy(fp(att), ps[:, 1, 0:S]).then_inc(*dve.end("att"))
                nc.vector.tensor_tensor(fp(xatt), ps[:, 1, 0:S], fp(xT), ALU.mult).then_inc(*dve.end("xatt"))
                eng.wait_ge(*act.done("rowexp", b))
                nc.vector.reciprocal(rowden[:, 1:2], rowden[:, 0:1]).then_inc(*dve.end("rowden"))
                eng.wait_ge(*dve.done("rowden", b))
                nc.vector.tensor_scalar(fp(row), fp(row), rowden[:, 1:2], None, ALU.mult).then_inc(*dve.end("rown"))
                eng.wait_ge(*pe.done("col", b))
                nc.vector.tensor_copy(fp(col), ps[:, 2, 0:QT]).then_inc(*dve.end("col"))
                eng.wait_ge(*pe.done("q2c", b))
                nc.vector.tensor_copy(fp(q2c), ps[:, 2, 4:5]).then_inc(*dve.end("q2c"))
                eng.wait_ge(*dve.done("q2c", b))
                nc.vector.tensor_scalar(fp(xq), fp(xT), q2c[:, 0:1], None, ALU.mult).then_inc(*dve.end("xq"))
                eng.wait_ge(*pe.done("z", b))
                tail_dve(nc, eng, chip, t, dve, pool, b, ps[:, 7, 0:S].rearrange("p (t d) -> p t d", t=QT), fp(xb))

        @block.tensor
        def _(eng):
            with eng.Fori(0, B) as b:
                eng.wait_ge(*dve.done("x", b))
                for qt in range(QT):
                    last = nc.tensor.transpose(ps[:, 6, qt * P:(qt + 1) * P], xb[:, qt, :], chip.ident[:, :])
                last.then_inc(*pe.end("xT"))
                eng.wait_ge(*dve.done("xw", b))
                for qt in range(QT):
                    nc.tensor.matmul(ps[:, 3 + qt, :], xw[:, qt * P:(qt + 1) * P], fp(cT), start=True, stop=True)
                    last = nc.tensor.matmul(ps[:, 7, qt:qt + 1], xT[:, qt * P:(qt + 1) * P], w["L2_xattn_w_c"], start=True, stop=True)
                last.then_inc(*pe.end("s"))
                eng.wait_ge(*dve.done("top", b))
                for qt in range(QT):
                    last = nc.tensor.transpose(ps[0:1, 2, qt * P:(qt + 1) * P], top[:, qt:qt + 1], chip.ident[:, :])
                last.then_inc(*pe.end("toprow"))
                eng.wait_ge(*dve.done("norm", b))
                for qt, bank in enumerate((5, 0)):
                    for kt in range(CT):
                        last = nc.tensor.transpose(ps[:, bank, kt * P:(kt + 1) * P], pr[:, qt, kt * P:(kt + 1) * P], chip.ident[:, :])
                last.then_inc(*pe.end("prT"))
                eng.wait_ge(*dve.done("prT", b))
                for kt in range(CT):
                    last = nc.tensor.matmul(ps[:, 1, 0:S], cb[:, kt, :], prT[:, kt, :, :].rearrange("p t q -> p (t q)"),
                                            start=(kt == 0), stop=(kt == CT - 1))
                last.then_inc(*pe.end("att"))
                eng.wait_ge(*dve.done("rown", b))
                for qt in range(QT):
                    last = nc.tensor.matmul(ps[:, 2, qt:qt + 1], row[:, qt * P:(qt + 1) * P], chip.ones[0:1, 0:1], start=True, stop=True)
                last.then_inc(*pe.end("col"))
                eng.wait_ge(*dve.done("col", b))
                for qt in range(QT):
                    last = nc.tensor.matmul(ps[:, 2, 4:5], xb[:, qt, :], col[:, qt:qt + 1], start=(qt == 0), stop=(qt == QT - 1))
                last.then_inc(*pe.end("q2c"))
                eng.wait_ge(*dve.done("xq", b))
                for qt in range(QT):
                    out = ps[:, 7, qt * P:(qt + 1) * P]
                    for c, part in enumerate((xT, att, xatt, xq)):
                        nc.tensor.matmul(out, part[:, qt * P:(qt + 1) * P], w["L2_xattn_W_l"][:, c, :], start=(c == 0), stop=False)
                    last = nc.tensor.matmul(out, chip.ones[0:1, 0:P], w["L2_xattn_b_l"], start=False, stop=True)
                last.then_inc(*pe.end("z"))


def l0_xattn(nc, chip):
    H, DH, NK = 8, 64, S2 + S
    KT = NK // P
    with ExitStack() as ctx:
        sb = lambda n, s, dt=F32: ctx.enter_context(nc.sbuf_tensor(f"l0x_{n}", s, dt))
        pe_s, dve_s, act_s, pool_s, ready = stage_sems(nc, ctx, "l0x")
        t = Tail(nc, ctx, "l0x")
        xb = sb("xb", [P, QT, D])
        z = sb("z", [P, KT, D])
        zs, zmv, zr = sb("zs", [P, KT, 6]), sb("zmv", [P, KT, 2]), sb("zr", [P, KT])
        kvT = sb("kvT", [P, NK])
        qT, kT = sb("qT", [P, H, S]), sb("kT", [P, H, NK])
        v = sb("v", [P, KT, H, P])
        nm, e = sb("nm", [P, QT, H, P]), sb("e", [P, 4, 512])
        rec, attT = sb("rec", [P, 2, S]), sb("attT", [P, H // 2, S])
        mask_rows, rows = sb("mask_rows", [2, B, NK]), sb("rows", [2, NK])
        mask_u8 = sb("mask_u8", [1, B, S2], U8)
        ys, ymv, yr = sb("ys", [P, QT, 6]), sb("ymv", [P, QT, 2]), sb("yr", [P, QT])
        yn = sb("yn", [P, QT, D])
        ps, w = chip.ps, chip.w
        wq, wkv = w["L0_xattn_w_q"], w["L0_xattn_w_kv"]
        masked = ctx.enter_context(nc.semaphore("l0x_mask_rows"))
        units = [(h, kp) for h in range(H) for kp in range(KT // 2)]
        names = []
        for u in range(len(units) + 1):
            names += ([f"sT{u}"] if u < len(units) else []) + ([f"pv{u - 1}"] if u else [])
        pe = Steps(pe_s, ["zT", "rows", "q"] + [f"k{h}" for h in range(H)] + [f"v{i}" for i in range(KT)]
                   + [f"s{h}" for h in range(H)] + ["nmT"] + names + ["y"])
        dve = Steps(dve_s, ["x", "zstats", "zvar", "zn", "kvT", "qrows", "q"] + [f"k{h}" for h in range(0, H, 2)]
                    + [f"v{i}" for i in range(0, KT, 2)] + [f"max{h}" for h in range(H)] + ["guarded"]
                    + [f"{s}{h}" for h in range(H) for s in ("rec", "att")]
                    + ["ystats", "yvar", "yn", "yg", "yb"] + TAIL_DVE)
        act = Steps(act_s, ["rows"] + [f"k{h}" for h in range(1, H, 2)] + [f"v{i}" for i in range(1, KT, 2)]
                    + [f"exp{u}" for u in range(len(units))])
        pool = Steps(pool_s, ["zeps", "zr", "yeps", "yr"] + TAIL_POOL)
        kd = lambda h: dve.done if h % 2 == 0 else act.done
        block = ctx.enter_context(nc.Block())

        @block.sync
        def _(sp):
            sp.dma_start(fp(mask_u8), chip.a["mask_BxS2_bf1"].rearrange("(o b) k -> o b k", o=1)).then_inc(ready, 16)
            sp.wait_ge(ready, 16)

        @block.gpsimd
        def _(eng):
            nc.gpsimd.memset(fp(nm), 0.0)
            nc.gpsimd.memset(v[:, :, 0:H:2, DH:P], 1.0)
            nc.gpsimd.memset(v[:, :, 1:H:2, 0:DH], 1.0).then_inc(masked, 1)
            with eng.Fori(0, B) as b:
                eng.wait_ge(*dve.done("zvar", b))
                nc.gpsimd.tensor_tensor(fp(zr), zmv[:, :, 1], chip.eps[:, 0:KT], ALU.add).then_inc(*pool.end("zeps"))
                eng.wait_ge(*pool.done("zeps", b))
                nc.gpsimd.tensor_tensor(fp(zr), fp(zr), chip.neghalf[:, 0:KT], ALU.pow).then_inc(*pool.end("zr"))
                eng.wait_ge(*dve.done("yvar", b))
                nc.gpsimd.tensor_tensor(fp(yr), ymv[:, :, 1], chip.eps[:, 0:QT], ALU.add).then_inc(*pool.end("yeps"))
                eng.wait_ge(*pool.done("yeps", b))
                nc.gpsimd.tensor_tensor(fp(yr), fp(yr), chip.neghalf[:, 0:QT], ALU.pow).then_inc(*pool.end("yr"))
                tail_pool(nc, eng, chip, t, dve, pool, b)

        @block.vector
        def _(eng):
            nc.vector.memset(fp(mask_rows), 1.0).then_inc(masked, 1)
            eng.wait_ge(masked, 2)
            nc.vector.memset(mask_rows[0:1, :, S2:NK], 0.0)
            eng.wait_ge(ready, 16)
            nc.vector.tensor_scalar(mask_rows[0:1, :, 0:S2], fp(mask_u8), 0, MASKED, ALU.is_equal, ALU.mult).then_inc(masked, 1)
            eng.wait_ge(masked, 3)
            with eng.Fori(0, B) as b:
                nc.vector.tensor_copy(fp(rows), mask_rows[:, b, :])
                nc.vector.tensor_copy(fp(xb), chip.x_tok[:, b, :, :])
                nc.vector.tensor_copy(z[:, CT:KT, :], chip.x_tok[:, b, :, :])
                nc.vector.tensor_copy(z[:, 0:CT, :], chip.ctx_tok[:, b, :, :]).then_inc(*dve.end("x"))
                eng.wait_ge(*dve.done("x", b))
                for i in range(KT):
                    last = nc.vector.bn_stats(zs[:, i, :], z[:, i, :])
                last.then_inc(*dve.end("zstats"))
                eng.wait_ge(*dve.done("zstats", b))
                nc.vector.memset(chip.scratch[:, 2:3], 0.0)
                for i in range(KT):
                    last = nc.vector.bn_aggr(zmv[:, i, :], zs[:, i, :])
                last.then_inc(*dve.end("zvar"))
                eng.wait_ge(*pool.done("zr", b))
                for i in range(KT):
                    last = nc.vector.tensor_scalar(z[:, i, :], z[:, i, :], zmv[:, i, 0:1], zr[:, i:i + 1], ALU.subtract, ALU.mult)
                last.then_inc(*dve.end("zn"))
                eng.wait_ge(*pe.done("zT", b))
                nc.vector.tensor_scalar(kvT[:, 0:S2], ps[:, 0, :], w["L0_xattn_g_x"], w["L0_xattn_b_x"], ALU.mult, ALU.add)
                nc.vector.tensor_scalar(kvT[:, S2:NK], ps[:, 1, 0:S], w["L0_xattn_g_l"], w["L0_xattn_b_l"], ALU.mult, ALU.add)\
                    .then_inc(*dve.end("kvT"))
                wide_const = w["c_qrows"][DH:P, :].unsqueeze(1).to_broadcast([P - DH, H, S])
                nc.vector.tensor_copy(qT[DH:P, :, :], wide_const).then_inc(*dve.end("qrows"))
                eng.wait_ge(*pe.done("q", b))
                nc.vector.tensor_scalar(qT[0:DH, :, :], ps[0:DH, 4:8, :].rearrange("p a (h q) -> p (a h) q", q=S),
                                        DH ** -0.5, None, ALU.mult).then_inc(*dve.end("q"))
                for h in range(0, H, 2):
                    eng.wait_ge(*pe.done(f"k{h}", b))
                    nc.vector.tensor_copy(kT[0:DH, h, :], ps[0:DH, 0:2, :].rearrange("p a k -> p (a k)")[:, 0:NK])\
                        .then_inc(*dve.end(f"k{h}"))
                for i in range(0, KT, 2):
                    eng.wait_ge(*pe.done(f"v{i}", b))
                    src = ps[:, 4 + i % 4, :].rearrange("p (h d) -> p h d", d=DH)
                    nc.vector.tensor_copy(v[:, i, 0:H:2, 0:DH], src[:, 0:H:2, :])
                    nc.vector.tensor_copy(v[:, i, 1:H:2, DH:P], src[:, 1:H:2, :]).then_inc(*dve.end(f"v{i}"))
                for h in range(H):
                    eng.wait_ge(*pe.done(f"s{h}", b))
                    bank = 4 * (h % 2)
                    nc.vector.tensor_reduce(nm[:, :, h, DH], ps[:, bank:bank + 4, :].rearrange("p (q a) k -> p q (a k)", a=2)[:, :, 0:NK],
                                            AX.X, ALU.max, negate=True).then_inc(*dve.end(f"max{h}"))
                eng.wait_ge(*pe.done("nmT", b))
                nc.vector.tensor_tensor(qT[DH:P, :, :], ps[DH:P, 0:4, :].rearrange("p a (h q) -> p (a h) q", q=S), wide_const, ALU.add)\
                    .then_inc(*dve.end("guarded"))
                for h in range(H):
                    eng.wait_ge(*pe.done(f"pv{(KT // 2) * h + KT // 2 - 1}", b))
                    dims, den = (slice(0, DH), slice(DH, P)) if h % 2 == 0 else (slice(DH, P), slice(0, DH))
                    nc.vector.reciprocal(rec[dims, h % 2, :], ps[den, 4 + h % 2, 0:S]).then_inc(*dve.end(f"rec{h}"))
                    eng.wait_ge(*dve.done(f"rec{h}", b))
                    nc.vector.tensor_tensor(attT[dims, h // 2, :], ps[dims, 4 + h % 2, 0:S], rec[dims, h % 2, :], ALU.mult)\
                        .then_inc(*dve.end(f"att{h}"))
                eng.wait_ge(*pe.done("y", b))
                for q in range(QT):
                    last = nc.vector.bn_stats(ys[:, q, :], ps[:, 6, q * P:(q + 1) * P])
                last.then_inc(*dve.end("ystats"))
                eng.wait_ge(*dve.done("ystats", b))
                nc.vector.memset(chip.scratch[:, 3:4], 0.0)
                for q in range(QT):
                    last = nc.vector.bn_aggr(ymv[:, q, :], ys[:, q, :])
                last.then_inc(*dve.end("yvar"))
                eng.wait_ge(*pool.done("yr", b))
                for q in range(QT):
                    last = nc.vector.tensor_scalar(yn[:, q, :], ps[:, 6, q * P:(q + 1) * P], ymv[:, q, 0:1], yr[:, q:q + 1],
                                                   ALU.subtract, ALU.mult)
                last.then_inc(*dve.end("yn"))
                eng.wait_ge(*dve.done("yn", b))
                nc.vector.tensor_tensor(fp(yn), fp(yn), w["L0_xattn_g_o"].unsqueeze(1).to_broadcast([P, QT, D]), ALU.mult)\
                    .then_inc(*dve.end("yg"))
                eng.wait_ge(*dve.done("yg", b))
                nc.vector.tensor_tensor(fp(yn), fp(yn), w["L0_xattn_b_o"].unsqueeze(1).to_broadcast([P, QT, D]), ALU.add)\
                    .then_inc(*dve.end("yb"))
                eng.wait_ge(*dve.done("yb", b))
                tail_dve(nc, eng, chip, t, dve, pool, b, fp(yn), fp(xb))

        @block.scalar
        def _(eng):
            with eng.Fori(0, B) as b:
                eng.wait_ge(*pe.done("rows", b))
                nc.scalar.activation(kT[DH:P, :, :], ps[DH:P, 2:4, :].rearrange("p a k -> p (a k)")[:, 0:NK].unsqueeze(1)
                                     .to_broadcast([P - DH, H, NK]), ACT.Copy).then_inc(*act.end("rows"))
                for h in range(1, H, 2):
                    eng.wait_ge(*pe.done(f"k{h}", b))
                    nc.scalar.activation(kT[0:DH, h, :], ps[0:DH, 2:4, :].rearrange("p a k -> p (a k)")[:, 0:NK], ACT.Copy)\
                        .then_inc(*act.end(f"k{h}"))
                for i in range(1, KT, 2):
                    eng.wait_ge(*pe.done(f"v{i}", b))
                    src = ps[:, 4 + i % 4, :].rearrange("p (h d) -> p h d", d=DH)
                    nc.scalar.activation(v[:, i, 0:H:2, 0:DH], src[:, 0:H:2, :], ACT.Copy)
                    nc.scalar.activation(v[:, i, 1:H:2, DH:P], src[:, 1:H:2, :], ACT.Copy).then_inc(*act.end(f"v{i}"))
                for u in range(len(units)):
                    eng.wait_ge(*pe.done(f"sT{u}", b))
                    if u >= 4:
                        eng.wait_ge(*pe.done(f"pv{u - 4}", b))
                    nc.scalar.activation(e[:, u % 4, :], ps[:, u % 4, :], ACT.Exp).then_inc(*act.end(f"exp{u}"))

        @block.tensor
        def _(eng):
            eng.wait_ge(masked, 3)
            with eng.Fori(0, B) as b:
                eng.wait_ge(*dve.done("zn", b))
                for i in range(KT):
                    last = nc.tensor.transpose(ps[:, i // 4, (i % 4) * P:(i % 4 + 1) * P], z[:, i, :], chip.ident[:, :])
                last.then_inc(*pe.end("zT"))
                nc.tensor.matmul(ps[:, 2, :], w["c_krows"], rows[:, 0:512], start=True, stop=True)
                nc.tensor.matmul(ps[:, 3, 0:S], w["c_krows"], rows[:, 512:NK], start=True, stop=True).then_inc(*pe.end("rows"))
                eng.wait_ge(*dve.done("kvT", b))
                for h in range(H):
                    last = nc.tensor.matmul(ps[0:DH, 4 + h // 2, (h % 2) * S:(h % 2 + 1) * S], wq[:, h * DH:(h + 1) * DH],
                                            kvT[:, S2:NK], start=True, stop=True)
                last.then_inc(*pe.end("q"))
                for h in range(H):
                    if h == 1:
                        eng.wait_ge(*act.done("rows", b))
                    if h >= 2:
                        eng.wait_ge(*kd(h)(f"k{h - 2}", b))
                    wk = wkv[:, h * DH:(h + 1) * DH]
                    bank = 2 * (h % 2)
                    nc.tensor.matmul(ps[0:DH, bank, :], wk, kvT[:, 0:512], start=True, stop=True)
                    nc.tensor.matmul(ps[0:DH, bank + 1, 0:S], wk, kvT[:, 512:NK], start=True, stop=True).then_inc(*pe.end(f"k{h}"))
                eng.wait_ge(*dve.done("q", b))
                for i in range(KT):
                    if i >= 4:
                        eng.wait_ge(*kd(i)(f"v{i - 4}", b))
                    nc.tensor.matmul(ps[:, 4 + i % 4, :], kvT[:, i * P:(i + 1) * P], wkv[:, 512:1024], start=True, stop=True)\
                        .then_inc(*pe.end(f"v{i}"))
                eng.wait_ge(*dve.done(f"v{KT - 2}", b))
                eng.wait_ge(*act.done(f"v{KT - 1}", b))
                for h in range(H):
                    if h >= 2:
                        eng.wait_ge(*dve.done(f"max{h - 2}", b))
                    for q in range(QT):
                        bank = 4 * (h % 2) + 2 * q
                        lhs = qT[:, h, q * P:(q + 1) * P]
                        nc.tensor.matmul(ps[:, bank, :], lhs, kT[:, h, 0:512], start=True, stop=True)
                        last = nc.tensor.matmul(ps[:, bank + 1, 0:S], lhs, kT[:, h, 512:NK], start=True, stop=True)
                    last.then_inc(*pe.end(f"s{h}"))
                eng.wait_ge(*dve.done(f"max{H - 1}", b))
                for h in range(H):
                    for q in range(QT):
                        at = (h % 2) * S + q * P
                        last = nc.tensor.transpose(ps[:, h // 2, at:at + P], nm[:, q, h, :], chip.ident[:, :])
                last.then_inc(*pe.end("nmT"))
                eng.wait_ge(*dve.done("guarded", b))
                for u in range(len(units) + 1):
                    if u < len(units):
                        h, kp = units[u]
                        if u >= 4:
                            eng.wait_ge(*act.done(f"exp{u - 4}", b))
                        for i in range(2):
                            kt = 2 * kp + i
                            last = nc.tensor.matmul(ps[:, u % 4, i * S:(i + 1) * S], kT[:, h, kt * P:(kt + 1) * P], qT[:, h, :],
                                                    start=True, stop=True)
                        last.then_inc(*pe.end(f"sT{u}"))
                    if u:
                        h, kp = units[u - 1]
                        eng.wait_ge(*act.done(f"exp{u - 1}", b))
                        if kp == 0 and h >= 2:
                            eng.wait_ge(*dve.done(f"att{h - 2}", b))
                        for i in range(2):
                            kt = 2 * kp + i
                            last = nc.tensor.matmul(ps[:, 4 + h % 2, 0:S], v[:, kt, h, :], e[:, (u - 1) % 4, i * S:(i + 1) * S],
                                                    start=(kt == 0), stop=(kt == KT - 1))
                        last.then_inc(*pe.end(f"pv{u - 1}"))
                eng.wait_ge(*dve.done(f"att{H - 1}", b))
                for q in range(QT):
                    for c in range(H // 2):
                        last = nc.tensor.matmul(ps[:, 6, q * P:(q + 1) * P], attT[:, c, q * P:(q + 1) * P],
                                                w["L0_xattn_w_out"][:, c, :], start=(c == 0), stop=(c == H // 2 - 1))
                last.then_inc(*pe.end("y"))


def l2_ffn(nc, chip):
    E, F, T = 8, 512, B * S
    C = F // P
    with ExitStack() as ctx:
        sb = lambda n, s, dt=F32: ctx.enter_context(nc.sbuf_tensor(f"l2f_{n}", s, dt))
        pe_s, dve_s, act_s, pool_s, ready = stage_sems(nc, ctx, "l2f")
        t, k = Tail(nc, ctx, "l2f"), Pick(nc, ctx, "l2f", E)
        xb, xTb, xT = sb("xb", [P, QT, D]), sb("xTb", [P, S]), sb("xT", [P, T])
        logits, one = sb("logits", [P, QT, E]), sb("one", [P, QT, E])
        oneT, shut, sel = sb("oneT", [E, T]), sb("shut", [P, T], BF16), sb("sel", [P, E, P], BF16)
        w1, w2 = sb("w1", [P, 2, F]), sb("w2", [P, 2, C, D])
        b1 = sb("b1", [P, 2 * C])
        hT, yT = sb("hT", [P, 4, 512]), sb("yT", [P, T])
        ps, w = chip.ps, chip.w
        nxt = [ctx.enter_context(nc.semaphore(f"l2f_{e}")) for e in ("gate_pe", "gate_dve", "main_pe", "main_dve", "main_act",
                                                                      "end_pe", "weights0", "weights1", "bias")]
        gpe, gdve = Steps(nxt[0], ["xT", "logits", "oneT"]), Steps(nxt[1], ["x", "xT", "xTall", "logits"] + pick_steps("top") + ["oneT", "shut"])
        units = [(e, c, half) for e in range(2) for c in range(C) for half in range(2)]
        n = len(units)
        names = []
        for u in range(n + 2):
            names += ([f"h{u}"] if u < n else []) + ([f"acc{u - 2}"] if u >= 2 else [])
        mpe = Steps(nxt[2], names)
        mdve, mact = Steps(nxt[3], ["b1"] + [f"r{u}" for u in range(1, n, 2)]), Steps(nxt[4], [f"r{u}" for u in range(0, n, 2)])
        relu = lambda u: (mact if u % 2 == 0 else mdve).done
        pe, dve, pool = Steps(pe_s, ["y"]), Steps(dve_s, ["x"] + TAIL_DVE), Steps(pool_s, TAIL_POOL)
        weights = nxt[6:8]
        block = ctx.enter_context(nc.Block())

        @block.sync
        def _(sp):
            for e in range(E):
                if e >= 2:
                    sp.wait_ge(*mpe.done(f"acc{n // 2 * (e % 2 + 1) - 1}", e // 2 - 1))
                sp.dma_start(w1[:, e % 2, :], chip.a["L2_ffn_W1"][e, :, :]).then_inc(weights[e % 2], 16)
                sp.dma_start(w2[:, e % 2, :, :], chip.a["L2_ffn_W2"][e, :, :].rearrange("(c p) d -> p c d", p=P))\
                    .then_inc(weights[e % 2], 16)

        @block.gpsimd
        def _(eng):
            nc.gpsimd.memset(fp(shut), 0.0)
            nc.gpsimd.memset(fp(sel), 0.0).then_inc(ready, 1)
            with eng.Fori(0, B) as b:
                tail_pool(nc, eng, chip, t, dve, pool, b)

        @block.vector
        def _(eng):
            eng.wait_ge(ready, 1)
            nc.vector.tensor_copy(sel[0:E, :, :], w["c_sel8"]).then_inc(ready, 1)
            with eng.Fori(0, B) as b:
                nc.vector.tensor_copy(fp(xb), chip.x_tok[:, b, :, :]).then_inc(*gdve.end("x"))
                eng.wait_ge(*gpe.done("xT", b))
                nc.vector.tensor_copy(fp(xTb), ps[:, 6, 0:S]).then_inc(*gdve.end("xT"))
                nc.vector.tensor_copy(xT[:, bass.ts(b, S)], ps[:, 6, 0:S]).then_inc(*gdve.end("xTall"))
                eng.wait_ge(*gpe.done("logits", b))
                nc.vector.tensor_copy(fp(logits), ps[:, 7, 0:QT * E].rearrange("p (t e) -> p t e", e=E)).then_inc(*gdve.end("logits"))
                eng.wait_ge(*gdve.done("logits", b))
                pick_first(nc, eng, chip, k, gdve, b, "top", fp(logits), fp(one))
                eng.wait_ge(*gpe.done("oneT", b))
                nc.vector.tensor_scalar(oneT[:, bass.ts(b, S)], ps[0:E, 5, 0:S], 1.0, None, ALU.mult).then_inc(*gdve.end("oneT"))
                nc.vector.tensor_scalar(shut[0:E, bass.ts(b, S)], ps[0:E, 5, 0:S], -1.0, -MASKED, ALU.add, ALU.mult)\
                    .then_inc(*gdve.end("shut"))
            with eng.Fori(0, E // 2) as i:
                nc.vector.tensor_copy(fp(b1), w["L2_ffn_b1"][:, bass.ts(i, 2 * C)]).then_inc(*mdve.end("b1"))
                eng.wait_ge(*mdve.done("b1", i))
                for u, (e, c, half) in enumerate(units):
                    if u % 2:
                        eng.wait_ge(*mpe.done(f"h{u}", i))
                        if u >= 4:
                            eng.wait_ge(*mpe.done(f"acc{u - 4}", i))
                        nc.vector.tensor_scalar(hT[:, u % 4, :], ps[:, u % 4, :], b1[:, e * C + c:e * C + c + 1], 0.0, ALU.add, ALU.max)\
                            .then_inc(*mdve.end(f"r{u}"))
                eng.wait_ge(*mdve.done(f"r{n - 1}", i))
                eng.wait_ge(*mact.done(f"r{n - 2}", i))
            eng.wait_ge(*mpe.passed(E // 2))
            eng.wait_ge(nxt[5], 1)
            nc.vector.tensor_copy(fp(yT), ps[:, 6:8, :].rearrange("p a t -> p (a t)")).then_inc(nxt[8], 1)
            for b in range(B):
                nc.vector.tensor_copy(fp(xb), chip.x_tok[:, b, :, :]).then_inc(*dve.end("x"))
                eng.wait_ge(*dve.done("x", b))
                eng.wait_ge(*pe.done("y", b))
                tail_dve(nc, eng, chip, t, dve, pool, b, ps[:, b % 2, 0:S].rearrange("p (t d) -> p t d", t=QT), fp(xb))

        @block.scalar
        def _(eng):
            with eng.Fori(0, E // 2) as i:
                eng.wait_ge(*mdve.done("b1", i))
                for u, (e, c, half) in enumerate(units):
                    if u % 2 == 0:
                        eng.wait_ge(*mpe.done(f"h{u}", i))
                        if u >= 4:
                            eng.wait_ge(*mpe.done(f"acc{u - 4}", i))
                        nc.scalar.activation(hT[:, u % 4, :], ps[:, u % 4, :], ACT.Relu, bias=b1[:, e * C + c:e * C + c + 1])\
                            .then_inc(*mact.end(f"r{u}"))

        @block.tensor
        def _(eng):
            with eng.Fori(0, B) as b:
                eng.wait_ge(*gdve.done("x", b))
                for qt in range(QT):
                    last = nc.tensor.transpose(ps[:, 6, qt * P:(qt + 1) * P], xb[:, qt, :], chip.ident[:, :])
                last.then_inc(*gpe.end("xT"))
                eng.wait_ge(*gdve.done("xT", b))
                for qt in range(QT):
                    out = ps[:, 7, qt * E:(qt + 1) * E]
                    nc.tensor.matmul(out, xTb[:, qt * P:(qt + 1) * P], w["L2_ffn_Wg"], start=True, stop=False)
                    last = nc.tensor.matmul(out, chip.ones[0:1, 0:P], w["L2_ffn_bg"], start=False, stop=True)
                last.then_inc(*gpe.end("logits"))
                eng.wait_ge(*gdve.done("toppick", b))
                for qt in range(QT):
                    last = nc.tensor.transpose(ps[0:E, 5, qt * P:(qt + 1) * P], one[:, qt, :], chip.ident[:, :])
                last.then_inc(*gpe.end("oneT"))
            eng.wait_ge(*gdve.passed(B))
            eng.wait_ge(ready, 2)
            for half in range(2):
                nc.tensor.matmul(ps[:, 6 + half, :], w["L2_ffn_b2"], oneT[:, half * 512:(half + 1) * 512], start=True, stop=False)
            with eng.Fori(0, E // 2) as i:
                for u in range(n + 2):
                    if u < n:
                        e, c, half = units[u]
                        if u % (n // 2) == 0:
                            eng.wait_ge(weights[e], i * 32 + 32)
                        if u >= 4:
                            eng.wait_ge(*relu(u)(f"r{u - 4}", i))
                        cols = slice(half * 512, (half + 1) * 512)
                        nc.tensor.matmul(ps[:, u % 4, :], w1[:, e, c * P:(c + 1) * P], xT[:, cols], start=True, stop=False)
                        nc.tensor.matmul(ps[:, u % 4, :], sel[:, i * 2 + e, :], shut[:, cols], start=False, stop=True)\
                            .then_inc(*mpe.end(f"h{u}"))
                    if u >= 2:
                        e, c, half = units[u - 2]
                        eng.wait_ge(*relu(u)(f"r{u - 2}", i))
                        nc.tensor.matmul(ps[:, 6 + half, :], w2[:, e, c, :], hT[:, (u - 2) % 4, :], start=False, stop=False)\
                            .then_inc(*mpe.end(f"acc{u - 2}"))
            for half in range(2):
                last = nc.tensor.matmul(ps[:, 6 + half, :], chip.zeros[0:1, 0:P], chip.ones[0:1, 0:512], start=False, stop=True)
            last.then_inc(nxt[5], 1)
            eng.wait_ge(nxt[8], 1)
            for b in range(B):
                if b >= 2:
                    eng.wait_ge(*dve.done("sum", b - 2))
                for qt in range(QT):
                    last = nc.tensor.transpose(ps[:, b % 2, qt * P:(qt + 1) * P], yT[:, b * S + qt * P:b * S + (qt + 1) * P], chip.ident[:, :])
                last.then_inc(*pe.end("y"))


def l3_ffn(nc, chip):
    E, F, T, TILES = 7, 512, B * S, B * QT
    C = F // P
    CAPACITY = -(-5 * T * 2 // (4 * E))
    with ExitStack() as ctx:
        sb = lambda n, s, dt=F32: ctx.enter_context(nc.sbuf_tensor(f"l3f_{n}", s, dt))
        pe_s, dve_s, act_s, pool_s, ready = stage_sems(nc, ctx, "l3f")
        t, k = Tail(nc, ctx, "l3f"), Pick(nc, ctx, "l3f", E)
        xb, z = sb("xb", [P, QT, D]), sb("z", [P, QT, D])
        zs, zmv, zr = sb("zs", [P, QT, 6]), sb("zmv", [P, QT, 2]), sb("zr", [P, QT])
        hb, hT = sb("hb", [P, S]), sb("hT", [P, T])
        lg, one, two = sb("lg", [P, QT, E]), sb("one", [P, QT, E]), sb("two", [P, QT, E])
        m1, ex, den = sb("m1", [P, QT]), sb("ex", [P, QT]), sb("den", [P, QT])
        picks, gates = sb("picks", [P, 2 * TILES, E]), sb("gates", [P, 2, TILES])
        offs, keep = sb("offs", [P, 2 * TILES, E]), sb("keep", [P, 2 * TILES, E])
        weight, weightT = sb("weight", [P, TILES, 8]), sb("weightT", [8, T])
        mine, hg = sb("mine", [8, 2, T]), sb("hg", [P, 2, T])
        w1, w3, w2 = sb("w1", [P, 2, F]), sb("w3", [P, 2, F]), sb("w2", [P, 2, C, D])
        act1, mid = sb("act1", [P, 2, 512]), sb("mid", [P, 2, 512])
        yT = sb("yT", [P, T])
        ps, w = chip.ps, chip.w
        sem = lambda n: ctx.enter_context(nc.semaphore(f"l3f_{n}"))
        weights = [sem("weights0"), sem("weights1")]
        closed, copied = sem("closed"), sem("copied")
        rpe = Steps(sem("route_pe"), ["zT", "logits"])
        rdve = Steps(sem("route_dve"), ["x", "stats", "var", "z", "hb", "hT", "logits"] + pick_steps("first") + ["m1", "rest"]
                     + pick_steps("second") + ["gap", "den", "gate1", "gate2", "picks"])
        ract, rpool = Steps(sem("route_act"), ["exp"]), Steps(sem("route_pool"), ["eps", "rstd"])
        cpe = Steps(sem("count_pe"), ["counts", "weightT"])
        cdve = Steps(sem("count_dve"), ["shared", "off0"] + [f"off{i}" for i in range(1, 2 * TILES)]
                     + ["pos", "keep", "kept", "weighed", "weight", "weightT"])
        units = [(e, c, half) for e in range(2) for c in range(C) for half in range(2)]
        n = len(units)
        names = []
        for u in range(n + 2):
            if u < n and u % (n // 2) == 0:
                names.append(f"spread{units[u][0]}")
            names += ([f"ab{u}"] if u < n else []) + ([f"acc{u - 2}"] if u >= 2 else [])
        mpe = Steps(sem("main_pe"), names)
        names = []
        for u in range(n):
            if u % (n // 2) == 0:
                names += [f"mine{units[u][0]}", f"hg{units[u][0]}"]
            names.append(f"mid{u}")
        mdve, mact = Steps(sem("main_dve"), names), Steps(sem("main_act"), [f"silu{u}" for u in range(n)])
        pe, dve, pool = Steps(pe_s, ["y"]), Steps(dve_s, ["x"] + TAIL_DVE), Steps(pool_s, TAIL_POOL)
        a = chip.a
        block = ctx.enter_context(nc.Block())

        @block.sync
        def _(sp):
            for e in range(E + 1):
                if e >= 2:
                    sp.wait_ge(*mpe.done(f"acc{n // 2 * (e % 2 + 1) - 1}", e // 2 - 1))
                one_of = lambda m: a[f"L3_ffn_{m}"][e, :, :] if e < E else a[f"L3_ffn_{m}s"]
                sp.dma_start(w1[:, e % 2, :], one_of("W1")).then_inc(weights[e % 2], 16)
                sp.dma_start(w3[:, e % 2, :], one_of("W3")).then_inc(weights[e % 2], 16)
                sp.dma_start(w2[:, e % 2, :, :], one_of("W2").rearrange("(c p) d -> p c d", p=P)).then_inc(weights[e % 2], 16)

        @block.gpsimd
        def _(eng):
            with eng.Fori(0, B) as b:
                eng.wait_ge(*rdve.done("var", b))
                nc.gpsimd.tensor_tensor(fp(zr), zmv[:, :, 1], chip.eps[:, 0:QT], ALU.add).then_inc(*rpool.end("eps"))
                eng.wait_ge(*rpool.done("eps", b))
                nc.gpsimd.tensor_tensor(fp(zr), fp(zr), chip.neghalf[:, 0:QT], ALU.pow).then_inc(*rpool.end("rstd"))
            with eng.Fori(0, B) as b:
                tail_pool(nc, eng, chip, t, dve, pool, b)

        @block.vector
        def _(eng):
            with eng.Fori(0, B) as b:
                nc.vector.tensor_copy(fp(xb), chip.x_tok[:, b, :, :]).then_inc(*rdve.end("x"))
                eng.wait_ge(*rdve.done("x", b))
                for q in range(QT):
                    last = nc.vector.bn_stats(zs[:, q, :], xb[:, q, :])
                last.then_inc(*rdve.end("stats"))
                eng.wait_ge(*rdve.done("stats", b))
                nc.vector.memset(chip.scratch[:, 4:5], 0.0)
                for q in range(QT):
                    last = nc.vector.bn_aggr(zmv[:, q, :], zs[:, q, :])
                last.then_inc(*rdve.end("var"))
                eng.wait_ge(*rpool.done("rstd", b))
                for q in range(QT):
                    last = nc.vector.tensor_scalar(z[:, q, :], xb[:, q, :], zmv[:, q, 0:1], zr[:, q:q + 1], ALU.subtract, ALU.mult)
                last.then_inc(*rdve.end("z"))
                eng.wait_ge(*rpe.done("zT", b))
                nc.vector.tensor_scalar(fp(hb), ps[:, 6, 0:S], w["L3_ffn_ln_g"], w["L3_ffn_ln_b"], ALU.mult, ALU.add)\
                    .then_inc(*rdve.end("hb"))
                nc.vector.tensor_scalar(hT[:, bass.ts(b, S)], ps[:, 6, 0:S], w["L3_ffn_ln_g"], w["L3_ffn_ln_b"], ALU.mult, ALU.add)\
                    .then_inc(*rdve.end("hT"))
                eng.wait_ge(*rpe.done("logits", b))
                nc.vector.tensor_copy(fp(lg), ps[:, 7, 0:QT * E].rearrange("p (t e) -> p t e", e=E)).then_inc(*rdve.end("logits"))
                eng.wait_ge(*rdve.done("logits", b))
                pick_first(nc, eng, chip, k, rdve, b, "first", fp(lg), fp(one))
                nc.vector.tensor_copy(fp(m1), fp(k.m)).then_inc(*rdve.end("m1"))
                eng.wait_ge(*rdve.done("m1", b))
                nc.vector.scalar_tensor_tensor(fp(two), fp(one), MASKED, fp(lg), ALU.mult, ALU.add).then_inc(*rdve.end("rest"))
                eng.wait_ge(*rdve.done("rest", b))
                pick_first(nc, eng, chip, k, rdve, b, "second", fp(two), fp(two))
                nc.vector.tensor_tensor(fp(ex), fp(k.m), fp(m1), ALU.subtract).then_inc(*rdve.end("gap"))
                eng.wait_ge(*ract.done("exp", b))
                nc.vector.tensor_scalar(fp(den), fp(ex), 1.0, None, ALU.add).then_inc(*rdve.end("den"))
                eng.wait_ge(*rdve.done("den", b))
                nc.vector.reciprocal(fp(den), fp(den)).then_inc(*rdve.end("gate1"))
                eng.wait_ge(*rdve.done("gate1", b))
                nc.vector.tensor_scalar(gates[:, 0, bass.ts(b, QT)], fp(den), 1.0, None, ALU.mult)
                nc.vector.tensor_tensor(gates[:, 1, bass.ts(b, QT)], fp(ex), fp(den), ALU.mult).then_inc(*rdve.end("gate2"))
                eng.wait_ge(*rdve.done("gate2", b))
                nc.vector.tensor_scalar(picks[:, bass.ts(b, QT), :], fp(one), 1.0, None, ALU.mult)
                nc.vector.tensor_scalar(picks[:, bass.ds(b * QT + TILES, QT), :], fp(two), 1.0, None, ALU.mult)\
                    .then_inc(*rdve.end("picks"))
            nc.vector.memset(weight[:, :, E:8], 1.0).then_inc(*cdve.end("shared"))
            nc.vector.memset(offs[:, 0, :], 0.0).then_inc(*cdve.end("off0"))
            eng.wait_ge(*cpe.done("counts"))
            totals = ps[:, 1, 0:2 * TILES * E].rearrange("p (i e) -> p i e", e=E)
            for i in range(1, 2 * TILES):
                eng.wait_ge(*cdve.done(f"off{i - 1}"))
                nc.vector.tensor_tensor(offs[:, i, :], offs[:, i - 1, :], totals[:, i - 1, :], ALU.add).then_inc(*cdve.end(f"off{i}"))
            eng.wait_ge(*cdve.done(f"off{2 * TILES - 1}"))
            nc.vector.tensor_tensor(fp(offs), ps[:, 0, 0:2 * TILES * E].rearrange("p (i e) -> p i e", e=E), fp(offs), ALU.add)\
                .then_inc(*cdve.end("pos"))
            eng.wait_ge(*cdve.done("pos"))
            nc.vector.tensor_scalar(fp(keep), fp(offs), float(CAPACITY), None, ALU.is_lt).then_inc(*cdve.end("keep"))
            eng.wait_ge(*cdve.done("keep"))
            nc.vector.tensor_tensor(fp(keep), fp(keep), fp(picks), ALU.mult).then_inc(*cdve.end("kept"))
            eng.wait_ge(*cdve.done("kept"))
            nc.vector.tensor_tensor(fp(keep), fp(keep), fp(gates).rearrange("p s t -> p (s t)").unsqueeze(2)
                                    .to_broadcast([P, 2 * TILES, E]), ALU.mult).then_inc(*cdve.end("weighed"))
            eng.wait_ge(*cdve.done("weighed"))
            nc.vector.tensor_tensor(weight[:, :, 0:E], keep[:, 0:TILES, :], keep[:, TILES:2 * TILES, :], ALU.add)\
                .then_inc(*cdve.end("weight"))
            eng.wait_ge(*cpe.done("weightT"))
            nc.vector.tensor_copy(fp(weightT), ps[0:8, 2:4, :].rearrange("p a t -> p (a t)")).then_inc(*cdve.end("weightT"))
            eng.wait_ge(*cdve.done("weightT"))
            with eng.Fori(0, (E + 1) // 2) as i:
                for u, (e, c, half) in enumerate(units):
                    if u % (n // 2) == 0:
                        nc.vector.tensor_scalar(mine[:, e, :], fp(weightT), chip.ident[0:8, bass.ds(i * 2 + e, 1)], None, ALU.mult)\
                            .then_inc(*mdve.end(f"mine{e}"))
                        eng.wait_ge(*mpe.done(f"spread{e}", i))
                        nc.vector.tensor_tensor(hg[:, e, :], ps[:, 4:6, :].rearrange("p a t -> p (a t)"), fp(hT), ALU.mult)\
                            .then_inc(*mdve.end(f"hg{e}"))
                    eng.wait_ge(*mact.done(f"silu{u}", i))
                    if u >= 2:
                        eng.wait_ge(*mpe.done(f"acc{u - 2}", i))
                    nc.vector.tensor_tensor(mid[:, u % 2, :], ps[:, 2 + u % 2, :], act1[:, u % 2, :], ALU.mult)\
                        .then_inc(*mdve.end(f"mid{u}"))
                eng.wait_ge(*mpe.done(f"acc{n - 1}", i))
            eng.wait_ge(closed, 1)
            nc.vector.tensor_copy(fp(yT), ps[:, 6:8, :].rearrange("p a t -> p (a t)")).then_inc(copied, 1)
            for b in range(B):
                nc.vector.tensor_copy(fp(xb), chip.x_tok[:, b, :, :]).then_inc(*dve.end("x"))
                eng.wait_ge(*dve.done("x", b))
                eng.wait_ge(*pe.done("y", b))
                tail_dve(nc, eng, chip, t, dve, pool, b, ps[:, b % 2, 0:S].rearrange("p (t d) -> p t d", t=QT), fp(xb))

        @block.scalar
        def _(eng):
            with eng.Fori(0, B) as b:
                eng.wait_ge(*rdve.done("gap", b))
                nc.scalar.activation(fp(ex), fp(ex), ACT.Exp).then_inc(*ract.end("exp"))
            with eng.Fori(0, (E + 1) // 2) as i:
                for u, (e, c, half) in enumerate(units):
                    eng.wait_ge(*mpe.done(f"ab{u}", i))
                    if u >= 2:
                        eng.wait_ge(*mdve.done(f"mid{u - 2}", i))
                    nc.scalar.activation(act1[:, u % 2, :], ps[:, u % 2, :], ACT.Silu).then_inc(*mact.end(f"silu{u}"))

        @block.tensor
        def _(eng):
            with eng.Fori(0, B) as b:
                eng.wait_ge(*rdve.done("z", b))
                for q in range(QT):
                    last = nc.tensor.transpose(ps[:, 6, q * P:(q + 1) * P], z[:, q, :], chip.ident[:, :])
                last.then_inc(*rpe.end("zT"))
                eng.wait_ge(*rdve.done("hb", b))
                for q in range(QT):
                    last = nc.tensor.matmul(ps[:, 7, q * E:(q + 1) * E], hb[:, q * P:(q + 1) * P], w["L3_ffn_Wr"], start=True, stop=True)
                last.then_inc(*rpe.end("logits"))
            eng.wait_ge(*rdve.passed(B))
            flat = fp(picks).rearrange("p i e -> p (i e)")
            nc.tensor.matmul(ps[:, 0, 0:2 * TILES * E], w["c_before"], flat, start=True, stop=True)
            nc.tensor.matmul(ps[:, 1, 0:2 * TILES * E], chip.ones[:, 0:P], flat, start=True, stop=True).then_inc(*cpe.end("counts"))
            eng.wait_ge(*cdve.done("weight"))
            for i in range(TILES):
                last = nc.tensor.transpose(ps[0:8, 2 + i // 4, (i % 4) * P:(i % 4 + 1) * P], weight[:, i, :], chip.ident[:, :])
            last.then_inc(*cpe.end("weightT"))
            for half in range(2):
                nc.tensor.matmul(ps[:, 6 + half, :], chip.zeros[0:1, 0:P], chip.ones[0:1, 0:512], start=True, stop=False)
            eng.wait_ge(*cdve.done("weightT"))
            with eng.Fori(0, (E + 1) // 2) as i:
                for u in range(n + 2):
                    if u < n:
                        e, c, half = units[u]
                        cols = slice(half * 512, (half + 1) * 512)
                        if u % (n // 2) == 0:
                            eng.wait_ge(*mdve.done(f"mine{e}", i))
                            for x in range(2):
                                last = nc.tensor.matmul(ps[:, 4 + x, :], chip.ones[0:8, 0:P], mine[:, e, x * 512:(x + 1) * 512],
                                                        start=True, stop=True)
                            last.then_inc(*mpe.end(f"spread{e}"))
                            eng.wait_ge(weights[e], i * 48 + 48)
                            eng.wait_ge(*mdve.done(f"hg{e}", i))
                        if u >= 2:
                            eng.wait_ge(*mdve.done(f"mid{u - 2}", i))
                        nc.tensor.matmul(ps[:, u % 2, :], w1[:, e, c * P:(c + 1) * P], hT[:, cols], start=True, stop=True)
                        nc.tensor.matmul(ps[:, 2 + u % 2, :], w3[:, e, c * P:(c + 1) * P], hg[:, e, cols], start=True, stop=True)\
                            .then_inc(*mpe.end(f"ab{u}"))
                    if u >= 2:
                        e, c, half = units[u - 2]
                        eng.wait_ge(*mdve.done(f"mid{u - 2}", i))
                        nc.tensor.matmul(ps[:, 6 + half, :], w2[:, e, c, :], mid[:, (u - 2) % 2, :], start=False, stop=False)\
                            .then_inc(*mpe.end(f"acc{u - 2}"))
            for half in range(2):
                last = nc.tensor.matmul(ps[:, 6 + half, :], chip.zeros[0:1, 0:P], chip.ones[0:1, 0:512], start=False, stop=True)
            last.then_inc(closed, 1)
            eng.wait_ge(copied, 1)
            for b in range(B):
                if b >= 2:
                    eng.wait_ge(*dve.done("sum", b - 2))
                for q in range(QT):
                    last = nc.tensor.transpose(ps[:, b % 2, q * P:(q + 1) * P], yT[:, b * S + q * P:b * S + (q + 1) * P], chip.ident[:, :])
                last.then_inc(*pe.end("y"))


FFN_LAYERS, FFN_HEADS, FFN_DH, FFN_IN = 6, 16, 64, 341
FFN_CHUNKS = [(0, P), (P, P), (2 * P, FFN_IN - 2 * P)]
EDGE = 32
SEEN = P + EDGE


def l1_ffn_constants():
    f = np.float32
    half = np.arange(0, FFN_DH, 2, dtype=f)
    inv_freq = (f(1) / np.power(f(10000), half / f(FFN_DH)).astype(f)).astype(f)
    t = np.arange(S, dtype=f)
    freqs = (t[:, None] * inv_freq[None, :]).astype(f)
    freqs = np.concatenate([freqs, freqs], -1)
    base = ((half + f(0.4 * FFN_DH)) / f(1.4 * FFN_DH)).astype(f)
    power = ((t - S // 2) / f(EDGE // 2)).astype(f)
    scale = np.power(base[None, :], power[:, None]).astype(f)
    scale = np.concatenate([scale, scale], -1)
    inv = (f(1) / scale).astype(f)
    sign = np.where(np.arange(FFN_DH) < FFN_DH // 2, f(-1), f(1))[None, :]
    cos, sin = np.cos(freqs).astype(f), (np.sin(freqs) * sign).astype(f)
    tab = np.stack([np.stack([cos * scale * f(8), sin * scale * f(8)]), np.stack([cos * inv, sin * inv])]).astype(f)
    return {"c_xpos": np.ascontiguousarray(tab.reshape(2, 2, QT, P, FFN_DH).transpose(3, 0, 1, 2, 4))}


class FfnState:
    pass


def l1_ffn(nc, chip):
    with ExitStack() as ctx:
        sb = lambda n, s, dt=F32: ctx.enter_context(nc.sbuf_tensor(f"l1f_{n}", s, dt))
        f = FfnState()
        f.xr = sb("xr", [P, B, S])
        f.cols = sb("cols", [P, 9, FFN_LAYERS])
        f.spread = sb("spread", [P, 2, FFN_LAYERS, FFN_DH])
        f.xpos = sb("xpos", [P, 2, 2, QT, FFN_DH])
        f.band = sb("band", [P, QT, SEEN], BF16)
        f.bandT = sb("bandT", [P, SEEN], BF16)
        f.pick = sb("pick", [P, FFN_HEADS // 2, P], BF16)
        f.mean_w = sb("mean_w", [P, P])
        l1_ffn_enter(nc, chip, f)
        l1_ffn_layers(nc, chip, f)
        l1_ffn_leave(nc, chip, f)


def l1_ffn_enter(nc, chip, f):
    with ExitStack() as ctx:
        sb = lambda n, s, dt=F32: ctx.enter_context(nc.sbuf_tensor(f"l1fe_{n}", s, dt))
        pe_s, dve_s, act_s, pool_s, loads = stage_sems(nc, ctx, "l1fe")
        raw = sb("raw", [FFN_LAYERS, 3, P])
        raw_b1 = sb("raw_b1", [FFN_LAYERS, 2 * FFN_IN])
        raw_band, raw_bandT, raw_pick = sb("raw_band", [P, QT, SEEN]), sb("raw_bandT", [P, SEEN]), sb("raw_pick", [P, FFN_HEADS // 2])
        pe, dve = Steps(pe_s, [f"x{b}" for b in range(B)] + ["cols"]), Steps(dve_s, ["clear"] + [f"x{b}" for b in range(B)])
        vectors = [(i, raw[:, i, :], P) for i in range(3)]
        vectors += [(3 + 3 * g + i, raw_b1[:, g * FFN_IN + at:g * FFN_IN + at + n], n)
                    for g in range(2) for i, (at, n) in enumerate(FFN_CHUNKS)]
        a, ps = chip.a, chip.ps
        block = ctx.enter_context(nc.Block())

        @block.sync
        def _(sp):
            n = 0
            for dst, src in [(raw[:, 0, :], a["L1_ffn_ln_g"]), (raw[:, 1, :], a["L1_ffn_ln_b"]), (raw[:, 2, :], a["L1_ffn_b2"]),
                             (fp(raw_b1), a["L1_ffn_b1"]), (fp(f.xpos), a["c_xpos"]),
                             (fp(raw_band), a["c_band"]), (fp(raw_bandT), a["c_bandT"]), (fp(raw_pick), a["c_pick"])]:
                sp.dma_start(dst, src).then_inc(loads, 16)
                n += 16
            for i, k in enumerate("qk"):
                sp.dma_start(f.spread[:, i, :, :].rearrange("p l d -> p (l d)"),
                             a[f"L1_ffn_{k}_scale"].rearrange("l d -> (l d)").partition_broadcast(P)).then_inc(loads, 16)
                n += 16
            sp.wait_ge(loads, n)

        @block.tensor
        def _(eng):
            for b in range(B):
                for q in range(QT):
                    last = nc.tensor.transpose(ps[:, b, q * P:(q + 1) * P], chip.x_tok[:, b, q, :], chip.ident[:, :])
                last.then_inc(*pe.end(f"x{b}"))
            eng.wait_ge(loads, 10 * 16)
            for i, src, n in vectors:
                last = nc.tensor.transpose(ps[0:n, 4, 8 * i:8 * i + FFN_LAYERS], src, chip.ident[0:FFN_LAYERS, 0:FFN_LAYERS])
            last.then_inc(*pe.end("cols"))

        @block.vector
        def _(eng):
            nc.vector.memset(fp(f.mean_w), 1.0 / D)
            nc.vector.memset(fp(f.cols), 0.0).then_inc(*dve.end("clear"))
            for b in range(B):
                eng.wait_ge(*pe.done(f"x{b}"))
                nc.vector.tensor_copy(f.xr[:, b, :], ps[:, b, 0:S]).then_inc(*dve.end(f"x{b}"))
            eng.wait_ge(*pe.done("cols"))
            eng.wait_ge(*dve.done("clear"))
            for i, src, n in vectors:
                nc.vector.tensor_copy(f.cols[0:n, i, :], ps[0:n, 4, 8 * i:8 * i + FFN_LAYERS])
            nc.vector.tensor_copy(fp(f.band), fp(raw_band))
            nc.vector.tensor_copy(fp(f.bandT), fp(raw_bandT))
            nc.vector.tensor_copy(fp(f.pick), fp(raw_pick).unsqueeze(2).to_broadcast([P, FFN_HEADS // 2, P]))


def l1_ffn_leave(nc, chip, f):
    with ExitStack() as ctx:
        sb = lambda n, s, dt=F32: ctx.enter_context(nc.sbuf_tensor(f"l1fl_{n}", s, dt))
        pe_s, dve_s, act_s, pool_s, loads = stage_sems(nc, ctx, "l1fl")
        t = Tail(nc, ctx, "l1fl")
        xb = sb("xb", [P, QT, D])
        pe, dve, pool = Steps(pe_s, ["y"]), Steps(dve_s, ["x"] + TAIL_DVE), Steps(pool_s, TAIL_POOL)
        block = ctx.enter_context(nc.Block())

        @block.gpsimd
        def _(eng):
            with eng.Fori(0, B) as b:
                tail_pool(nc, eng, chip, t, dve, pool, b)

        @block.vector
        def _(eng):
            for b in range(B):
                nc.vector.tensor_copy(fp(xb), chip.x_tok[:, b, :, :]).then_inc(*dve.end("x"))
                eng.wait_ge(*dve.done("x", b))
                eng.wait_ge(*pe.done("y", b))
                tail_dve(nc, eng, chip, t, dve, pool, b, chip.ps[:, b, 0:S].rearrange("p (t d) -> p t d", t=QT), fp(xb))

        @block.tensor
        def _(eng):
            for b in range(B):
                for q in range(QT):
                    last = nc.tensor.transpose(chip.ps[:, b, q * P:(q + 1) * P], f.xr[:, b, q * P:(q + 1) * P], chip.ident[:, :])
                last.then_inc(*pe.end("y"))


class FfnWork:
    pass


def l1_ffn_layers(nc, chip, f):
    H, DH, L = FFN_HEADS, FFN_DH, FFN_LAYERS
    PAIRS = H // 2
    with ExitStack() as ctx:
        sb = lambda n, s, dt=F32: ctx.enter_context(nc.sbuf_tensor(f"l1fb_{n}", s, dt))
        w = FfnWork()
        w.wqkv, w.wo = sb("wqkv", [P, 3 * H * DH]), sb("wo", [P, PAIRS, D])
        w.w1, w.w2 = sb("w1", [P, 2 * FFN_IN]), sb("w2", [P, 3, D])
        w.turn_tab, w.col = sb("turn_tab", [P, 2, 2, QT, DH]), sb("col", [P, 9])
        w.xs = sb("xs", [P, 2, S])
        w.sq, w.ssq, w.rinv = sb("sq", [P, 2, 512]), sb("ssq", [P, 2, 8, 8]), sb("rinv", [P, 2, 8, 8])
        w.r1, w.r2 = sb("r1", [P, 4, 512]), sb("r2", [P, 2, 512])
        w.qk = sb("qk", [P, 4, 512])
        w.qT, w.kT = sb("qT", [P, 2, H, S]), sb("kT", [P, 2, PAIRS, S])
        w.v = sb("v", [P, 2, QT, H, DH])
        w.nm, w.den = sb("nm", [P, 2, H, QT]), sb("den", [P, 2, H, QT])
        w.shift = sb("shift", [P, 2, 2, QT, H])
        w.low, w.mid = w.r2[0:H, 0, :], sb("mid", [H, 2 * S], BF16)
        w.parts = sb("parts", [P, 2, 2 * S], BF16)
        w.p0, w.p1 = sb("p0", [P, 2, 2, S]), sb("p1", [P, 2, 2, P])
        w.attT = sb("attT", [P, PAIRS, 2, S])
        w.x1, w.x1s = sb("x1", [P, 2, S]), sb("x1s", [P, 2, S])
        w.diff, w.dsq = sb("diff", [P, 2, S]), sb("dsq", [P, 4, P])
        w.rstd = sb("rstd", [P, 4])
        w.g = sb("g", [P, 3, 2, S])
        sem = lambda n: ctx.enter_context(nc.semaphore(f"l1fb_{n}"))
        a = chip.a
        w.ready, w.qkv_in, w.out_in = sem("ready"), sem("qkv_in"), sem("out_in")
        w.tables = Steps(sem("table_steps"), ["tables"])
        l1_ffn_steps(w, sem)
        block = ctx.enter_context(nc.Block())

        def slots(attention, unit):
            attention(0, 0, 0, None)
            with attention.eng.Fori(0, L - 1) as j:
                attention(j * 2 + 1, 1, j, unit(j * 2, 0, j))
                attention(j * 2 + 2, 0, j + 1, unit(j * 2 + 1, 1, j))
            attention(2 * L - 1, 1, L - 1, unit(2 * L - 2, 0, L - 1))
            for piece in unit(2 * L - 1, 1, L - 1):
                piece()

        @block.sync
        def _(sp):
            for l in range(L):
                if l:
                    sp.wait_ge(*w.a_pe.done("proj1_11", 2 * l - 1))
                sp.dma_start(fp(w.wqkv), a["L1_ffn_Wqkv"][l, :, :]).then_inc(w.qkv_in, 16)
                if l:
                    sp.wait_ge(*w.g_pe.done("y2", 2 * l - 1))
                for dst, src in [(fp(w.wo), a["L1_ffn_Wo"][l, :, :].rearrange("(c p) d -> p c d", p=P)),
                                 (fp(w.w1), a["L1_ffn_W1"][l, :, :]),
                                 (w.w2[:, 0:2, :], a["L1_ffn_W2"][l, 0:2 * P, :].rearrange("(c p) d -> p c d", p=P)),
                                 (w.w2[0:FFN_IN - 2 * P, 2, :], a["L1_ffn_W2"][l, 2 * P:FFN_IN, :])]:
                    sp.dma_start(dst, src).then_inc(w.out_in, 16)

        @block.gpsimd
        def _(eng):
            l1_ffn_pool(nc, eng, chip, f, w, slots)

        @block.vector
        def _(eng):
            l1_ffn_dve(nc, eng, chip, f, w, slots)

        @block.scalar
        def _(eng):
            l1_ffn_act(nc, eng, chip, f, w, slots)

        @block.tensor
        def _(eng):
            l1_ffn_pe(nc, eng, chip, f, w, slots)


PROJ = [(k, hh, q) for k in range(3) for hh in range(2) for q in range(QT)]
QK = 4 * QT
PAIRS_OF = lambda n: ((n // 2) % 2 * 4 + n % 2 * 2, (n // 2) % 2 * 4 + n % 2 * 2 + 2)
SCORES = [(i, c) for i in range(2) for c in range(FFN_HEADS // 2)]
SOFTEN_AFTER = {11: 0}


def l1_ffn_steps(w, sem):
    pe = []
    for i in range(2):
        for m in range(4):
            pe += [f"proj{i}_{u}" for u in ((0, 1, 2, 3) if m == 0 else (4, 5) if m == 1 else (6, 7) if m == 2 else (8, 9, 10, 11))]
            pe += [f"turn{i}_{2 * m}", f"turn{i}_{2 * m + 1}"]
    for u in range(len(SCORES)):
        pe += [f"s{u}"] + (["shift0"] if u == 11 else [])
    for u in range(len(SCORES)):
        pe += [f"t{u}_0", f"t{u}_1"] + (["shift1"] if u == 1 else []) + ([f"pv{u - 1}"] if u else [])
    w.a_pe = Steps(sem("a_pe_steps"), pe + [f"pv{len(SCORES) - 1}"])
    dve = ["xs"]
    unit = lambda i, u: [f"rot{i}_{u}", f"ssq{i}_{u}", f"add{i}_{u}", f"clamp{i}_{u}"]
    for i in range(2):
        for m in range(3):
            for u in ((0, 1, 2, 3) if m == 0 else (4, 5) if m == 1 else (6, 7)):
                dve += unit(i, u)
            if m < 2:
                dve += [f"q{i}_{2 * m}", f"q{i}_{2 * m + 1}"]
    for u in range(len(SCORES)):
        dve += [f"max{u}"] + ([f"shift0"] if u == 9 else []) + (["hi0", "low0", "mid0", "parts0"] if u == 11 else [])
    dve += ["shift1", "hi1", "low1", "mid1", "parts1"]
    w.a_dve = Steps(sem("a_dve_steps"), dve + [f"att{u}" for u in range(len(SCORES))])
    act = []
    for i in range(2):
        for m in range(4):
            act += [f"sq{i}_{u}" for u in ((0, 1, 2, 3) if m == 0 else (4, 5) if m == 1 else (6, 7) if m == 2 else ())]
            act += [f"v{i}_{u}" for u in (8, 9, 10, 11)] if m == 3 else []
            act += [f"turned{i}_{2 * m}", f"turned{i}_{2 * m + 1}"]
    for u in range(len(SCORES)):
        act += [f"exp{u}"] + (["ln0"] if u == 7 else [])
    act += ["ln1"]
    for u in range(len(SCORES)):
        act += [f"p{u}_0", f"p{u}_1"]
    w.a_act = Steps(sem("a_act_steps"), act)
    pool = []
    for i in range(2):
        for u in range(QK):
            pool += [f"rinv{i}_{u}", f"qk{i}_{u}"]
    w.a_pool = Steps(sem("a_pool_steps"), pool)
    w.g_pe = Steps(sem("g_pe_steps"), ["y1", "mean", "var", "rstd"] + [f"{k}{i}" for i in range(3) for k in ("gate", "value")] + ["y2"])
    w.g_dve = Steps(sem("g_dve_steps"), ["x1", "x1s", "diff", "dsq", "vareps", "diag", "xn0", "xn", "g0", "g1", "g2", "x2"])
    w.g_act = Steps(sem("g_act_steps"), ["gelu0", "gelu1", "gelu2"])
    w.g_pool = Steps(sem("g_pool_steps"), ["rstd"])


class Slot:

    def __init__(self, eng, body):
        self.eng, self.body = eng, body

    def __call__(self, t, half, layer, pieces):
        pieces = list(pieces or [])

        def between():
            if pieces:
                pieces.pop(0)()

        self.body(t, half, layer, between)
        assert not pieces


def l1_ffn_pool(nc, eng, chip, f, w, slots):
    a_dve, a_pool = w.a_dve, w.a_pool
    heads = lambda r: r.rearrange("p (h d) -> p h d", d=FFN_DH)
    nc.gpsimd.memset(fp(w.p0), 0.0)
    nc.gpsimd.memset(fp(w.shift), 0.0)
    nc.gpsimd.memset(fp(w.parts), 0.0).then_inc(w.ready, 1)

    def attention(t, half, layer, between):
        for i in range(2):
            for u in range(QK):
                eng.wait_ge(*a_dve.done(f"clamp{i}_{u}", t))
                nc.gpsimd.tensor_tensor(w.rinv[:, i, u, :], w.ssq[:, i, u, :], chip.neghalf[:, 0:8], ALU.pow)\
                    .then_inc(*a_pool.end(f"rinv{i}_{u}"))
                eng.wait_ge(*a_pool.done(f"rinv{i}_{u}", t))
                if u >= 4 or i:
                    eng.wait_ge(*w.a_pe.done(f"turn{i}_{2 * (u // 2) - 3}" if u >= 4 else f"turn{i - 1}_{2 * (u // 2) + 5}", t))
                nc.gpsimd.tensor_tensor(heads(w.qk[:, u % 4, :]), heads(w.r1[:, u % 4, :]),
                                        w.rinv[:, i, u, :].unsqueeze(2).to_broadcast([P, 8, FFN_DH]), ALU.mult).then_inc(*a_pool.end(f"qk{i}_{u}"))
                if i == 0 and u == 5:
                    between()

    def unit(t, half, layer):
        def rstd():
            eng.wait_ge(*w.g_dve.done("vareps", t))
            nc.gpsimd.tensor_tensor(fp(w.rstd), fp(w.rstd), chip.neghalf[:, 0:4], ALU.pow).then_inc(*w.g_pool.end("rstd"))

        return [rstd]

    slots(Slot(eng, attention), unit)


def l1_ffn_dve(nc, eng, chip, f, w, slots):
    DH, H = FFN_DH, FFN_HEADS
    ps, a_pe, a_dve, a_act, a_pool = chip.ps, w.a_pe, w.a_dve, w.a_act, w.a_pool
    g_pe, g_dve, g_act, g_pool = w.g_pe, w.g_dve, w.g_act, w.g_pool
    heads = lambda r: r.rearrange("p (h d) -> p h d", d=DH)
    nc.vector.memset(w.qT[0:DH, :, 1:H:2, :], 0.0)
    nc.vector.memset(w.qT[DH:P, :, 0:H:2, :], 0.0)
    nc.vector.memset(w.xs[DH:P, :, 0:1], 0.0)
    nc.vector.memset(w.x1s[DH:P, :, 0:1], 0.0).then_inc(w.ready, 1)
    eng.wait_ge(w.ready, 2)

    def tables(l):
        for k in range(2):
            for part, (lo, hi) in ((0, (0, DH)), (1, (DH // 2, DH)), (1, (0, DH // 2))):
                o = slice(0, DH) if part == 0 else slice(DH // 2 - lo, DH - lo)
                last = nc.vector.tensor_tensor(w.turn_tab[:, k, part, :, o], f.xpos[:, k, part, :, o],
                                               f.spread[:, k, l, lo:hi].unsqueeze(1).to_broadcast([P, QT, hi - lo]), ALU.mult)
        last.then_inc(*w.tables.end("tables"))

    def rotate(t, i, u):
        k, hh, q = PROJ[u]
        eng.wait_ge(*a_act.done(f"sq{i}_{u}", t))
        if i or u >= 4:
            eng.wait_ge(*a_pool.done(f"qk{i}_{u - 4}" if u >= 4 else f"qk{i - 1}_{u + 4}", t))
        src, r1, r2 = heads(ps[:, u % 3, :]), heads(w.r1[:, u % 4, :]), heads(w.r2[:, u % 2, :])
        tab = lambda part, o: w.turn_tab[:, k, part, q, o].unsqueeze(1).to_broadcast([P, 8, o.stop - o.start])
        nc.vector.tensor_tensor(r1, src, tab(0, slice(0, DH)), ALU.mult)
        for lo in (0, DH // 2):
            o, other = slice(lo, lo + DH // 2), slice(DH // 2 - lo, DH - lo)
            last = nc.vector.tensor_tensor(r2[:, :, o], src[:, :, other], tab(1, o), ALU.mult)
        last.then_inc(*a_dve.end(f"rot{i}_{u}"))
        nc.vector.tensor_reduce(w.ssq[:, i, u, :], heads(w.sq[:, u % 2, :]), AX.X, ALU.add).then_inc(*a_dve.end(f"ssq{i}_{u}"))
        eng.wait_ge(*a_dve.done(f"rot{i}_{u}", t))
        nc.vector.tensor_tensor(r1, r1, r2, ALU.add).then_inc(*a_dve.end(f"add{i}_{u}"))
        eng.wait_ge(*a_dve.done(f"ssq{i}_{u}", t))
        nc.vector.tensor_scalar(w.ssq[:, i, u, :], w.ssq[:, i, u, :], 1e-24, None, ALU.max).then_inc(*a_dve.end(f"clamp{i}_{u}"))

    def second_heads(t, i, n):
        lo, hi = PAIRS_OF(n)
        eng.wait_ge(*a_pe.done(f"turn{i}_{n}", t))
        nc.vector.tensor_copy(w.qT[DH:P, i, 2 * lo + 1:2 * hi:2, :], ps[DH:P, 4 + n % 2, :].rearrange("p (h t) -> p h t", t=S))\
            .then_inc(*a_dve.end(f"q{i}_{n}"))

    def shifts(t, i):
        eng.wait_ge(*a_act.done(f"ln{i}", t))
        for odd in range(2):
            last = nc.vector.tensor_tensor(w.shift[:, i, odd, :, odd:H:2], w.nm[:, i, odd:H:2, :].rearrange("p h q -> p q h"),
                                           w.den[:, i, odd:H:2, :].rearrange("p h q -> p q h"), ALU.subtract)
        last.then_inc(*a_dve.end(f"shift{i}"))

    def split(t, i):
        eng.wait_ge(*a_pe.done(f"shift{i}", t))
        src = ps[0:H, 7, :]
        nc.vector.tensor_copy(w.parts[0:H, i, :], src).then_inc(*a_dve.end(f"hi{i}"))
        eng.wait_ge(*a_dve.done(f"hi{i}", t))
        nc.vector.tensor_tensor(w.low, src, w.parts[0:H, i, :], ALU.subtract).then_inc(*a_dve.end(f"low{i}"))
        eng.wait_ge(*a_dve.done(f"low{i}", t))
        nc.vector.tensor_copy(w.parts[EDGE:EDGE + H, i, :], w.low)
        nc.vector.tensor_copy(fp(w.mid), w.low).then_inc(*a_dve.end(f"mid{i}"))
        eng.wait_ge(*a_dve.done(f"mid{i}", t))
        nc.vector.tensor_tensor(w.parts[2 * EDGE:2 * EDGE + H, i, :], w.low, fp(w.mid), ALU.subtract).then_inc(*a_dve.end(f"parts{i}"))

    def attention(t, half, layer, between):
        x = f.xr[:, 2 * half:2 * half + 2, :]
        nc.vector.tensor_copy(w.xs[0:DH, :, :], x[0:DH, :, :])
        nc.vector.tensor_copy(w.xs[DH:P, :, 1:S], x[DH:P, :, 0:S - 1]).then_inc(*a_dve.end("xs"))
        if half == 0:
            tables(layer)
        eng.wait_ge(*w.tables.done("tables", layer))
        for i in range(2):
            for u in (0, 1):
                rotate(t, i, u)
            between()
            for u in (2, 3):
                rotate(t, i, u)
            between()
            second_heads(t, i, 0)
            second_heads(t, i, 1)
            between()
            for u in (4, 5):
                rotate(t, i, u)
            between()
            second_heads(t, i, 2)
            second_heads(t, i, 3)
            between()
            for u in (6, 7):
                rotate(t, i, u)
            between()
        for u, (i, c) in enumerate(SCORES):
            eng.wait_ge(*a_pe.done(f"s{u}", t))
            bank = 2 * (u % 2)
            nc.vector.tensor_reduce(w.nm[:, i, 2 * c:2 * c + 2, 0], ps[:, bank:bank + 2, 0:P], AX.X, ALU.max, negate=True)
            nc.vector.tensor_reduce(w.nm[:, i, 2 * c:2 * c + 2, 1], ps[:, bank:bank + 2, P:P + SEEN], AX.X, ALU.max, negate=True)\
                .then_inc(*a_dve.end(f"max{u}"))
            if u == 9:
                shifts(t, 0)
            if u == 11:
                split(t, 0)
        shifts(t, 1)
        split(t, 1)
        for u, (i, c) in enumerate(SCORES):
            eng.wait_ge(*a_pe.done(f"pv{u}", t))
            nc.vector.tensor_copy(w.attT[:, c, i, :], ps[:, 7, 0:S]).then_inc(*a_dve.end(f"att{u}"))

    def unit(t, half, layer):
        x = f.xr[:, 2 * half:2 * half + 2, :]
        tokens = lambda bank: ps[:, bank, :].rearrange("p (b t) -> p b t", b=2)
        flat = lambda h: fp(h).rearrange("p b t -> p (b t)")

        def residual():
            if half == 0:
                nc.vector.tensor_copy(fp(w.col), f.cols[:, :, layer])
            eng.wait_ge(*g_pe.done("y1", t))
            nc.vector.tensor_tensor(fp(w.x1), tokens(3), x, ALU.add).then_inc(*g_dve.end("x1"))
            eng.wait_ge(*g_dve.done("x1", t))
            nc.vector.tensor_copy(w.x1s[0:DH, :, :], w.x1[0:DH, :, :])
            nc.vector.tensor_copy(w.x1s[DH:P, :, 1:S], w.x1[DH:P, :, 0:S - 1]).then_inc(*g_dve.end("x1s"))

        def centred():
            eng.wait_ge(*g_pe.done("mean", t))
            nc.vector.tensor_tensor(fp(w.diff), fp(w.x1s), tokens(6), ALU.subtract).then_inc(*g_dve.end("diff"))
            eng.wait_ge(*g_dve.done("diff", t))
            nc.vector.tensor_tensor(flat(w.dsq), flat(w.diff), flat(w.diff), ALU.mult).then_inc(*g_dve.end("dsq"))

        def variance():
            eng.wait_ge(*g_pe.done("var", t))
            nc.vector.tensor_scalar(fp(w.rstd), ps[:, 7, 0:4], EPS, None, ALU.add).then_inc(*g_dve.end("vareps"))

        def diagonals():
            eng.wait_ge(*g_pool.done("rstd", t))
            nc.vector.tensor_tensor(fp(w.dsq), chip.ident[:, :].unsqueeze(1).to_broadcast([P, 4, P]),
                                    w.rstd[:, :].unsqueeze(2).to_broadcast([P, 4, P]), ALU.mult).then_inc(*g_dve.end("diag"))

        def normed():
            eng.wait_ge(*g_pe.done("rstd", t))
            nc.vector.tensor_tensor(fp(w.diff), fp(w.diff), tokens(7), ALU.mult).then_inc(*g_dve.end("xn0"))
            eng.wait_ge(*g_dve.done("xn0", t))
            nc.vector.tensor_scalar(fp(w.diff), fp(w.diff), w.col[:, 0:1], w.col[:, 1:2], ALU.mult, ALU.add).then_inc(*g_dve.end("xn"))

        def gated(i):
            n, bank = FFN_CHUNKS[i][1], (6, 3, 7)[i]
            eng.wait_ge(*g_pe.done(f"value{i}", t))
            eng.wait_ge(*g_act.done(f"gelu{i}", t))
            nc.vector.scalar_tensor_tensor(w.g[0:n, i, :, :], tokens(bank)[0:n], w.col[0:n, 3 + i:4 + i], w.g[0:n, i, :, :], ALU.add, ALU.mult)\
                .then_inc(*g_dve.end(f"g{i}"))

        def out():
            eng.wait_ge(*g_pe.done("y2", t))
            nc.vector.scalar_tensor_tensor(x, tokens(3), w.col[:, 2:3], fp(w.x1), ALU.add, ALU.add).then_inc(*g_dve.end("x2"))
            eng.wait_ge(*g_dve.done("x2", t))

        nothing = lambda: None
        return [residual, nothing, centred, variance, diagonals, normed,
                lambda: gated(0), lambda: gated(1), nothing, lambda: gated(2), nothing, out]

    slots(Slot(eng, attention), unit)


def l1_ffn_act(nc, eng, chip, f, w, slots):
    DH = FFN_DH
    ps, a_pe, a_dve, a_act = chip.ps, w.a_pe, w.a_dve, w.a_act

    def attention(t, half, layer, between):
        def square(i, u):
            eng.wait_ge(*a_pe.done(f"proj{i}_{u}", t))
            if u >= 2 or i:
                eng.wait_ge(*a_dve.done(f"ssq{i}_{u - 2}" if u >= 2 else f"ssq{i - 1}_{u + 6}", t))
            nc.scalar.activation(w.sq[:, u % 2, :], ps[:, u % 3, :], ACT.Square).then_inc(*a_act.end(f"sq{i}_{u}"))

        def turned(i, n):
            lo, hi = PAIRS_OF(n)
            eng.wait_ge(*a_pe.done(f"turn{i}_{n}", t))
            src = ps[:, 4 + n % 2, :].rearrange("p (h t) -> p h t", t=S)
            if n < 4:
                last = nc.scalar.activation(w.qT[0:DH, i, 2 * lo:2 * hi:2, :], src[0:DH, :, :], ACT.Copy)
            else:
                last = nc.scalar.activation(w.kT[:, i, lo:hi, :], src, ACT.Copy)
            last.then_inc(*a_act.end(f"turned{i}_{n}"))

        for i in range(2):
            for u in range(4):
                square(i, u)
            if i:
                between()
            turned(i, 0)
            turned(i, 1)
            if i:
                between()
            for m in (1, 2):
                square(i, 2 * m + 2)
                square(i, 2 * m + 3)
                turned(i, 2 * m)
                turned(i, 2 * m + 1)
            for u in range(QK, len(PROJ)):
                k, hh, q = PROJ[u]
                eng.wait_ge(*a_pe.done(f"proj{i}_{u}", t))
                nc.scalar.activation(w.v[:, i, q, 8 * hh:8 * hh + 8, :], ps[:, u % 3, :].rearrange("p (h d) -> p h d", d=DH), ACT.Copy)\
                    .then_inc(*a_act.end(f"v{i}_{u}"))
            if i == 0:
                between()
            turned(i, 6)
            turned(i, 7)

        def log(i):
            eng.wait_ge(*a_act.done(f"exp{8 * i + 7}", t))
            nc.scalar.activation(w.den[:, i, :, :], w.den[:, i, :, :], ACT.Ln).then_inc(*a_act.end(f"ln{i}"))

        for u, (i, c) in enumerate(SCORES):
            eng.wait_ge(*a_dve.done(f"max{u}", t))
            for j in range(2):
                for q, (lo, hi) in enumerate(((0, P), (P, P + SEEN))):
                    h, s = 2 * c + j, ps[:, 2 * (u % 2) + j, lo:hi]
                    last = nc.scalar.activation(s, s, ACT.Exp, bias=w.nm[:, i, h, q:q + 1], accum_out=w.den[:, i, h, q:q + 1])
            last.then_inc(*a_act.end(f"exp{u}"))
            if u == 7:
                log(0)
        log(1)
        for u, (i, c) in enumerate(SCORES):
            for tile, (dst, n) in enumerate(((w.p0, SEEN), (w.p1, P))):
                eng.wait_ge(*a_pe.done(f"t{u}_{tile}", t))
                if u >= 2 and tile == 0:
                    eng.wait_ge(*a_pe.done(f"pv{u - 2}", t))
                nc.scalar.activation(dst[:, u % 2, :, 0:n], ps[:, 4 + (2 * u + tile) % 3, 0:2 * n].rearrange("p (j t) -> p j t", j=2), ACT.Exp)\
                    .then_inc(*a_act.end(f"p{u}_{tile}"))

    def unit(t, half, layer):
        def gelu(i):
            n, bank = FFN_CHUNKS[i][1], (3, 7, 6)[i]
            eng.wait_ge(*w.g_pe.done(f"gate{i}", t))
            nc.scalar.activation(w.g[0:n, i, :, :], ps[0:n, bank, :].rearrange("p (b t) -> p b t", b=2), ACT.Gelu, bias=w.col[0:n, 6 + i:7 + i])\
                .then_inc(*w.g_act.end(f"gelu{i}"))

        return [lambda: gelu(0), lambda: gelu(1), lambda: gelu(2)]

    slots(Slot(eng, attention), unit)


def l1_ffn_pe(nc, eng, chip, f, w, slots):
    H, DH = FFN_HEADS, FFN_DH
    PAIRS = H // 2
    ps, a_pe, a_dve, a_act, a_pool = chip.ps, w.a_pe, w.a_dve, w.a_act, w.a_pool
    g_pe, g_dve, g_act = w.g_pe, w.g_dve, w.g_act
    eng.wait_ge(w.ready, 2)

    def attention(t, half, layer, between):
        def project(i, units):
            for u in units:
                k, hh, q = PROJ[u]
                if u >= 3:
                    v = u - 3
                    eng.wait_ge(*a_act.done(f"sq{i}_{v}" if v < QK else f"v{i}_{v}", t))
                    if v < QK:
                        eng.wait_ge(*a_dve.done(f"rot{i}_{v}", t))
                elif i:
                    eng.wait_ge(*a_act.done(f"v{i - 1}_{u + 9}", t))
                at = k * H * DH + hh * 512
                nc.tensor.matmul(ps[:, u % 3, :], w.xs[:, i, q * P:(q + 1) * P], w.wqkv[:, at:at + 512], start=True, stop=True)\
                    .then_inc(*a_pe.end(f"proj{i}_{u}"))

        def turn(i, n):
            even = 2 * (n // 2)
            eng.wait_ge(*a_pool.done(f"qk{i}_{even + 1}", t))
            if n >= 2:
                eng.wait_ge(*a_act.done(f"turned{i}_{n - 2}", t))
                if n < 6:
                    eng.wait_ge(*a_dve.done(f"q{i}_{n - 2}", t))
            elif i:
                eng.wait_ge(*a_act.done(f"turned{i - 1}_{n + 6}", t))
            for c in range(2):
                for q in range(QT):
                    at = (n % 2 * 2 + c) * P
                    last = nc.tensor.transpose(ps[:, 4 + n % 2, c * S + q * P:c * S + (q + 1) * P],
                                               w.qk[:, (even + q) % 4, at:at + P], chip.ident[:, :])
            last.then_inc(*a_pe.end(f"turn{i}_{n}"))

        eng.wait_ge(w.qkv_in, layer * 16 + 16)
        eng.wait_ge(*a_dve.done("xs", t))
        project(0, (0, 1, 2))
        between()
        project(0, (3,))
        turn(0, 0)
        turn(0, 1)
        between()
        project(0, (4, 5))
        between()
        turn(0, 2)
        turn(0, 3)
        project(0, (6, 7))
        between()
        turn(0, 4)
        turn(0, 5)
        project(0, (8, 9, 10, 11))
        between()
        turn(0, 6)
        turn(0, 7)
        project(1, (0, 1))
        between()
        project(1, (2, 3))
        turn(1, 0)
        turn(1, 1)
        between()
        project(1, (4, 5))
        turn(1, 2)
        turn(1, 3)
        between()
        project(1, (6, 7))
        turn(1, 4)
        turn(1, 5)
        project(1, (8, 9, 10, 11))
        turn(1, 6)
        turn(1, 7)

        def shift(i):
            eng.wait_ge(*a_dve.done(f"shift{i}", t))
            for odd in range(2):
                for q in range(QT):
                    at = odd * S + q * P
                    last = nc.tensor.transpose(ps[0:H, 7, at:at + P], w.shift[:, i, odd, q, :], chip.ident[:, :])
            last.then_inc(*a_pe.end(f"shift{i}"))

        for u, (i, c) in enumerate(SCORES):
            if u == 0:
                eng.wait_ge(*a_dve.done("q1_3", t))
                eng.wait_ge(*a_act.done("turned1_7", t))
                after_unit(t)
            if u >= 2:
                eng.wait_ge(*a_act.done(f"exp{u - 2}", t))
            for j in range(2):
                h, bank = 2 * c + j, 2 * (u % 2) + j
                for q, (lo, hi, key) in enumerate(((0, P, 0), (P, P + SEEN, P - EDGE))):
                    nc.tensor.matmul(ps[:, bank, lo:hi], w.qT[:, i, h, q * P:(q + 1) * P], w.kT[:, i, c, key:key + hi - lo],
                                     start=True, stop=False)
                    last = nc.tensor.matmul(ps[:, bank, lo:hi], chip.ident_b[:, :], f.band[:, q, 0:hi - lo], start=False, stop=True)
            last.then_inc(*a_pe.end(f"s{u}"))
            if u == 11:
                shift(0)

        def values(u):
            i, c = SCORES[u]
            eng.wait_ge(*a_act.done(f"p{u}_1", t))
            eng.wait_ge(*a_dve.done(f"att{u - 1}" if u else "parts1", t))
            for j in range(2):
                h, out, place = 2 * c + j, ps[DH * j:DH * j + DH, 7, 0:S], (0, DH * j)
                nc.tensor.matmul(out[:, 0:P], w.v[:, i, 0, h, :], w.p0[:, u % 2, j, 0:P], start=True, stop=True, tile_position=place)
                nc.tensor.matmul(out[:, P:S], w.v[:, i, 0, h, :], w.p0[:, u % 2, j, P:S], start=True, stop=False, tile_position=place)
                last = nc.tensor.matmul(out[:, P:S], w.v[:, i, 1, h, :], w.p1[:, u % 2, j, :], start=False, stop=True, tile_position=place)
            last.then_inc(*a_pe.end(f"pv{u}"))

        for u, (i, c) in enumerate(SCORES):
            for tile, (at, n) in enumerate(((0, SEEN), (P, P))):
                k = 2 * u + tile
                if c == 0 and tile == 0:
                    eng.wait_ge(*a_dve.done(f"parts{i}", t))
                if k >= 3:
                    eng.wait_ge(*a_act.done(f"p{(k - 3) // 2}_{(k - 3) % 2}", t))
                out = ps[:, 4 + k % 3, 0:2 * n].rearrange("p (j t) -> p j t", j=2)
                nc.tensor.matmul(out, w.kT[:, i, c, tile * P:(tile + 1) * P], w.qT[:, i, 2 * c:2 * c + 2, at:at + n], start=True, stop=False)
                nc.tensor.matmul(out, chip.ident_b[:, :], f.bandT[:, 0:n].unsqueeze(1).to_broadcast([P, 2, n]), start=False, stop=False)
                nc.tensor.matmul(out, f.pick[:, c, :], w.parts[:, i, :].rearrange("p (j t) -> p j t", j=2)[:, :, at:at + n],
                                 start=False, stop=True).then_inc(*a_pe.end(f"t{u}_{tile}"))
            if u == 1:
                shift(1)
            if u:
                values(u - 1)
        values(len(SCORES) - 1)

    def after_unit(t):
        if not isinstance(t, int) or t:
            eng.wait_ge(*g_dve.done("x2", t - 1))

    def unit(t, half, layer):
        def attended():
            eng.wait_ge(w.out_in, layer * 64 + 64)
            eng.wait_ge(*a_dve.done(f"att{len(SCORES) - 1}", t))
            for c in range(PAIRS):
                last = nc.tensor.matmul(ps[:, 3, :], w.wo[:, c, :], w.attT[:, c, :, :].rearrange("p b t -> p (b t)"),
                                        start=(c == 0), stop=(c == PAIRS - 1))
            last.then_inc(*g_pe.end("y1"))

        flat = lambda h: fp(h).rearrange("p b t -> p (b t)")

        def mean():
            eng.wait_ge(*g_dve.done("x1s", t))
            nc.tensor.matmul(ps[:, 6, :], fp(f.mean_w), flat(w.x1s), start=True, stop=True).then_inc(*g_pe.end("mean"))

        def variance():
            eng.wait_ge(*g_dve.done("dsq", t))
            for k in range(4):
                last = nc.tensor.matmul(ps[:, 7, k:k + 1], w.dsq[:, k, :], f.mean_w[:, 0:1], start=True, stop=True)
            last.then_inc(*g_pe.end("var"))

        def spread():
            eng.wait_ge(*g_dve.done("diag", t))
            nc.tensor.matmul(ps[:, 7, :], chip.ones[:, 0:P], flat(w.dsq), start=True, stop=True).then_inc(*g_pe.end("rstd"))

        def chunk(i):
            at, n = FFN_CHUNKS[i]
            if i == 0:
                eng.wait_ge(*g_dve.done("xn", t))
            if i == 2:
                eng.wait_ge(*g_dve.done("g0", t))
            nc.tensor.matmul(ps[0:n, (3, 7, 6)[i], :], w.w1[:, FFN_IN + at:FFN_IN + at + n], flat(w.diff), start=True, stop=True)\
                .then_inc(*g_pe.end(f"gate{i}"))
            if i:
                eng.wait_ge(*g_act.done(f"gelu{i - 1}", t))
            nc.tensor.matmul(ps[0:n, (6, 3, 7)[i], :], w.w1[:, at:at + n], flat(w.diff), start=True, stop=True)\
                .then_inc(*g_pe.end(f"value{i}"))

        def out():
            for i, (at, n) in enumerate(FFN_CHUNKS):
                eng.wait_ge(*g_dve.done(f"g{i}", t))
            for i, (at, n) in enumerate(FFN_CHUNKS):
                last = nc.tensor.matmul(ps[:, 3, :], w.w2[0:n, i, :], w.g[0:n, i, :, :].rearrange("p b t -> p (b t)"), start=(i == 0), stop=(i == 2))
            last.then_inc(*g_pe.end("y2"))

        return [attended, mean, variance, spread, lambda: chunk(0), lambda: chunk(1), lambda: chunk(2), out]

    slots(Slot(eng, attention), unit)





def constants():
    f = np.float32
    pos, feat = np.arange(S, dtype=f)[:, None], np.arange(D)
    freq = (f(1) / np.power(f(0.0001), f(2) * np.arange(2, dtype=f) / f(4)).astype(f)).astype(f)
    ang = (pos * freq[(feat % 4) // 2][None, :]).astype(f)
    sign = np.where(feat % 2 == 0, f(-1), f(1))[None, :]
    turn = np.stack([np.cos(ang), np.sin(ang) * sign]).astype(f)
    rope = np.stack([turn * f(0.5), turn])
    rope = rope.reshape(2, 2, QT, P, D).transpose(3, 0, 1, 2, 4)
    heads = (np.arange(P)[:, None] // 8 == np.arange(16)[None, :]).astype(f)
    see = lambda i, j: np.where((j <= i) & (j >= i - 32), f(0), f(MASKED))
    p = np.arange(P)[:, None]
    w = np.arange(160)[None, :]
    band = np.stack([see(p, w), see(P + p, 96 + w)], axis=1)
    row = np.arange(P)[:, None]
    pick = ((row % 32 // 2 == np.arange(8)[None, :]) & (row < 96)).astype(f)
    sel8 = np.repeat(np.eye(8, dtype=f)[:, :, None], P, axis=2)
    before = (np.arange(P)[:, None] < np.arange(P)[None, :]).astype(f)
    qrows = np.zeros((P, S), f)
    qrows[65] = 1
    krows = np.zeros((2, P), f)
    krows[0, 65], krows[1, 64] = 1, 1
    return {"c_ident": np.eye(P, dtype=f), "c_rope": np.ascontiguousarray(rope), "c_heads": heads,
            "c_band": band.astype(f), "c_bandT": np.ascontiguousarray(see(w, p)).astype(f), "c_pick": pick, "c_sel8": sel8, "c_before": before, "c_qrows": qrows, "c_krows": krows, "c_rank": np.tile(np.arange(8, 0, -1, dtype=f), (P, 1)),
            **l1_ffn_constants()}


def program(nc, a, out, stages):
    with ExitStack() as ctx:
        sb = lambda n, s, dt=F32: ctx.enter_context(nc.sbuf_tensor(n, s, dt))
        chip = Chip()
        chip.a = a
        chip.ps = ctx.enter_context(nc.psum_tensor("ps", [P, 8, 512], F32))
        chip.x_tok = sb("x_tok", [P, B, QT, D])
        chip.ctx_tok = sb("ctx_tok", [P, B, CT, D])
        chip.ctxT = sb("ctxT", [P, B, S2])
        chip.ident, chip.ident_b = sb("ident", [P, P]), sb("ident_b", [P, P], BF16)
        chip.ones = sb("ones", [P, 512])
        chip.neghalf, chip.eps = sb("neghalf", [P, S]), sb("eps", [P, 8])
        chip.zeros = sb("zeros", [P, P])
        chip.scratch = sb("scratch", [P, 8])
        chip.w = {}
        chip.initial_loads = [
            (fp(chip.ident), a["c_ident"]),
            (fp(chip.x_tok), a["x"].rearrange("b (t p) d -> p b t d", p=P)),
            (fp(chip.ctx_tok), a["ctx_1024"].rearrange("b (t p) d -> p b t d", p=P)),
        ]
        chip.turned_weights = []
        early = ExitStack()
        shared = lambda name: not name.startswith(("L0_", "L1_", "c_rope", "c_qrows", "c_krows"))
        for of_all in (True, False):
            stack = ctx if of_all else early
            add = lambda name, shape, dt=F32: chip.w.__setitem__(name, fp(stack.enter_context(nc.sbuf_tensor(f"w_{name}", list(shape), dt))))
            load = lambda name, src: chip.initial_loads.append((chip.w[name], src))
            for name, shape in LOADS.items():
                if shared(name) == of_all:
                    add(name, shape)
                    load(name, a[name])
            for name, n in ROWS.items():
                if shared(name) == of_all:
                    add(name, [1, n])
                    flat = a[name] if len(a[name].shape) == 1 else a[name].rearrange("e n -> (e n)")
                    load(name, flat.rearrange("(o n) -> o n", o=1))
            for name in COLS:
                if shared(name) == of_all:
                    add(name, [P, 1])
                    load(name, a[name].rearrange("(d o) -> d o", o=1))
            for name, n in SPREAD.items():
                if shared(name) == of_all:
                    add(name, [P, n])
                    load(name, a[name].partition_broadcast(P))
            for name, n in TURNED.items():
                if shared(name) == of_all:
                    add(name, [P, n, D])
            for name in ("c_rope", "c_heads", "c_sel8", "c_before", "c_rank", "c_qrows", "c_krows"):
                if shared(name) == of_all:
                    add(name, a[name].shape)
                    load(name, a[name])
            if of_all:
                add("L2_ffn_b1", [P, 32])
                add("L2_attn_Wp", [P, 8])
                for head in range(16):
                    chip.initial_loads.append((chip.w["L2_attn_Wp"][8 * head:8 * head + 8, :], a["L2_attn_Wp"]))
            else:
                add("L0_xattn_w_out", [P, 4, D])
                load("L0_xattn_w_out", a["L0_xattn_w_out"].rearrange("(c p) d -> p c d", p=P))
                add("L0_attn_mask", [P, QT, S], I32)
                load("L0_attn_mask", a["L0_attn_mask"][0, 0, :, :].rearrange("(t p) k -> p t k", p=P))
        with ExitStack() as stay:
            for name, n in TURNED.items():
                raw = stay.enter_context(nc.sbuf_tensor(f"raw_{name}", [P, n, D], F32))
                src = {"L0_ffn_We": "e o i -> o e i"}.get(name)
                chip.initial_loads.append((fp(raw), a[name].rearrange(src) if src else
                                           a[name].rearrange("o (c i) -> o c i", i=D)))
                chip.turned_weights += [(chip.w[name][:, c, :], raw[:, c, :]) for c in range(n)]
            raw = stay.enter_context(nc.sbuf_tensor("raw_b1", [32, D], F32))
            chip.initial_loads.append((fp(raw), a["L2_ffn_b1"].rearrange("e (c p) -> (e c) p", p=P)))
            chip.turned_weights.append((chip.w["L2_ffn_b1"], fp(raw)))
            setup(nc, chip, a)
            context_stage(nc, chip)
        for stage in stages:
            if stage is l1_ffn:
                early.close()
            stage(nc, chip)
        early.close()
        stored = ctx.enter_context(nc.semaphore("stored"))
        with nc.Block() as block:
            @block.sync
            def _(sp):
                sp.dma_start(out.rearrange("b (t p) d -> p b t d", p=P), fp(chip.x_tok)).then_inc(stored, 16)
                sp.wait_ge(stored, 16)


def kernel(**inputs):
    import concourse.bacc as bacc
    from concourse.bass_utils import run_bass_kernel_spmd

    nc = bacc.Bacc("TRN2", target_bir_lowering=False, num_devices=1)
    arrays, aps = {}, {}
    for name, value in list(inputs.items()) + list(constants().items()):
        v = np.ascontiguousarray(value)
        if v.dtype == np.bool_:
            v = v.view(np.uint8)
        arrays[f"in_{name}"] = v
        shape = v.shape if v.shape else (1,)
        arrays[f"in_{name}"] = v.reshape(shape)
        aps[name] = nc.dram_tensor(f"in_{name}", shape, mybir.dt.from_np(v.dtype), kind="ExternalInput").ap()
    out = nc.dram_tensor("out_0", (B, S, D), F32, kind="ExternalOutput").ap()
    program(nc, aps, out, STAGES)
    r = run_bass_kernel_spmd(nc, [arrays], core_ids=[0])
    return r.results[0]["out_0"]
STAGES = [l0_attn, l0_xattn, l0_ffn, l1_attn, l1_xattn, l1_ffn, l2_attn, l2_xattn, l2_ffn, l3_attn, l3_xattn, l3_ffn]
```

```python
from contextlib import ExitStack

import numpy as np

import concourse.bass as bass
from concourse import mybir

F32 = mybir.dt.float32
BF16 = mybir.dt.bfloat16
I32 = mybir.dt.int32
U8 = mybir.dt.uint8
ALU = mybir.AluOpType
ACT = mybir.ActivationFunctionType
AX = mybir.AxisListType

P = 128
D = 128
B = 4
S = 256
QT = S // P
S2 = 512
CT = S2 // P
EPS = 1e-5
MASKED = -1e30
STRIP = 32


class Steps:

    def __init__(self, sem, names):
        self.sem, self.names, self.turn = sem, list(names), 0
        self.place = {n: k + 1 for k, n in enumerate(self.names)}
        assert len(self.place) == len(self.names)

    def end(self, name):
        assert self.names[self.turn % len(self.names)] == name, (self.names[self.turn % len(self.names)], name)
        self.turn += 1
        return self.sem, 1

    def done(self, name, turn=0):
        return self.sem, turn * len(self.names) + self.place[name]

    def passed(self, turn):
        return self.sem, turn * len(self.names)


class Chip:
    pass


def fp(handle):
    return handle[tuple(slice(None) for _ in handle.shape)]


def stage_sems(nc, ctx, label):
    return [ctx.enter_context(nc.semaphore(f"{label}_{e}_steps")) for e in ("pe", "dve", "act", "pool")] + \
        [ctx.enter_context(nc.semaphore(f"{label}_loads"))]



TAIL_DVE = ["sum", "stats", "var", "normed"]
TAIL_POOL = ["vareps", "rstd"]


class Tail:

    def __init__(self, nc, ctx, label):
        sb = lambda n, s: ctx.enter_context(nc.sbuf_tensor(f"{label}_{n}", s, F32))
        self.y = sb("y", [P, QT, D])
        self.stats = sb("stats", [P, QT, 6])
        self.mv = sb("mv", [P, QT, 2])
        self.rstd = sb("rstd", [P, QT])


def tail_dve(nc, eng, chip, t, dve, pool, turn, addend, residual, seq=None, of=""):
    seq = turn if seq is None else seq
    nc.vector.tensor_tensor(fp(t.y), addend, residual, ALU.add).then_inc(*dve.end("sum" + of))
    eng.wait_ge(*dve.done("sum" + of, turn))
    for q in range(QT):
        last = nc.vector.bn_stats(t.stats[:, q, :], t.y[:, q, :])
    last.then_inc(*dve.end("stats" + of))
    eng.wait_ge(*dve.done("stats" + of, turn))
    nc.vector.memset(chip.scratch[:, 0:1], 0.0)
    for q in range(QT):
        last = nc.vector.bn_aggr(t.mv[:, q, :], t.stats[:, q, :])
    last.then_inc(*dve.end("var" + of))
    eng.wait_ge(*pool.done("rstd" + of, turn))
    for q in range(QT):
        last = nc.vector.tensor_scalar(chip.x_tok[:, seq, q, :], t.y[:, q, :], t.mv[:, q, 0:1], t.rstd[:, q:q + 1],
                                       ALU.subtract, ALU.mult)
    last.then_inc(*dve.end("normed" + of))


def tail_pool(nc, eng, chip, t, dve, pool, turn, of=""):
    eng.wait_ge(*dve.done("var" + of, turn))
    nc.gpsimd.tensor_tensor(fp(t.rstd), t.mv[:, :, 1], chip.eps[:, 0:QT], ALU.add).then_inc(*pool.end("vareps" + of))
    eng.wait_ge(*pool.done("vareps" + of, turn))
    nc.gpsimd.tensor_tensor(fp(t.rstd), fp(t.rstd), chip.neghalf[:, 0:QT], ALU.pow).then_inc(*pool.end("rstd" + of))


def named(names, i):
    return [f"{n}{i}" for n in names]


PAIR = 2
STRIPS = 4


class Heads:

    def __init__(self, nc, ctx, label, NH, NK):
        sb = lambda n, s, dt=F32: ctx.enter_context(nc.sbuf_tensor(f"{label}_{n}", s, dt))
        self.NH, self.NK, self.KT, self.hd = NH, NK, NK // P, D // NH
        self.G, self.JH = D // STRIP, NH * STRIP // D
        G, JH = self.G, self.JH
        self.spread = sb("spread", [P, 2, JH, P], BF16)
        self.pick = sb("pick", [P, NH, P], BF16)
        self.qp, self.kp = sb("qp", [P, PAIR, G, S], BF16), sb("kp", [P, PAIR, G, NK], BF16)
        self.rem = sb("rem", [P, G * NK])
        self.qs, self.ks = sb("qs", [P, PAIR, G, JH, S], BF16), sb("ks", [P, PAIR, G, JH, NK], BF16)
        self.v = sb("v", [P, PAIR, NK // P, 16, STRIP])
        self.nm = sb("nm", [P, PAIR, QT, NH])
        self.low, self.mid = sb("max_rem", [STRIP, S]), sb("max_mid", [STRIP, S], BF16)
        self.parts = sb("parts", [P, PAIR, S], BF16)
        self.e = sb("e", [P, 2, 2, 512])
        self.raw_spread = fp(self.e).rearrange("p a j n -> p (a j n)")[:, 0:2 * JH * P]
        self.converted = ctx.enter_context(nc.semaphore(f"{label}_converted"))
        self.raw_pick = sb("raw_pick", [P, NH])
        self.oT = sb("oT", [P, PAIR, NH // 4, S])
        self.rec = sb("rec", [P, QT, 16])
        self.att = sb("att", [P, PAIR, QT, NH, 8])
        self.q_units = [(j, 2 * g, 2) for j in range(JH) for g in range(G // 2)]
        self.k_units = [(j, g, 2) for j in range(JH) for g in range(0, G, 2)] if NK == S else [(j, g, 1) for j in range(JH) for g in range(G)]
        self.s_units = [(h, q) for h in range(0, NH, 2) for q in ([None] if NK == S else range(QT))]
        self.t_units = [(h, k) for h in range(0, NH, 2) for k in range(NK // S)]
        self.rounds = NH // 16
        stacks = [("q", u) for u in range(len(self.q_units))] + [("k", u) for u in range(len(self.k_units))]
        self.merged, every = [], -(-len(stacks) // len(self.s_units))
        for u in range(len(self.s_units)):
            self.merged += [("s", u)] + stacks[every * u:every * (u + 1)]

    def stack_of(self, s, i, h):
        return s[:, i, h // self.JH, h % self.JH, :]

    def last_t(self, g):
        return max(u for u, (h, k) in enumerate(self.t_units) if h // 4 == g)

    def pe_steps(self, qk, late=()):
        q, k = [f"spreadq{u}_" for u in range(len(self.q_units))], [f"spreadk{u}_" for u in range(len(self.k_units))]
        names = named(qk, 0) + named(q, 0) + named(qk, 1) + named(k, 0)
        names += [f"scores{u}_0" if k == "s" else f"spread{k}{u}_1" for k, u in self.merged]
        for u in range(len(self.s_units)):
            names += [f"scores{u}_1"] + (["negmax0"] if u == 2 else [])
        n = len(self.t_units)
        for i in range(PAIR):
            for u in range(n + 1):
                names += ([f"scoresT{u}_{i}"] if u < n else []) + ([f"pv{u - 1}_{i}"] if u else []) + (["negmax1"] if (u, i) == (1, 0) else [])
                names += [f"heads{r}_0" for r in range(self.rounds) if (u, i) == (3 + r, 1)] + (named(late, 0) if (u, i) == (n - 1, 1) else [])
        return names + [f"heads{r}_1" for r in range(self.rounds)] + named(late, 1)

    def split_steps(self, i):
        return named(["qrem", "qmid", "qlo", "krem", "kmid", "klo"], i)

    def dve_steps(self, middle=(), late=()):
        names, split = [f"max{u}_0" for u in range(len(self.s_units))], ["maxhi", "maxrem", "maxmid", "maxlo"]
        for u in range(len(self.s_units)):
            names += [f"max{u}_1"] + (named(split, 0) if u == 2 else [])
        rounds = lambda i: [f"{k}{r}_{i}" for r in range(self.rounds) for k in ("rec", "att")]
        out = lambda i: [f"out{g}_{i}" for g in range(self.NH // 4)]
        names += named(split, 1) + out(0) + rounds(0) + named(middle, 0) + out(1)[:-1] + named(late, 0) + out(1)[-1:]
        return names + rounds(1) + named(middle, 1) + named(late, 1)

    def act_steps(self, before=lambda i: []):
        q, k = [f"stackq{u}_" for u in range(len(self.q_units))], [f"stackk{u}_" for u in range(len(self.k_units))]
        hi = lambda i: before(i) + [f"qhi{i}", f"khi{i}"]
        return hi(0) + named(q, 0) + hi(1) + named(k, 0) + named(q, 1) + named(k, 1) + \
            [f"exp{u}_{i}" for i in range(PAIR) for u in range(len(self.t_units))]


QK_BANKS = {"q": slice(4, 6), "k": slice(0, 4)}


def heads_source(chip, h, k):
    n = S if k == "q" else h.NK
    return chip.ps[:, QK_BANKS[k], :].rearrange("p a n -> p (a n)")[:, 0:h.G * n]


def heads_start(sp, h, a, loads):
    sp.dma_start(h.raw_spread, a[f"c_spread{h.hd}"].rearrange("p s j n -> p (s j n)")).then_inc(loads, 16)
    sp.dma_start(fp(h.raw_pick), a["c_pick_head"][:, 0:h.NH]).then_inc(loads, 16)
    sp.wait_ge(loads, 32)


def heads_convert(nc, eng, h, loads):
    eng.wait_ge(loads, 32)
    nc.scalar.activation(fp(h.spread).rearrange("p s j n -> p (s j n)"), h.raw_spread, ACT.Copy)
    nc.scalar.activation(fp(h.pick), fp(h.raw_pick).unsqueeze(2).to_broadcast([P, h.NH, P]), ACT.Copy).then_inc(h.converted, 1)
    eng.wait_ge(h.converted, 1)


def heads_spread(nc, eng, chip, h, pe, dve, act, turn, i, k, u):
    units, parts = (h.q_units, h.qp) if k == "q" else (h.k_units, h.kp)
    j, g, n = units[u]
    if u == 0:
        eng.wait_ge(*dve.done(f"{k}lo{i}", turn))
    if u >= 2:
        eng.wait_ge(*act.done(f"stack{k}{u - 2}_{i}", turn))
    elif (k, i) != ("q", 0):
        before = {("k", 0): ("q", 0), ("q", 1): ("k", 0), ("k", 1): ("q", 1)}[k, i]
        m = len(h.q_units if before[0] == "q" else h.k_units)
        eng.wait_ge(*act.done(f"stack{before[0]}{m - 2 + u}_{before[1]}", turn))
    nc.tensor.matmul(chip.ps[:, 6 + u % 2, :], h.spread[:, "qk".index(k), j, :], parts[:, i, g:g + n, :].rearrange("p g t -> p (g t)"),
                     start=True, stop=True).then_inc(*pe.end(f"spread{k}{u}_{i}"))


def heads_pe(nc, eng, chip, h, pe, dve, act, turn, queries_and_keys, vhead, late, mask=None):
    ps = chip.ps
    spread = lambda i, k, u: heads_spread(nc, eng, chip, h, pe, dve, act, turn, i, k, u)

    def scores(i, u):
        h0, q = h.s_units[u]
        if u == 0:
            eng.wait_ge(*act.done(f"stackk{len(h.k_units) - 1}_{i}", turn))
            if i == 0:
                eng.wait_ge(*dve.done(f"krem{PAIR - 1}", turn))
        if u >= 2 or i:
            w, wi = (u - 2, i) if u >= 2 else (len(h.s_units) - 2 + u, i - 1)
            eng.wait_ge(*dve.done(f"max{w}_{wi}", turn))
        for j in range(2):
            for qt in (range(QT) if q is None else [q]):
                col = 0 if q is not None else qt * S
                out = ps[:, 2 * (u % 2) + j, col:col + h.NK]
                last = nc.tensor.matmul(out, h.stack_of(h.qs, i, h0 + j)[:, qt * P:(qt + 1) * P], h.stack_of(h.ks, i, h0 + j),
                                        start=True, stop=mask is None)
                if mask is not None:
                    last = nc.tensor.matmul(out, chip.ident_b[:, :], mask[0][:, qt, :], start=False, stop=True)
        last.then_inc(*pe.end(f"scores{u}_{i}"))

    def negmax(i):
        eng.wait_ge(*dve.done(f"max{len(h.s_units) - 1}_{i}", turn))
        for qt in range(QT):
            last = nc.tensor.transpose(ps[0:h.NH, 4 + i, qt * P:(qt + 1) * P], h.nm[:, i, qt, :], chip.ident[:, :])
        last.then_inc(*pe.end(f"negmax{i}"))

    def heads(i, r):
        if r:
            eng.wait_ge(*dve.done(f"att{r - 1}_{i}", turn))
        elif i:
            eng.wait_ge(*dve.done("normed0", turn))
        eng.wait_ge(*dve.done(f"out{4 * r + 3}_{i}", turn))
        for g in range(4 * r, 4 * r + 4):
            for qt in range(QT):
                last = nc.tensor.transpose(ps[:, 4 + qt, (g % 4) * P:(g % 4 + 1) * P], h.oT[:, i, g, qt * P:(qt + 1) * P],
                                           chip.ident[:, :])
        last.then_inc(*pe.end(f"heads{r}_{i}"))

    queries_and_keys(turn, 0)
    for u in range(len(h.q_units)):
        spread(0, "q", u)
    queries_and_keys(turn, 1)
    for u in range(len(h.k_units)):
        spread(0, "k", u)
    for k, u in h.merged:
        scores(0, u) if k == "s" else spread(1, k, u)
    for u in range(len(h.s_units)):
        scores(1, u)
        if u == 2:
            negmax(0)
    n = len(h.t_units)
    for i in range(PAIR):
        for u in range(n + 1):
            if u < n:
                h0, kh = h.t_units[u]
                if u == 0:
                    eng.wait_ge(*dve.done(f"maxlo{i}", turn))
                    eng.wait_ge(*dve.done(f"max{len(h.s_units) - 1}_{PAIR - 1}", turn))
                if u >= 2 or i:
                    w, wi = (u - 2, i) if u >= 2 else (n - 2 + u, i - 1)
                    eng.wait_ge(*act.done(f"exp{w}_{wi}", turn))
                for j in range(2):
                    for kk in range(2):
                        kt = 2 * kh + kk
                        out = ps[:, 2 * (u % 2) + j, kk * S:(kk + 1) * S]
                        nc.tensor.matmul(out, h.stack_of(h.ks, i, h0 + j)[:, kt * P:(kt + 1) * P], h.stack_of(h.qs, i, h0 + j),
                                         start=True, stop=False)
                        last = nc.tensor.matmul(out, h.pick[:, h0 + j, :], h.parts[:, i, :], start=False, stop=mask is None)
                        if mask is not None:
                            last = nc.tensor.matmul(out, chip.ident_b[:, :], mask[1][:, kt, :], start=False, stop=True)
                last.then_inc(*pe.end(f"scoresT{u}_{i}"))
            if u:
                w = u - 1
                h0, kh = h.t_units[w]
                g = h0 // 4
                eng.wait_ge(*act.done(f"exp{w}_{i}", turn))
                if h0 % 4 == 0 and kh == 0:
                    if g >= 2 or i:
                        v, vi = (g - 2, i) if g >= 2 else (h.NH // 4 - 2 + g, i - 1)
                        eng.wait_ge(*dve.done(f"out{v}_{vi}", turn))
                for j in range(2):
                    s0 = STRIP * (h0 % 4 + j)
                    for kk in range(2):
                        kt = 2 * kh + kk
                        last = nc.tensor.matmul(ps[s0:s0 + STRIP, 6 + g % 2, 0:S], h.v[:, i, kt, vhead(h0 + j), :],
                                                h.e[:, w % 2, j, kk * S:(kk + 1) * S], start=(kt == 0),
                                                stop=(kt == h.KT - 1), tile_position=(0, s0))
                last.then_inc(*pe.end(f"pv{w}_{i}"))
                if (u, i) == (1, 0):
                    negmax(1)
                for r in range(h.rounds):
                    if (u, i) == (3 + r, 1):
                        heads(0, r)
                if (u, i) == (n - 1, 1):
                    late(turn, 0)
    for r in range(h.rounds):
        heads(1, r)
    late(turn, 1)


def heads_split(nc, eng, chip, h, dve, act, turn, i, k, scale):
    src, dst = heads_source(chip, h, k), (h.qp if k == "q" else h.kp)[:, i, :, :].rearrange("p g t -> p (g t)")
    rem = h.rem[:, 0:src.shape[1]]
    last = STRIPS - 1
    eng.wait_ge(*act.done(f"{k}hi{i}", turn))
    if (k, i) != ("q", 0):
        eng.wait_ge(*dve.done(f"qlo{i}" if k == "k" else f"klo{i - 1}", turn))
    nc.vector.scalar_tensor_tensor(rem[2 * STRIP:P, :], src[2 * STRIP:P, :], scale, dst[2 * STRIP:P, :], ALU.mult, ALU.subtract)\
        .then_inc(*dve.end(f"{k}rem{i}"))
    eng.wait_ge(*dve.done(f"{k}rem{i}", turn))
    nc.vector.tensor_scalar(dst[2 * STRIP:P, :], rem[2 * STRIP:P, :], 1.0, None, ALU.mult).then_inc(*dve.end(f"{k}mid{i}"))
    eng.wait_ge(*dve.done(f"{k}mid{i}", turn))
    nc.vector.tensor_tensor(dst[last * STRIP:P, :], rem[last * STRIP:P, :], dst[last * STRIP:P, :], ALU.subtract).then_inc(*dve.end(f"{k}lo{i}"))


def heads_dve(nc, eng, chip, h, pe, dve, turn, middle, late):
    ps = chip.ps

    def split(i):
        eng.wait_ge(*pe.done(f"negmax{i}", turn))
        src, part = ps[0:h.NH, 4 + i, 0:S], lambda n: h.parts[n * STRIP:n * STRIP + h.NH, i, :]
        low, mid = h.low[0:h.NH, :], h.mid[0:h.NH, :]
        nc.vector.tensor_copy(part(0), src).then_inc(*dve.end(f"maxhi{i}"))
        eng.wait_ge(*dve.done(f"maxhi{i}", turn))
        nc.vector.tensor_tensor(low, src, part(0), ALU.subtract).then_inc(*dve.end(f"maxrem{i}"))
        eng.wait_ge(*dve.done(f"maxrem{i}", turn))
        nc.vector.tensor_copy(part(1), low)
        nc.vector.tensor_copy(mid, low).then_inc(*dve.end(f"maxmid{i}"))
        eng.wait_ge(*dve.done(f"maxmid{i}", turn))
        nc.vector.tensor_tensor(part(2), low, mid, ALU.subtract).then_inc(*dve.end(f"maxlo{i}"))

    for i in range(PAIR):
        for u, (h0, q) in enumerate(h.s_units):
            eng.wait_ge(*pe.done(f"scores{u}_{i}", turn))
            bank = 2 * (u % 2)
            if q is None:
                src = ps[:, bank:bank + 2, :].rearrange("p j (t k) -> p j t k", t=QT)
                dst = h.nm[:, i, :, h0:h0 + 2].rearrange("p t j -> p j t")
            else:
                src, dst = ps[:, bank:bank + 2, :], h.nm[:, i, q, h0:h0 + 2]
            nc.vector.tensor_reduce(dst, src, AX.X, ALU.max, negate=True).then_inc(*dve.end(f"max{u}_{i}"))
            if (u, i) == (2, 1):
                split(0)
    split(1)

    def out(i, g):
        eng.wait_ge(*pe.done(f"pv{h.last_t(g)}_{i}", turn))
        nc.vector.tensor_copy(h.oT[:, i, g, :], ps[:, 6 + g % 2, 0:S]).then_inc(*dve.end(f"out{g}_{i}"))

    def rounds(i):
        for r in range(h.rounds):
            eng.wait_ge(*pe.done(f"heads{r}_{i}", turn))
            o = ps[:, 4:6, :].rearrange("p t (h c) -> p t h c", c=STRIP)
            nc.vector.reciprocal(h.rec[:, :, :], o[:, :, :, 8]).then_inc(*dve.end(f"rec{r}_{i}"))
            eng.wait_ge(*dve.done(f"rec{r}_{i}", turn))
            nc.vector.tensor_tensor(h.att[:, i, :, 16 * r:16 * r + 16, :], o[:, :, :, 0:8],
                                    h.rec[:, :, :].unsqueeze(3).to_broadcast([P, QT, 16, 8]), ALU.mult)                .then_inc(*dve.end(f"att{r}_{i}"))

    groups = h.NH // 4
    for g in range(groups):
        out(0, g)
    rounds(0)
    middle(turn, 0)
    for g in range(groups - 1):
        out(1, g)
    late(turn, 0)
    out(1, groups - 1)
    rounds(1)
    middle(turn, 1)
    late(turn, 1)


def heads_act(nc, eng, chip, h, pe, dve, act, turn, qk, scale, before=None):
    def first_parts(i):
        if before is not None:
            before(turn, i)
        for k, dst, by in (("q", h.qp, scale), ("k", h.kp, 1.0)):
            eng.wait_ge(*pe.done(qk[k] + str(i), turn))
            nc.scalar.activation(dst[:, i, :, :].rearrange("p g t -> p (g t)"), heads_source(chip, h, k), ACT.Copy, scale=by)\
                .then_inc(*act.end(f"{k}hi{i}"))

    def stacks(i, k):
        units, dst, n_t = (h.q_units, h.qs, S) if k == "q" else (h.k_units, h.ks, h.NK)
        for u, (j, g, n) in enumerate(units):
            eng.wait_ge(*pe.done(f"spread{k}{u}_{i}", turn))
            nc.scalar.activation(dst[:, i, g:g + n, j, :], chip.ps[:, 6 + u % 2, :].rearrange("p (g t) -> p g t", t=n_t), ACT.Copy)\
                .then_inc(*act.end(f"stack{k}{u}_{i}"))

    first_parts(0)
    stacks(0, "q")
    first_parts(1)
    stacks(0, "k")
    stacks(1, "q")
    stacks(1, "k")
    for i in range(PAIR):
        for u in range(len(h.t_units)):
            eng.wait_ge(*pe.done(f"scoresT{u}_{i}", turn))
            if u >= 2 or i:
                w, wi = (u - 2, i) if u >= 2 else (len(h.t_units) - 2 + u, i - 1)
                eng.wait_ge(*pe.done(f"pv{w}_{wi}", turn))
            bank = 2 * (u % 2)
            nc.scalar.activation(h.e[:, u % 2, :, :], chip.ps[:, bank:bank + 2, :], ACT.Exp).then_inc(*act.end(f"exp{u}_{i}"))


def clear_heads(nc, eng, h, cleared):
    nc.gpsimd.memset(fp(h.parts), 0.0)
    nc.gpsimd.memset(h.v[:, :, :, :, 9:STRIP], 0.0)
    nc.gpsimd.memset(h.v[:, :, :, :, 8:9], 1.0).then_inc(cleared, 1)


def four_times(src):
    return src.rearrange("k (g c) -> k g c", c=STRIP).unsqueeze(2).to_broadcast([src.shape[0], D // STRIP, STRIPS, STRIP])




LOADS = {
    "L0_attn_w_kvc": (P, D), "L0_attn_w_kvu": (P, 2 * D), "L0_attn_w_qc": (P, 32), "L0_attn_w_qu": (32, D),
    "L0_attn_w_o": (P, D), "L0_xattn_w_q": (P, 512), "L0_xattn_w_kv": (P, 1024), "L0_ffn_Wg": (P, 8),
    "L1_attn_Wq": (P, D), "L1_attn_Wk": (P, D), "L1_attn_Wv": (P, D), "L1_attn_Wo": (P, D),
    "L2_attn_Wq": (P, D), "L2_attn_Wk": (P, D), "L2_attn_Wv": (P, D),
    "L2_ffn_Wg": (P, 8), "L2_ffn_b2": (8, D),
    "L3_attn_Wq": (P, D), "L3_attn_Wk": (P, D), "L3_attn_Wv": (P, D), "L3_attn_Wp": (P, D),
    "L3_ffn_Wr": (P, 7),
}
ROWS = {
    "L0_attn_b_kvc": D, "L0_attn_b_kvu": 2 * D, "L0_attn_b_qc": 32, "L0_attn_b_qu": D, "L0_attn_b_o": D,
    "L0_ffn_bg": 8, "L0_ffn_be": 8 * D, "L1_xattn_Wv_b": D, "L2_attn_bv": D, "L2_xattn_b_l": D, "L2_ffn_bg": 8,
    "L3_attn_bq": D, "L3_attn_bk": D, "L3_attn_bv": D, "L3_attn_bp": D, "L3_xattn_bo": D,
}
COLS = [
    "L0_xattn_g_x", "L0_xattn_b_x", "L0_xattn_g_l", "L0_xattn_b_l", "L1_xattn_Wq_b", "L1_xattn_Wk_b",
    "L2_attn_bq", "L2_attn_bk", "L2_xattn_w_cq", "L2_xattn_w_c", "L2_xattn_w_q", "L3_ffn_ln_g", "L3_ffn_ln_b",
]
SPREAD = {
    "L0_xattn_g_o": D, "L0_xattn_b_o": D, "L1_attn_lambda_q1": 4, "L1_attn_lambda_k1": 4, "L1_attn_lambda_q2": 4,
    "L1_attn_lambda_k2": 4, "L1_attn_subln_g": 8, "L2_xattn_b_cq": 1, "L2_xattn_b_c": 1, "L2_xattn_b_q": 1,
}
TURNED = {
    "L0_ffn_We": 8, "L1_xattn_Wq_w": 1, "L1_xattn_Wk_w": 1, "L1_xattn_Wv_w": 1, "L2_xattn_W_l": 4,
    "L3_xattn_Wv": 1, "L3_xattn_Wk": 1, "L3_xattn_Wq": 1, "L3_xattn_Wo": 1,
}


def setup(nc, chip, a):
    with ExitStack() as ctx:
        pe_s, dve_s, act_s, pool_s, loads = stage_sems(nc, ctx, "setup")
        fetched = []

        block = ctx.enter_context(nc.Block())

        @block.sync
        def _(sp):
            n = 0
            for dst, src in chip.initial_loads:
                sp.dma_start(dst, src).then_inc(loads, 16)
                n += 16
            sp.wait_ge(loads, n)

        @block.gpsimd
        def _(pool):
            nc.gpsimd.memset(fp(chip.neghalf), -0.5)
            nc.gpsimd.memset(fp(chip.eps), EPS)
            nc.gpsimd.memset(fp(chip.zeros), 0.0)
            nc.gpsimd.memset(fp(chip.ones), 1.0)


def context_stage(nc, chip):
    with ExitStack() as ctx:
        pe_s, dve_s, act_s, pool_s, loads = stage_sems(nc, ctx, "context")
        jobs = [(chip.ctxT[:, b, c * P:(c + 1) * P], chip.ctx_tok[:, b, c, :]) for b in range(B) for c in range(CT)]
        jobs += chip.turned_weights
        full = 4
        units = [jobs[i:i + full] for i in range(0, len(jobs), full)]
        pe = Steps(pe_s, [f"turn{u}" for u in range(len(units))])
        dve = Steps(dve_s, [f"copy{u}" for u in range(len(units))])
        block = ctx.enter_context(nc.Block())

        @block.tensor
        def _(eng):
            for u, unit in enumerate(units):
                if u >= 8:
                    eng.wait_ge(*dve.done(f"copy{u - 8}"))
                for i, (dst, src) in enumerate(unit):
                    n = src.shape[0]
                    last = nc.tensor.transpose(chip.ps[:, u % 8, i * P:i * P + n], src, chip.ident[0:n, 0:n])
                last.then_inc(*pe.end(f"turn{u}"))

        @block.vector
        def _(eng):
            nc.vector.tensor_copy(fp(chip.ident_b), fp(chip.ident))
            for u, unit in enumerate(units):
                eng.wait_ge(*pe.done(f"turn{u}"))
                for i, (dst, src) in enumerate(unit):
                    last = nc.vector.tensor_copy(dst, chip.ps[:, u % 8, i * P:i * P + src.shape[0]])
                last.then_inc(*dve.end(f"copy{u}"))


def l0_attn(nc, chip):
    with ExitStack() as ctx:
        sb = lambda n, s, dt=F32: ctx.enter_context(nc.sbuf_tensor(f"l0a_{n}", s, dt))
        pe_s, dve_s, act_s, pool_s, ready = stage_sems(nc, ctx, "l0a")
        h = Heads(nc, ctx, "l0a", 16, S)
        t = Tail(nc, ctx, "l0a")
        G = h.G
        wq, wk = sb("wq", [32, G, STRIPS, STRIP]), sb("wk", [P, G, STRIPS, STRIP])
        bq, bk = sb("bq", [1, G, STRIPS, STRIP]), sb("bk", [1, G, STRIPS, STRIP])
        mq, mf, mk = sb("mq", [P, QT, S], BF16), sb("mf", [P, QT, S]), sb("mk", [P, QT, S], BF16)
        xb, xT = sb("xb", [P, PAIR, QT, D]), sb("xT", [P, PAIR, S])
        latent, low, attT = sb("latent", [P, PAIR, S]), sb("low", [32, PAIR, S]), sb("attT", [P, PAIR, S])
        ps, w = chip.ps, chip.w
        pre = Steps(ctx.enter_context(nc.semaphore("l0a_prepared")), ["mask", "maskb", "maskT", "weights"])
        turned, loads = ctx.enter_context(nc.semaphore("l0a_mask_turned")), ctx.enter_context(nc.semaphore("l0a_matrices"))
        first = ["xT", "latent", "low", "v"]
        pe = Steps(pe_s, named(first, 0) + named(first, 1) + h.pe_steps(["q", "k"], ["attT", "y"]))
        first = ["x"] + first
        last = ["attT"] + TAIL_DVE
        dve = Steps(dve_s, named(first, 0) + named(first, 1) + h.split_steps(0) + h.split_steps(1) + h.dve_steps(late=last))
        act = Steps(act_s, h.act_steps())
        pool = Steps(pool_s, named(TAIL_POOL, 0) + named(TAIL_POOL, 1))
        scale = float(1 / np.sqrt(np.float32(h.hd)))
        block = ctx.enter_context(nc.Block())

        @block.sync
        def _(sp):
            heads_start(sp, h, chip.a, loads)
            for dst, src in chip.later_loads:
                sp.dma_start(dst, src).then_inc(chip.later_loaded, 16)
            sp.wait_ge(chip.later_loaded, 16 * len(chip.later_loads))

        @block.gpsimd
        def _(eng):
            clear_heads(nc, eng, h, ready)
            with eng.Fori(0, B // PAIR) as n:
                for i in range(PAIR):
                    tail_pool(nc, eng, chip, t, dve, pool, n, of=str(i))

        @block.vector
        def _(eng):
            nc.vector.tensor_scalar(fp(mf), w["L0_attn_mask"], 0, MASKED, ALU.is_equal, ALU.mult).then_inc(*pre.end("mask"))
            eng.wait_ge(*pre.done("mask"))
            nc.vector.tensor_copy(fp(mq), fp(mf)).then_inc(*pre.end("maskb"))
            eng.wait_ge(turned, 1)
            nc.vector.tensor_copy(fp(mk), ps[:, 0:2, 0:S]).then_inc(*pre.end("maskT"))
            for dst, src in ((wq, w["L0_attn_w_qu"]), (wk, w["L0_attn_w_kvu"][:, 0:D]), (bq, w["L0_attn_b_qu"]),
                             (bk, w["L0_attn_b_kvu"][:, 0:D])):
                last = nc.vector.tensor_copy(fp(dst), four_times(src))
            last.then_inc(*pre.end("weights"))
            with eng.Fori(0, B // PAIR) as n:
                for i in range(PAIR):
                    nc.vector.tensor_copy(xb[:, i, :, :], chip.x_tok[:, n * PAIR + i, :, :]).then_inc(*dve.end(f"x{i}"))
                    eng.wait_ge(*pe.done(f"xT{i}", n))
                    nc.vector.tensor_copy(xT[:, i, :], ps[:, 6, 0:S]).then_inc(*dve.end(f"xT{i}"))
                    eng.wait_ge(*pe.done(f"latent{i}", n))
                    nc.vector.tensor_copy(latent[:, i, :], ps[:, 7, 0:S]).then_inc(*dve.end(f"latent{i}"))
                    eng.wait_ge(*pe.done(f"low{i}", n))
                    nc.vector.tensor_copy(low[:, i, :], ps[0:32, 6, 0:S]).then_inc(*dve.end(f"low{i}"))
                    eng.wait_ge(*pe.done(f"v{i}", n))
                    eng.wait_ge(ready, 1)
                    nc.vector.tensor_copy(h.v[:, i, :, :, 0:8], ps[:, 2, 0:S].rearrange("p (t h c) -> p t h c", t=QT, c=8))\
                        .then_inc(*dve.end(f"v{i}"))
                for i in range(PAIR):
                    heads_split(nc, eng, chip, h, dve, act, n, i, "q", scale)
                    heads_split(nc, eng, chip, h, dve, act, n, i, "k", 1.0)
                heads_dve(nc, eng, chip, h, pe, dve, n, lambda n, i: None,
                          lambda n, i: out_dve(nc, eng, chip, t, pe, dve, pool, n, i, attT, xb))

        @block.scalar
        def _(eng):
            heads_convert(nc, eng, h, loads)
            with eng.Fori(0, B // PAIR) as n:
                heads_act(nc, eng, chip, h, pe, dve, act, n, {"q": "q", "k": "k"}, scale)

        @block.tensor
        def _(eng):
            eng.wait_ge(*pre.done("mask"))
            for kt in range(QT):
                for qt in range(QT):
                    last = nc.tensor.transpose(ps[:, kt, qt * P:(qt + 1) * P], mf[:, qt, kt * P:(kt + 1) * P],
                                               chip.ident[:, :])
            last.then_inc(turned, 1)
            eng.wait_ge(*pre.done("weights"))

            def queries_and_keys(n, i):
                eng.wait_ge(*dve.done(f"v{i}", n))
                if i:
                    eng.wait_ge(*dve.done(f"qrem{i - 1}", n))
                for g in range(G):
                    out = ps[:, 4 + g // 2, (g % 2) * S:(g % 2 + 1) * S]
                    nc.tensor.matmul(out, wq[:, g, :, :].rearrange("k s c -> k (s c)"), low[:, i, :], start=True, stop=False)
                    last = nc.tensor.matmul(out, bq[:, g, :, :].rearrange("k s c -> k (s c)"), chip.ones[0:1, 0:S], start=False, stop=True)
                last.then_inc(*pe.end(f"q{i}"))
                if i:
                    eng.wait_ge(*dve.done(f"krem{i - 1}", n))
                for g in range(G):
                    out = ps[:, g // 2, (g % 2) * S:(g % 2 + 1) * S]
                    nc.tensor.matmul(out, wk[:, g, :, :].rearrange("k s c -> k (s c)"), latent[:, i, :], start=True, stop=False)
                    last = nc.tensor.matmul(out, bk[:, g, :, :].rearrange("k s c -> k (s c)"), chip.ones[0:1, 0:S], start=False, stop=True)
                last.then_inc(*pe.end(f"k{i}"))

            with eng.Fori(0, B // PAIR) as n:
                for i in range(PAIR):
                    eng.wait_ge(*dve.done(f"x{i}", n))
                    for qt in range(QT):
                        last = nc.tensor.transpose(ps[:, 6, qt * P:(qt + 1) * P], xb[:, i, qt, :], chip.ident[:, :])
                    last.then_inc(*pe.end(f"xT{i}"))
                    eng.wait_ge(*dve.done(f"xT{i}", n))
                    nc.tensor.matmul(ps[:, 7, 0:S], w["L0_attn_w_kvc"], xT[:, i, :], start=True, stop=False)
                    nc.tensor.matmul(ps[:, 7, 0:S], w["L0_attn_b_kvc"], chip.ones[0:1, 0:S], start=False, stop=True)\
                        .then_inc(*pe.end(f"latent{i}"))
                    nc.tensor.matmul(ps[0:32, 6, 0:S], w["L0_attn_w_qc"], xT[:, i, :], start=True, stop=False)
                    nc.tensor.matmul(ps[0:32, 6, 0:S], w["L0_attn_b_qc"], chip.ones[0:1, 0:S], start=False, stop=True)\
                        .then_inc(*pe.end(f"low{i}"))
                    eng.wait_ge(*dve.done(f"latent{i}", n))
                    for kt in range(QT):
                        out = ps[:, 2, kt * P:(kt + 1) * P]
                        nc.tensor.matmul(out, latent[:, i, kt * P:(kt + 1) * P], w["L0_attn_w_kvu"][:, D:2 * D], start=True, stop=False)
                        last = nc.tensor.matmul(out, chip.ones[0:1, 0:P], w["L0_attn_b_kvu"][:, D:2 * D], start=False, stop=True)
                    last.then_inc(*pe.end(f"v{i}"))
                heads_pe(nc, eng, chip, h, pe, dve, act, n, queries_and_keys, lambda i: i,
                         lambda n, i: project_out(nc, eng, chip, h.att[:, i, :, :, :].rearrange("p t h c -> p t (h c)"), attT, pe, dve, n, i,
                                                  w["L0_attn_w_o"], w["L0_attn_b_o"], f"att{h.rounds - 1}_{i}"), mask=(mq, mk))


OUT_BANKS = ((4, 5), (2, 3))


def project_out(nc, eng, chip, att, attT, pe, dve, turn, i, wo, bo, ready):
    ps, (turned, out_bank) = chip.ps, OUT_BANKS[i]
    eng.wait_ge(*dve.done(ready, turn))
    for qt in range(QT):
        last = nc.tensor.transpose(ps[:, turned, qt * P:(qt + 1) * P], att[:, qt, :], chip.ident[:, :])
    last.then_inc(*pe.end(f"attT{i}"))
    eng.wait_ge(*dve.done(f"attT{i}", turn))
    for qt in range(QT):
        out = ps[:, out_bank, qt * P:(qt + 1) * P]
        last = nc.tensor.matmul(out, attT[:, i, qt * P:(qt + 1) * P], wo, start=True, stop=bo is None)
        if bo is not None:
            last = nc.tensor.matmul(out, chip.ones[0:1, 0:P], bo, start=False, stop=True)
    last.then_inc(*pe.end(f"y{i}"))


def out_dve(nc, eng, chip, t, pe, dve, pool, turn, i, attT, xb):
    turned, out_bank = OUT_BANKS[i]
    eng.wait_ge(*pe.done(f"attT{i}", turn))
    nc.vector.tensor_copy(attT[:, i, :], chip.ps[:, turned, 0:S]).then_inc(*dve.end(f"attT{i}"))
    eng.wait_ge(*pe.done(f"y{i}", turn))
    tail_dve(nc, eng, chip, t, dve, pool, turn, chip.ps[:, out_bank, 0:S].rearrange("p (t d) -> p t d", t=QT), xb[:, i, :, :],
             seq=turn * PAIR + i, of=str(i))


def l3_xattn(nc, chip):
    with ExitStack() as ctx:
        sb = lambda n, s, dt=F32: ctx.enter_context(nc.sbuf_tensor(f"l3x_{n}", s, dt))
        pe_s, dve_s, act_s, pool_s, ready = stage_sems(nc, ctx, "l3x")
        h = Heads(nc, ctx, "l3x", 16, S2)
        t = Tail(nc, ctx, "l3x")
        wq, wk = sb("wq", [P, h.G, STRIPS, STRIP]), sb("wk", [P, h.G, STRIPS, STRIP])
        xb, xT, cT, attT = sb("xb", [P, PAIR, QT, D]), sb("xT", [P, PAIR, S]), sb("cT", [P, PAIR, S2]), sb("attT", [P, PAIR, S])
        ps, w = chip.ps, chip.w
        prepared, loads = ctx.enter_context(nc.semaphore("l3x_prepared")), ctx.enter_context(nc.semaphore("l3x_matrices"))
        pe = Steps(pe_s, named(["xT", "v"], 0) + named(["xT", "v"], 1) + h.pe_steps(["q", "k"], ["attT", "y"]))
        first, last = ["x", "xT", "v"], ["attT"] + TAIL_DVE
        dve = Steps(dve_s, named(first, 0) + named(first, 1) + h.split_steps(0) + h.split_steps(1) + h.dve_steps(late=last))
        act = Steps(act_s, h.act_steps())
        pool = Steps(pool_s, named(TAIL_POOL, 0) + named(TAIL_POOL, 1))
        scale = float(np.float32(1) / np.sqrt(np.float32(D)))
        block = ctx.enter_context(nc.Block())

        @block.sync
        def _(sp):
            heads_start(sp, h, chip.a, loads)

        @block.gpsimd
        def _(eng):
            clear_heads(nc, eng, h, ready)
            with eng.Fori(0, B // PAIR) as n:
                for i in range(PAIR):
                    tail_pool(nc, eng, chip, t, dve, pool, n, of=str(i))

        @block.vector
        def _(eng):
            for dst, src in ((wq, w["L3_xattn_Wq"]), (wk, w["L3_xattn_Wk"])):
                last = nc.vector.tensor_copy(fp(dst), four_times(src[:, 0, :]))
            last.then_inc(prepared, 1)
            with eng.Fori(0, B // PAIR) as n:
                for i in range(PAIR):
                    nc.vector.tensor_copy(xb[:, i, :, :], chip.x_tok[:, n * PAIR + i, :, :])
                    nc.vector.tensor_copy(cT[:, i, :], chip.ctxT[:, n * PAIR + i, :]).then_inc(*dve.end(f"x{i}"))
                    eng.wait_ge(*pe.done(f"xT{i}", n))
                    nc.vector.tensor_copy(xT[:, i, :], ps[:, 6, 0:S]).then_inc(*dve.end(f"xT{i}"))
                    eng.wait_ge(*pe.done(f"v{i}", n))
                    eng.wait_ge(ready, 1)
                    nc.vector.tensor_copy(h.v[:, i, :, :, 0:8], ps[:, 7, :].rearrange("p (t h c) -> p t h c", t=CT, c=8))\
                        .then_inc(*dve.end(f"v{i}"))
                for i in range(PAIR):
                    heads_split(nc, eng, chip, h, dve, act, n, i, "q", scale)
                    heads_split(nc, eng, chip, h, dve, act, n, i, "k", 1.0)
                heads_dve(nc, eng, chip, h, pe, dve, n, lambda n, i: None,
                          lambda n, i: out_dve(nc, eng, chip, t, pe, dve, pool, n, i, attT, xb))

        @block.scalar
        def _(eng):
            heads_convert(nc, eng, h, loads)
            with eng.Fori(0, B // PAIR) as n:
                heads_act(nc, eng, chip, h, pe, dve, act, n, {"q": "q", "k": "k"}, scale)

        @block.tensor
        def _(eng):
            eng.wait_ge(prepared, 1)

            def queries_and_keys(n, i):
                eng.wait_ge(*dve.done(f"xT{i}", n))
                if i:
                    eng.wait_ge(*dve.done(f"qrem{i - 1}", n))
                for g in range(h.G):
                    last = nc.tensor.matmul(ps[:, 4 + g // 2, (g % 2) * S:(g % 2 + 1) * S], wq[:, g, :, :].rearrange("k s c -> k (s c)"),
                                            xT[:, i, :], start=True, stop=True)
                last.then_inc(*pe.end(f"q{i}"))
                if i:
                    eng.wait_ge(*dve.done(f"krem{i - 1}", n))
                for g in range(h.G):
                    last = nc.tensor.matmul(ps[:, g, :], wk[:, g, :, :].rearrange("k s c -> k (s c)"), cT[:, i, :], start=True, stop=True)
                last.then_inc(*pe.end(f"k{i}"))

            with eng.Fori(0, B // PAIR) as n:
                for i in range(PAIR):
                    eng.wait_ge(*dve.done(f"x{i}", n))
                    for qt in range(QT):
                        last = nc.tensor.transpose(ps[:, 6, qt * P:(qt + 1) * P], xb[:, i, qt, :], chip.ident[:, :])
                    last.then_inc(*pe.end(f"xT{i}"))
                    for kt in range(CT):
                        last = nc.tensor.matmul(ps[:, 7, kt * P:(kt + 1) * P], cT[:, i, kt * P:(kt + 1) * P],
                                                w["L3_xattn_Wv"][:, 0, :], start=True, stop=True)
                    last.then_inc(*pe.end(f"v{i}"))
                eng.wait_ge(*dve.done("v1", n))
                heads_pe(nc, eng, chip, h, pe, dve, act, n, queries_and_keys, lambda i: i,
                         lambda n, i: project_out(nc, eng, chip, h.att[:, i, :, :, :].rearrange("p t h c -> p t (h c)"), attT, pe, dve, n, i,
                                                  w["L3_xattn_Wo"][:, 0, :], w["L3_xattn_bo"], f"att{h.rounds - 1}_{i}"))


def l2_attn(nc, chip):
    with ExitStack() as ctx:
        sb = lambda n, s, dt=F32: ctx.enter_context(nc.sbuf_tensor(f"l2a_{n}", s, dt))
        pe_s, dve_s, act_s, pool_s, ready = stage_sems(nc, ctx, "l2a")
        h = Heads(nc, ctx, "l2a", 16, S)
        t = Tail(nc, ctx, "l2a")
        block_diag, wp = sb("block_diag", [P, 16, 8]), sb("wp", [P, h.G, STRIPS, STRIP])
        xb, xT = sb("xb", [P, PAIR, QT, D]), sb("xT", [P, PAIR, S])
        q0, k0 = sb("q0", [P, PAIR, S]), sb("k0", [P, PAIR, S])
        ps, w = chip.ps, chip.w
        prepared, loads = ctx.enter_context(nc.semaphore("l2a_prepared")), ctx.enter_context(nc.semaphore("l2a_matrices"))
        first, last = ["xT", "q0", "k0", "v"], TAIL_DVE
        pe = Steps(pe_s, named(first, 0) + named(first, 1) + h.pe_steps(["q", "k"]))
        first = ["x"] + first
        dve = Steps(dve_s, named(first, 0) + named(first, 1) + h.split_steps(0) + h.split_steps(1) + h.dve_steps(late=last))
        act = Steps(act_s, h.act_steps())
        pool = Steps(pool_s, named(TAIL_POOL, 0) + named(TAIL_POOL, 1))
        scale = float(1 / np.sqrt(h.hd))
        block = ctx.enter_context(nc.Block())

        @block.sync
        def _(sp):
            heads_start(sp, h, chip.a, loads)

        @block.gpsimd
        def _(eng):
            clear_heads(nc, eng, h, ready)
            with eng.Fori(0, B // PAIR) as n:
                for i in range(PAIR):
                    tail_pool(nc, eng, chip, t, dve, pool, n, of=str(i))

        @block.vector
        def _(eng):
            nc.vector.tensor_tensor(fp(block_diag), w["L2_attn_Wp"].unsqueeze(1).to_broadcast([P, 16, 8]),
                                    w["c_heads"].unsqueeze(2).to_broadcast([P, 16, 8]), ALU.mult).then_inc(prepared, 1)
            eng.wait_ge(prepared, 1)
            nc.vector.tensor_copy(fp(wp), four_times(fp(block_diag).rearrange("p h c -> p (h c)"))).then_inc(prepared, 1)

            def close(n, i):
                eng.wait_ge(*dve.done(f"att{h.rounds - 1}_{i}", n))
                tail_dve(nc, eng, chip, t, dve, pool, n, h.att[:, i, :, :, :].rearrange("p t h c -> p t (h c)"), xb[:, i, :, :],
                         seq=n * PAIR + i, of=str(i))

            with eng.Fori(0, B // PAIR) as n:
                for i in range(PAIR):
                    nc.vector.tensor_copy(xb[:, i, :, :], chip.x_tok[:, n * PAIR + i, :, :]).then_inc(*dve.end(f"x{i}"))
                    eng.wait_ge(*pe.done(f"xT{i}", n))
                    nc.vector.tensor_copy(xT[:, i, :], ps[:, 6, 0:S]).then_inc(*dve.end(f"xT{i}"))
                    eng.wait_ge(*pe.done(f"q0{i}", n))
                    nc.vector.tensor_scalar(q0[:, i, :], ps[:, 3, 0:S], w["L2_attn_bq"], None, ALU.add).then_inc(*dve.end(f"q0{i}"))
                    eng.wait_ge(*pe.done(f"k0{i}", n))
                    nc.vector.tensor_scalar(k0[:, i, :], ps[:, 7, 0:S], w["L2_attn_bk"], None, ALU.add).then_inc(*dve.end(f"k0{i}"))
                    eng.wait_ge(*pe.done(f"v{i}", n))
                    eng.wait_ge(ready, 1)
                    nc.vector.tensor_copy(h.v[:, i, :, :, 0:8], ps[:, 2, 0:S].rearrange("p (t h c) -> p t h c", t=QT, c=8))\
                        .then_inc(*dve.end(f"v{i}"))
                for i in range(PAIR):
                    heads_split(nc, eng, chip, h, dve, act, n, i, "q", scale)
                    heads_split(nc, eng, chip, h, dve, act, n, i, "k", 1.0)
                heads_dve(nc, eng, chip, h, pe, dve, n, lambda n, i: None, close)

        @block.scalar
        def _(eng):
            heads_convert(nc, eng, h, loads)
            with eng.Fori(0, B // PAIR) as n:
                heads_act(nc, eng, chip, h, pe, dve, act, n, {"q": "q", "k": "k"}, scale)

        @block.tensor
        def _(eng):
            eng.wait_ge(prepared, 2)

            def queries_and_keys(n, i):
                eng.wait_ge(*dve.done(f"k0{i}", n))
                if i:
                    eng.wait_ge(*dve.done(f"qrem{i - 1}", n))
                for g in range(h.G):
                    last = nc.tensor.matmul(ps[:, 4 + g // 2, (g % 2) * S:(g % 2 + 1) * S], wp[:, g, :, :].rearrange("k s c -> k (s c)"),
                                            q0[:, i, :], start=True, stop=True)
                last.then_inc(*pe.end(f"q{i}"))
                if i:
                    eng.wait_ge(*dve.done(f"krem{i - 1}", n))
                for g in range(h.G):
                    last = nc.tensor.matmul(ps[:, g // 2, (g % 2) * S:(g % 2 + 1) * S], wp[:, g, :, :].rearrange("k s c -> k (s c)"),
                                            k0[:, i, :], start=True, stop=True)
                last.then_inc(*pe.end(f"k{i}"))

            with eng.Fori(0, B // PAIR) as n:
                for i in range(PAIR):
                    eng.wait_ge(*dve.done(f"x{i}", n))
                    for qt in range(QT):
                        last = nc.tensor.transpose(ps[:, 6, qt * P:(qt + 1) * P], xb[:, i, qt, :], chip.ident[:, :])
                    last.then_inc(*pe.end(f"xT{i}"))
                    eng.wait_ge(*dve.done(f"xT{i}", n))
                    nc.tensor.matmul(ps[:, 3, 0:S], w["L2_attn_Wq"], xT[:, i, :], start=True, stop=True).then_inc(*pe.end(f"q0{i}"))
                    nc.tensor.matmul(ps[:, 7, 0:S], w["L2_attn_Wk"], xT[:, i, :], start=True, stop=True).then_inc(*pe.end(f"k0{i}"))
                    for kt in range(QT):
                        out = ps[:, 2, kt * P:(kt + 1) * P]
                        nc.tensor.matmul(out, xT[:, i, kt * P:(kt + 1) * P], w["L2_attn_Wv"], start=True, stop=False)
                        last = nc.tensor.matmul(out, chip.ones[0:1, 0:P], w["L2_attn_bv"], start=False, stop=True)
                    last.then_inc(*pe.end(f"v{i}"))
                heads_pe(nc, eng, chip, h, pe, dve, act, n, queries_and_keys, lambda i: i, lambda n, i: None)


LAMBDA_INIT = 0.8 - 0.6 * float(np.exp(-0.3 * 12))


def l1_attn(nc, chip):
    with ExitStack() as ctx:
        sb = lambda n, s, dt=F32: ctx.enter_context(nc.sbuf_tensor(f"l1a_{n}", s, dt))
        pe_s, dve_s, act_s, pool_s, ready = stage_sems(nc, ctx, "l1a")
        h = Heads(nc, ctx, "l1a", 32, S)
        t = Tail(nc, ctx, "l1a")
        xb, xT, attT = sb("xb", [P, PAIR, QT, D]), sb("xT", [P, S]), sb("attT", [P, PAIR, S])
        rot, rot2 = sb("rot", [P, PAIR, 2, QT, D]), sb("rot2", [P, QT, D])
        four = fp(h.e).rearrange("p a j n -> p (a j n)").rearrange("p (m t g s c) -> p m t g s c", m=2, t=QT, g=h.G, s=STRIPS)
        lam, lam2, neglam = sb("lam", [P, 2, 4]), sb("lam2", [P, 2]), sb("neglam", [P, 1])
        gain = sb("gain", [P, 8])
        diff, sq = sb("diff", [P, QT, 16, 8]), sb("sq", [P, QT, 16, 8])
        ms, rms = sb("ms", [P, QT, 16]), sb("rms", [P, QT, 16])
        heads = sb("heads", [P, PAIR, QT, D])
        ps, w = chip.ps, chip.w
        lam_steps = Steps(ctx.enter_context(nc.semaphore("l1a_lambda_steps")), ["products", "sums", "neglam"])
        lam_exp, loads = ctx.enter_context(nc.semaphore("l1a_lambda_exp")), ctx.enter_context(nc.semaphore("l1a_matrices"))
        first = ["xT", "qkv"]
        pe = Steps(pe_s, named(first, 0) + named(first, 1) + h.pe_steps(["q", "k"], ["attT", "y"]))
        first = ["x", "xT", "v"] + [f"{k}{n}" for k in "qk" for n in ("cos", "sin", "turned")]
        dve = Steps(dve_s, named(first, 0) + named(first, 1) + h.split_steps(0) + h.split_steps(1) + h.dve_steps(["diff", "sq", "ms"], ["rms", "gained", "attT"] + TAIL_DVE))
        act = Steps(act_s, h.act_steps(before=lambda i: named(["qfour", "kfour"], i)))
        pool = Steps(pool_s, named(["rmseps", "rmspow"] + TAIL_POOL, 0) + named(["rmseps", "rmspow"] + TAIL_POOL, 1))
        block = ctx.enter_context(nc.Block())

        @block.sync
        def _(sp):
            heads_start(sp, h, chip.a, loads)

        @block.gpsimd
        def _(eng):
            clear_heads(nc, eng, h, ready)
            with eng.Fori(0, B // PAIR) as n:
                for i in range(PAIR):
                    eng.wait_ge(*dve.done(f"ms{i}", n))
                    nc.gpsimd.tensor_tensor(fp(rms), fp(ms), chip.eps[:, 0:1].unsqueeze(2).to_broadcast([P, QT, 16]), ALU.add)\
                        .then_inc(*pool.end(f"rmseps{i}"))
                    eng.wait_ge(*pool.done(f"rmseps{i}", n))
                    nc.gpsimd.tensor_tensor(fp(rms), fp(rms), chip.neghalf[:, 0:32].rearrange("p (t h) -> p t h", t=QT), ALU.pow)\
                        .then_inc(*pool.end(f"rmspow{i}"))
                    tail_pool(nc, eng, chip, t, dve, pool, n, of=str(i))

        @block.vector
        def _(eng):
            nc.vector.tensor_tensor(lam[:, 0, :], w["L1_attn_lambda_q1"], w["L1_attn_lambda_k1"], ALU.mult)
            nc.vector.tensor_tensor(lam[:, 1, :], w["L1_attn_lambda_q2"], w["L1_attn_lambda_k2"], ALU.mult)\
                .then_inc(*lam_steps.end("products"))
            nc.vector.tensor_scalar(fp(gain), w["L1_attn_subln_g"], 1.0 - LAMBDA_INIT, None, ALU.mult)
            eng.wait_ge(*lam_steps.done("products"))
            nc.vector.tensor_reduce(fp(lam2), fp(lam), AX.X, ALU.add).then_inc(*lam_steps.end("sums"))
            eng.wait_ge(lam_exp, 1)
            nc.vector.scalar_tensor_tensor(fp(neglam), lam2[:, 1:2], -LAMBDA_INIT, lam2[:, 0:1], ALU.add, ALU.subtract)\
                .then_inc(*lam_steps.end("neglam"))
            eng.wait_ge(*lam_steps.done("neglam"))

            def rotate(n, i):
                for m, k in enumerate("qk"):
                    src = ps[:, m, 0:S].rearrange("p (t d) -> p t d", t=QT)
                    pairs = ps[:, m, 0:S].rearrange("p (n c) -> p n c", c=2)
                    sin = w["c_rope"][:, m, 1, :, :].rearrange("p t (n c) -> p (t n) c", c=2)
                    out = fp(rot2).rearrange("p t (n c) -> p (t n) c", c=2)
                    if m or i:
                        eng.wait_ge(*dve.done(f"qturned{i}" if m else f"kturned{i - 1}", n))
                    nc.vector.tensor_tensor(rot[:, i, m, :, :], src, w["c_rope"][:, m, 0, :, :], ALU.mult).then_inc(*dve.end(f"{k}cos{i}"))
                    nc.vector.tensor_tensor(out[:, :, 0], pairs[:, :, 1], sin[:, :, 0], ALU.mult)
                    nc.vector.tensor_tensor(out[:, :, 1], pairs[:, :, 0], sin[:, :, 1], ALU.mult).then_inc(*dve.end(f"{k}sin{i}"))
                    eng.wait_ge(*dve.done(f"{k}sin{i}", n))
                    nc.vector.tensor_tensor(rot[:, i, m, :, :], rot[:, i, m, :, :], fp(rot2), ALU.add).then_inc(*dve.end(f"{k}turned{i}"))

            def difference(n, i):
                eng.wait_ge(*dve.done(f"att{h.rounds - 1}_{i}", n))
                pair = h.att[:, i, :, :, :].rearrange("p t (h two) c -> p (t h) two c", two=2)
                nc.vector.scalar_tensor_tensor(fp(diff).rearrange("p t h c -> p (t h) c"), pair[:, :, 1, :], neglam[:, 0:1],
                                               pair[:, :, 0, :], ALU.mult, ALU.add).then_inc(*dve.end(f"diff{i}"))
                eng.wait_ge(*dve.done(f"diff{i}", n))
                nc.vector.scalar_tensor_tensor(fp(sq), fp(diff), 1.0 / 8, fp(diff), ALU.mult, ALU.mult).then_inc(*dve.end(f"sq{i}"))
                eng.wait_ge(*dve.done(f"sq{i}", n))
                nc.vector.tensor_reduce(fp(ms), fp(sq), AX.X, ALU.add).then_inc(*dve.end(f"ms{i}"))

            def close(n, i):
                eng.wait_ge(*pool.done(f"rmspow{i}", n))
                nc.vector.tensor_tensor(fp(sq), fp(diff), fp(rms).unsqueeze(3).to_broadcast([P, QT, 16, 8]), ALU.mult)\
                    .then_inc(*dve.end(f"rms{i}"))
                eng.wait_ge(*dve.done(f"rms{i}", n))
                nc.vector.tensor_tensor(heads[:, i, :, :].rearrange("p t (h c) -> p (t h) c", c=8),
                                        fp(sq).rearrange("p t h c -> p (t h) c"),
                                        fp(gain).unsqueeze(1).to_broadcast([P, 32, 8]), ALU.mult).then_inc(*dve.end(f"gained{i}"))
                eng.wait_ge(*dve.done(f"gained{i}", n))
                out_dve(nc, eng, chip, t, pe, dve, pool, n, i, attT, xb)

            with eng.Fori(0, B // PAIR) as n:
                for i in range(PAIR):
                    nc.vector.tensor_copy(xb[:, i, :, :], chip.x_tok[:, n * PAIR + i, :, :]).then_inc(*dve.end(f"x{i}"))
                    eng.wait_ge(*pe.done(f"xT{i}", n))
                    nc.vector.tensor_copy(fp(xT), ps[:, 6, 0:S]).then_inc(*dve.end(f"xT{i}"))
                    eng.wait_ge(*pe.done(f"qkv{i}", n))
                    eng.wait_ge(ready, 1)
                    nc.vector.tensor_copy(h.v[:, i, :, :, 0:8], ps[:, 2, 0:S].rearrange("p (t h c) -> p t h c", t=QT, c=8))\
                        .then_inc(*dve.end(f"v{i}"))
                    rotate(n, i)
                for i in range(PAIR):
                    heads_split(nc, eng, chip, h, dve, act, n, i, "q", 1.0)
                    heads_split(nc, eng, chip, h, dve, act, n, i, "k", 1.0)
                heads_dve(nc, eng, chip, h, pe, dve, n, difference, close)

        @block.scalar
        def _(eng):
            eng.wait_ge(*lam_steps.done("sums"))
            nc.scalar.activation(fp(lam2), fp(lam2), ACT.Exp).then_inc(lam_exp, 1)
            heads_convert(nc, eng, h, loads)

            def four_copies(n, i):
                eng.wait_ge(*dve.done(f"kturned{i}", n))
                if i:
                    eng.wait_ge(*pe.done(f"k{i - 1}", n))
                for m, k in enumerate("qk"):
                    for q in range(QT):
                        last = nc.scalar.activation(four[:, m, q, :, :, :], four_times(rot[:, i, m, q, :]), ACT.Copy)
                    last.then_inc(*act.end(f"{k}four{i}"))

            with eng.Fori(0, B // PAIR) as n:
                heads_act(nc, eng, chip, h, pe, dve, act, n, {"q": "q", "k": "k"}, 1.0, before=four_copies)

        @block.tensor
        def _(eng):
            eng.wait_ge(*lam_steps.done("neglam"))

            def queries_and_keys(n, i):
                for m, k in enumerate("qk"):
                    eng.wait_ge(*act.done(f"{k}four{i}", n))
                    if i:
                        eng.wait_ge(*dve.done(f"{k}rem{i - 1}", n))
                    for g in range(h.G):
                        for qt in range(QT):
                            at = (g % 2) * S + qt * P
                            last = nc.tensor.transpose(ps[:, (4, 0)[m] + g // 2, at:at + P],
                                                       four[:, m, qt, g, :, :].rearrange("p s c -> p (s c)"), chip.ident[:, :])
                    last.then_inc(*pe.end(f"{k}{i}"))

            with eng.Fori(0, B // PAIR) as n:
                for i in range(PAIR):
                    eng.wait_ge(*dve.done(f"x{i}", n))
                    for qt in range(QT):
                        last = nc.tensor.transpose(ps[:, 6, qt * P:(qt + 1) * P], xb[:, i, qt, :], chip.ident[:, :])
                    last.then_inc(*pe.end(f"xT{i}"))
                    eng.wait_ge(*dve.done(f"xT{i}", n))
                    if i:
                        eng.wait_ge(*dve.done(f"kturned{i - 1}", n))
                    for m, name in enumerate(("L1_attn_Wq", "L1_attn_Wk", "L1_attn_Wv")):
                        for qt in range(QT):
                            last = nc.tensor.matmul(ps[:, m, qt * P:(qt + 1) * P], xT[:, qt * P:(qt + 1) * P], w[name],
                                                    start=True, stop=True)
                    last.then_inc(*pe.end(f"qkv{i}"))
                eng.wait_ge(*dve.done("kturned1", n))
                heads_pe(nc, eng, chip, h, pe, dve, act, n, queries_and_keys, lambda i: i // 2,
                         lambda n, i: project_out(nc, eng, chip, heads[:, i, :, :], attT, pe, dve, n, i, w["L1_attn_Wo"], None, f"gained{i}"))


def paired(names):
    return [f"{n}{i}" for n in names for i in range(PAIR)]


def tails_dve(nc, eng, chip, t, dve, pool, turn, ready, addend, residual):
    for i in range(PAIR):
        eng.wait_ge(*ready(i))
        nc.vector.tensor_tensor(fp(t[i].y), addend(i), residual(i), ALU.add).then_inc(*dve.end(f"sum{i}"))
    for i in range(PAIR):
        eng.wait_ge(*dve.done(f"sum{i}", turn))
        for q in range(QT):
            last = nc.vector.bn_stats(t[i].stats[:, q, :], t[i].y[:, q, :])
        last.then_inc(*dve.end(f"stats{i}"))
    for i in range(PAIR):
        eng.wait_ge(*dve.done(f"stats{i}", turn))
        nc.vector.memset(chip.scratch[:, 4 + i:5 + i], 0.0)
        for q in range(QT):
            last = nc.vector.bn_aggr(t[i].mv[:, q, :], t[i].stats[:, q, :])
        last.then_inc(*dve.end(f"var{i}"))
    for i in range(PAIR):
        eng.wait_ge(*pool.done(f"rstd{i}", turn))
        for q in range(QT):
            last = nc.vector.tensor_scalar(chip.x_tok[:, PAIR * turn + i, q, :], t[i].y[:, q, :], t[i].mv[:, q, 0:1],
                                           t[i].rstd[:, q:q + 1], ALU.subtract, ALU.mult)
        last.then_inc(*dve.end(f"normed{i}"))


def tails_pool(nc, eng, chip, t, dve, pool, turn):
    for i in range(PAIR):
        eng.wait_ge(*dve.done(f"var{i}", turn))
        nc.gpsimd.tensor_tensor(fp(t[i].rstd), t[i].mv[:, :, 1], chip.eps[:, 0:QT], ALU.add).then_inc(*pool.end(f"vareps{i}"))
    for i in range(PAIR):
        eng.wait_ge(*pool.done(f"vareps{i}", turn))
        nc.gpsimd.tensor_tensor(fp(t[i].rstd), fp(t[i].rstd), chip.neghalf[:, 0:QT], ALU.pow).then_inc(*pool.end(f"rstd{i}"))


def l3_attn(nc, chip):
    with ExitStack() as ctx:
        sb = lambda n, s: [ctx.enter_context(nc.sbuf_tensor(f"l3a_{n}{i}", s, F32)) for i in range(PAIR)]
        pe_s, dve_s, act_s, pool_s, ready = stage_sems(nc, ctx, "l3a")
        t = [Tail(nc, ctx, f"l3a{i}") for i in range(PAIR)]
        xb, xT = sb("xb", [P, QT, D]), sb("xT", [P, S])
        low, qk, v = sb("low", [P, 2, S]), sb("qk", [P, 2, S]), sb("v", [P, S])
        ex = sb("ex", [P, 2, S])
        kv, oT = sb("kv", [P, D]), sb("oT", [P, S])
        ps, w = chip.ps, chip.w
        pe = Steps(pe_s, paired(["xT", "qkv", "kv", "oT", "y"]))
        dve = Steps(dve_s, paired(["x", "xT", "low", "v", "qk", "kv", "oT"] + TAIL_DVE))
        act = Steps(act_s, paired(["exp"]))
        pool = Steps(pool_s, paired(TAIL_POOL))
        block = ctx.enter_context(nc.Block())

        @block.gpsimd
        def _(eng):
            with eng.Fori(0, B // PAIR) as b:
                tails_pool(nc, eng, chip, t, dve, pool, b)

        @block.scalar
        def _(eng):
            with eng.Fori(0, B // PAIR) as b:
                for i in range(PAIR):
                    eng.wait_ge(*dve.done(f"low{i}", b))
                    nc.scalar.activation(fp(ex[i]), fp(low[i]), ACT.Exp).then_inc(*act.end(f"exp{i}"))

        @block.vector
        def _(eng):
            with eng.Fori(0, B // PAIR) as b:
                for i in range(PAIR):
                    nc.vector.tensor_copy(fp(xb[i]), chip.x_tok[:, PAIR * b + i, :, :]).then_inc(*dve.end(f"x{i}"))
                for i in range(PAIR):
                    eng.wait_ge(*pe.done(f"xT{i}", b))
                    nc.vector.tensor_copy(fp(xT[i]), ps[:, 4 * i + 1, S:2 * S]).then_inc(*dve.end(f"xT{i}"))
                for i in range(PAIR):
                    eng.wait_ge(*pe.done(f"qkv{i}", b))
                    nc.vector.tensor_scalar(fp(low[i]), ps[:, 4 * i, :].rearrange("p (a s) -> p a s", a=2), 0.0, None, ALU.min).then_inc(*dve.end(f"low{i}"))
                for i in range(PAIR):
                    nc.vector.tensor_copy(fp(v[i]), ps[:, 4 * i + 1, 0:S]).then_inc(*dve.end(f"v{i}"))
                for i in range(PAIR):
                    eng.wait_ge(*act.done(f"exp{i}", b))
                    nc.vector.scalar_tensor_tensor(fp(qk[i]), ps[:, 4 * i, :].rearrange("p (a s) -> p a s", a=2), 0.0, fp(ex[i]), ALU.max, ALU.add)\
                        .then_inc(*dve.end(f"qk{i}"))
                for i in range(PAIR):
                    eng.wait_ge(*pe.done(f"kv{i}", b))
                    nc.vector.tensor_tensor(fp(kv[i]).rearrange("p (h c) -> p h c", c=8),
                                            ps[:, 4 * i + 2, 0:D].rearrange("p (h c) -> p h c", c=8),
                                            w["c_heads"].unsqueeze(2).to_broadcast([P, 16, 8]), ALU.mult).then_inc(*dve.end(f"kv{i}"))
                for i in range(PAIR):
                    eng.wait_ge(*pe.done(f"oT{i}", b))
                    nc.vector.tensor_copy(fp(oT[i]), ps[:, 4 * i + 3, 0:S]).then_inc(*dve.end(f"oT{i}"))
                tails_dve(nc, eng, chip, t, dve, pool, b, lambda i: pe.done(f"y{i}", b),
                          lambda i: ps[:, 4 * i + 2, 0:S].rearrange("p (t d) -> p t d", t=QT), lambda i: fp(xb[i]))

        @block.tensor
        def _(eng):
            with eng.Fori(0, B // PAIR) as b:
                for i in range(PAIR):
                    eng.wait_ge(*dve.done(f"x{i}", b))
                    for qt in range(QT):
                        last = nc.tensor.transpose(ps[:, 4 * i + 1, S + qt * P:S + (qt + 1) * P], xb[i][:, qt, :], chip.ident[:, :])
                    last.then_inc(*pe.end(f"xT{i}"))
                for i in range(PAIR):
                    eng.wait_ge(*dve.done(f"xT{i}", b))
                    nc.tensor.matmul(ps[:, 4 * i, 0:S], w["L3_attn_Wq"], fp(xT[i]), start=True, stop=False)
                    nc.tensor.matmul(ps[:, 4 * i, 0:S], w["L3_attn_bq"], chip.ones[0:1, 0:S], start=False, stop=True)
                    for c, k in ((1, "k"), (2, "v")):
                        for kt in range(QT):
                            out = ps[:, 4 * i + c // 2, c % 2 * S + kt * P:c % 2 * S + (kt + 1) * P]
                            nc.tensor.matmul(out, xT[i][:, kt * P:(kt + 1) * P], w[f"L3_attn_W{k}"], start=True, stop=False)
                            last = nc.tensor.matmul(out, chip.ones[0:1, 0:P], w[f"L3_attn_b{k}"], start=False, stop=True)
                    last.then_inc(*pe.end(f"qkv{i}"))
                for i in range(PAIR):
                    eng.wait_ge(*dve.done(f"qk{i}", b))
                    for kt in range(QT):
                        last = nc.tensor.matmul(ps[:, 4 * i + 2, 0:D], qk[i][:, 1, kt * P:(kt + 1) * P], v[i][:, kt * P:(kt + 1) * P],
                                                start=(kt == 0), stop=(kt == QT - 1))
                    last.then_inc(*pe.end(f"kv{i}"))
                for i in range(PAIR):
                    eng.wait_ge(*dve.done(f"kv{i}", b))
                    nc.tensor.matmul(ps[:, 4 * i + 3, 0:S], fp(kv[i]), qk[i][:, 0, :], start=True, stop=True).then_inc(*pe.end(f"oT{i}"))
                for i in range(PAIR):
                    eng.wait_ge(*dve.done(f"oT{i}", b))
                    for qt in range(QT):
                        out = ps[:, 4 * i + 2, qt * P:(qt + 1) * P]
                        nc.tensor.matmul(out, oT[i][:, qt * P:(qt + 1) * P], w["L3_attn_Wp"], start=True, stop=False)
                        last = nc.tensor.matmul(out, chip.ones[0:1, 0:P], w["L3_attn_bp"], start=False, stop=True)
                    last.then_inc(*pe.end(f"y{i}"))


class Pick:

    def __init__(self, nc, ctx, label, n, tiles=QT):
        sb = lambda k, s: ctx.enter_context(nc.sbuf_tensor(f"{label}_{k}", s, F32))
        self.n, self.tiles = n, tiles
        self.m, self.eq, self.best = sb("m", [P, tiles]), sb("eq", [P, tiles, n]), sb("best", [P, tiles])


def pick_steps(p):
    return [p + s for s in ("max", "eq", "cand", "best", "pick")]


def pick_first(nc, eng, chip, k, dve, b, p, v, out):
    wide = lambda x: fp(x).unsqueeze(2).to_broadcast([P, k.tiles, k.n])
    nc.vector.tensor_reduce(fp(k.m), v, AX.X, ALU.max).then_inc(*dve.end(p + "max"))
    eng.wait_ge(*dve.done(p + "max", b))
    nc.vector.tensor_tensor(fp(k.eq), v, wide(k.m), ALU.is_equal).then_inc(*dve.end(p + "eq"))
    eng.wait_ge(*dve.done(p + "eq", b))
    nc.vector.tensor_tensor(fp(k.eq), fp(k.eq), chip.w["c_rank"][:, 0:k.n].unsqueeze(1).to_broadcast([P, k.tiles, k.n]), ALU.mult)\
        .then_inc(*dve.end(p + "cand"))
    eng.wait_ge(*dve.done(p + "cand", b))
    nc.vector.tensor_reduce(fp(k.best), fp(k.eq), AX.X, ALU.max).then_inc(*dve.end(p + "best"))
    eng.wait_ge(*dve.done(p + "best", b))
    nc.vector.tensor_tensor(out, fp(k.eq), wide(k.best), ALU.is_equal).then_inc(*dve.end(p + "pick"))


def pick_first_paired(nc, eng, chip, k, dve, turn, p, ready, v, out):
    for i in range(PAIR):
        eng.wait_ge(*dve.done(f"{ready}{i}", turn))
        nc.vector.tensor_reduce(fp(k[i].m), fp(v[i]), AX.X, ALU.max).then_inc(*dve.end(f"{p}max{i}"))
    n = k[0].n
    wide = lambda x: fp(x).unsqueeze(2).to_broadcast([P, QT, n])
    for i in range(PAIR):
        eng.wait_ge(*dve.done(f"{p}max{i}", turn))
        nc.vector.tensor_tensor(fp(k[i].eq), fp(v[i]), wide(k[i].m), ALU.is_equal).then_inc(*dve.end(f"{p}eq{i}"))
    for i in range(PAIR):
        eng.wait_ge(*dve.done(f"{p}eq{i}", turn))
        nc.vector.tensor_tensor(fp(k[i].eq), fp(k[i].eq), chip.w["c_rank"][:, 0:n].unsqueeze(1).to_broadcast([P, QT, n]), ALU.mult)\
            .then_inc(*dve.end(f"{p}cand{i}"))
    for i in range(PAIR):
        eng.wait_ge(*dve.done(f"{p}cand{i}", turn))
        nc.vector.tensor_reduce(fp(k[i].best), fp(k[i].eq), AX.X, ALU.max).then_inc(*dve.end(f"{p}best{i}"))
    for i in range(PAIR):
        eng.wait_ge(*dve.done(f"{p}best{i}", turn))
        nc.vector.tensor_tensor(fp(out[i]), fp(k[i].eq), wide(k[i].best), ALU.is_equal).then_inc(*dve.end(f"{p}pick{i}"))


def l0_ffn(nc, chip):
    E = 8
    with ExitStack() as ctx:
        sb = lambda n, s: [ctx.enter_context(nc.sbuf_tensor(f"l0f_{n}{i}", s, F32)) for i in range(PAIR)]
        pe_s, dve_s, act_s, pool_s, ready = stage_sems(nc, ctx, "l0f")
        t, k = [Tail(nc, ctx, f"l0f{i}") for i in range(PAIR)], [Pick(nc, ctx, f"l0f{i}", E) for i in range(PAIR)]
        xb, xT = sb("xb", [P, QT, D]), sb("xT", [P, S])
        gate, one, two = sb("gate", [P, QT, E]), sb("one", [P, QT, E]), sb("two", [P, QT, E])
        mx, den = sb("mx", [P, QT]), sb("den", [P, QT])
        prod, mixed = sb("prod", [P, QT, E, D]), sb("mixed", [P, QT, D])
        ps, w = chip.ps, chip.w
        pe = Steps(pe_s, paired(["xT", "logits", "experts"]))
        dve = Steps(dve_s, paired(["x", "xT", "gmax", "shift", "den", "rden", "gate"] + pick_steps("first") + ["rest"]
                    + pick_steps("second") + ["sel", "kept", "kden", "rkden", "weight", "prod", "mixed"] + TAIL_DVE))
        act = Steps(act_s, paired(["exp"]))
        pool = Steps(pool_s, paired(TAIL_POOL))
        wide = lambda x: fp(x).unsqueeze(2).to_broadcast([P, QT, E])
        logits = lambda i: ps[:, 4 * i + 1, 0:QT * E].rearrange("p (t e) -> p t e", e=E)
        block = ctx.enter_context(nc.Block())

        @block.gpsimd
        def _(eng):
            with eng.Fori(0, B // PAIR) as b:
                tails_pool(nc, eng, chip, t, dve, pool, b)

        @block.scalar
        def _(eng):
            with eng.Fori(0, B // PAIR) as b:
                for i in range(PAIR):
                    eng.wait_ge(*dve.done(f"shift{i}", b))
                    nc.scalar.activation(fp(gate[i]), fp(gate[i]), ACT.Exp).then_inc(*act.end(f"exp{i}"))

        @block.vector
        def _(eng):
            with eng.Fori(0, B // PAIR) as b:
                for i in range(PAIR):
                    nc.vector.tensor_copy(fp(xb[i]), chip.x_tok[:, PAIR * b + i, :, :]).then_inc(*dve.end(f"x{i}"))
                for i in range(PAIR):
                    eng.wait_ge(*pe.done(f"xT{i}", b))
                    nc.vector.tensor_copy(fp(xT[i]), ps[:, 4 * i, 0:S]).then_inc(*dve.end(f"xT{i}"))
                for i in range(PAIR):
                    eng.wait_ge(*pe.done(f"logits{i}", b))
                    nc.vector.tensor_reduce(fp(mx[i]), logits(i), AX.X, ALU.max).then_inc(*dve.end(f"gmax{i}"))
                for i in range(PAIR):
                    eng.wait_ge(*dve.done(f"gmax{i}", b))
                    nc.vector.tensor_tensor(fp(gate[i]), logits(i), wide(mx[i]), ALU.subtract).then_inc(*dve.end(f"shift{i}"))
                for i in range(PAIR):
                    eng.wait_ge(*act.done(f"exp{i}", b))
                    nc.vector.tensor_reduce(fp(den[i]), fp(gate[i]), AX.X, ALU.add).then_inc(*dve.end(f"den{i}"))
                for i in range(PAIR):
                    eng.wait_ge(*dve.done(f"den{i}", b))
                    nc.vector.reciprocal(fp(den[i]), fp(den[i])).then_inc(*dve.end(f"rden{i}"))
                for i in range(PAIR):
                    eng.wait_ge(*dve.done(f"rden{i}", b))
                    nc.vector.tensor_tensor(fp(gate[i]), fp(gate[i]), wide(den[i]), ALU.mult).then_inc(*dve.end(f"gate{i}"))
                pick_first_paired(nc, eng, chip, k, dve, b, "first", "gate", gate, one)
                for i in range(PAIR):
                    eng.wait_ge(*dve.done(f"firstpick{i}", b))
                    nc.vector.scalar_tensor_tensor(fp(two[i]), fp(one[i]), -2.0, fp(gate[i]), ALU.mult, ALU.add).then_inc(*dve.end(f"rest{i}"))
                pick_first_paired(nc, eng, chip, k, dve, b, "second", "rest", two, two)
                for i in range(PAIR):
                    eng.wait_ge(*dve.done(f"secondpick{i}", b))
                    nc.vector.tensor_tensor(fp(one[i]), fp(one[i]), fp(two[i]), ALU.add).then_inc(*dve.end(f"sel{i}"))
                for i in range(PAIR):
                    eng.wait_ge(*dve.done(f"sel{i}", b))
                    nc.vector.tensor_tensor(fp(gate[i]), fp(gate[i]), fp(one[i]), ALU.mult).then_inc(*dve.end(f"kept{i}"))
                for i in range(PAIR):
                    eng.wait_ge(*dve.done(f"kept{i}", b))
                    nc.vector.tensor_reduce(fp(den[i]), fp(gate[i]), AX.X, ALU.add).then_inc(*dve.end(f"kden{i}"))
                for i in range(PAIR):
                    eng.wait_ge(*dve.done(f"kden{i}", b))
                    nc.vector.reciprocal(fp(den[i]), fp(den[i])).then_inc(*dve.end(f"rkden{i}"))
                for i in range(PAIR):
                    eng.wait_ge(*dve.done(f"rkden{i}", b))
                    nc.vector.tensor_tensor(fp(gate[i]), fp(gate[i]), wide(den[i]), ALU.mult).then_inc(*dve.end(f"weight{i}"))
                for i in range(PAIR):
                    eng.wait_ge(*dve.done(f"weight{i}", b))
                    eng.wait_ge(*pe.done(f"experts{i}", b))
                    for qt in range(QT):
                        last = nc.vector.tensor_tensor(prod[i][:, qt, :, :],
                                                       ps[:, 4 * i + 2 * qt:4 * i + 2 * qt + 2, :].rearrange("p a (e d) -> p (a e) d", d=D),
                                                       gate[i][:, qt, :].unsqueeze(2).to_broadcast([P, E, D]), ALU.mult)
                    last.then_inc(*dve.end(f"prod{i}"))
                for i in range(PAIR):
                    eng.wait_ge(*dve.done(f"prod{i}", b))
                    for qt in range(QT):
                        last = nc.vector.tensor_reduce(mixed[i][:, qt, :], prod[i][:, qt, :, :].rearrange("p e d -> p d e"), AX.X, ALU.add)
                    last.then_inc(*dve.end(f"mixed{i}"))
                tails_dve(nc, eng, chip, t, dve, pool, b, lambda i: dve.done(f"mixed{i}", b),
                          lambda i: fp(mixed[i]), lambda i: fp(xb[i]))

        @block.tensor
        def _(eng):
            with eng.Fori(0, B // PAIR) as b:
                for i in range(PAIR):
                    eng.wait_ge(*dve.done(f"x{i}", b))
                    for qt in range(QT):
                        last = nc.tensor.transpose(ps[:, 4 * i, qt * P:(qt + 1) * P], xb[i][:, qt, :], chip.ident[:, :])
                    last.then_inc(*pe.end(f"xT{i}"))
                for i in range(PAIR):
                    eng.wait_ge(*dve.done(f"xT{i}", b))
                    for qt in range(QT):
                        out = ps[:, 4 * i + 1, qt * E:(qt + 1) * E]
                        nc.tensor.matmul(out, xT[i][:, qt * P:(qt + 1) * P], w["L0_ffn_Wg"], start=True, stop=False)
                        last = nc.tensor.matmul(out, chip.ones[0:1, 0:P], w["L0_ffn_bg"], start=False, stop=True)
                    last.then_inc(*pe.end(f"logits{i}"))
                for i in range(PAIR):
                    eng.wait_ge(*dve.done(f"shift{i}", b))
                    for qt in range(QT):
                        for a in range(2):
                            out = ps[:, 4 * i + 2 * qt + a, :]
                            nc.tensor.matmul(out, xT[i][:, qt * P:(qt + 1) * P],
                                             w["L0_ffn_We"][:, 4 * a:4 * a + 4, :].rearrange("p e d -> p (e d)"), start=True, stop=False)
                            last = nc.tensor.matmul(out, chip.ones[0:1, 0:P], w["L0_ffn_be"][:, 512 * a:512 * a + 512],
                                                    start=False, stop=True)
                    last.then_inc(*pe.end(f"experts{i}"))


def l1_xattn(nc, chip):
    with ExitStack() as ctx:
        sb = lambda n, s: [ctx.enter_context(nc.sbuf_tensor(f"l1x_{n}{i}", s, F32)) for i in range(PAIR)]
        pe_s, dve_s, act_s, pool_s, ready = stage_sems(nc, ctx, "l1x")
        t = [Tail(nc, ctx, f"l1x{i}") for i in range(PAIR)]
        xb, xT, cT = sb("xb", [P, QT, D]), sb("xT", [P, S]), sb("cT", [P, S2])
        qT, kT, v = sb("qT", [P, S]), sb("kT", [P, S2]), sb("v", [P, CT, D])
        nm, den, rden = sb("nm", [P, QT]), sb("den", [P, QT]), sb("rden", [P, QT])
        pr, prT, out_sb = sb("pr", [P, QT, S2]), sb("prT", [P, QT, CT, P]), sb("out", [P, QT, D])
        ps, w = chip.ps, chip.w
        pe = Steps(pe_s, paired(["xT", "kv", "q", "s", "prT", "o"]))
        dve = Steps(dve_s, paired(["x", "xT", "k", "v", "q", "nm", "rden", "prT", "o"] + TAIL_DVE))
        act = Steps(act_s, paired(["exp"]))
        pool = Steps(pool_s, paired(TAIL_POOL))
        block = ctx.enter_context(nc.Block())

        @block.gpsimd
        def _(eng):
            with eng.Fori(0, B // PAIR) as b:
                tails_pool(nc, eng, chip, t, dve, pool, b)

        @block.scalar
        def _(eng):
            with eng.Fori(0, B // PAIR) as b:
                for i in range(PAIR):
                    eng.wait_ge(*dve.done(f"nm{i}", b))
                    for qt in range(QT):
                        last = nc.scalar.activation(pr[i][:, qt, :], ps[:, 4 * i + 2 + qt, :], ACT.Exp, bias=nm[i][:, qt:qt + 1],
                                                    accum_out=den[i][:, qt:qt + 1])
                    last.then_inc(*act.end(f"exp{i}"))

        @block.vector
        def _(eng):
            with eng.Fori(0, B // PAIR) as b:
                for i in range(PAIR):
                    nc.vector.tensor_copy(fp(xb[i]), chip.x_tok[:, PAIR * b + i, :, :])
                    nc.vector.tensor_copy(fp(cT[i]), chip.ctxT[:, PAIR * b + i, :]).then_inc(*dve.end(f"x{i}"))
                for i in range(PAIR):
                    eng.wait_ge(*pe.done(f"xT{i}", b))
                    nc.vector.tensor_copy(fp(xT[i]), ps[:, 4 * i, 0:S]).then_inc(*dve.end(f"xT{i}"))
                for i in range(PAIR):
                    eng.wait_ge(*pe.done(f"kv{i}", b))
                    nc.vector.tensor_scalar(fp(kT[i]), ps[:, 4 * i + 1, :], w["L1_xattn_Wk_b"], None, ALU.add).then_inc(*dve.end(f"k{i}"))
                for i in range(PAIR):
                    nc.vector.tensor_copy(fp(v[i]), ps[:, 4 * i + 2, :].rearrange("p (t d) -> p t d", t=CT)).then_inc(*dve.end(f"v{i}"))
                for i in range(PAIR):
                    eng.wait_ge(*pe.done(f"q{i}", b))
                    nc.vector.tensor_scalar(fp(qT[i]), ps[:, 4 * i, S:2 * S], w["L1_xattn_Wq_b"], float(np.float32(1) / np.sqrt(np.float32(D))),
                                            ALU.add, ALU.mult).then_inc(*dve.end(f"q{i}"))
                for i in range(PAIR):
                    eng.wait_ge(*pe.done(f"s{i}", b))
                    nc.vector.tensor_reduce(fp(nm[i]), ps[:, 4 * i + 2:4 * i + 4, :], AX.X, ALU.max, negate=True).then_inc(*dve.end(f"nm{i}"))
                for i in range(PAIR):
                    eng.wait_ge(*act.done(f"exp{i}", b))
                    nc.vector.reciprocal(fp(rden[i]), fp(den[i])).then_inc(*dve.end(f"rden{i}"))
                for i in range(PAIR):
                    eng.wait_ge(*pe.done(f"prT{i}", b))
                    for qt in range(QT):
                        last = nc.vector.tensor_copy(prT[i][:, qt, :, :], ps[:, 4 * i + qt, :].rearrange("p (t q) -> p t q", t=CT))
                    last.then_inc(*dve.end(f"prT{i}"))
                for i in range(PAIR):
                    eng.wait_ge(*pe.done(f"o{i}", b))
                    eng.wait_ge(*dve.done(f"rden{i}", b))
                    for qt in range(QT):
                        last = nc.vector.tensor_scalar(out_sb[i][:, qt, :], ps[:, 4 * i + 2, qt * P:(qt + 1) * P], rden[i][:, qt:qt + 1], None, ALU.mult)
                    last.then_inc(*dve.end(f"o{i}"))
                tails_dve(nc, eng, chip, t, dve, pool, b, lambda i: dve.done(f"o{i}", b),
                          lambda i: fp(out_sb[i]), lambda i: fp(xb[i]))

        @block.tensor
        def _(eng):
            with eng.Fori(0, B // PAIR) as b:
                for i in range(PAIR):
                    eng.wait_ge(*dve.done(f"x{i}", b))
                    for qt in range(QT):
                        last = nc.tensor.transpose(ps[:, 4 * i, qt * P:(qt + 1) * P], xb[i][:, qt, :], chip.ident[:, :])
                    last.then_inc(*pe.end(f"xT{i}"))
                for i in range(PAIR):
                    nc.tensor.matmul(ps[:, 4 * i + 1, :], w["L1_xattn_Wk_w"][:, 0, :], fp(cT[i]), start=True, stop=True)
                    for kt in range(CT):
                        out = ps[:, 4 * i + 2, kt * P:(kt + 1) * P]
                        nc.tensor.matmul(out, cT[i][:, kt * P:(kt + 1) * P], w["L1_xattn_Wv_w"][:, 0, :], start=True, stop=False)
                        last = nc.tensor.matmul(out, chip.ones[0:1, 0:P], w["L1_xattn_Wv_b"], start=False, stop=True)
                    last.then_inc(*pe.end(f"kv{i}"))
                for i in range(PAIR):
                    eng.wait_ge(*dve.done(f"xT{i}", b))
                    nc.tensor.matmul(ps[:, 4 * i, S:2 * S], w["L1_xattn_Wq_w"][:, 0, :], fp(xT[i]), start=True, stop=True).then_inc(*pe.end(f"q{i}"))
                for i in range(PAIR):
                    eng.wait_ge(*dve.done(f"q{i}", b))
                    for qt in range(QT):
                        last = nc.tensor.matmul(ps[:, 4 * i + 2 + qt, :], qT[i][:, qt * P:(qt + 1) * P], fp(kT[i]), start=True, stop=True)
                    last.then_inc(*pe.end(f"s{i}"))
                for i in range(PAIR):
                    eng.wait_ge(*act.done(f"exp{i}", b))
                    for qt in range(QT):
                        for kt in range(CT):
                            last = nc.tensor.transpose(ps[:, 4 * i + qt, kt * P:(kt + 1) * P], pr[i][:, qt, kt * P:(kt + 1) * P], chip.ident[:, :])
                    last.then_inc(*pe.end(f"prT{i}"))
                for i in range(PAIR):
                    eng.wait_ge(*dve.done(f"prT{i}", b))
                    for qt in range(QT):
                        for kt in range(CT):
                            last = nc.tensor.matmul(ps[:, 4 * i + 2, qt * P:(qt + 1) * P], prT[i][:, qt, kt, :], v[i][:, kt, :],
                                                    start=(kt == 0), stop=(kt == CT - 1))
                    last.then_inc(*pe.end(f"o{i}"))


def l2_xattn(nc, chip):
    with ExitStack() as ctx:
        sb = lambda n, s: [ctx.enter_context(nc.sbuf_tensor(f"l2x_{n}{i}", s, F32)) for i in range(PAIR)]
        pe_s, dve_s, act_s, pool_s, ready = stage_sems(nc, ctx, "l2x")
        t = [Tail(nc, ctx, f"l2x{i}") for i in range(PAIR)]
        xb, xT, cT, cb = sb("xb", [P, QT, D]), sb("xT", [P, S]), sb("cT", [P, S2]), sb("cb", [P, CT, D])
        xw, bsum = sb("xw", [P, S]), sb("bsum", [P, 1])
        nm, den, rden, top = sb("nm", [P, QT]), sb("den", [P, QT]), sb("rden", [P, QT]), sb("top", [P, QT])
        pr, prT = sb("pr", [P, QT, S2]), sb("prT", [P, CT, QT, P])
        att, xatt, xq = sb("att", [P, S]), sb("xatt", [P, S]), sb("xq", [P, S])
        rowmax, rowden, row = sb("rowmax", [1, 1]), sb("rowden", [1, 2]), sb("row", [1, S])
        col, q2c = sb("col", [P, QT]), sb("q2c", [P, 1])
        ps, w = chip.ps, chip.w
        pe = Steps(pe_s, paired(["xT", "s", "toprow", "prT", "att", "col", "q2c", "z"]))
        dve = Steps(dve_s, paired(["bsum1", "x", "xT", "xw", "nm", "top", "rowmax", "rden", "norm", "prT", "att", "xatt",
                            "rowden", "rown", "col", "q2c", "xq"] + TAIL_DVE))
        act = Steps(act_s, paired(["exp", "rowexp"]))
        pool = Steps(pool_s, paired(TAIL_POOL))
        block = ctx.enter_context(nc.Block())

        @block.gpsimd
        def _(eng):
            with eng.Fori(0, B // PAIR) as b:
                tails_pool(nc, eng, chip, t, dve, pool, b)

        @block.scalar
        def _(eng):
            with eng.Fori(0, B // PAIR) as b:
                for i in range(PAIR):
                    eng.wait_ge(*dve.done(f"nm{i}", b))
                    for qt in range(QT):
                        last = nc.scalar.activation(pr[i][:, qt, :], ps[:, 4 * i + 2 + qt, :], ACT.Exp, bias=nm[i][:, qt:qt + 1],
                                                    accum_out=den[i][:, qt:qt + 1])
                    last.then_inc(*act.end(f"exp{i}"))
                for i in range(PAIR):
                    eng.wait_ge(*dve.done(f"rowmax{i}", b))
                    nc.scalar.activation(fp(row[i]), ps[0:1, 4 * i, 0:S], ACT.Exp, bias=fp(rowmax[i]), accum_out=rowden[i][:, 0:1])\
                        .then_inc(*act.end(f"rowexp{i}"))

        @block.vector
        def _(eng):
            with eng.Fori(0, B // PAIR) as b:
                for i in range(PAIR):
                    nc.vector.tensor_copy(fp(xb[i]), chip.x_tok[:, PAIR * b + i, :, :])
                    nc.vector.tensor_copy(fp(cb[i]), chip.ctx_tok[:, PAIR * b + i, :, :])
                    nc.vector.tensor_copy(fp(cT[i]), chip.ctxT[:, PAIR * b + i, :])
                    nc.vector.tensor_tensor(fp(bsum[i]), w["L2_xattn_b_c"], w["L2_xattn_b_q"], ALU.add).then_inc(*dve.end(f"bsum1{i}"))
                for i in range(PAIR):
                    eng.wait_ge(*dve.done(f"bsum1{i}", b))
                    nc.vector.tensor_tensor(fp(bsum[i]), fp(bsum[i]), w["L2_xattn_b_cq"], ALU.add).then_inc(*dve.end(f"x{i}"))
                for i in range(PAIR):
                    eng.wait_ge(*pe.done(f"xT{i}", b))
                    nc.vector.tensor_copy(fp(xT[i]), ps[:, 4 * i, 0:S]).then_inc(*dve.end(f"xT{i}"))
                for i in range(PAIR):
                    nc.vector.tensor_scalar(fp(xw[i]), ps[:, 4 * i, 0:S], w["L2_xattn_w_cq"], w["L2_xattn_w_q"], ALU.mult, ALU.add)\
                        .then_inc(*dve.end(f"xw{i}"))
                for i in range(PAIR):
                    eng.wait_ge(*pe.done(f"s{i}", b))
                    nc.vector.tensor_reduce(fp(nm[i]), ps[:, 4 * i + 2:4 * i + 4, :], AX.X, ALU.max, negate=True).then_inc(*dve.end(f"nm{i}"))
                for i in range(PAIR):
                    eng.wait_ge(*dve.done(f"nm{i}", b))
                    eng.wait_ge(*dve.done(f"x{i}", b))
                    nc.vector.scalar_tensor_tensor(fp(top[i]), ps[:, 4 * i + 1, 0:QT], bsum[i][:, 0:1], fp(nm[i]), ALU.add, ALU.subtract)\
                        .then_inc(*dve.end(f"top{i}"))
                for i in range(PAIR):
                    eng.wait_ge(*pe.done(f"toprow{i}", b))
                    nc.vector.tensor_reduce(fp(rowmax[i]), ps[0:1, 4 * i, 0:S], AX.X, ALU.max, negate=True).then_inc(*dve.end(f"rowmax{i}"))
                for i in range(PAIR):
                    eng.wait_ge(*act.done(f"exp{i}", b))
                    nc.vector.reciprocal(fp(rden[i]), fp(den[i])).then_inc(*dve.end(f"rden{i}"))
                for i in range(PAIR):
                    eng.wait_ge(*dve.done(f"rden{i}", b))
                    for qt in range(QT):
                        last = nc.vector.tensor_scalar(pr[i][:, qt, :], pr[i][:, qt, :], rden[i][:, qt:qt + 1], None, ALU.mult)
                    last.then_inc(*dve.end(f"norm{i}"))
                for i in range(PAIR):
                    eng.wait_ge(*pe.done(f"prT{i}", b))
                    for qt in range(QT):
                        last = nc.vector.tensor_copy(prT[i][:, :, qt, :], ps[:, 4 * i + 2 + qt, :].rearrange("p (t q) -> p t q", t=CT))
                    last.then_inc(*dve.end(f"prT{i}"))
                for i in range(PAIR):
                    eng.wait_ge(*pe.done(f"att{i}", b))
                    nc.vector.tensor_copy(fp(att[i]), ps[:, 4 * i + 1, 0:S]).then_inc(*dve.end(f"att{i}"))
                for i in range(PAIR):
                    nc.vector.tensor_tensor(fp(xatt[i]), ps[:, 4 * i + 1, 0:S], fp(xT[i]), ALU.mult).then_inc(*dve.end(f"xatt{i}"))
                for i in range(PAIR):
                    eng.wait_ge(*act.done(f"rowexp{i}", b))
                    nc.vector.reciprocal(rowden[i][:, 1:2], rowden[i][:, 0:1]).then_inc(*dve.end(f"rowden{i}"))
                for i in range(PAIR):
                    eng.wait_ge(*dve.done(f"rowden{i}", b))
                    nc.vector.tensor_scalar(fp(row[i]), fp(row[i]), rowden[i][:, 1:2], None, ALU.mult).then_inc(*dve.end(f"rown{i}"))
                for i in range(PAIR):
                    eng.wait_ge(*pe.done(f"col{i}", b))
                    nc.vector.tensor_copy(fp(col[i]), ps[:, 4 * i + 1, S:S + QT]).then_inc(*dve.end(f"col{i}"))
                for i in range(PAIR):
                    eng.wait_ge(*pe.done(f"q2c{i}", b))
                    nc.vector.tensor_copy(fp(q2c[i]), ps[:, 4 * i + 1, S + QT:S + QT + 1]).then_inc(*dve.end(f"q2c{i}"))
                for i in range(PAIR):
                    eng.wait_ge(*dve.done(f"q2c{i}", b))
                    nc.vector.tensor_scalar(fp(xq[i]), fp(xT[i]), q2c[i][:, 0:1], None, ALU.mult).then_inc(*dve.end(f"xq{i}"))
                tails_dve(nc, eng, chip, t, dve, pool, b, lambda i: pe.done(f"z{i}", b),
                          lambda i: ps[:, 4 * i, 0:S].rearrange("p (t d) -> p t d", t=QT), lambda i: fp(xb[i]))

        @block.tensor
        def _(eng):
            with eng.Fori(0, B // PAIR) as b:
                for i in range(PAIR):
                    eng.wait_ge(*dve.done(f"x{i}", b))
                    for qt in range(QT):
                        last = nc.tensor.transpose(ps[:, 4 * i, qt * P:(qt + 1) * P], xb[i][:, qt, :], chip.ident[:, :])
                    last.then_inc(*pe.end(f"xT{i}"))
                for i in range(PAIR):
                    eng.wait_ge(*dve.done(f"xw{i}", b))
                    for qt in range(QT):
                        nc.tensor.matmul(ps[:, 4 * i + 2 + qt, :], xw[i][:, qt * P:(qt + 1) * P], fp(cT[i]), start=True, stop=True)
                        last = nc.tensor.matmul(ps[:, 4 * i + 1, qt:qt + 1], xT[i][:, qt * P:(qt + 1) * P], w["L2_xattn_w_c"], start=True, stop=True)
                    last.then_inc(*pe.end(f"s{i}"))
                for i in range(PAIR):
                    eng.wait_ge(*dve.done(f"top{i}", b))
                    for qt in range(QT):
                        last = nc.tensor.transpose(ps[0:1, 4 * i, qt * P:(qt + 1) * P], top[i][:, qt:qt + 1], chip.ident[:, :])
                    last.then_inc(*pe.end(f"toprow{i}"))
                for i in range(PAIR):
                    eng.wait_ge(*dve.done(f"norm{i}", b))
                    for qt in range(QT):
                        for kt in range(CT):
                            last = nc.tensor.transpose(ps[:, 4 * i + 2 + qt, kt * P:(kt + 1) * P], pr[i][:, qt, kt * P:(kt + 1) * P], chip.ident[:, :])
                    last.then_inc(*pe.end(f"prT{i}"))
                for i in range(PAIR):
                    eng.wait_ge(*dve.done(f"prT{i}", b))
                    for kt in range(CT):
                        last = nc.tensor.matmul(ps[:, 4 * i + 1, 0:S], cb[i][:, kt, :], prT[i][:, kt, :, :].rearrange("p t q -> p (t q)"),
                                                start=(kt == 0), stop=(kt == CT - 1))
                    last.then_inc(*pe.end(f"att{i}"))
                for i in range(PAIR):
                    eng.wait_ge(*dve.done(f"rown{i}", b))
                    for qt in range(QT):
                        last = nc.tensor.matmul(ps[:, 4 * i + 1, S + qt:S + qt + 1], row[i][:, qt * P:(qt + 1) * P], chip.ones[0:1, 0:1], start=True, stop=True)
                    last.then_inc(*pe.end(f"col{i}"))
                for i in range(PAIR):
                    eng.wait_ge(*dve.done(f"col{i}", b))
                    for qt in range(QT):
                        last = nc.tensor.matmul(ps[:, 4 * i + 1, S + QT:S + QT + 1], xb[i][:, qt, :], col[i][:, qt:qt + 1], start=(qt == 0), stop=(qt == QT - 1))
                    last.then_inc(*pe.end(f"q2c{i}"))
                for i in range(PAIR):
                    eng.wait_ge(*dve.done(f"xq{i}", b))
                    for qt in range(QT):
                        out = ps[:, 4 * i, qt * P:(qt + 1) * P]
                        for c, part in enumerate((xT[i], att[i], xatt[i], xq[i])):
                            nc.tensor.matmul(out, part[:, qt * P:(qt + 1) * P], w["L2_xattn_W_l"][:, c, :], start=(c == 0), stop=False)
                        last = nc.tensor.matmul(out, chip.ones[0:1, 0:P], w["L2_xattn_b_l"], start=False, stop=True)
                    last.then_inc(*pe.end(f"z{i}"))


def l0_xattn(nc, chip):
    H, DH, NK = 8, 64, S2 + S
    KT = NK // P
    with ExitStack() as ctx:
        sb = lambda n, s, dt=F32: ctx.enter_context(nc.sbuf_tensor(f"l0x_{n}", s, dt))
        pe_s, dve_s, act_s, pool_s, ready = stage_sems(nc, ctx, "l0x")
        t = Tail(nc, ctx, "l0x")
        xb = sb("xb", [P, QT, D])
        z = sb("z", [P, KT, D])
        zs, zmv, zr = sb("zs", [P, KT, 6]), sb("zmv", [P, KT, 2]), sb("zr", [P, KT])
        kvT = sb("kvT", [P, NK])
        qT, kT = sb("qT", [P, H, S]), sb("kT", [P, H, NK])
        v = sb("v", [P, KT, H, P])
        nm, e = sb("nm", [P, QT, H, P]), sb("e", [P, 4, 512])
        rec, attT = sb("rec", [P, 2, S]), sb("attT", [P, H // 2, S])
        mask_rows, rows = sb("mask_rows", [2, B, NK]), sb("rows", [2, NK])
        mask_u8 = sb("mask_u8", [1, B, S2], U8)
        ys, ymv, yr = sb("ys", [P, QT, 6]), sb("ymv", [P, QT, 2]), sb("yr", [P, QT])
        y, yn = sb("yo", [P, QT, D]), sb("yn", [P, QT, D])
        ps, w = chip.ps, chip.w
        wq, wkv = w["L0_xattn_w_q"], w["L0_xattn_w_kv"]
        masked, padded = ctx.enter_context(nc.semaphore("l0x_mask_rows")), ctx.enter_context(nc.semaphore("l0x_padded"))
        units = [(h, kp) for h in range(H) for kp in range(KT // 2)]
        names = []
        for u in range(len(units) + 1):
            names += ([f"sT{u}"] if u < len(units) else []) + ([f"pv{u - 1}"] if u else [])
        pe = Steps(pe_s, ["zT", "rows", "q"] + [f"k{h}" for h in range(H)] + [f"v{i}" for i in range(KT)]
                   + [f"s{h}" for h in range(H)] + ["nmT0", "nmT1"] + names + ["y"])
        dve = Steps(dve_s, ["kvT", "qrows", "q"] + [f"k{h}" for h in range(0, H, 2)]
                    + [f"v{i}" for i in range(0, KT, 2)] + [f"max{h}" for h in range(H)] + ["guarded0", "guarded1"]
                    + [f"{s}{h}" for h in range(H) for s in ("rec", "att")]
                    + ["y"])
        act = Steps(act_s, ["rows"] + [f"k{h}" for h in range(1, H, 2)] + [f"v{i}" for i in range(1, KT, 2)]
                    + [f"exp{u}" for u in range(len(units))])
        sem = lambda n: ctx.enter_context(nc.semaphore(f"l0x_{n}"))
        open_dve, open_pool = Steps(sem("dve_open_steps"), ["x", "zstats", "zvar", "zn", "rows"]), Steps(sem("pool_open_steps"), ["zeps", "zr"])
        close_dve = Steps(sem("dve_close_steps"), ["ystats", "yvar", "yn", "yg", "yb"] + TAIL_DVE)
        close_pool = Steps(pool_s, ["yeps", "yr"] + TAIL_POOL)
        kd = lambda h: dve.done if h % 2 == 0 else act.done
        block = ctx.enter_context(nc.Block())

        @block.sync
        def _(sp):
            sp.dma_start(fp(mask_u8), chip.a["mask_BxS2_bf1"].rearrange("(o b) k -> o b k", o=1)).then_inc(ready, 16)
            sp.wait_ge(ready, 16)

        @block.gpsimd
        def _(eng):

            def opening(b):
                eng.wait_ge(*open_dve.done("zvar", b))
                nc.gpsimd.tensor_tensor(fp(zr), zmv[:, :, 1], chip.eps[:, 0:KT], ALU.add).then_inc(*open_pool.end("zeps"))
                eng.wait_ge(*open_pool.done("zeps", b))
                nc.gpsimd.tensor_tensor(fp(zr), fp(zr), chip.neghalf[:, 0:KT], ALU.pow).then_inc(*open_pool.end("zr"))

            def closing(b):
                eng.wait_ge(*close_dve.done("yvar", b))
                nc.gpsimd.tensor_tensor(fp(yr), ymv[:, :, 1], chip.eps[:, 0:QT], ALU.add).then_inc(*close_pool.end("yeps"))
                eng.wait_ge(*close_pool.done("yeps", b))
                nc.gpsimd.tensor_tensor(fp(yr), fp(yr), chip.neghalf[:, 0:QT], ALU.pow).then_inc(*close_pool.end("yr"))
                tail_pool(nc, eng, chip, t, close_dve, close_pool, b)

            opening(0)
            nc.gpsimd.memset(fp(nm), 0.0)
            nc.gpsimd.memset(v[:, :, 0:H:2, DH:P], 1.0)
            nc.gpsimd.memset(v[:, :, 1:H:2, 0:DH], 1.0).then_inc(padded, 1)
            opening(1)
            with eng.Fori(1, B - 1) as b:
                closing(b - 1)
                opening(b + 1)
            closing(B - 2)
            closing(B - 1)

        @block.vector
        def _(eng):
            def opened(b):
                nc.vector.tensor_copy(z[:, CT:KT, :], chip.x_tok[:, b, :, :])
                nc.vector.tensor_copy(z[:, 0:CT, :], chip.ctx_tok[:, b, :, :]).then_inc(*open_dve.end("x"))
                eng.wait_ge(*open_dve.done("x", b))
                for i in range(KT):
                    last = nc.vector.bn_stats(zs[:, i, :], z[:, i, :])
                last.then_inc(*open_dve.end("zstats"))

            def variances(b):
                eng.wait_ge(*open_dve.done("zstats", b))
                nc.vector.memset(chip.scratch[:, 2:3], 0.0)
                for i in range(KT):
                    last = nc.vector.bn_aggr(zmv[:, i, :], zs[:, i, :])
                last.then_inc(*open_dve.end("zvar"))

            def normed(b):
                eng.wait_ge(*open_pool.done("zr", b))
                for i in range(KT):
                    last = nc.vector.tensor_scalar(z[:, i, :], z[:, i, :], zmv[:, i, 0:1], zr[:, i:i + 1], ALU.subtract, ALU.mult)
                last.then_inc(*open_dve.end("zn"))

            def row_of_masks(b):
                nc.vector.tensor_copy(fp(rows), mask_rows[:, b, :]).then_inc(*open_dve.end("rows"))

            wide_const = lambda heads: w["c_qrows"][DH:P, :].unsqueeze(1).to_broadcast([P - DH, heads, S])

            def start(b):
                eng.wait_ge(*pe.done("zT", b))
                nc.vector.tensor_scalar(kvT[:, 0:S2], ps[:, 0, :], w["L0_xattn_g_x"], w["L0_xattn_b_x"], ALU.mult, ALU.add)
                nc.vector.tensor_scalar(kvT[:, S2:NK], ps[:, 1, 0:S], w["L0_xattn_g_l"], w["L0_xattn_b_l"], ALU.mult, ALU.add)\
                    .then_inc(*dve.end("kvT"))
                nc.vector.tensor_copy(qT[DH:P, :, :], wide_const(H)).then_inc(*dve.end("qrows"))
                eng.wait_ge(padded, 1)
                eng.wait_ge(*pe.done("q", b))
                nc.vector.tensor_scalar(qT[0:DH, :, :], ps[0:DH, 4:8, :].rearrange("p a (h q) -> p (a h) q", q=S),
                                        DH ** -0.5, None, ALU.mult).then_inc(*dve.end("q"))

            def close_stats(b):
                nc.vector.tensor_copy(fp(xb), chip.x_tok[:, b, :, :])
                eng.wait_ge(*dve.done("y", b))
                for q in range(QT):
                    last = nc.vector.bn_stats(ys[:, q, :], y[:, q, :])
                last.then_inc(*close_dve.end("ystats"))
                eng.wait_ge(*close_dve.done("ystats", b))
                nc.vector.memset(chip.scratch[:, 3:4], 0.0)
                for q in range(QT):
                    last = nc.vector.bn_aggr(ymv[:, q, :], ys[:, q, :])
                last.then_inc(*close_dve.end("yvar"))

            def close_norm(b):
                eng.wait_ge(*close_pool.done("yr", b))
                for q in range(QT):
                    last = nc.vector.tensor_scalar(yn[:, q, :], y[:, q, :], ymv[:, q, 0:1], yr[:, q:q + 1],
                                                   ALU.subtract, ALU.mult)
                last.then_inc(*close_dve.end("yn"))

            def close_gain(b):
                eng.wait_ge(*close_dve.done("yn", b))
                nc.vector.tensor_tensor(fp(yn), fp(yn), w["L0_xattn_g_o"].unsqueeze(1).to_broadcast([P, QT, D]), ALU.mult)\
                    .then_inc(*close_dve.end("yg"))

            def close_offset(b):
                eng.wait_ge(*close_dve.done("yg", b))
                nc.vector.tensor_tensor(fp(yn), fp(yn), w["L0_xattn_b_o"].unsqueeze(1).to_broadcast([P, QT, D]), ALU.add)\
                    .then_inc(*close_dve.end("yb"))

            def attend(b, before, ahead):
                for h in range(0, H, 2):
                    eng.wait_ge(*pe.done(f"k{h}", b))
                    nc.vector.tensor_copy(kT[0:DH, h, :], ps[0:DH, 0:2, :].rearrange("p a k -> p (a k)")[:, 0:NK])\
                        .then_inc(*dve.end(f"k{h}"))
                for i in range(0, KT, 2):
                    eng.wait_ge(*pe.done(f"v{i}", b))
                    src = ps[:, 4 + i % 4, :].rearrange("p (h d) -> p h d", d=DH)
                    nc.vector.tensor_copy(v[:, i, 0:H:2, 0:DH], src[:, 0:H:2, :])
                    nc.vector.tensor_copy(v[:, i, 1:H:2, DH:P], src[:, 1:H:2, :]).then_inc(*dve.end(f"v{i}"))
                for h in range(H):
                    eng.wait_ge(*pe.done(f"s{h}", b))
                    bank = 4 * (h % 2)
                    nc.vector.tensor_reduce(nm[:, :, h, DH], ps[:, bank:bank + 4, :].rearrange("p (q a) k -> p q (a k)", a=2)[:, :, 0:NK],
                                            AX.X, ALU.max, negate=True).then_inc(*dve.end(f"max{h}"))
                    if before:
                        for at, part in ((0, close_stats), (2, close_norm), (3, close_gain), (4, close_offset)):
                            if h == at:
                                part(b - 1)
                for n in range(2):
                    heads = slice(n * H // 2, (n + 1) * H // 2)
                    eng.wait_ge(*pe.done(f"nmT{n}", b))
                    nc.vector.tensor_tensor(qT[DH:P, heads, :], ps[DH:P, 2 * n:2 * n + 2, :].rearrange("p a (h q) -> p (a h) q", q=S),
                                            wide_const(H // 2), ALU.add).then_inc(*dve.end(f"guarded{n}"))
                if before:
                    eng.wait_ge(*close_dve.done("yb", b - 1))
                    tail_dve(nc, eng, chip, t, close_dve, close_pool, b - 1, fp(yn), fp(xb))
                for h in range(H):
                    eng.wait_ge(*pe.done(f"pv{(KT // 2) * h + KT // 2 - 1}", b))
                    dims, den = (slice(0, DH), slice(DH, P)) if h % 2 == 0 else (slice(DH, P), slice(0, DH))
                    nc.vector.reciprocal(rec[dims, h % 2, :], ps[den, 4 + h % 2, 0:S]).then_inc(*dve.end(f"rec{h}"))
                    eng.wait_ge(*dve.done(f"rec{h}", b))
                    nc.vector.tensor_tensor(attT[dims, h // 2, :], ps[dims, 4 + h % 2, 0:S], rec[dims, h % 2, :], ALU.mult)\
                        .then_inc(*dve.end(f"att{h}"))
                    if ahead:
                        for at, part in ((1, opened), (2, variances), (3, normed), (4, row_of_masks)):
                            if h == at:
                                part(b + 1)
                eng.wait_ge(*pe.done("y", b))
                nc.vector.tensor_copy(fp(y), ps[:, 6:6 + QT, 0:D]).then_inc(*dve.end("y"))

            opened(0)
            variances(0)
            nc.vector.memset(fp(mask_rows), 1.0).then_inc(masked, 1)
            eng.wait_ge(masked, 1)
            nc.vector.memset(mask_rows[0:1, :, S2:NK], 0.0)
            eng.wait_ge(ready, 16)
            nc.vector.tensor_scalar(mask_rows[0:1, :, 0:S2], fp(mask_u8), 0, MASKED, ALU.is_equal, ALU.mult).then_inc(masked, 1)
            eng.wait_ge(masked, 2)
            normed(0)
            row_of_masks(0)
            start(0)
            attend(0, False, True)
            with eng.Fori(1, B - 1) as b:
                start(b)
                attend(b, True, True)
            start(B - 1)
            attend(B - 1, True, False)
            for part in (close_stats, close_norm, close_gain, close_offset):
                part(B - 1)
            eng.wait_ge(*close_dve.done("yb", B - 1))
            tail_dve(nc, eng, chip, t, close_dve, close_pool, B - 1, fp(yn), fp(xb))

        @block.scalar
        def _(eng):
            with eng.Fori(0, B) as b:
                eng.wait_ge(*pe.done("rows", b))
                nc.scalar.activation(kT[DH:P, :, :], ps[DH:P, 2:4, :].rearrange("p a k -> p (a k)")[:, 0:NK].unsqueeze(1)
                                     .to_broadcast([P - DH, H, NK]), ACT.Copy).then_inc(*act.end("rows"))
                for h in range(1, H, 2):
                    eng.wait_ge(*pe.done(f"k{h}", b))
                    nc.scalar.activation(kT[0:DH, h, :], ps[0:DH, 2:4, :].rearrange("p a k -> p (a k)")[:, 0:NK], ACT.Copy)\
                        .then_inc(*act.end(f"k{h}"))
                for i in range(1, KT, 2):
                    eng.wait_ge(*pe.done(f"v{i}", b))
                    src = ps[:, 4 + i % 4, :].rearrange("p (h d) -> p h d", d=DH)
                    nc.scalar.activation(v[:, i, 0:H:2, 0:DH], src[:, 0:H:2, :], ACT.Copy)
                    nc.scalar.activation(v[:, i, 1:H:2, DH:P], src[:, 1:H:2, :], ACT.Copy).then_inc(*act.end(f"v{i}"))
                for u in range(len(units)):
                    eng.wait_ge(*pe.done(f"sT{u}", b))
                    if u >= 4:
                        eng.wait_ge(*pe.done(f"pv{u - 4}", b))
                    nc.scalar.activation(e[:, u % 4, :], ps[:, u % 4, :], ACT.Exp).then_inc(*act.end(f"exp{u}"))

        @block.tensor
        def _(eng):
            with eng.Fori(0, B) as b:
                eng.wait_ge(*open_dve.done("zn", b))
                for i in range(KT):
                    last = nc.tensor.transpose(ps[:, i // 4, (i % 4) * P:(i % 4 + 1) * P], z[:, i, :], chip.ident[:, :])
                last.then_inc(*pe.end("zT"))
                eng.wait_ge(*open_dve.done("rows", b))
                nc.tensor.matmul(ps[:, 2, :], w["c_krows"], rows[:, 0:512], start=True, stop=True)
                nc.tensor.matmul(ps[:, 3, 0:S], w["c_krows"], rows[:, 512:NK], start=True, stop=True).then_inc(*pe.end("rows"))
                eng.wait_ge(*dve.done("kvT", b))
                for h in range(H):
                    last = nc.tensor.matmul(ps[0:DH, 4 + h // 2, (h % 2) * S:(h % 2 + 1) * S], wq[:, h * DH:(h + 1) * DH],
                                            kvT[:, S2:NK], start=True, stop=True)
                last.then_inc(*pe.end("q"))
                for h in range(H):
                    if h == 1:
                        eng.wait_ge(*act.done("rows", b))
                    if h >= 2:
                        eng.wait_ge(*kd(h)(f"k{h - 2}", b))
                    wk = wkv[:, h * DH:(h + 1) * DH]
                    bank = 2 * (h % 2)
                    nc.tensor.matmul(ps[0:DH, bank, :], wk, kvT[:, 0:512], start=True, stop=True)
                    nc.tensor.matmul(ps[0:DH, bank + 1, 0:S], wk, kvT[:, 512:NK], start=True, stop=True).then_inc(*pe.end(f"k{h}"))
                eng.wait_ge(*dve.done("q", b))
                for i in range(KT):
                    if i >= 4:
                        eng.wait_ge(*kd(i)(f"v{i - 4}", b))
                    nc.tensor.matmul(ps[:, 4 + i % 4, :], kvT[:, i * P:(i + 1) * P], wkv[:, 512:1024], start=True, stop=True)\
                        .then_inc(*pe.end(f"v{i}"))
                eng.wait_ge(*dve.done(f"v{KT - 2}", b))
                eng.wait_ge(*act.done(f"v{KT - 1}", b))
                for h in range(H):
                    if h >= 2:
                        eng.wait_ge(*dve.done(f"max{h - 2}", b))
                    for q in range(QT):
                        bank = 4 * (h % 2) + 2 * q
                        lhs = qT[:, h, q * P:(q + 1) * P]
                        nc.tensor.matmul(ps[:, bank, :], lhs, kT[:, h, 0:512], start=True, stop=True)
                        last = nc.tensor.matmul(ps[:, bank + 1, 0:S], lhs, kT[:, h, 512:NK], start=True, stop=True)
                    last.then_inc(*pe.end(f"s{h}"))
                for n in range(2):
                    eng.wait_ge(*dve.done(f"max{H - 2 + n}", b))
                    for h in range(n * H // 2, (n + 1) * H // 2):
                        for q in range(QT):
                            at = (h % 2) * S + q * P
                            last = nc.tensor.transpose(ps[:, h // 2, at:at + P], nm[:, q, h, :], chip.ident[:, :])
                    last.then_inc(*pe.end(f"nmT{n}"))
                eng.wait_ge(*dve.done("guarded0", b))
                for u in range(len(units) + 1):
                    if u < len(units):
                        h, kp = units[u]
                        if u == 2:
                            eng.wait_ge(*dve.done("guarded1", b))
                        if u >= 4:
                            eng.wait_ge(*act.done(f"exp{u - 4}", b))
                        for i in range(2):
                            kt = 2 * kp + i
                            last = nc.tensor.matmul(ps[:, u % 4, i * S:(i + 1) * S], kT[:, h, kt * P:(kt + 1) * P], qT[:, h, :],
                                                    start=True, stop=True)
                        last.then_inc(*pe.end(f"sT{u}"))
                    if u:
                        h, kp = units[u - 1]
                        eng.wait_ge(*act.done(f"exp{u - 1}", b))
                        if kp == 0 and h >= 2:
                            eng.wait_ge(*dve.done(f"att{h - 2}", b))
                        for i in range(2):
                            kt = 2 * kp + i
                            last = nc.tensor.matmul(ps[:, 4 + h % 2, 0:S], v[:, kt, h, :], e[:, (u - 1) % 4, i * S:(i + 1) * S],
                                                    start=(kt == 0), stop=(kt == KT - 1))
                        last.then_inc(*pe.end(f"pv{u - 1}"))
                for c in range(H // 2):
                    eng.wait_ge(*dve.done(f"att{2 * c + 1}", b))
                    for q in range(QT):
                        last = nc.tensor.matmul(ps[:, 6 + q, 0:P], attT[:, c, q * P:(q + 1) * P], w["L0_xattn_w_out"][:, c, :],
                                                start=(c == 0), stop=(c == H // 2 - 1))
                last.then_inc(*pe.end("y"))


def l2_ffn(nc, chip):
    E, F, T, TILES = 8, 512, B * S, B * QT
    C = F // P
    with ExitStack() as ctx:
        sb = lambda n, s, dt=F32: ctx.enter_context(nc.sbuf_tensor(f"l2f_{n}", s, dt))
        pe_s, dve_s, act_s, pool_s, ready = stage_sems(nc, ctx, "l2f")
        t, k = [Tail(nc, ctx, f"l2f{i}") for i in range(B)], Pick(nc, ctx, "l2f", E, TILES)
        xT = sb("xT", [P, T])
        logits, one = sb("logits", [P, TILES, E]), sb("one", [P, TILES, E])
        oneT, shut, sel = sb("oneT", [E, T]), sb("shut", [P, T], BF16), sb("sel", [P, E, P], BF16)
        w1, w2 = sb("w1", [P, 2, F]), sb("w2", [P, 2, C, D])
        b1 = sb("b1", [P, 2 * C])
        hT, yT = sb("hT", [P, 4, 512]), sb("yT", [P, T])
        ps, w = chip.ps, chip.w
        nxt = [ctx.enter_context(nc.semaphore(f"l2f_{e}")) for e in ("gate_pe", "gate_dve", "main_pe", "main_dve", "main_act",
                                                                      "end_pe", "weights0", "weights1", "bias")]
        gpe, gdve = Steps(nxt[0], ["xT", "logits", "oneT"]), Steps(nxt[1], ["xT", "logits"] + pick_steps("top") + ["oneT", "shut"])
        units = [(e, c, half) for e in range(2) for c in range(C) for half in range(2)]
        n = len(units)
        names = []
        for u in range(n + 2):
            names += ([f"h{u}"] if u < n else []) + ([f"acc{u - 2}"] if u >= 2 else [])
        mpe = Steps(nxt[2], names)
        mdve, mact = Steps(nxt[3], ["b1"] + [f"r{u}" for u in range(1, n, 2)]), Steps(nxt[4], [f"r{u}" for u in range(0, n, 2)])
        relu = lambda u: (mact if u % 2 == 0 else mdve).done
        pe, dve, pool = Steps(pe_s, [f"y{b}" for b in range(B)]), Steps(dve_s, paired(TAIL_DVE)), Steps(pool_s, paired(TAIL_POOL))
        weights = nxt[6:8]
        block = ctx.enter_context(nc.Block())

        @block.sync
        def _(sp):
            for e in range(E):
                if e >= 2:
                    sp.wait_ge(*mpe.done(f"acc{n // 2 * (e % 2 + 1) - 1}", e // 2 - 1))
                sp.dma_start(w1[:, e % 2, :], chip.a["L2_ffn_W1"][e, :, :]).then_inc(weights[e % 2], 16)
                sp.dma_start(w2[:, e % 2, :, :], chip.a["L2_ffn_W2"][e, :, :].rearrange("(c p) d -> p c d", p=P))\
                    .then_inc(weights[e % 2], 16)

        @block.gpsimd
        def _(eng):
            nc.gpsimd.memset(fp(shut), 0.0)
            nc.gpsimd.memset(fp(sel), 0.0).then_inc(ready, 1)
            for pair in range(B // PAIR):
                tails_pool(nc, eng, chip, t[PAIR * pair:], dve, pool, pair)

        @block.vector
        def _(eng):
            eng.wait_ge(ready, 1)
            nc.vector.tensor_copy(sel[0:E, :, :], w["c_sel8"]).then_inc(ready, 1)
            eng.wait_ge(*gpe.done("xT"))
            nc.vector.tensor_copy(fp(xT), ps[:, 2:4, :].rearrange("p a t -> p (a t)")).then_inc(*gdve.end("xT"))
            eng.wait_ge(*gpe.done("logits"))
            nc.vector.tensor_copy(fp(logits), ps[:, 7, 0:TILES * E].rearrange("p (t e) -> p t e", e=E)).then_inc(*gdve.end("logits"))
            eng.wait_ge(*gdve.done("logits"))
            pick_first(nc, eng, chip, k, gdve, 0, "top", fp(logits), fp(one))
            eng.wait_ge(*gpe.done("oneT"))
            oneT_ps = ps[0:E, 4:6, :].rearrange("p a t -> p (a t)")
            nc.vector.tensor_scalar(fp(oneT), oneT_ps, 1.0, None, ALU.mult).then_inc(*gdve.end("oneT"))
            nc.vector.tensor_scalar(shut[0:E, :], oneT_ps, -1.0, -MASKED, ALU.add, ALU.mult).then_inc(*gdve.end("shut"))
            with eng.Fori(0, E // 2) as i:
                nc.vector.tensor_copy(fp(b1), w["L2_ffn_b1"][:, bass.ts(i, 2 * C)]).then_inc(*mdve.end("b1"))
                eng.wait_ge(*mdve.done("b1", i))
                for u, (e, c, half) in enumerate(units):
                    if u % 2:
                        eng.wait_ge(*mpe.done(f"h{u}", i))
                        if u >= 4:
                            eng.wait_ge(*mpe.done(f"acc{u - 4}", i))
                        nc.vector.tensor_scalar(hT[:, u % 4, :], ps[:, u % 4, :], b1[:, e * C + c:e * C + c + 1], 0.0, ALU.add, ALU.max)\
                            .then_inc(*mdve.end(f"r{u}"))
                eng.wait_ge(*mdve.done(f"r{n - 1}", i))
                eng.wait_ge(*mact.done(f"r{n - 2}", i))
            eng.wait_ge(*mpe.passed(E // 2))
            eng.wait_ge(nxt[5], 1)
            nc.vector.tensor_copy(fp(yT), ps[:, 6:8, :].rearrange("p a t -> p (a t)")).then_inc(nxt[8], 1)
            for pair in range(B // PAIR):
                tails_dve(nc, eng, chip, t[PAIR * pair:], dve, pool, pair, lambda i: pe.done(f"y{PAIR * pair + i}"),
                          lambda i: ps[:, PAIR * pair + i, 0:S].rearrange("p (t d) -> p t d", t=QT), lambda i: chip.x_tok[:, PAIR * pair + i, :, :])

        @block.scalar
        def _(eng):
            with eng.Fori(0, E // 2) as i:
                eng.wait_ge(*mdve.done("b1", i))
                for u, (e, c, half) in enumerate(units):
                    if u % 2 == 0:
                        eng.wait_ge(*mpe.done(f"h{u}", i))
                        if u >= 4:
                            eng.wait_ge(*mpe.done(f"acc{u - 4}", i))
                        nc.scalar.activation(hT[:, u % 4, :], ps[:, u % 4, :], ACT.Relu, bias=b1[:, e * C + c:e * C + c + 1])\
                            .then_inc(*mact.end(f"r{u}"))

        @block.tensor
        def _(eng):
            for q in range(TILES):
                last = nc.tensor.transpose(ps[:, 2 + q // 4, q % 4 * P:(q % 4 + 1) * P], chip.x_tok[:, q // QT, q % QT, :], chip.ident[:, :])
            last.then_inc(*gpe.end("xT"))
            eng.wait_ge(*gdve.done("xT"))
            for q in range(TILES):
                out = ps[:, 7, q * E:(q + 1) * E]
                nc.tensor.matmul(out, xT[:, q * P:(q + 1) * P], w["L2_ffn_Wg"], start=True, stop=False)
                last = nc.tensor.matmul(out, chip.ones[0:1, 0:P], w["L2_ffn_bg"], start=False, stop=True)
            last.then_inc(*gpe.end("logits"))
            eng.wait_ge(*gdve.done("toppick"))
            for q in range(TILES):
                last = nc.tensor.transpose(ps[0:E, 4 + q // 4, q % 4 * P:(q % 4 + 1) * P], one[:, q, :], chip.ident[:, :])
            last.then_inc(*gpe.end("oneT"))
            eng.wait_ge(*gdve.done("shut"))
            eng.wait_ge(ready, 2)
            for half in range(2):
                nc.tensor.matmul(ps[:, 6 + half, :], w["L2_ffn_b2"], oneT[:, half * 512:(half + 1) * 512], start=True, stop=False)
            with eng.Fori(0, E // 2) as i:
                for u in range(n + 2):
                    if u < n:
                        e, c, half = units[u]
                        if u % (n // 2) == 0:
                            eng.wait_ge(weights[e], i * 32 + 32)
                        if u >= 4:
                            eng.wait_ge(*relu(u)(f"r{u - 4}", i))
                        cols = slice(half * 512, (half + 1) * 512)
                        nc.tensor.matmul(ps[:, u % 4, :], w1[:, e, c * P:(c + 1) * P], xT[:, cols], start=True, stop=False)
                        nc.tensor.matmul(ps[:, u % 4, :], sel[:, i * 2 + e, :], shut[:, cols], start=False, stop=True)\
                            .then_inc(*mpe.end(f"h{u}"))
                    if u >= 2:
                        e, c, half = units[u - 2]
                        eng.wait_ge(*relu(u)(f"r{u - 2}", i))
                        nc.tensor.matmul(ps[:, 6 + half, :], w2[:, e, c, :], hT[:, (u - 2) % 4, :], start=False, stop=False)\
                            .then_inc(*mpe.end(f"acc{u - 2}"))
            for half in range(2):
                last = nc.tensor.matmul(ps[:, 6 + half, :], chip.zeros[0:1, 0:P], chip.ones[0:1, 0:512], start=False, stop=True)
            last.then_inc(nxt[5], 1)
            eng.wait_ge(nxt[8], 1)
            for b in range(B):
                for qt in range(QT):
                    last = nc.tensor.transpose(ps[:, b, qt * P:(qt + 1) * P], yT[:, b * S + qt * P:b * S + (qt + 1) * P], chip.ident[:, :])
                last.then_inc(*pe.end(f"y{b}"))


def l3_ffn(nc, chip):
    E, F, T, TILES = 7, 512, B * S, B * QT
    C = F // P
    CAPACITY = -(-5 * T * 2 // (4 * E))
    with ExitStack() as ctx:
        sb = lambda n, s, dt=F32: ctx.enter_context(nc.sbuf_tensor(f"l3f_{n}", s, dt))
        pe_s, dve_s, act_s, pool_s, ready = stage_sems(nc, ctx, "l3f")
        t, k = [Tail(nc, ctx, f"l3f{i}") for i in range(B)], Pick(nc, ctx, "l3f", E, TILES)
        z = sb("z", [P, TILES, D])
        zs, zmv, zr = sb("zs", [P, TILES, 6]), sb("zmv", [P, TILES, 2]), sb("zr", [P, TILES])
        hT = sb("hT", [P, T])
        lg, two = sb("lg", [P, TILES, E]), sb("two", [P, TILES, E])
        m1, ex, den = sb("m1", [P, TILES]), sb("ex", [P, TILES]), sb("den", [P, TILES])
        picks, gates = sb("picks", [P, 2 * TILES, E]), sb("gates", [P, 2, TILES])
        offs, keep = sb("offs", [P, 2 * TILES, E]), sb("keep", [P, 2 * TILES, E])
        weight, weightT = sb("weight", [P, TILES, 8]), sb("weightT", [8, T])
        mine, hg = sb("mine", [8, 2, T]), sb("hg", [P, 2, T])
        w1, w3, w2 = sb("w1", [P, 2, F]), sb("w3", [P, 2, F]), sb("w2", [P, 2, C, D])
        act1, mid = sb("act1", [P, 2, 512]), sb("mid", [P, 2, 512])
        yT = sb("yT", [P, T])
        ps, w = chip.ps, chip.w
        sem = lambda n: ctx.enter_context(nc.semaphore(f"l3f_{n}"))
        weights = [sem("weights0"), sem("weights1")]
        closed, copied = sem("closed"), sem("copied")
        rpe = Steps(sem("route_pe"), ["zT", "logits"])
        rdve = Steps(sem("route_dve"), ["stats", "var", "z", "hT", "logits"] + pick_steps("first") + ["m1", "rest"]
                     + pick_steps("second") + ["gap", "den", "gate1", "gates"])
        ract, rpool = Steps(sem("route_act"), ["exp"]), Steps(sem("route_pool"), ["eps", "rstd"])
        cpe = Steps(sem("count_pe"), ["counts", "weightT"])
        cdve = Steps(sem("count_dve"), ["shared", "off0"] + [f"off{i}" for i in range(1, 2 * TILES)]
                     + ["pos", "keep", "kept", "weighed", "weight", "weightT"])
        units = [(e, c, half) for e in range(2) for c in range(C) for half in range(2)]
        n = len(units)
        names = []
        for u in range(n + 2):
            names += ([f"ab{u}"] if u < n else []) + ([f"acc{u - 2}"] if u >= 2 else [])
        mpe = Steps(sem("main_pe"), names)
        gpe, gdve = Steps(sem("gate_pe"), ["spread"]), Steps(sem("gate_dve"), ["mine", "hg"])
        ahead = [n // 2 * e + n // 4 for e in range(2)]
        mdve, mact = Steps(sem("main_dve"), [f"mid{u}" for u in range(n)]), Steps(sem("main_act"), [f"silu{u}" for u in range(n)])
        pe, dve, pool = Steps(pe_s, [f"y{b}" for b in range(B)]), Steps(dve_s, paired(TAIL_DVE)), Steps(pool_s, paired(TAIL_POOL))
        a = chip.a
        block = ctx.enter_context(nc.Block())

        @block.sync
        def _(sp):
            for e in range(E + 1):
                if e >= 2:
                    sp.wait_ge(*mpe.done(f"acc{n // 2 * (e % 2 + 1) - 1}", e // 2 - 1))
                one_of = lambda m: a[f"L3_ffn_{m}"][e, :, :] if e < E else a[f"L3_ffn_{m}s"]
                sp.dma_start(w1[:, e % 2, :], one_of("W1")).then_inc(weights[e % 2], 16)
                sp.dma_start(w3[:, e % 2, :], one_of("W3")).then_inc(weights[e % 2], 16)
                sp.dma_start(w2[:, e % 2, :, :], one_of("W2").rearrange("(c p) d -> p c d", p=P)).then_inc(weights[e % 2], 16)

        @block.gpsimd
        def _(eng):
            eng.wait_ge(*rdve.done("var"))
            nc.gpsimd.tensor_tensor(fp(zr), zmv[:, :, 1], chip.eps[:, 0:TILES], ALU.add).then_inc(*rpool.end("eps"))
            eng.wait_ge(*rpool.done("eps"))
            nc.gpsimd.tensor_tensor(fp(zr), fp(zr), chip.neghalf[:, 0:TILES], ALU.pow).then_inc(*rpool.end("rstd"))
            for pair in range(B // PAIR):
                tails_pool(nc, eng, chip, t[PAIR * pair:], dve, pool, pair)

        @block.vector
        def _(eng):
            x_tiles = fp(chip.x_tok).rearrange("p b t d -> p (b t) d")
            for q in range(TILES):
                last = nc.vector.bn_stats(zs[:, q, :], x_tiles[:, q, :])
            last.then_inc(*rdve.end("stats"))
            eng.wait_ge(*rdve.done("stats"))
            for q in range(TILES):
                last = nc.vector.bn_aggr(zmv[:, q, :], zs[:, q, :])
            last.then_inc(*rdve.end("var"))
            eng.wait_ge(*rpool.done("rstd"))
            for q in range(TILES):
                last = nc.vector.tensor_scalar(z[:, q, :], x_tiles[:, q, :], zmv[:, q, 0:1], zr[:, q:q + 1], ALU.subtract, ALU.mult)
            last.then_inc(*rdve.end("z"))
            eng.wait_ge(*rpe.done("zT"))
            nc.vector.tensor_scalar(fp(hT), ps[:, 4:6, :].rearrange("p a t -> p (a t)"), w["L3_ffn_ln_g"], w["L3_ffn_ln_b"],
                                    ALU.mult, ALU.add).then_inc(*rdve.end("hT"))
            eng.wait_ge(*rpe.done("logits"))
            nc.vector.tensor_copy(fp(lg), ps[:, 7, 0:TILES * E].rearrange("p (t e) -> p t e", e=E)).then_inc(*rdve.end("logits"))
            eng.wait_ge(*rdve.done("logits"))
            one, second = picks[:, 0:TILES, :], picks[:, TILES:2 * TILES, :]
            pick_first(nc, eng, chip, k, rdve, 0, "first", fp(lg), one)
            nc.vector.tensor_copy(fp(m1), fp(k.m)).then_inc(*rdve.end("m1"))
            eng.wait_ge(*rdve.done("m1"))
            nc.vector.scalar_tensor_tensor(fp(two), one, MASKED, fp(lg), ALU.mult, ALU.add).then_inc(*rdve.end("rest"))
            eng.wait_ge(*rdve.done("rest"))
            pick_first(nc, eng, chip, k, rdve, 0, "second", fp(two), second)
            nc.vector.tensor_tensor(fp(ex), fp(k.m), fp(m1), ALU.subtract).then_inc(*rdve.end("gap"))
            eng.wait_ge(*ract.done("exp"))
            nc.vector.tensor_scalar(fp(den), fp(ex), 1.0, None, ALU.add).then_inc(*rdve.end("den"))
            eng.wait_ge(*rdve.done("den"))
            nc.vector.reciprocal(gates[:, 0, :], fp(den)).then_inc(*rdve.end("gate1"))
            eng.wait_ge(*rdve.done("gate1"))
            nc.vector.tensor_tensor(gates[:, 1, :], fp(ex), gates[:, 0, :], ALU.mult).then_inc(*rdve.end("gates"))
            nc.vector.memset(weight[:, :, E:8], 1.0).then_inc(*cdve.end("shared"))
            nc.vector.memset(offs[:, 0, :], 0.0).then_inc(*cdve.end("off0"))
            eng.wait_ge(*cpe.done("counts"))
            totals = ps[:, 1, 0:2 * TILES * E].rearrange("p (i e) -> p i e", e=E)
            for i in range(1, 2 * TILES):
                eng.wait_ge(*cdve.done(f"off{i - 1}"))
                nc.vector.tensor_tensor(offs[:, i, :], offs[:, i - 1, :], totals[:, i - 1, :], ALU.add).then_inc(*cdve.end(f"off{i}"))
            eng.wait_ge(*cdve.done(f"off{2 * TILES - 1}"))
            nc.vector.tensor_tensor(fp(offs), ps[:, 0, 0:2 * TILES * E].rearrange("p (i e) -> p i e", e=E), fp(offs), ALU.add)\
                .then_inc(*cdve.end("pos"))
            eng.wait_ge(*cdve.done("pos"))
            nc.vector.tensor_scalar(fp(keep), fp(offs), float(CAPACITY), None, ALU.is_lt).then_inc(*cdve.end("keep"))
            eng.wait_ge(*cdve.done("keep"))
            nc.vector.tensor_tensor(fp(keep), fp(keep), fp(picks), ALU.mult).then_inc(*cdve.end("kept"))
            eng.wait_ge(*cdve.done("kept"))
            eng.wait_ge(*rdve.done("gates"))
            nc.vector.tensor_tensor(fp(keep), fp(keep), fp(gates).rearrange("p s t -> p (s t)").unsqueeze(2)
                                    .to_broadcast([P, 2 * TILES, E]), ALU.mult).then_inc(*cdve.end("weighed"))
            eng.wait_ge(*cdve.done("weighed"))
            nc.vector.tensor_tensor(weight[:, :, 0:E], keep[:, 0:TILES, :], keep[:, TILES:2 * TILES, :], ALU.add)\
                .then_inc(*cdve.end("weight"))
            eng.wait_ge(*cpe.done("weightT"))
            nc.vector.tensor_copy(fp(weightT), ps[0:8, 2:4, :].rearrange("p a t -> p (a t)")).then_inc(*cdve.end("weightT"))
            eng.wait_ge(*cdve.done("weightT"))

            def row(expert, e):
                nc.vector.tensor_scalar(mine[:, e, :], fp(weightT), chip.ident[0:8, bass.ds(expert, 1)], None, ALU.mult)\
                    .then_inc(*gdve.end("mine"))

            def gated(expert, e):
                eng.wait_ge(*gpe.done("spread", expert))
                nc.vector.tensor_tensor(hg[:, e, :], ps[:, 4:6, :].rearrange("p a t -> p (a t)"), fp(hT), ALU.mult)\
                    .then_inc(*gdve.end("hg"))

            row(0, 0)
            gated(0, 0)
            with eng.Fori(0, (E + 1) // 2) as i:
                for u, (e, c, half) in enumerate(units):
                    if u in ahead:
                        row(i * 2 + e + 1, 1 - e)
                    if u - 3 in ahead:
                        gated(i * 2 + e + 1, 1 - e)
                    eng.wait_ge(*mact.done(f"silu{u}", i))
                    if u >= 2:
                        eng.wait_ge(*mpe.done(f"acc{u - 2}", i))
                    nc.vector.tensor_tensor(mid[:, u % 2, :], ps[:, 2 + u % 2, :], act1[:, u % 2, :], ALU.mult)\
                        .then_inc(*mdve.end(f"mid{u}"))
                eng.wait_ge(*mpe.done(f"acc{n - 1}", i))
            eng.wait_ge(closed, 1)
            nc.vector.tensor_copy(fp(yT), ps[:, 6:8, :].rearrange("p a t -> p (a t)")).then_inc(copied, 1)
            for pair in range(B // PAIR):
                tails_dve(nc, eng, chip, t[PAIR * pair:], dve, pool, pair, lambda i: pe.done(f"y{PAIR * pair + i}"),
                          lambda i: ps[:, PAIR * pair + i, 0:S].rearrange("p (t d) -> p t d", t=QT), lambda i: chip.x_tok[:, PAIR * pair + i, :, :])

        @block.scalar
        def _(eng):
            eng.wait_ge(*rdve.done("gap"))
            nc.scalar.activation(fp(ex), fp(ex), ACT.Exp).then_inc(*ract.end("exp"))
            with eng.Fori(0, (E + 1) // 2) as i:
                for u, (e, c, half) in enumerate(units):
                    eng.wait_ge(*mpe.done(f"ab{u}", i))
                    if u >= 2:
                        eng.wait_ge(*mdve.done(f"mid{u - 2}", i))
                    nc.scalar.activation(act1[:, u % 2, :], ps[:, u % 2, :], ACT.Silu).then_inc(*mact.end(f"silu{u}"))

        @block.tensor
        def _(eng):
            eng.wait_ge(*rdve.done("z"))
            for q in range(TILES):
                last = nc.tensor.transpose(ps[:, 4 + q // 4, q % 4 * P:(q % 4 + 1) * P], z[:, q, :], chip.ident[:, :])
            last.then_inc(*rpe.end("zT"))
            eng.wait_ge(*rdve.done("hT"))
            for q in range(TILES):
                last = nc.tensor.matmul(ps[:, 7, q * E:(q + 1) * E], hT[:, q * P:(q + 1) * P], w["L3_ffn_Wr"], start=True, stop=True)
            last.then_inc(*rpe.end("logits"))
            eng.wait_ge(*rdve.done("secondpick"))
            flat = fp(picks).rearrange("p i e -> p (i e)")
            nc.tensor.matmul(ps[:, 0, 0:2 * TILES * E], w["c_before"], flat, start=True, stop=True)
            nc.tensor.matmul(ps[:, 1, 0:2 * TILES * E], chip.ones[:, 0:P], flat, start=True, stop=True).then_inc(*cpe.end("counts"))
            eng.wait_ge(*cdve.done("weight"))
            for i in range(TILES):
                last = nc.tensor.transpose(ps[0:8, 2 + i // 4, (i % 4) * P:(i % 4 + 1) * P], weight[:, i, :], chip.ident[:, :])
            last.then_inc(*cpe.end("weightT"))
            for half in range(2):
                nc.tensor.matmul(ps[:, 6 + half, :], chip.zeros[0:1, 0:P], chip.ones[0:1, 0:512], start=True, stop=False)
            eng.wait_ge(*cdve.done("weightT"))

            def spread(expert, e):
                eng.wait_ge(*gdve.done("mine", expert))
                for x in range(2):
                    last = nc.tensor.matmul(ps[:, 4 + x, :], chip.ones[0:8, 0:P], mine[:, e, x * 512:(x + 1) * 512], start=True, stop=True)
                last.then_inc(*gpe.end("spread"))

            spread(0, 0)
            with eng.Fori(0, (E + 1) // 2) as i:
                for u in range(n + 2):
                    if u - 1 in ahead:
                        e = units[u][0]
                        spread(i * 2 + e + 1, 1 - e)
                    if u < n:
                        e, c, half = units[u]
                        cols = slice(half * 512, (half + 1) * 512)
                        if u % (n // 2) == 0:
                            eng.wait_ge(weights[e], i * 48 + 48)
                            eng.wait_ge(*gdve.done("hg", i * 2 + e))
                        if u >= 2:
                            eng.wait_ge(*mdve.done(f"mid{u - 2}", i))
                        nc.tensor.matmul(ps[:, u % 2, :], w1[:, e, c * P:(c + 1) * P], hT[:, cols], start=True, stop=True)
                        nc.tensor.matmul(ps[:, 2 + u % 2, :], w3[:, e, c * P:(c + 1) * P], hg[:, e, cols], start=True, stop=True)\
                            .then_inc(*mpe.end(f"ab{u}"))
                    if u >= 2:
                        e, c, half = units[u - 2]
                        eng.wait_ge(*mdve.done(f"mid{u - 2}", i))
                        nc.tensor.matmul(ps[:, 6 + half, :], w2[:, e, c, :], mid[:, (u - 2) % 2, :], start=False, stop=False)\
                            .then_inc(*mpe.end(f"acc{u - 2}"))
            for half in range(2):
                last = nc.tensor.matmul(ps[:, 6 + half, :], chip.zeros[0:1, 0:P], chip.ones[0:1, 0:512], start=False, stop=True)
            last.then_inc(closed, 1)
            eng.wait_ge(copied, 1)
            for b in range(B):
                for q in range(QT):
                    last = nc.tensor.transpose(ps[:, b, q * P:(q + 1) * P], yT[:, b * S + q * P:b * S + (q + 1) * P], chip.ident[:, :])
                last.then_inc(*pe.end(f"y{b}"))


FFN_LAYERS, FFN_HEADS, FFN_DH, FFN_IN = 6, 16, 64, 341
FFN_CHUNKS = [(0, P), (P, P), (2 * P, FFN_IN - 2 * P)]
EDGE = 32
SEEN = P + EDGE


def l1_ffn_constants():
    f = np.float32
    half = np.arange(0, FFN_DH, 2, dtype=f)
    inv_freq = (f(1) / np.power(f(10000), half / f(FFN_DH)).astype(f)).astype(f)
    t = np.arange(S, dtype=f)
    freqs = (t[:, None] * inv_freq[None, :]).astype(f)
    freqs = np.concatenate([freqs, freqs], -1)
    base = ((half + f(0.4 * FFN_DH)) / f(1.4 * FFN_DH)).astype(f)
    power = ((t - S // 2) / f(EDGE // 2)).astype(f)
    scale = np.power(base[None, :], power[:, None]).astype(f)
    scale = np.concatenate([scale, scale], -1)
    inv = (f(1) / scale).astype(f)
    sign = np.where(np.arange(FFN_DH) < FFN_DH // 2, f(-1), f(1))[None, :]
    cos, sin = np.cos(freqs).astype(f), (np.sin(freqs) * sign).astype(f)
    tab = np.stack([np.stack([cos * scale * f(8), sin * scale * f(8)]), np.stack([cos * inv, sin * inv])]).astype(f)
    return {"c_xpos": np.ascontiguousarray(tab.reshape(2, 2, QT, P, FFN_DH).transpose(3, 0, 1, 2, 4))}


class FfnState:
    pass


def l1_ffn(nc, chip):
    with ExitStack() as ctx:
        sb = lambda n, s, dt=F32: ctx.enter_context(nc.sbuf_tensor(f"l1f_{n}", s, dt))
        f = FfnState()
        f.xr = sb("xr", [P, B, S])
        f.cols = sb("cols", [P, 9, FFN_LAYERS])
        f.spread = sb("spread", [P, 2, FFN_LAYERS, FFN_DH])
        f.xpos = sb("xpos", [P, 2, 2, QT, FFN_DH])
        f.band = sb("band", [P, QT, SEEN], BF16)
        f.bandT = sb("bandT", [P, SEEN], BF16)
        f.pick = sb("pick", [P, FFN_HEADS // 2, P], BF16)
        f.pick_half = sb("pick_half", [P, FFN_HEADS // 2, P], BF16)
        f.mean_w = sb("mean_w", [P, P])
        l1_ffn_enter(nc, chip, f)
        l1_ffn_layers(nc, chip, f)
        l1_ffn_leave(nc, chip, f)


def l1_ffn_enter(nc, chip, f):
    with ExitStack() as ctx:
        sb = lambda n, s, dt=F32: ctx.enter_context(nc.sbuf_tensor(f"l1fe_{n}", s, dt))
        pe_s, dve_s, act_s, pool_s, loads = stage_sems(nc, ctx, "l1fe")
        raw = sb("raw", [FFN_LAYERS, 3, P])
        raw_b1 = sb("raw_b1", [FFN_LAYERS, 2 * FFN_IN])
        raw_band, raw_bandT, raw_pick = sb("raw_band", [P, QT, SEEN]), sb("raw_bandT", [P, SEEN]), sb("raw_pick", [P, FFN_HEADS // 2, 2])
        pe, dve = Steps(pe_s, [f"x{b}" for b in range(B)] + ["cols"]), Steps(dve_s, ["clear"] + [f"x{b}" for b in range(B)])
        vectors = [(i, raw[:, i, :], P) for i in range(3)]
        vectors += [(3 + 3 * g + i, raw_b1[:, g * FFN_IN + at:g * FFN_IN + at + n], n)
                    for g in range(2) for i, (at, n) in enumerate(FFN_CHUNKS)]
        a, ps = chip.a, chip.ps
        block = ctx.enter_context(nc.Block())

        @block.sync
        def _(sp):
            n = 0
            for dst, src in [(raw[:, 0, :], a["L1_ffn_ln_g"]), (raw[:, 1, :], a["L1_ffn_ln_b"]), (raw[:, 2, :], a["L1_ffn_b2"]),
                             (fp(raw_b1), a["L1_ffn_b1"]), (fp(f.xpos), a["c_xpos"]),
                             (fp(raw_band), a["c_band"]), (fp(raw_bandT), a["c_bandT"]), (fp(raw_pick), a["c_pick"])]:
                sp.dma_start(dst, src).then_inc(loads, 16)
                n += 16
            for i, k in enumerate("qk"):
                sp.dma_start(f.spread[:, i, :, :].rearrange("p l d -> p (l d)"),
                             a[f"L1_ffn_{k}_scale"].rearrange("l d -> (l d)").partition_broadcast(P)).then_inc(loads, 16)
                n += 16
            sp.wait_ge(loads, n)

        @block.tensor
        def _(eng):
            for b in range(B):
                for q in range(QT):
                    last = nc.tensor.transpose(ps[:, b, q * P:(q + 1) * P], chip.x_tok[:, b, q, :], chip.ident[:, :])
                last.then_inc(*pe.end(f"x{b}"))
            eng.wait_ge(loads, 10 * 16)
            for i, src, n in vectors:
                last = nc.tensor.transpose(ps[0:n, 4, 8 * i:8 * i + FFN_LAYERS], src, chip.ident[0:FFN_LAYERS, 0:FFN_LAYERS])
            last.then_inc(*pe.end("cols"))

        @block.vector
        def _(eng):
            nc.vector.memset(fp(f.mean_w), 1.0 / D)
            nc.vector.memset(fp(f.cols), 0.0).then_inc(*dve.end("clear"))
            for b in range(B):
                eng.wait_ge(*pe.done(f"x{b}"))
                nc.vector.tensor_copy(f.xr[:, b, :], ps[:, b, 0:S]).then_inc(*dve.end(f"x{b}"))
            eng.wait_ge(*pe.done("cols"))
            eng.wait_ge(*dve.done("clear"))
            for i, src, n in vectors:
                nc.vector.tensor_copy(f.cols[0:n, i, :], ps[0:n, 4, 8 * i:8 * i + FFN_LAYERS])
            nc.vector.tensor_copy(fp(f.band), fp(raw_band))
            nc.vector.tensor_copy(fp(f.bandT), fp(raw_bandT))
            for odd in range(2):
                nc.vector.tensor_copy(f.pick_half[:, :, odd * FFN_DH:(odd + 1) * FFN_DH],
                                      raw_pick[:, :, odd:odd + 1].to_broadcast([P, FFN_HEADS // 2, FFN_DH]))
            nc.vector.tensor_tensor(fp(f.pick), raw_pick[:, :, 0:1].to_broadcast([P, FFN_HEADS // 2, P]),
                                    raw_pick[:, :, 1:2].to_broadcast([P, FFN_HEADS // 2, P]), ALU.add)


def l1_ffn_leave(nc, chip, f):
    with ExitStack() as ctx:
        sb = lambda n, s, dt=F32: ctx.enter_context(nc.sbuf_tensor(f"l1fl_{n}", s, dt))
        pe_s, dve_s, act_s, pool_s, loads = stage_sems(nc, ctx, "l1fl")
        t = Tail(nc, ctx, "l1fl")
        xb = sb("xb", [P, QT, D])
        pe, dve, pool = Steps(pe_s, ["y"]), Steps(dve_s, ["x"] + TAIL_DVE), Steps(pool_s, TAIL_POOL)
        block = ctx.enter_context(nc.Block())

        @block.gpsimd
        def _(eng):
            with eng.Fori(0, B) as b:
                tail_pool(nc, eng, chip, t, dve, pool, b)

        @block.vector
        def _(eng):
            for b in range(B):
                nc.vector.tensor_copy(fp(xb), chip.x_tok[:, b, :, :]).then_inc(*dve.end("x"))
                eng.wait_ge(*dve.done("x", b))
                eng.wait_ge(*pe.done("y", b))
                tail_dve(nc, eng, chip, t, dve, pool, b, chip.ps[:, b, 0:S].rearrange("p (t d) -> p t d", t=QT), fp(xb))

        @block.tensor
        def _(eng):
            for b in range(B):
                for q in range(QT):
                    last = nc.tensor.transpose(chip.ps[:, b, q * P:(q + 1) * P], f.xr[:, b, q * P:(q + 1) * P], chip.ident[:, :])
                last.then_inc(*pe.end("y"))


class FfnWork:
    pass


def l1_ffn_layers(nc, chip, f):
    H, DH, L = FFN_HEADS, FFN_DH, FFN_LAYERS
    PAIRS = H // 2
    with ExitStack() as ctx:
        sb = lambda n, s, dt=F32: ctx.enter_context(nc.sbuf_tensor(f"l1fb_{n}", s, dt))
        w = FfnWork()
        w.wqkv, w.wo = sb("wqkv", [P, 3 * H * DH]), sb("wo", [P, PAIRS, D])
        w.w1, w.w2 = sb("w1", [P, 2 * FFN_IN]), sb("w2", [P, 3, D])
        w.turn_tab, w.col = sb("turn_tab", [P, 2, 2, QT, DH]), sb("col", [P, 9])
        w.xs = sb("xs", [P, 2, S])
        w.sq, w.ssq, w.rinv = sb("sq", [P, 2, 512]), sb("ssq", [P, 2, 8, 8]), sb("rinv", [P, 2, 8, 8])
        w.qk, w.r2 = sb("qk", [P, QK, 512]), sb("r2", [P, 2, 512])
        w.qT, w.kT = sb("qT", [P, 2, H, S]), sb("kT", [P, 2, PAIRS, S])
        w.v = sb("v", [P, 2, QT, H, DH])
        w.shift = sb("shift", [P, 2, 2 * QT * H])
        w.den, w.rden = sb("den", [P, 2, H, QT]), sb("rden", [P, 2, QT, H])
        w.low = w.r2[3 * EDGE:3 * EDGE + H, 0, :]
        w.parts = sb("parts", [P, 2, 2 * S], BF16)
        w.rparts = sb("rparts", [P, 2, S], BF16)
        w.p0, w.p1 = sb("p0", [P, 2, 2, S]), sb("p1", [P, 2, 2, P])
        w.attT = sb("attT", [P, PAIRS, 2, S])
        w.x1, w.x1s = sb("x1", [P, 2, S]), sb("x1s", [P, 2, S])
        w.diff, w.dsq = sb("diff", [P, 2, S]), sb("dsq", [P, 4, P])
        w.rstd = sb("rstd", [P, 4])
        g = sb("g", [P, 2, 2, S])
        w.g = [g[:, 0, :, :], g[:, 1, :, :], fp(w.p1).rearrange("p a j n -> p (a j n)").rearrange("p (b t) -> p b t", b=2)]
        sem = lambda n: ctx.enter_context(nc.semaphore(f"l1fb_{n}"))
        a = chip.a
        w.ready, w.qkv_in, w.out_in = sem("ready"), sem("qkv_in"), sem("out_in")
        w.tables = Steps(sem("table_steps"), ["tables"])
        l1_ffn_steps(w, sem)
        block = ctx.enter_context(nc.Block())

        def slots(attention, unit):
            attention(0, 0, 0, None)
            with attention.eng.Fori(0, L - 1) as j:
                attention(j * 2 + 1, 1, j, unit(j * 2, 0, j))
                attention(j * 2 + 2, 0, j + 1, unit(j * 2 + 1, 1, j))
            attention(2 * L - 1, 1, L - 1, unit(2 * L - 2, 0, L - 1))
            for piece in unit(2 * L - 1, 1, L - 1).values():
                piece()

        @block.sync
        def _(sp):
            for l in range(L):
                if l:
                    sp.wait_ge(*w.a_pe.done("proj1_11", 2 * l - 1))
                sp.dma_start(fp(w.wqkv), a["L1_ffn_Wqkv"][l, :, :]).then_inc(w.qkv_in, 16)
                if l:
                    sp.wait_ge(*w.g_pe.done("y2", 2 * l - 1))
                for dst, src in [(fp(w.wo), a["L1_ffn_Wo"][l, :, :].rearrange("(c p) d -> p c d", p=P)),
                                 (fp(w.w1), a["L1_ffn_W1"][l, :, :]),
                                 (w.w2[:, 0:2, :], a["L1_ffn_W2"][l, 0:2 * P, :].rearrange("(c p) d -> p c d", p=P)),
                                 (w.w2[0:FFN_IN - 2 * P, 2, :], a["L1_ffn_W2"][l, 2 * P:FFN_IN, :])]:
                    sp.dma_start(dst, src).then_inc(w.out_in, 16)

        @block.gpsimd
        def _(eng):
            l1_ffn_pool(nc, eng, chip, f, w, slots)

        @block.vector
        def _(eng):
            l1_ffn_dve(nc, eng, chip, f, w, slots)

        @block.scalar
        def _(eng):
            l1_ffn_act(nc, eng, chip, f, w, slots)

        @block.tensor
        def _(eng):
            l1_ffn_pe(nc, eng, chip, f, w, slots)


PROJ = [(k, hh, q) for k in range(3) for hh in range(2) for q in range(QT)]
QK = 4 * QT
PAIRS_OF = lambda n: ((n // 2) % 2 * 4 + n % 2 * 2, (n // 2) % 2 * 4 + n % 2 * 2 + 2)
WEIGHT_BANKS = (6, 4, 5)
SCORES = [(i, c) for i in range(2) for c in range(FFN_HEADS // 2)]
PE_PLAN = """p0.0 p0.1 p0.2 y1 p0.3 p0.4 p0.5 t0.0 t0.1 mean p0.6 p0.7 t0.2 t0.3 var p0.8 p0.9 t0.4 t0.5 p0.10 p0.11
             p1.0 p1.1 rstd t0.6 t0.7 p1.2 p1.3 chunk0 p1.4 p1.5 t1.0 t1.1 chunk1 p1.6 p1.7 t1.2 t1.3 chunk2
             p1.8 p1.9 t1.4 t1.5 y2 p1.10 p1.11 t1.6 t1.7""".split()
DVE_PLAN = """r0.0 r0.1 r0.2 x1 r0.3 r0.4 r0.5 centre r0.6 r0.7 vareps r1.0 diag r1.1 xn r1.2 r1.3 r1.4 g0 r1.5 r1.6 g1 r1.7
              g2 x2""".split()
ACT_PLAN = """s0.0 s0.1 s0.2 s0.3 s0.4 s0.5 e0.0 e0.1 s0.6 s0.7 e0.2 e0.3 v0.8 v0.9 e0.4 e0.5 v0.10 v0.11
              s1.0 s1.1 e0.6 e0.7 s1.2 s1.3 gelu0 s1.4 s1.5 e1.0 e1.1 gelu1 s1.6 s1.7 e1.2 e1.3 gelu2
              v1.8 v1.9 e1.4 e1.5 v1.10 v1.11 e1.6 e1.7""".split()


def planned(plan):
    for step in plan:
        if "." in step:
            i, n = step[1:].split(".")
            yield step[0], int(i), int(n)
        else:
            yield step, None, None


def l1_ffn_steps(w, sem):
    pe = [{"p": "proj", "t": "turn"}[k] + f"{i}_{n}" for k, i, n in planned(PE_PLAN) if n is not None]
    for u in range(len(SCORES)):
        pe += [f"s{u}"] + (["shift0"] if u == 9 else ["rden0"] if u == 15 else [])
    for u in range(len(SCORES)):
        pe += [f"t{u}_0", f"t{u}_1"] + (["shift1"] if u == 2 else ["rden1"] if u == 4 else []) + ([f"pv{u - 1}"] if u else [])
    w.a_pe = Steps(sem("a_pe_steps"), pe + [f"pv{len(SCORES) - 1}"])
    dve = ["xs"]
    for k, i, n in planned(DVE_PLAN):
        if n is not None:
            dve += [f"rot{i}_{n}", f"ssq{i}_{n}", f"add{i}_{n}", f"clamp{i}_{n}"]
    split = lambda of: [f"hi_{of}", f"low_{of}", f"mid_{of}", f"parts_{of}"]
    for u in range(len(SCORES)):
        dve += [f"max{u}"] + (["rden0"] if u == 9 else split("shift0") if u == 10 else split("rden0") if u == 15 else [])
    for u in range(len(SCORES)):
        dve += [f"sum{u}", f"att{u}"] + (split("shift1") if u == 0 else ["rden1"] + split("rden1") if u == 2 else [])
    w.a_dve = Steps(sem("a_dve_steps"), dve)
    act = [{"s": "sq", "e": "turned", "v": "v"}[k] + f"{i}_{n}" for k, i, n in planned(ACT_PLAN) if n is not None]
    for u in range(len(SCORES)):
        act += [f"exp{u}"]
    for u in range(len(SCORES)):
        act += [f"p{u}_0", f"p{u}_1"]
    w.a_act = Steps(sem("a_act_steps"), act)
    pool = []
    for i in range(2):
        for u in range(QK):
            pool += [f"rinv{i}_{u}", f"qk{i}_{u}"]
    w.a_pool = Steps(sem("a_pool_steps"), pool)
    w.g_pe = Steps(sem("g_pe_steps"), ["y1", "mean", "var", "rstd"] + [f"{k}{i}" for i in range(3) for k in ("gate", "value")] + ["y2"])
    w.g_dve = Steps(sem("g_dve_steps"), ["x1", "x1s", "diff", "dsq", "vareps", "diag", "xn0", "xn", "g0", "g1", "g2", "x2"])
    w.g_act = Steps(sem("g_act_steps"), ["gelu0", "gelu1", "gelu2"])
    w.g_pool = Steps(sem("g_pool_steps"), ["rstd"])


class Slot:

    def __init__(self, eng, body):
        self.eng, self.body = eng, body

    def __call__(self, t, half, layer, pieces):
        self.body(t, half, layer, pieces or {})


def l1_ffn_pool(nc, eng, chip, f, w, slots):
    a_dve, a_pool = w.a_dve, w.a_pool
    heads = lambda r: r.rearrange("p (h d) -> p h d", d=FFN_DH)
    nc.gpsimd.memset(fp(w.p0), 0.0)
    nc.gpsimd.memset(fp(w.shift), 0.0)
    nc.gpsimd.memset(fp(w.rparts), 0.0)
    nc.gpsimd.memset(fp(w.parts), 0.0).then_inc(w.ready, 1)

    def attention(t, half, layer, pieces):
        for i in range(2):
            for u in range(QK):
                eng.wait_ge(*a_dve.done(f"clamp{i}_{u}", t))
                nc.gpsimd.tensor_tensor(w.rinv[:, i, u, :], w.ssq[:, i, u, :], chip.neghalf[:, 0:8], ALU.pow)\
                    .then_inc(*a_pool.end(f"rinv{i}_{u}"))
                eng.wait_ge(*a_pool.done(f"rinv{i}_{u}", t))
                nc.gpsimd.tensor_tensor(heads(w.qk[:, u, :]), heads(w.qk[:, u, :]),
                                        w.rinv[:, i, u, :].unsqueeze(2).to_broadcast([P, 8, FFN_DH]), ALU.mult).then_inc(*a_pool.end(f"qk{i}_{u}"))
                if i == 0 and u == 6 and pieces:
                    pieces["rstd"]()

    def unit(t, half, layer):
        def rstd():
            eng.wait_ge(*w.g_dve.done("vareps", t))
            nc.gpsimd.tensor_tensor(fp(w.rstd), fp(w.rstd), chip.neghalf[:, 0:4], ALU.pow).then_inc(*w.g_pool.end("rstd"))

        return {"rstd": rstd}

    slots(Slot(eng, attention), unit)


def l1_ffn_dve(nc, eng, chip, f, w, slots):
    DH, H = FFN_DH, FFN_HEADS
    ps, a_pe, a_dve, a_act, a_pool = chip.ps, w.a_pe, w.a_dve, w.a_act, w.a_pool
    g_pe, g_dve, g_act, g_pool = w.g_pe, w.g_dve, w.g_act, w.g_pool
    heads = lambda r: r.rearrange("p (h d) -> p h d", d=DH)
    nc.vector.memset(w.qT[0:DH, :, 1:H:2, :], 0.0)
    nc.vector.memset(w.qT[DH:P, :, 0:H:2, :], 0.0)
    nc.vector.memset(w.xs[DH:P, :, 0:1], 0.0)
    nc.vector.memset(w.x1s[DH:P, :, 0:1], 0.0).then_inc(w.ready, 1)
    eng.wait_ge(w.ready, 2)

    def tables(l):
        for k in range(2):
            for part, (lo, hi) in ((0, (0, DH)), (1, (DH // 2, DH)), (1, (0, DH // 2))):
                o = slice(0, DH) if part == 0 else slice(DH // 2 - lo, DH - lo)
                last = nc.vector.tensor_tensor(w.turn_tab[:, k, part, :, o], f.xpos[:, k, part, :, o],
                                               f.spread[:, k, l, lo:hi].unsqueeze(1).to_broadcast([P, QT, hi - lo]), ALU.mult)
        last.then_inc(*w.tables.end("tables"))

    def rotate(t, i, u):
        k, hh, q = PROJ[u]
        eng.wait_ge(*a_act.done(f"sq{i}_{u}", t))
        if i:
            eng.wait_ge(*a_pe.done(f"turn{i - 1}_{2 * (u // 2) + 1}", t))
        src, r1, r2 = heads(ps[:, u % 3, :]), heads(w.qk[:, u, :]), heads(w.r2[:, u % 2, :])
        tab = lambda part, o: w.turn_tab[:, k, part, q, o].unsqueeze(1).to_broadcast([P, 8, o.stop - o.start])
        nc.vector.tensor_tensor(r1, src, tab(0, slice(0, DH)), ALU.mult)
        for lo in (0, DH // 2):
            o, other = slice(lo, lo + DH // 2), slice(DH // 2 - lo, DH - lo)
            last = nc.vector.tensor_tensor(r2[:, :, o], src[:, :, other], tab(1, o), ALU.mult)
        last.then_inc(*a_dve.end(f"rot{i}_{u}"))
        nc.vector.tensor_reduce(w.ssq[:, i, u, :], heads(w.sq[:, u % 2, :]), AX.X, ALU.add).then_inc(*a_dve.end(f"ssq{i}_{u}"))
        eng.wait_ge(*a_dve.done(f"rot{i}_{u}", t))
        nc.vector.tensor_tensor(r1, r1, r2, ALU.add).then_inc(*a_dve.end(f"add{i}_{u}"))
        eng.wait_ge(*a_dve.done(f"ssq{i}_{u}", t))
        nc.vector.tensor_scalar(w.ssq[:, i, u, :], w.ssq[:, i, u, :], 1e-24, None, ALU.max).then_inc(*a_dve.end(f"clamp{i}_{u}"))

    def inverses(t, i):
        eng.wait_ge(*a_act.done(f"exp{8 * i + 7}", t))
        nc.vector.reciprocal(w.rden[:, i, :, :], w.den[:, i, :, :].rearrange("p h q -> p q h")).then_inc(*a_dve.end(f"rden{i}"))

    def split(t, i, of, bank, dst):
        n = dst.shape[2]
        eng.wait_ge(*a_pe.done(of, t))
        src, low, mid = ps[0:H, bank, 0:n], w.low[:, 0:n], dst[3 * EDGE:3 * EDGE + H, i, :]
        nc.vector.tensor_copy(dst[0:H, i, :], src).then_inc(*a_dve.end(f"hi_{of}"))
        eng.wait_ge(*a_dve.done(f"hi_{of}", t))
        nc.vector.tensor_tensor(low, src, dst[0:H, i, :], ALU.subtract).then_inc(*a_dve.end(f"low_{of}"))
        eng.wait_ge(*a_dve.done(f"low_{of}", t))
        nc.vector.tensor_copy(dst[EDGE:EDGE + H, i, :], low)
        nc.vector.tensor_copy(mid, low).then_inc(*a_dve.end(f"mid_{of}"))
        eng.wait_ge(*a_dve.done(f"mid_{of}", t))
        nc.vector.tensor_tensor(dst[2 * EDGE:2 * EDGE + H, i, :], low, mid, ALU.subtract).then_inc(*a_dve.end(f"parts_{of}"))

    def attention(t, half, layer, pieces):
        x = f.xr[:, 2 * half:2 * half + 2, :]
        nc.vector.tensor_copy(w.xs[0:DH, :, :], x[0:DH, :, :])
        nc.vector.tensor_copy(w.xs[DH:P, :, 1:S], x[DH:P, :, 0:S - 1]).then_inc(*a_dve.end("xs"))
        if half == 0:
            tables(layer)
        eng.wait_ge(*w.tables.done("tables", layer))
        for k, i, n in planned(DVE_PLAN):
            if k == "r":
                rotate(t, i, n)
            elif pieces:
                pieces[k]()
        for u, (i, c) in enumerate(SCORES):
            eng.wait_ge(*a_pe.done(f"s{u}", t))
            bank = 2 * (u % 3)
            for q, (lo, hi) in enumerate(((0, P), (P, P + SEEN))):
                at = q * H + 2 * c
                last = nc.vector.tensor_reduce(w.shift[:, i, at:at + QT * H + 2:QT * H + 1], ps[:, bank:bank + 2, lo:hi], AX.X, ALU.max, negate=True)
            last.then_inc(*a_dve.end(f"max{u}"))
            if u == 9:
                inverses(t, 0)
            if u == 10:
                split(t, 0, "shift0", 7, w.parts)
            if u == 15:
                split(t, 0, "rden0", 7, w.rparts)
        for u, (i, c) in enumerate(SCORES):
            eng.wait_ge(*a_pe.done(f"pv{u}", t))
            att = w.attT[:, c, i, :]
            nc.vector.tensor_copy(att, ps[:, 7, 0:S]).then_inc(*a_dve.end(f"sum{u}"))
            eng.wait_ge(*a_dve.done(f"sum{u}", t))
            nc.vector.tensor_tensor(att, att, ps[:, 7, S:2 * S], ALU.mult).then_inc(*a_dve.end(f"att{u}"))
            if u == 0:
                split(t, 1, "shift1", 0, w.parts)
            if u == 2:
                inverses(t, 1)
                split(t, 1, "rden1", 1, w.rparts)

    def unit(t, half, layer):
        x = f.xr[:, 2 * half:2 * half + 2, :]
        tokens = lambda bank: ps[:, bank, :].rearrange("p (b t) -> p b t", b=2)
        flat = lambda h: fp(h).rearrange("p b t -> p (b t)")

        def residual():
            if half == 0:
                nc.vector.tensor_copy(fp(w.col), f.cols[:, :, layer])
            eng.wait_ge(*g_pe.done("y1", t))
            nc.vector.tensor_tensor(fp(w.x1), tokens(3), x, ALU.add).then_inc(*g_dve.end("x1"))
            eng.wait_ge(*g_dve.done("x1", t))
            nc.vector.tensor_copy(w.x1s[0:DH, :, :], w.x1[0:DH, :, :])
            nc.vector.tensor_copy(w.x1s[DH:P, :, 1:S], w.x1[DH:P, :, 0:S - 1]).then_inc(*g_dve.end("x1s"))

        def centred():
            eng.wait_ge(*g_pe.done("mean", t))
            nc.vector.tensor_tensor(fp(w.diff), fp(w.x1s), tokens(6), ALU.subtract).then_inc(*g_dve.end("diff"))
            eng.wait_ge(*g_dve.done("diff", t))
            nc.vector.tensor_tensor(flat(w.dsq), flat(w.diff), flat(w.diff), ALU.mult).then_inc(*g_dve.end("dsq"))

        def variance():
            eng.wait_ge(*g_pe.done("var", t))
            nc.vector.tensor_scalar(fp(w.rstd), ps[:, 7, 0:4], EPS, None, ALU.add).then_inc(*g_dve.end("vareps"))

        def diagonals():
            eng.wait_ge(*g_pool.done("rstd", t))
            nc.vector.tensor_tensor(fp(w.dsq), chip.ident[:, :].unsqueeze(1).to_broadcast([P, 4, P]),
                                    w.rstd[:, :].unsqueeze(2).to_broadcast([P, 4, P]), ALU.mult).then_inc(*g_dve.end("diag"))

        def normed():
            eng.wait_ge(*g_pe.done("rstd", t))
            nc.vector.tensor_tensor(fp(w.diff), fp(w.diff), tokens(7), ALU.mult).then_inc(*g_dve.end("xn0"))
            eng.wait_ge(*g_dve.done("xn0", t))
            nc.vector.tensor_scalar(fp(w.diff), fp(w.diff), w.col[:, 0:1], w.col[:, 1:2], ALU.mult, ALU.add).then_inc(*g_dve.end("xn"))

        def gated(i):
            n, bank = FFN_CHUNKS[i][1], (6, 3, 7)[i]
            eng.wait_ge(*g_pe.done(f"value{i}", t))
            eng.wait_ge(*g_act.done(f"gelu{i}", t))
            nc.vector.scalar_tensor_tensor(w.g[i][0:n], tokens(bank)[0:n], w.col[0:n, 3 + i:4 + i], w.g[i][0:n], ALU.add, ALU.mult)\
                .then_inc(*g_dve.end(f"g{i}"))

        def out():
            eng.wait_ge(*g_pe.done("y2", t))
            nc.vector.scalar_tensor_tensor(x, tokens(3), w.col[:, 2:3], fp(w.x1), ALU.add, ALU.add).then_inc(*g_dve.end("x2"))
            eng.wait_ge(*g_dve.done("x2", t))

        return {"x1": residual, "centre": centred, "vareps": variance, "diag": diagonals, "xn": normed,
                "g0": lambda: gated(0), "g1": lambda: gated(1), "g2": lambda: gated(2), "x2": out}

    slots(Slot(eng, attention), unit)


def l1_ffn_act(nc, eng, chip, f, w, slots):
    DH = FFN_DH
    ps, a_pe, a_dve, a_act = chip.ps, w.a_pe, w.a_dve, w.a_act

    def attention(t, half, layer, pieces):
        def square(i, u):
            eng.wait_ge(*a_pe.done(f"proj{i}_{u}", t))
            if u >= 2 or i:
                eng.wait_ge(*a_dve.done(f"ssq{i}_{u - 2}" if u >= 2 else f"ssq{i - 1}_{u + 6}", t))
            nc.scalar.activation(w.sq[:, u % 2, :], ps[:, u % 3, :], ACT.Square).then_inc(*a_act.end(f"sq{i}_{u}"))

        def turned(i, n):
            lo, hi = PAIRS_OF(n)
            eng.wait_ge(*a_pe.done(f"turn{i}_{n}", t))
            src = ps[:, 4 + n % 2, :].rearrange("p (h t) -> p h t", t=S)
            if n < 4:
                nc.scalar.activation(w.qT[0:DH, i, 2 * lo:2 * hi:2, :], src[0:DH, :, :], ACT.Copy)
                last = nc.scalar.activation(w.qT[DH:P, i, 2 * lo + 1:2 * hi:2, :], src[DH:P, :, :], ACT.Copy)
            else:
                last = nc.scalar.activation(w.kT[:, i, lo:hi, :], src, ACT.Copy)
            last.then_inc(*a_act.end(f"turned{i}_{n}"))

        def values(i, u):
            k, hh, q = PROJ[u]
            eng.wait_ge(*a_pe.done(f"proj{i}_{u}", t))
            nc.scalar.activation(w.v[:, i, q, 8 * hh:8 * hh + 8, :], ps[:, u % 3, :].rearrange("p (h d) -> p h d", d=DH), ACT.Copy)\
                .then_inc(*a_act.end(f"v{i}_{u}"))

        for k, i, n in planned(ACT_PLAN):
            if n is not None:
                {"s": square, "e": turned, "v": values}[k](i, n)
            elif pieces:
                pieces[k]()

        place = lambda h, q: h % 2 * QT * FFN_HEADS + q * FFN_HEADS + h
        for u, (i, c) in enumerate(SCORES):
            eng.wait_ge(*a_dve.done(f"max{u}", t))
            for j in range(2):
                for q, (lo, hi) in enumerate(((0, P), (P, P + SEEN))):
                    h, s = 2 * c + j, ps[:, 2 * (u % 3) + j, lo:hi]
                    last = nc.scalar.activation(s, s, ACT.Exp, bias=w.shift[:, i, place(h, q):place(h, q) + 1], accum_out=w.den[:, i, h, q:q + 1])
            last.then_inc(*a_act.end(f"exp{u}"))
        for u, (i, c) in enumerate(SCORES):
            for tile, (dst, n) in enumerate(((w.p0, SEEN), (w.p1, P))):
                eng.wait_ge(*a_pe.done(f"t{u}_{tile}", t))
                if u >= 2 and tile == 0:
                    eng.wait_ge(*a_pe.done(f"pv{u - 2}", t))
                nc.scalar.activation(dst[:, u % 2, :, 0:n], ps[:, WEIGHT_BANKS[(2 * u + tile) % 3], 0:2 * n].rearrange("p (j t) -> p j t", j=2), ACT.Exp)\
                    .then_inc(*a_act.end(f"p{u}_{tile}"))

    def unit(t, half, layer):
        def gelu(i):
            n, bank = FFN_CHUNKS[i][1], (3, 7, 6)[i]
            eng.wait_ge(*w.g_pe.done(f"gate{i}", t))
            nc.scalar.activation(w.g[i][0:n], ps[0:n, bank, :].rearrange("p (b t) -> p b t", b=2), ACT.Gelu, bias=w.col[0:n, 6 + i:7 + i])\
                .then_inc(*w.g_act.end(f"gelu{i}"))

        return {f"gelu{i}": (lambda i=i: gelu(i)) for i in range(3)}

    slots(Slot(eng, attention), unit)


def l1_ffn_pe(nc, eng, chip, f, w, slots):
    H, DH = FFN_HEADS, FFN_DH
    PAIRS = H // 2
    ps, a_pe, a_dve, a_act, a_pool = chip.ps, w.a_pe, w.a_dve, w.a_act, w.a_pool
    g_pe, g_dve, g_act = w.g_pe, w.g_dve, w.g_act
    eng.wait_ge(w.ready, 2)

    def attention(t, half, layer, pieces):
        def project(i, u):
            k, hh, q = PROJ[u]
            if u >= 3:
                before = u - 3
                eng.wait_ge(*a_act.done(f"sq{i}_{before}" if before < QK else f"v{i}_{before}", t))
                if before < QK:
                    eng.wait_ge(*a_dve.done(f"rot{i}_{before}", t))
            elif i:
                eng.wait_ge(*a_act.done(f"v{i - 1}_{u + 9}", t))
            at = k * H * DH + hh * 512
            nc.tensor.matmul(ps[:, u % 3, :], w.xs[:, i, q * P:(q + 1) * P], w.wqkv[:, at:at + 512], start=True, stop=True)\
                .then_inc(*a_pe.end(f"proj{i}_{u}"))

        def turn(i, n):
            even = 2 * (n // 2)
            eng.wait_ge(*a_pool.done(f"qk{i}_{even + 1}", t))
            if n >= 2:
                eng.wait_ge(*a_act.done(f"turned{i}_{n - 2}", t))
            elif i:
                eng.wait_ge(*a_act.done(f"turned{i - 1}_{n + 6}", t))
            for c in range(2):
                for q in range(QT):
                    at = (n % 2 * 2 + c) * P
                    last = nc.tensor.transpose(ps[:, 4 + n % 2, c * S + q * P:c * S + (q + 1) * P],
                                               w.qk[:, even + q, at:at + P], chip.ident[:, :])
            last.then_inc(*a_pe.end(f"turn{i}_{n}"))

        eng.wait_ge(w.qkv_in, layer * 16 + 16)
        eng.wait_ge(*a_dve.done("xs", t))
        for k, i, n in planned(PE_PLAN):
            if n is not None:
                {"p": project, "t": turn}[k](i, n)
            elif pieces:
                pieces[k]()

        def shift(i):
            eng.wait_ge(*a_dve.done(f"max{8 * i + 7}", t))
            if i:
                eng.wait_ge(*a_act.done("exp15", t))
            for k in range(2 * QT):
                last = nc.tensor.transpose(ps[0:H, 0 if i else 7, k * P:(k + 1) * P], w.shift[:, i, k * H:(k + 1) * H], chip.ident[:, :])
            last.then_inc(*a_pe.end(f"shift{i}"))

        def inverses(i):
            eng.wait_ge(*a_dve.done(f"rden{i}", t))
            eng.wait_ge(*a_dve.done(f"parts_shift{i}", t))
            for q in range(QT):
                last = nc.tensor.transpose(ps[0:H, 1 if i else 7, q * P:(q + 1) * P], w.rden[:, i, q, :], chip.ident[:, :])
            last.then_inc(*a_pe.end(f"rden{i}"))

        for u, (i, c) in enumerate(SCORES):
            if u == 0:
                eng.wait_ge(*a_act.done("turned1_7", t))
                after_unit(t)
            if u >= 3:
                eng.wait_ge(*a_act.done(f"exp{u - 3}", t))
            for j in range(2):
                h, bank = 2 * c + j, 2 * (u % 3) + j
                for q, (lo, hi, key) in enumerate(((0, P, 0), (P, P + SEEN, P - EDGE))):
                    nc.tensor.matmul(ps[:, bank, lo:hi], w.qT[:, i, h, q * P:(q + 1) * P], w.kT[:, i, c, key:key + hi - lo],
                                     start=True, stop=False)
                    last = nc.tensor.matmul(ps[:, bank, lo:hi], chip.ident_b[:, :], f.band[:, q, 0:hi - lo], start=False, stop=True)
            last.then_inc(*a_pe.end(f"s{u}"))
            if u == 9:
                shift(0)
            if u == 15:
                inverses(0)

        def values(u):
            i, c = SCORES[u]
            eng.wait_ge(*a_act.done(f"p{u}_1", t))
            eng.wait_ge(*a_dve.done(f"att{u - 1}" if u else "parts_rden0", t))
            if u == 8:
                eng.wait_ge(*a_dve.done("parts_rden1", t))
            nc.tensor.matmul(ps[:, 7, S:2 * S], f.pick_half[:, c, :], w.rparts[:, i, :], start=True, stop=True)
            for j in range(2):
                h, out, place = 2 * c + j, ps[DH * j:DH * j + DH, 7, 0:S], (0, DH * j)
                nc.tensor.matmul(out[:, 0:P], w.v[:, i, 0, h, :], w.p0[:, u % 2, j, 0:P], start=True, stop=True, tile_position=place)
                nc.tensor.matmul(out[:, P:S], w.v[:, i, 0, h, :], w.p0[:, u % 2, j, P:S], start=True, stop=False, tile_position=place)
                last = nc.tensor.matmul(out[:, P:S], w.v[:, i, 1, h, :], w.p1[:, u % 2, j, :], start=False, stop=True, tile_position=place)
            last.then_inc(*a_pe.end(f"pv{u}"))

        for u, (i, c) in enumerate(SCORES):
            for tile, (at, n) in enumerate(((0, SEEN), (P, P))):
                k = 2 * u + tile
                if c == 0 and tile == 0:
                    eng.wait_ge(*a_dve.done(f"parts_shift{i}", t))
                if k == 1:
                    eng.wait_ge(*a_act.done("exp14", t))
                if k >= 3:
                    eng.wait_ge(*a_act.done(f"p{(k - 3) // 2}_{(k - 3) % 2}", t))
                out = ps[:, WEIGHT_BANKS[k % 3], 0:2 * n].rearrange("p (j t) -> p j t", j=2)
                nc.tensor.matmul(out, w.kT[:, i, c, tile * P:(tile + 1) * P], w.qT[:, i, 2 * c:2 * c + 2, at:at + n], start=True, stop=False)
                nc.tensor.matmul(out, chip.ident_b[:, :], f.bandT[:, 0:n].unsqueeze(1).to_broadcast([P, 2, n]), start=False, stop=False)
                nc.tensor.matmul(out, f.pick[:, c, :], w.parts[:, i, :].rearrange("p (j t) -> p j t", j=2)[:, :, at:at + n],
                                 start=False, stop=True).then_inc(*a_pe.end(f"t{u}_{tile}"))
            if u == 2:
                shift(1)
            if u == 4:
                inverses(1)
            if u:
                values(u - 1)
        values(len(SCORES) - 1)

    def after_unit(t):
        if not isinstance(t, int) or t:
            eng.wait_ge(*g_dve.done("x2", t - 1))

    def unit(t, half, layer):
        def attended():
            eng.wait_ge(w.out_in, layer * 64 + 64)
            eng.wait_ge(*a_dve.done(f"att{len(SCORES) - 1}", t))
            for c in range(PAIRS):
                last = nc.tensor.matmul(ps[:, 3, :], w.wo[:, c, :], w.attT[:, c, :, :].rearrange("p b t -> p (b t)"),
                                        start=(c == 0), stop=(c == PAIRS - 1))
            last.then_inc(*g_pe.end("y1"))

        flat = lambda h: fp(h).rearrange("p b t -> p (b t)")

        def mean():
            eng.wait_ge(*g_dve.done("x1s", t))
            nc.tensor.matmul(ps[:, 6, :], fp(f.mean_w), flat(w.x1s), start=True, stop=True).then_inc(*g_pe.end("mean"))

        def variance():
            eng.wait_ge(*g_dve.done("dsq", t))
            for k in range(4):
                last = nc.tensor.matmul(ps[:, 7, k:k + 1], w.dsq[:, k, :], f.mean_w[:, 0:1], start=True, stop=True)
            last.then_inc(*g_pe.end("var"))

        def spread():
            eng.wait_ge(*g_dve.done("diag", t))
            nc.tensor.matmul(ps[:, 7, :], chip.ones[:, 0:P], flat(w.dsq), start=True, stop=True).then_inc(*g_pe.end("rstd"))

        def chunk(i):
            at, n = FFN_CHUNKS[i]
            if i == 0:
                eng.wait_ge(*g_dve.done("xn", t))
            if i == 2:
                eng.wait_ge(*g_dve.done("g0", t))
            nc.tensor.matmul(ps[0:n, (3, 7, 6)[i], :], w.w1[:, FFN_IN + at:FFN_IN + at + n], flat(w.diff), start=True, stop=True)\
                .then_inc(*g_pe.end(f"gate{i}"))
            if i:
                eng.wait_ge(*g_act.done(f"gelu{i - 1}", t))
            nc.tensor.matmul(ps[0:n, (6, 3, 7)[i], :], w.w1[:, at:at + n], flat(w.diff), start=True, stop=True)\
                .then_inc(*g_pe.end(f"value{i}"))

        def out():
            for i, (at, n) in enumerate(FFN_CHUNKS):
                eng.wait_ge(*g_dve.done(f"g{i}", t))
            for i, (at, n) in enumerate(FFN_CHUNKS):
                last = nc.tensor.matmul(ps[:, 3, :], w.w2[0:n, i, :], w.g[i][0:n].rearrange("p b t -> p (b t)"), start=(i == 0), stop=(i == 2))
            last.then_inc(*g_pe.end("y2"))

        return {"y1": attended, "mean": mean, "var": variance, "rstd": spread,
                "chunk0": lambda: chunk(0), "chunk1": lambda: chunk(1), "chunk2": lambda: chunk(2), "y2": out}

    slots(Slot(eng, attention), unit)





def constants():
    f = np.float32
    pos, feat = np.arange(S, dtype=f)[:, None], np.arange(D)
    freq = (f(1) / np.power(f(0.0001), f(2) * np.arange(2, dtype=f) / f(4)).astype(f)).astype(f)
    ang = (pos * freq[(feat % 4) // 2][None, :]).astype(f)
    sign = np.where(feat % 2 == 0, f(-1), f(1))[None, :]
    turn = np.stack([np.cos(ang), np.sin(ang) * sign]).astype(f)
    rope = np.stack([turn * f(0.5), turn])
    rope = rope.reshape(2, 2, QT, P, D).transpose(3, 0, 1, 2, 4)
    heads = (np.arange(P)[:, None] // 8 == np.arange(16)[None, :]).astype(f)
    see = lambda i, j: np.where((j <= i) & (j >= i - 32), f(0), f(MASKED))
    p = np.arange(P)[:, None]
    w = np.arange(160)[None, :]
    band = np.stack([see(p, w), see(P + p, 96 + w)], axis=1)
    row = np.arange(P)[:, None]
    pick = ((row % 32 == np.arange(16)[None, :]) & (row < 96)).astype(f).reshape(P, 8, 2)
    pick_head = ((row % 32 == np.arange(32)[None, :]) & (row < 96)).astype(f)

    def spread(hd):
        strip = (0, 2, 3)
        m = np.zeros((2, 32 // hd, P, P), f)
        for j in range(32 // hd):
            for a in range(3):
                for b in range(3):
                    for d in range(hd):
                        for side, part in ((0, a), (1, b)):
                            m[side, j, 32 * strip[part] + j * hd + d, (3 * a + b) * hd + d] = 1
        return np.ascontiguousarray(m.transpose(2, 0, 1, 3))

    sel8 = np.repeat(np.eye(8, dtype=f)[:, :, None], P, axis=2)
    before = (np.arange(P)[:, None] < np.arange(P)[None, :]).astype(f)
    qrows = np.zeros((P, S), f)
    qrows[65] = 1
    krows = np.zeros((2, P), f)
    krows[0, 65], krows[1, 64] = 1, 1
    return {"c_ident": np.eye(P, dtype=f), "c_rope": np.ascontiguousarray(rope), "c_heads": heads,
            "c_band": band.astype(f), "c_bandT": np.ascontiguousarray(see(w, p)).astype(f), "c_pick": pick, "c_pick_head": pick_head, "c_spread8": spread(8), "c_spread4": spread(4), "c_sel8": sel8, "c_before": before, "c_qrows": qrows, "c_krows": krows, "c_rank": np.tile(np.arange(8, 0, -1, dtype=f), (P, 1)),
            **l1_ffn_constants()}


LAYER_1 = ("l1_attn", "l1_xattn")


def program(nc, a, out, stages):
    with ExitStack() as ctx:
        sb = lambda n, s, dt=F32: ctx.enter_context(nc.sbuf_tensor(n, s, dt))
        chip = Chip()
        chip.a = a
        chip.ps = ctx.enter_context(nc.psum_tensor("ps", [P, 8, 512], F32))
        chip.x_tok = sb("x_tok", [P, B, QT, D])
        chip.ctx_tok = sb("ctx_tok", [P, B, CT, D])
        chip.ctxT = sb("ctxT", [P, B, S2])
        chip.ident, chip.ident_b = sb("ident", [P, P]), sb("ident_b", [P, P], BF16)
        chip.ones = sb("ones", [P, 512])
        chip.neghalf, chip.eps = sb("neghalf", [P, S]), sb("eps", [P, 8])
        chip.zeros = sb("zeros", [P, P])
        chip.scratch = sb("scratch", [P, 8])
        chip.w = {}
        chip.initial_loads = [
            (fp(chip.ident), a["c_ident"]),
            (fp(chip.x_tok), a["x"].rearrange("b (t p) d -> p b t d", p=P)),
            (fp(chip.ctx_tok), a["ctx_1024"].rearrange("b (t p) d -> p b t d", p=P)),
        ]
        chip.turned_weights, chip.later_loads = [], []
        layer_0, layer_1 = ExitStack(), ExitStack()
        life = lambda name: 0 if name.startswith(("L0_", "c_qrows", "c_krows")) else 1 if name.startswith(("L1_", "c_rope")) else 2
        for of, stack in ((2, ctx), (1, layer_1), (0, layer_0)):
            add = lambda name, shape, dt=F32: chip.w.__setitem__(name, fp(stack.enter_context(nc.sbuf_tensor(f"w_{name}", list(shape), dt))))
            load = lambda name, src: (chip.initial_loads if name.startswith("L0_attn") else chip.later_loads).append((chip.w[name], src))
            for name, shape in LOADS.items():
                if life(name) == of:
                    add(name, shape)
                    load(name, a[name])
            for name, n in ROWS.items():
                if life(name) == of:
                    add(name, [1, n])
                    flat = a[name] if len(a[name].shape) == 1 else a[name].rearrange("e n -> (e n)")
                    load(name, flat.rearrange("(o n) -> o n", o=1))
            for name in COLS:
                if life(name) == of:
                    add(name, [P, 1])
                    load(name, a[name].rearrange("(d o) -> d o", o=1))
            for name, n in SPREAD.items():
                if life(name) == of:
                    add(name, [P, n])
                    load(name, a[name].partition_broadcast(P))
            for name, n in TURNED.items():
                if life(name) == of:
                    add(name, [P, n, D])
            for name in ("c_rope", "c_heads", "c_sel8", "c_before", "c_rank", "c_qrows", "c_krows"):
                if life(name) == of:
                    add(name, a[name].shape)
                    load(name, a[name])
            if of == 2:
                add("L2_ffn_b1", [P, 32])
                add("L2_attn_Wp", [P, 8])
                for head in range(16):
                    chip.later_loads.append((chip.w["L2_attn_Wp"][8 * head:8 * head + 8, :], a["L2_attn_Wp"]))
            if of == 0:
                add("L0_xattn_w_out", [P, 4, D])
                load("L0_xattn_w_out", a["L0_xattn_w_out"].rearrange("(c p) d -> p c d", p=P))
                add("L0_attn_mask", [P, QT, S], I32)
                load("L0_attn_mask", a["L0_attn_mask"][0, 0, :, :].rearrange("(t p) k -> p t k", p=P))
        with ExitStack() as stay:
            for name, n in TURNED.items():
                raw = stay.enter_context(nc.sbuf_tensor(f"raw_{name}", [P, n, D], F32))
                src = {"L0_ffn_We": "e o i -> o e i"}.get(name)
                chip.initial_loads.append((fp(raw), a[name].rearrange(src) if src else
                                           a[name].rearrange("o (c i) -> o c i", i=D)))
                chip.turned_weights += [(chip.w[name][:, c, :], raw[:, c, :]) for c in range(n)]
            raw = stay.enter_context(nc.sbuf_tensor("raw_b1", [32, D], F32))
            chip.initial_loads.append((fp(raw), a["L2_ffn_b1"].rearrange("e (c p) -> (e c) p", p=P)))
            chip.turned_weights.append((chip.w["L2_ffn_b1"], fp(raw)))
            setup(nc, chip, a)
            context_stage(nc, chip)
        chip.later_loaded = ctx.enter_context(nc.semaphore("later_loaded"))
        for stage in stages:
            if not stage.__name__.startswith("l0"):
                layer_0.close()
            if stage.__name__ not in LAYER_1 and not stage.__name__.startswith("l0"):
                layer_1.close()
            stage(nc, chip)
        layer_0.close()
        layer_1.close()
        stored = ctx.enter_context(nc.semaphore("stored"))
        with nc.Block() as block:
            @block.sync
            def _(sp):
                sp.dma_start(out.rearrange("b (t p) d -> p b t d", p=P), fp(chip.x_tok)).then_inc(stored, 16)
                sp.wait_ge(stored, 16)


def kernel(**inputs):
    import concourse.bacc as bacc
    from concourse.bass_utils import run_bass_kernel_spmd

    nc = bacc.Bacc("TRN2", target_bir_lowering=False, num_devices=1)
    arrays, aps = {}, {}
    for name, value in list(inputs.items()) + list(constants().items()):
        v = np.ascontiguousarray(value)
        if v.dtype == np.bool_:
            v = v.view(np.uint8)
        arrays[f"in_{name}"] = v
        shape = v.shape if v.shape else (1,)
        arrays[f"in_{name}"] = v.reshape(shape)
        aps[name] = nc.dram_tensor(f"in_{name}", shape, mybir.dt.from_np(v.dtype), kind="ExternalInput").ap()
    out = nc.dram_tensor("out_0", (B, S, D), F32, kind="ExternalOutput").ap()
    program(nc, aps, out, STAGES)
    r = run_bass_kernel_spmd(nc, [arrays], core_ids=[0])
    return r.results[0]["out_0"]
STAGES = [l0_attn, l0_xattn, l0_ffn, l1_attn, l1_xattn, l1_ffn, l2_attn, l2_xattn, l2_ffn, l3_attn, l3_xattn, l3_ffn]
```
